# Optimizing a Trainium2 kernel written in Bass

```python
import numpy as np
import jax
import jax.numpy as jnp

def _softmax(x, axis=-1):
    return jax.nn.softmax(x, axis=axis)

def _gelu(x):
    return jax.nn.gelu(x, approximate=True)

def _silu(x):
    return jax.nn.silu(x)

def _sigmoid(x):
    return jax.nn.sigmoid(x)

def _layernorm(x, axis=-1, eps=1e-05):
    m = jnp.mean(x, axis=axis, keepdims=True)
    v = jnp.var(x, axis=axis, keepdims=True)
    return (x - m) / jnp.sqrt(v + eps)

def _scatter_add(tgt, idx, src, axis=0):
    return tgt.at[idx].add(src)

def _segment_sum(src, seg, n):
    return jax.ops.segment_sum(src, seg, n)
kernel_name = 'mk_gps_d4_gnn_r8_85bdfe'

def setup_inputs(seed: int=0):
    np.random.seed(seed)
    _w = jnp.asarray

    def _rec_inputs():
        import jax
        import jax.numpy as jnp
        _gk = jax.random.key(seed)
        x = -0.0005207 + 1.001 * jax.random.normal(jax.random.fold_in(_gk, 1), (512, 512), jnp.float32)
        src = jax.random.randint(jax.random.fold_in(_gk, 2), (16384,), 0, 512, jnp.int32)
        dst = jnp.minimum((512 * jax.random.uniform(jax.random.fold_in(_gk, 3), (16384,)) ** 2.0).astype(jnp.int32), 4095)
        _o = jnp.argsort(dst, stable=True)
        src = src[_o]
        dst = dst[_o]
        edge_attr_4 = 0.00171547 + 0.999346 * jax.random.normal(jax.random.fold_in(_gk, 12), (16384, 4), jnp.float32)
        edge_attr_8 = 0.000126197 + 0.999763 * jax.random.normal(jax.random.fold_in(_gk, 13), (16384, 8), jnp.float32)
        return (x, src, dst, edge_attr_4, edge_attr_8)
    x, src, dst, edge_attr_4, edge_attr_8 = _rec_inputs()

    def _L0_gnn_setup():
        import jax, jax.numpy as jnp
        import numpy as np
        import math
        N, IN_DIM, OUT_DIM, H = (512, 512, 512, 8)
        HD = OUT_DIM // H
        E_RAND = 32 * N
        key = jax.random.key(seed)
        ks = jax.random.split(key, 12)
        x = jax.random.normal(ks[0], (N, IN_DIM), dtype=jnp.float32)
        src = jax.random.randint(ks[1], (E_RAND,), 0, N)
        dst = jax.random.randint(ks[2], (E_RAND,), 0, N)
        loops = jnp.arange(N)
        edge_index = jnp.stack([jnp.concatenate([src, loops]), jnp.concatenate([dst, loops])]).astype(jnp.int64)
        s = 1.0 / math.sqrt(IN_DIM)

        def lin(k):
            k1, k2 = jax.random.split(k)
            return (jax.random.uniform(k1, (OUT_DIM, IN_DIM), minval=-s, maxval=s), jax.random.uniform(k2, (OUT_DIM,), minval=-s, maxval=s))
        W_q, b_q = lin(ks[3])
        W_k, b_k = lin(ks[4])
        W_v, b_v = lin(ks[5])
        W_o, b_o = lin(ks[6])
        W_e, b_e = lin(ks[7])
        edge_emb = jax.random.normal(ks[8], (HD,)) / math.sqrt(HD)
        edge_attn = jax.random.normal(ks[9], (H, HD)) / math.sqrt(HD)
        ln_g = jnp.ones((OUT_DIM,), jnp.float32)
        ln_b = jnp.zeros((OUT_DIM,), jnp.float32)
        return dict(x=x, edge_index=edge_index, W_q=W_q, b_q=b_q, W_k=W_k, b_k=b_k, W_v=W_v, b_v=b_v, W_e=W_e, b_e=b_e, W_o=W_o, b_o=b_o, edge_emb=edge_emb, edge_attn=edge_attn, ln_g=ln_g, ln_b=ln_b)
    _L0_gnn_all = _L0_gnn_setup()
    _L0_gnn_in = {k: v for k, v in _L0_gnn_all.items() if k in ('W_q', 'b_q', 'W_k', 'b_k', 'W_v', 'b_v', 'W_e', 'b_e', 'W_o', 'b_o', 'edge_emb', 'edge_attn', 'ln_g', 'ln_b')}
    del _L0_gnn_all

    def _L0_mix_setup():
        import jax, jax.numpy as jnp
        import numpy as np
        N_HEADS = 8
        N_LANDMARKS = 256
        PINV_ITERS = 6

        def moore_penrose_iter_pinv(x, iters=PINV_ITERS):
            abs_x = jnp.abs(x)
            col = abs_x.sum(axis=-1)
            row = abs_x.sum(axis=-2)
            z = jnp.swapaxes(x, -1, -2) / (jnp.max(col) * jnp.max(row))
            m = x.shape[-1]
            Id = jnp.eye(m, dtype=x.dtype)
            for _ in range(iters):
                xz = x @ z
                z = 0.25 * z @ (13.0 * Id - xz @ (15.0 * Id - xz @ (7.0 * Id - xz)))
            return z
        key = jax.random.key(seed)
        k1, k2 = jax.random.split(key)
        B, S, D = (4, 512, 512)
        x = jax.random.normal(k1, (B, S, D), dtype=jnp.float32)
        Wqkv = jax.random.normal(k2, (D, 3 * D), dtype=jnp.float32) * D ** (-0.5)
        return {'x': x, 'Wqkv': Wqkv}
    _L0_mix_all = _L0_mix_setup()
    _L0_mix_in = {k: v for k, v in _L0_mix_all.items() if k in ('Wqkv',)}
    del _L0_mix_all

    def _L0_ffn_setup():
        import jax, jax.numpy as jnp
        import numpy as np
        D_MODEL = 512
        NUM_EXPERTS = 8
        TOP_K = 2
        FFN_MULT = 2
        HIDDEN = FFN_MULT * D_MODEL
        BATCH, SEQ = (4, 256)
        key = jax.random.key(seed)
        k_x, k_g, k_bg, k_w1, k_w3, k_w2 = jax.random.split(key, 6)
        sd = 1.0 / np.sqrt(D_MODEL).astype(np.float32)
        sh = 1.0 / np.sqrt(HIDDEN).astype(np.float32)
        return {'x': jax.random.normal(k_x, (BATCH, SEQ, D_MODEL), dtype=jnp.float32), 'Wg': jax.random.normal(k_g, (D_MODEL, NUM_EXPERTS), dtype=jnp.float32) * sd, 'bg': jax.random.normal(k_bg, (NUM_EXPERTS,), dtype=jnp.float32) * 0.01, 'W1': jax.random.normal(k_w1, (NUM_EXPERTS, D_MODEL, HIDDEN), dtype=jnp.float32) * sd, 'W3': jax.random.normal(k_w3, (NUM_EXPERTS, D_MODEL, HIDDEN), dtype=jnp.float32) * sd, 'W2': jax.random.normal(k_w2, (NUM_EXPERTS, HIDDEN, D_MODEL), dtype=jnp.float32) * sh}
    _L0_ffn_all = _L0_ffn_setup()
    _L0_ffn_in = {k: v for k, v in _L0_ffn_all.items() if k in ('Wg', 'bg', 'W1', 'W3', 'W2')}
    del _L0_ffn_all

    def _L1_gnn_setup():
        import jax, jax.numpy as jnp
        import numpy as np
        N_NODES = 1250
        N_EDGES = 20000
        D_IN = 512
        D_OUT = 512
        key = jax.random.key(seed)
        k1, k2, k3, k4, k5 = jax.random.split(key, 5)
        feature = jax.random.normal(k1, (N_NODES, D_IN), dtype=jnp.float32)
        src = jax.random.randint(k2, (N_EDGES,), 0, N_NODES, dtype=jnp.int64)
        dst = jax.random.randint(k3, (N_EDGES,), 0, N_NODES, dtype=jnp.int64)
        W = jax.random.normal(k4, (2 * D_IN, D_OUT), dtype=jnp.float32) * (1.0 / np.sqrt(2 * D_IN))
        b = jax.random.normal(k5, (D_OUT,), dtype=jnp.float32) * 0.01
        return {'feature': feature, 'src': src, 'dst': dst, 'W': W, 'b': b}
    _L1_gnn_all = _L1_gnn_setup()
    _L1_gnn_in = {k: v for k, v in _L1_gnn_all.items() if k in ('W', 'b')}
    del _L1_gnn_all

    def _L1_mix_setup():
        import jax, jax.numpy as jnp
        import numpy as np
        DIM = 512
        NUM_HEADS = 8
        HEAD_DIM = DIM // NUM_HEADS
        EPS = 1e-06

        def _feature_map(x):
            return jax.nn.elu(x) + 1.0
        key = jax.random.key(seed)
        k_x, k_qkv, k_out, k_b = jax.random.split(key, 4)
        B, N = (8, 512)
        x = jax.random.normal(k_x, (B, N, DIM), dtype=jnp.float32)
        s_qkv = 1.0 / np.sqrt(DIM)
        W_qkv = jax.random.uniform(k_qkv, (DIM, 3 * DIM), minval=-s_qkv, maxval=s_qkv, dtype=jnp.float32)
        W_out = jax.random.uniform(k_out, (DIM, DIM), minval=-s_qkv, maxval=s_qkv, dtype=jnp.float32)
        b_out = jax.random.uniform(k_b, (DIM,), minval=-s_qkv, maxval=s_qkv, dtype=jnp.float32)
        return {'x': x, 'W_qkv': W_qkv, 'W_out': W_out, 'b_out': b_out}
    _L1_mix_all = _L1_mix_setup()
    _L1_mix_in = {k: v for k, v in _L1_mix_all.items() if k in ('W_qkv', 'W_out', 'b_out')}
    del _L1_mix_all

    def _L1_ffn_setup():
        import jax, jax.numpy as jnp
        import numpy as np
        DIM = 512
        HID = 1024
        E = 8
        K = 2
        B, S = (4, 256)
        key = jax.random.key(seed)
        ks = jax.random.split(key, 10)
        sd = DIM ** (-0.5)
        sh = HID ** (-0.5)
        return {'x': jax.random.normal(ks[0], (B, S, DIM), dtype=jnp.float32), 'gate_w': jax.random.normal(ks[1], (E, DIM), dtype=jnp.float32) * sd, 'biases': jnp.zeros((E,), dtype=jnp.float32), 'w1': jax.random.normal(ks[2], (E, DIM, HID), dtype=jnp.float32) * sd, 'w3': jax.random.normal(ks[3], (E, DIM, HID), dtype=jnp.float32) * sd, 'w2': jax.random.normal(ks[4], (E, HID, DIM), dtype=jnp.float32) * sh, 'sw1': jax.random.normal(ks[5], (DIM, HID), dtype=jnp.float32) * sd, 'sw3': jax.random.normal(ks[6], (DIM, HID), dtype=jnp.float32) * sd, 'sw2': jax.random.normal(ks[7], (HID, DIM), dtype=jnp.float32) * sh}
    _L1_ffn_all = _L1_ffn_setup()
    _L1_ffn_in = {k: v for k, v in _L1_ffn_all.items() if k in ('gate_w', 'biases', 'w1', 'w3', 'w2', 'sw1', 'sw3', 'sw2')}
    del _L1_ffn_all

    def _L2_gnn_setup():
        import jax, jax.numpy as jnp
        import numpy as np
        N, IN_DIM, OUT_DIM, H = (1024, 512, 512, 4)
        E = 16384
        HC = H * OUT_DIM
        key = jax.random.key(seed)
        ks = jax.random.split(key, 12)
        s = 1.0 / np.sqrt(IN_DIM)
        return {'x': jax.random.normal(ks[0], (N, IN_DIM), dtype=jnp.float32), 'edge_index': jax.random.randint(ks[1], (2, E), 0, N, dtype=jnp.int64), 'Wq': jax.random.normal(ks[2], (IN_DIM, HC), dtype=jnp.float32) * s, 'bq': jnp.zeros((HC,), dtype=jnp.float32), 'Wk': jax.random.normal(ks[3], (IN_DIM, HC), dtype=jnp.float32) * s, 'bk': jnp.zeros((HC,), dtype=jnp.float32), 'Wv': jax.random.normal(ks[4], (IN_DIM, HC), dtype=jnp.float32) * s, 'bv': jnp.zeros((HC,), dtype=jnp.float32), 'Wskip': jax.random.normal(ks[5], (IN_DIM, HC), dtype=jnp.float32) * s, 'bskip': jnp.zeros((HC,), dtype=jnp.float32), 'Wlin': jax.random.normal(ks[6], (HC, OUT_DIM), dtype=jnp.float32) / np.sqrt(HC), 'blin': jnp.zeros((OUT_DIM,), dtype=jnp.float32), 'gamma': jnp.ones((OUT_DIM,), dtype=jnp.float32), 'beta': jnp.zeros((OUT_DIM,), dtype=jnp.float32)}
    _L2_gnn_all = _L2_gnn_setup()
    _L2_gnn_in = {k: v for k, v in _L2_gnn_all.items() if k in ('Wq', 'bq', 'Wk', 'bk', 'Wv', 'bv', 'Wskip', 'bskip', 'Wlin', 'blin', 'gamma', 'beta')}
    del _L2_gnn_all

    def _L2_mix_setup():
        import jax, jax.numpy as jnp
        import numpy as np
        HEADS = 8
        EPS_LN = 1e-05
        EPS_NORM = 1e-08
        key = jax.random.key(seed)
        ks = jax.random.split(key, 3)
        B, N, C = (4, 1024, 512)
        x = jax.random.normal(ks[0], (B, N, C), dtype=jnp.float32)
        qkv_w = jax.random.normal(ks[1], (3 * C, C), dtype=jnp.float32) / np.sqrt(C)
        qkv_b = jnp.zeros((3 * C,), dtype=jnp.float32)
        out_w = jax.random.normal(ks[2], (C, C), dtype=jnp.float32) / np.sqrt(C)
        out_b = jnp.zeros((C,), dtype=jnp.float32)
        ln_gamma = jnp.ones((C,), dtype=jnp.float32)
        ln_beta = jnp.zeros((C,), dtype=jnp.float32)
        return {'x': x, 'qkv_w': qkv_w, 'qkv_b': qkv_b, 'out_w': out_w, 'out_b': out_b, 'ln_gamma': ln_gamma, 'ln_beta': ln_beta}
    _L2_mix_all = _L2_mix_setup()
    _L2_mix_in = {k: v for k, v in _L2_mix_all.items() if k in ('qkv_w', 'qkv_b', 'out_w', 'out_b', 'ln_gamma', 'ln_beta')}
    del _L2_mix_all

    def _L2_ffn_setup():
        import jax, jax.numpy as jnp
        import numpy as np
        MIN_EXPERT_CAPACITY = 4
        EPS = 1e-09
        CAPACITY_FACTOR = 2.0

        def cumsum_exclusive(t, axis):
            return jnp.cumsum(t, axis=axis) - t

        def safe_one_hot(idx, depth):
            return jax.nn.one_hot(idx, depth + 1)[..., :depth]

        def top2_gating(x, w_gating):
            b, n, d = x.shape
            e = w_gating.shape[-1]
            raw_gates = jax.nn.softmax(jnp.einsum('bnd,de->bne', x, w_gating), axis=-1)
            gate_1 = jnp.max(raw_gates, axis=-1)
            index_1 = jnp.argmax(raw_gates, axis=-1)
            mask_1 = jax.nn.one_hot(index_1, e, dtype=raw_gates.dtype)
            gates_without_top1 = raw_gates * (1.0 - mask_1)
            gate_2 = jnp.max(gates_without_top1, axis=-1)
            index_2 = jnp.argmax(gates_without_top1, axis=-1)
            mask_2 = jax.nn.one_hot(index_2, e, dtype=raw_gates.dtype)
            denom = gate_1 + gate_2 + EPS
            gate_1 = gate_1 / denom
            gate_2 = gate_2 / denom
            density_1 = jnp.mean(mask_1, axis=-2)
            density_1_proxy = jnp.mean(raw_gates, axis=-2)
            loss = jnp.mean(density_1_proxy * density_1) * float(e * e)
            capacity = max(min(n, int(n * 2 * CAPACITY_FACTOR / e)), MIN_EXPERT_CAPACITY)
            cap_f = float(capacity)
            pos1 = cumsum_exclusive(mask_1, axis=-2) * mask_1
            mask_1 = mask_1 * (pos1 < cap_f).astype(mask_1.dtype)
            mask_1_count = jnp.sum(mask_1, axis=-2, keepdims=True)
            mask_1_flat = jnp.sum(mask_1, axis=-1)
            pos1 = jnp.sum(pos1, axis=-1)
            gate_1 = gate_1 * mask_1_flat
            pos2 = (cumsum_exclusive(mask_2, axis=-2) + mask_1_count) * mask_2
            mask_2 = mask_2 * (pos2 < cap_f).astype(mask_2.dtype)
            mask_2_flat = jnp.sum(mask_2, axis=-1)
            pos2 = jnp.sum(pos2, axis=-1)
            gate_2 = gate_2 * mask_2_flat
            combine = gate_1[..., None, None] * mask_1_flat[..., None, None] * jax.nn.one_hot(index_1, e, dtype=x.dtype)[..., None] * safe_one_hot(pos1.astype(jnp.int32), capacity)[..., None, :] + gate_2[..., None, None] * mask_2_flat[..., None, None] * jax.nn.one_hot(index_2, e, dtype=x.dtype)[..., None] * safe_one_hot(pos2.astype(jnp.int32), capacity)[..., None, :]
            dispatch = (combine > 0).astype(combine.dtype)
            return (dispatch, combine, loss)
        key = jax.random.key(seed)
        k_x, k_g, k_w1, k_w2 = jax.random.split(key, 4)
        b, n, d, e, h = (2, 512, 512, 16, 256)
        x = jax.random.normal(k_x, (b, n, d), dtype=jnp.float32)
        w_gating = jax.random.normal(k_g, (d, e), dtype=jnp.float32) / np.sqrt(d)
        w1 = jax.random.normal(k_w1, (e, d, h), dtype=jnp.float32) / np.sqrt(d)
        w2 = jax.random.normal(k_w2, (e, h, d), dtype=jnp.float32) / np.sqrt(h)
        return {'x': x, 'w_gating': w_gating, 'w1': w1, 'w2': w2}
    _L2_ffn_all = _L2_ffn_setup()
    _L2_ffn_in = {k: v for k, v in _L2_ffn_all.items() if k in ('w_gating', 'w1', 'w2')}
    del _L2_ffn_all

    def _L3_gnn_setup():
        import jax, jax.numpy as jnp
        import numpy as np
        MUL = 128
        N_NODES = 1250
        N_EDGES = 20000
        R_BASIS = 8
        HIDDEN = 64
        W_NUMEL = 4 * MUL
        SQRT3 = 3.0 ** 0.5
        SILU_2MOM = 1.679177
        AVG_NUM_NEIGHBORS = 10.0

        def _lin_irreps(x0, x1, W0, W1):
            y0 = x0 @ W0 / jnp.sqrt(jnp.float32(W0.shape[0]))
            y1 = jnp.einsum('num,uv->nvm', x1, W1) / jnp.sqrt(jnp.float32(W1.shape[0]))
            return (y0, y1)

        def _forward(node_feats, edge_attrs, edge_feats, edge_index, W_up0, W_up1, W_mlp1, W_mlp2, W_mlp3, W_mlp4, W_out0, W_out1):
            num_nodes = node_feats.shape[0]
            sender, receiver = (edge_index[0], edge_index[1])
            x0 = node_feats[:, :MUL]
            x1 = node_feats[:, MUL:].reshape(num_nodes, MUL, 3)
            x0, x1 = _lin_irreps(x0, x1, W_up0, W_up1)
            h = edge_feats
            for W in (W_mlp1, W_mlp2, W_mlp3):
                h = SILU_2MOM * jax.nn.silu(h @ W / jnp.sqrt(jnp.float32(W.shape[0])))
            tpw = h @ W_mlp4 / jnp.sqrt(jnp.float32(W_mlp4.shape[0]))
            w1, w2, w3, w4 = jnp.split(tpw, 4, axis=-1)
            s0 = x0[sender]
            s1 = x1[sender]
            y0 = edge_attrs[:, 0:1]
            y1 = edge_attrs[:, 1:4]
            p1 = w1 * s0 * y0
            p2 = (w2 * s0)[:, :, None] * y1[:, None, :]
            p3 = w3[:, :, None] * s1 * y0[:, None, :]
            p4 = w4 * jnp.einsum('eum,em->eu', s1, y1) / SQRT3
            m0 = jnp.concatenate([p1, p4], axis=-1)
            m1 = jnp.concatenate([p2, p3], axis=1)
            msg0 = jax.ops.segment_sum(m0, receiver, num_segments=num_nodes)
            msg1 = jax.ops.segment_sum(m1, receiver, num_segments=num_nodes)
            o0, o1 = _lin_irreps(msg0, msg1, W_out0, W_out1)
            out = jnp.concatenate([o0, o1.reshape(num_nodes, 3 * MUL)], axis=-1)
            return out / AVG_NUM_NEIGHBORS
        key = jax.random.key(seed)
        ks = jax.random.split(key, 12)
        rn = lambda k, s: jax.random.normal(k, s, dtype=jnp.float32)
        return {'node_feats': rn(ks[0], (N_NODES, 4 * MUL)), 'edge_attrs': rn(ks[1], (N_EDGES, 4)), 'edge_feats': rn(ks[2], (N_EDGES, R_BASIS)), 'edge_index': jax.random.randint(ks[3], (2, N_EDGES), 0, N_NODES), 'W_up0': rn(ks[4], (MUL, MUL)), 'W_up1': rn(ks[5], (MUL, MUL)), 'W_mlp1': rn(ks[6], (R_BASIS, HIDDEN)), 'W_mlp2': rn(ks[7], (HIDDEN, HIDDEN)), 'W_mlp3': rn(ks[8], (HIDDEN, HIDDEN)), 'W_mlp4': rn(ks[9], (HIDDEN, W_NUMEL)), 'W_out0': rn(ks[10], (2 * MUL, MUL)), 'W_out1': rn(ks[11], (2 * MUL, MUL))}
    _L3_gnn_all = _L3_gnn_setup()
    _L3_gnn_in = {k: v for k, v in _L3_gnn_all.items() if k in ('W_up0', 'W_up1', 'W_mlp1', 'W_mlp2', 'W_mlp3', 'W_mlp4', 'W_out0', 'W_out1')}
    del _L3_gnn_all

    def _L3_mix_setup():
        import jax, jax.numpy as jnp
        import numpy as np
        EPS = 1e-06
        H = 8
        DH = 64
        LN_EPS = 1e-05

        def _layernorm(x, g, b):
            m = jnp.mean(x, axis=-1, keepdims=True)
            v = jnp.mean(jnp.square(x - m), axis=-1, keepdims=True)
            return (x - m) / jnp.sqrt(v + LN_EPS) * g + b

        def _flow_attention(x, Wq, bq, Wk, bk, Wv, bv, Wo, bo):
            B, L, D = x.shape
            S = L
            q = jax.nn.sigmoid((x @ Wq + bq).reshape(B, L, H, DH).transpose(0, 2, 1, 3))
            k = jax.nn.sigmoid((x @ Wk + bk).reshape(B, S, H, DH).transpose(0, 2, 1, 3))
            v = (x @ Wv + bv).reshape(B, S, H, DH).transpose(0, 2, 1, 3)
            sink_incoming = 1.0 / jnp.einsum('nhld,nhd->nhl', q + EPS, k.sum(axis=2) + EPS)
            source_outgoing = 1.0 / jnp.einsum('nhld,nhd->nhl', k + EPS, q.sum(axis=2) + EPS)
            conserved_sink = jnp.einsum('nhld,nhd->nhl', q + EPS, (k * source_outgoing[..., None]).sum(axis=2) + EPS)
            conserved_source = jnp.einsum('nhld,nhd->nhl', k + EPS, (q * sink_incoming[..., None]).sum(axis=2) + EPS)
            conserved_source = jnp.clip(conserved_source, -1.0, 1.0)
            sink_allocation = jax.nn.sigmoid(conserved_sink * (float(L) / float(S)))
            source_competition = jax.nn.softmax(conserved_source, axis=-1) * float(S)
            kv = jnp.einsum('nhld,nhlm->nhdm', k, v * source_competition[..., None])
            o = jnp.einsum('nhld,nhdm->nhlm', q * sink_incoming[..., None], kv)
            o = o * sink_allocation[..., None]
            o = o.transpose(0, 2, 1, 3).reshape(B, L, D)
            return o @ Wo + bo
        key = jax.random.key(seed)
        ks = jax.random.split(key, 16)
        B, L, D, F = (2, 2048, 512, 256)
        s = 0.02
        inp = {'x': jax.random.normal(ks[0], (B, L, D), dtype=jnp.float32), 'Wq': jax.random.normal(ks[1], (D, D), dtype=jnp.float32) * s, 'bq': jnp.zeros((D,), jnp.float32), 'Wk': jax.random.normal(ks[2], (D, D), dtype=jnp.float32) * s, 'bk': jnp.zeros((D,), jnp.float32), 'Wv': jax.random.normal(ks[3], (D, D), dtype=jnp.float32) * s, 'bv': jnp.zeros((D,), jnp.float32), 'Wo': jax.random.normal(ks[4], (D, D), dtype=jnp.float32) * s, 'bo': jnp.zeros((D,), jnp.float32), 'W1': jax.random.normal(ks[5], (D, F), dtype=jnp.float32) * s, 'b1': jnp.zeros((F,), jnp.float32), 'W2': jax.random.normal(ks[6], (F, D), dtype=jnp.float32) * s, 'b2': jnp.zeros((D,), jnp.float32), 'g1': jnp.ones((D,), jnp.float32), 'be1': jnp.zeros((D,), jnp.float32), 'g2': jnp.ones((D,), jnp.float32), 'be2': jnp.zeros((D,), jnp.float32)}
        return inp
    _L3_mix_all = _L3_mix_setup()
    _L3_mix_in = {k: v for k, v in _L3_mix_all.items() if k in ('Wq', 'bq', 'Wk', 'bk', 'Wv', 'bv', 'Wo', 'bo', 'W1', 'b1', 'W2', 'b2', 'g1', 'be1', 'g2', 'be2')}
    del _L3_mix_all

    def _L3_ffn_setup():
        import jax, jax.numpy as jnp
        import numpy as np
        K_INPUT, K_PROCESS, K_OUTPUT = (256, 128, 256)

        def _gelu(x):
            return jax.nn.gelu(x, approximate=False)
        key = jax.random.key(seed)
        ks = jax.random.split(key, 6)
        d_model, n_in, n_proc, n_out, d_pv = (512, 256, 1024, 256, 256)
        B, S = (2, 1024)

        def xavier(k, shape):
            std = (2.0 / (shape[0] + shape[1])) ** 0.5
            return jax.random.normal(k, shape, dtype=jnp.float32) * std
        return {'x': jax.random.normal(ks[0], (B, S, d_model), dtype=jnp.float32), 'input_patterns': xavier(ks[1], (n_in, d_model)), 'process_input_weights': xavier(ks[2], (n_proc, n_in)), 'process_values': xavier(ks[3], (n_proc, d_pv)), 'output_input_weights': xavier(ks[4], (n_out, d_pv)), 'output_patterns': xavier(ks[5], (n_out, d_model))}
    _L3_ffn_all = _L3_ffn_setup()
    _L3_ffn_in = {k: v for k, v in _L3_ffn_all.items() if k in ('input_patterns', 'process_input_weights', 'process_values', 'output_input_weights', 'output_patterns')}
    del _L3_ffn_all
    return {'x': x, 'src': src, 'dst': dst, 'edge_attr_4': edge_attr_4, 'edge_attr_8': edge_attr_8, 'L0_gnn_W_q': _L0_gnn_in['W_q'], 'L0_gnn_b_q': _L0_gnn_in['b_q'], 'L0_gnn_W_k': _L0_gnn_in['W_k'], 'L0_gnn_b_k': _L0_gnn_in['b_k'], 'L0_gnn_W_v': _L0_gnn_in['W_v'], 'L0_gnn_b_v': _L0_gnn_in['b_v'], 'L0_gnn_W_e': _L0_gnn_in['W_e'], 'L0_gnn_b_e': _L0_gnn_in['b_e'], 'L0_gnn_W_o': _L0_gnn_in['W_o'], 'L0_gnn_b_o': _L0_gnn_in['b_o'], 'L0_gnn_edge_emb': _L0_gnn_in['edge_emb'], 'L0_gnn_edge_attn': _L0_gnn_in['edge_attn'], 'L0_gnn_ln_g': _L0_gnn_in['ln_g'], 'L0_gnn_ln_b': _L0_gnn_in['ln_b'], 'L0_mix_Wqkv': _L0_mix_in['Wqkv'], 'L0_ffn_Wg': _L0_ffn_in['Wg'], 'L0_ffn_bg': _L0_ffn_in['bg'], 'L0_ffn_W1': _L0_ffn_in['W1'], 'L0_ffn_W3': _L0_ffn_in['W3'], 'L0_ffn_W2': _L0_ffn_in['W2'], 'L1_gnn_W': _L1_gnn_in['W'], 'L1_gnn_b': _L1_gnn_in['b'], 'L1_mix_W_qkv': _L1_mix_in['W_qkv'], 'L1_mix_W_out': _L1_mix_in['W_out'], 'L1_mix_b_out': _L1_mix_in['b_out'], 'L1_ffn_gate_w': _L1_ffn_in['gate_w'], 'L1_ffn_biases': _L1_ffn_in['biases'], 'L1_ffn_w1': _L1_ffn_in['w1'], 'L1_ffn_w3': _L1_ffn_in['w3'], 'L1_ffn_w2': _L1_ffn_in['w2'], 'L1_ffn_sw1': _L1_ffn_in['sw1'], 'L1_ffn_sw3': _L1_ffn_in['sw3'], 'L1_ffn_sw2': _L1_ffn_in['sw2'], 'L2_gnn_Wq': _L2_gnn_in['Wq'], 'L2_gnn_bq': _L2_gnn_in['bq'], 'L2_gnn_Wk': _L2_gnn_in['Wk'], 'L2_gnn_bk': _L2_gnn_in['bk'], 'L2_gnn_Wv': _L2_gnn_in['Wv'], 'L2_gnn_bv': _L2_gnn_in['bv'], 'L2_gnn_Wskip': _L2_gnn_in['Wskip'], 'L2_gnn_bskip': _L2_gnn_in['bskip'], 'L2_gnn_Wlin': _L2_gnn_in['Wlin'], 'L2_gnn_blin': _L2_gnn_in['blin'], 'L2_gnn_gamma': _L2_gnn_in['gamma'], 'L2_gnn_beta': _L2_gnn_in['beta'], 'L2_mix_qkv_w': _L2_mix_in['qkv_w'], 'L2_mix_qkv_b': _L2_mix_in['qkv_b'], 'L2_mix_out_w': _L2_mix_in['out_w'], 'L2_mix_out_b': _L2_mix_in['out_b'], 'L2_mix_ln_gamma': _L2_mix_in['ln_gamma'], 'L2_mix_ln_beta': _L2_mix_in['ln_beta'], 'L2_ffn_w_gating': _L2_ffn_in['w_gating'], 'L2_ffn_w1': _L2_ffn_in['w1'], 'L2_ffn_w2': _L2_ffn_in['w2'], 'L3_gnn_W_up0': _L3_gnn_in['W_up0'], 'L3_gnn_W_up1': _L3_gnn_in['W_up1'], 'L3_gnn_W_mlp1': _L3_gnn_in['W_mlp1'], 'L3_gnn_W_mlp2': _L3_gnn_in['W_mlp2'], 'L3_gnn_W_mlp3': _L3_gnn_in['W_mlp3'], 'L3_gnn_W_mlp4': _L3_gnn_in['W_mlp4'], 'L3_gnn_W_out0': _L3_gnn_in['W_out0'], 'L3_gnn_W_out1': _L3_gnn_in['W_out1'], 'L3_mix_Wq': _L3_mix_in['Wq'], 'L3_mix_bq': _L3_mix_in['bq'], 'L3_mix_Wk': _L3_mix_in['Wk'], 'L3_mix_bk': _L3_mix_in['bk'], 'L3_mix_Wv': _L3_mix_in['Wv'], 'L3_mix_bv': _L3_mix_in['bv'], 'L3_mix_Wo': _L3_mix_in['Wo'], 'L3_mix_bo': _L3_mix_in['bo'], 'L3_mix_W1': _L3_mix_in['W1'], 'L3_mix_b1': _L3_mix_in['b1'], 'L3_mix_W2': _L3_mix_in['W2'], 'L3_mix_b2': _L3_mix_in['b2'], 'L3_mix_g1': _L3_mix_in['g1'], 'L3_mix_be1': _L3_mix_in['be1'], 'L3_mix_g2': _L3_mix_in['g2'], 'L3_mix_be2': _L3_mix_in['be2'], 'L3_ffn_input_patterns': _L3_ffn_in['input_patterns'], 'L3_ffn_process_input_weights': _L3_ffn_in['process_input_weights'], 'L3_ffn_process_values': _L3_ffn_in['process_values'], 'L3_ffn_output_input_weights': _L3_ffn_in['output_input_weights'], 'L3_ffn_output_patterns': _L3_ffn_in['output_patterns']}

def reference(x, src, dst, edge_attr_4, edge_attr_8, L0_gnn_W_q, L0_gnn_b_q, L0_gnn_W_k, L0_gnn_b_k, L0_gnn_W_v, L0_gnn_b_v, L0_gnn_W_e, L0_gnn_b_e, L0_gnn_W_o, L0_gnn_b_o, L0_gnn_edge_emb, L0_gnn_edge_attn, L0_gnn_ln_g, L0_gnn_ln_b, L0_mix_Wqkv, L0_ffn_Wg, L0_ffn_bg, L0_ffn_W1, L0_ffn_W3, L0_ffn_W2, L1_gnn_W, L1_gnn_b, L1_mix_W_qkv, L1_mix_W_out, L1_mix_b_out, L1_ffn_gate_w, L1_ffn_biases, L1_ffn_w1, L1_ffn_w3, L1_ffn_w2, L1_ffn_sw1, L1_ffn_sw3, L1_ffn_sw2, L2_gnn_Wq, L2_gnn_bq, L2_gnn_Wk, L2_gnn_bk, L2_gnn_Wv, L2_gnn_bv, L2_gnn_Wskip, L2_gnn_bskip, L2_gnn_Wlin, L2_gnn_blin, L2_gnn_gamma, L2_gnn_beta, L2_mix_qkv_w, L2_mix_qkv_b, L2_mix_out_w, L2_mix_out_b, L2_mix_ln_gamma, L2_mix_ln_beta, L2_ffn_w_gating, L2_ffn_w1, L2_ffn_w2, L3_gnn_W_up0, L3_gnn_W_up1, L3_gnn_W_mlp1, L3_gnn_W_mlp2, L3_gnn_W_mlp3, L3_gnn_W_mlp4, L3_gnn_W_out0, L3_gnn_W_out1, L3_mix_Wq, L3_mix_bq, L3_mix_Wk, L3_mix_bk, L3_mix_Wv, L3_mix_bv, L3_mix_Wo, L3_mix_bo, L3_mix_W1, L3_mix_b1, L3_mix_W2, L3_mix_b2, L3_mix_g1, L3_mix_be1, L3_mix_g2, L3_mix_be2, L3_ffn_input_patterns, L3_ffn_process_input_weights, L3_ffn_process_values, L3_ffn_output_input_weights, L3_ffn_output_patterns):
    import jax
    import jax.numpy as jnp

    def _L0_gnn_ref(x, edge_index, W_q, b_q, W_k, b_k, W_v, b_v, W_e, b_e, W_o, b_o, edge_emb, edge_attn, ln_g, ln_b):
        import jax, jax.numpy as jnp
        import numpy as np
        import math
        N, IN_DIM, OUT_DIM, H = (512, 512, 512, 8)
        HD = OUT_DIM // H
        E_RAND = 32 * N
        n = x.shape[0]
        q = (x @ W_q.T + b_q).reshape(n, H, HD)
        k = (x @ W_k.T + b_k).reshape(n, H, HD) + edge_emb
        x_e = (x @ W_e.T + b_e).reshape(n, H, HD)
        v = (x @ W_v.T + b_v).reshape(n, H, HD) + edge_attn[None] * x_e
        scores = jnp.einsum('nhd,mhd->hnm', q, k) / math.sqrt(HD)
        mask = jnp.zeros((n, n), jnp.float32).at[edge_index[0], edge_index[1]].set(1.0)
        scores = jnp.where(mask[None] > 0, scores, -jnp.inf)
        attn = jax.nn.softmax(scores, axis=-1)
        out = jnp.einsum('hnm,mhd->nhd', attn, v).reshape(n, OUT_DIM)
        out = out @ W_o.T + b_o
        out = out + x
        mu = jnp.mean(out, axis=-1, keepdims=True)
        var = jnp.mean(jnp.square(out - mu), axis=-1, keepdims=True)
        return (out - mu) / jnp.sqrt(var + 1e-05) * ln_g + ln_b

    def _L0_mix_ref(x, Wqkv):
        import jax, jax.numpy as jnp
        import numpy as np
        N_HEADS = 8
        N_LANDMARKS = 256
        PINV_ITERS = 6

        def moore_penrose_iter_pinv(x, iters=PINV_ITERS):
            abs_x = jnp.abs(x)
            col = abs_x.sum(axis=-1)
            row = abs_x.sum(axis=-2)
            z = jnp.swapaxes(x, -1, -2) / (jnp.max(col) * jnp.max(row))
            m = x.shape[-1]
            Id = jnp.eye(m, dtype=x.dtype)
            for _ in range(iters):
                xz = x @ z
                z = 0.25 * z @ (13.0 * Id - xz @ (15.0 * Id - xz @ (7.0 * Id - xz)))
            return z
        B, S, D = x.shape
        H = N_HEADS
        hd = D // H
        scale = hd ** (-0.5)
        qkv = x @ Wqkv
        q, k, v = jnp.split(qkv, 3, axis=-1)

        def to_heads(t):
            return t.reshape(B, S, H, hd).transpose(0, 2, 1, 3)
        q, k, v = (to_heads(q), to_heads(k), to_heads(v))
        q = q * scale
        lm = S // N_LANDMARKS
        q_lm = q.reshape(B, H, N_LANDMARKS, lm, hd).sum(axis=3) / lm
        k_lm = k.reshape(B, H, N_LANDMARKS, lm, hd).sum(axis=3) / lm
        sim1 = jnp.einsum('bhid,bhjd->bhij', q, k_lm)
        sim2 = jnp.einsum('bhid,bhjd->bhij', q_lm, k_lm)
        sim3 = jnp.einsum('bhid,bhjd->bhij', q_lm, k)
        attn1 = jax.nn.softmax(sim1, axis=-1)
        attn2 = jax.nn.softmax(sim2, axis=-1)
        attn3 = jax.nn.softmax(sim3, axis=-1)
        attn2_inv = moore_penrose_iter_pinv(attn2, PINV_ITERS)
        out = attn1 @ (attn2_inv @ (attn3 @ v))
        out = out.transpose(0, 2, 1, 3).reshape(B, S, D)
        return out

    def _L0_ffn_ref(x, Wg, bg, W1, W3, W2):
        import jax, jax.numpy as jnp
        import numpy as np
        D_MODEL = 512
        NUM_EXPERTS = 8
        TOP_K = 2
        FFN_MULT = 2
        HIDDEN = FFN_MULT * D_MODEL
        BATCH, SEQ = (4, 256)
        B, S, D = x.shape
        E = Wg.shape[1]
        xt = x.reshape(-1, D)
        T = xt.shape[0]
        logits = xt @ Wg + bg
        top_vals, top_idx = jax.lax.top_k(logits, TOP_K)
        top_probs = jax.nn.softmax(top_vals, axis=-1)
        gate_w = jnp.zeros((T, E), dtype=xt.dtype).at[jnp.arange(T)[:, None], top_idx].add(top_probs)

        def body(y, expert):
            w1, w3, w2, g = expert
            h = jax.nn.silu(xt @ w1) * (xt @ w3)
            return (y + g[:, None] * (h @ w2), None)
        y0 = jnp.zeros_like(xt)
        y, _ = jax.lax.scan(body, y0, (W1, W3, W2, gate_w.T))
        return y.reshape(B, S, D)

    def _L1_gnn_ref(feature, src, dst, W, b):
        import jax, jax.numpy as jnp
        import numpy as np
        N_NODES = 1250
        N_EDGES = 20000
        D_IN = 512
        D_OUT = 512
        n = feature.shape[0]
        neigh = jax.ops.segment_sum(feature[src], dst, num_segments=n)
        degs = jax.ops.segment_sum(jnp.ones_like(dst, dtype=feature.dtype), dst, num_segments=n)
        hk_neigh = neigh / jnp.maximum(degs, 1.0)[:, None]
        hk = jnp.concatenate([feature, hk_neigh], axis=-1) @ W + b
        return jax.nn.relu(hk)

    def _L1_mix_ref(x, W_qkv, W_out, b_out):
        import jax, jax.numpy as jnp
        import numpy as np
        DIM = 512
        NUM_HEADS = 8
        HEAD_DIM = DIM // NUM_HEADS
        EPS = 1e-06

        def _feature_map(x):
            return jax.nn.elu(x) + 1.0
        B, N, C = x.shape
        H, D = (NUM_HEADS, HEAD_DIM)
        qkv = x @ W_qkv
        qkv = qkv.reshape(B, N, 3, H, D).transpose(2, 0, 3, 1, 4)
        q, k, v = (qkv[0], qkv[1], qkv[2])
        q_phi = _feature_map(q)
        k_phi = _feature_map(k)
        KV = jnp.einsum('bhnd,bhne->bhde', k_phi, v)
        K_sum = k_phi.sum(axis=2)
        denom = jnp.einsum('bhnd,bhd->bhn', q_phi, K_sum)[..., None] + EPS
        out = jnp.einsum('bhnd,bhde->bhne', q_phi, KV) / denom
        out = out.transpose(0, 2, 1, 3).reshape(B, N, C)
        return out @ W_out + b_out

    def _L1_ffn_ref(x, gate_w, biases, w1, w3, w2, sw1, sw3, sw2):
        import jax, jax.numpy as jnp
        import numpy as np
        DIM = 512
        HID = 1024
        E = 8
        K = 2
        B, S = (4, 256)
        Bb, Ss, D = x.shape
        xt = x.reshape(Bb * Ss, D)
        shared = jax.nn.silu(xt @ sw1) * (xt @ sw3) @ sw2
        scores = xt @ gate_w.T
        _, idx = jax.lax.top_k(scores + biases, K)
        topv, _ = jax.lax.top_k(scores, K)
        p = jax.nn.sigmoid(topv)
        p = p / jnp.sum(p, axis=-1, keepdims=True)
        h = jax.nn.silu(jnp.einsum('td,edh->eth', xt, w1)) * jnp.einsum('td,edh->eth', xt, w3)
        y = jnp.einsum('eth,ehd->etd', h, w2)
        onehot = jax.nn.one_hot(idx, E, dtype=xt.dtype)
        comb = jnp.einsum('tk,tke->te', p, onehot)
        out = jnp.einsum('te,etd->td', comb, y) + shared
        return out.reshape(Bb, Ss, D)

    def _L2_gnn_ref(x, edge_index, Wq, bq, Wk, bk, Wv, bv, Wskip, bskip, Wlin, blin, gamma, beta):
        import jax, jax.numpy as jnp
        import numpy as np
        N, IN_DIM, OUT_DIM, H = (1024, 512, 512, 4)
        E = 16384
        HC = H * OUT_DIM
        n = x.shape[0]
        src, dst = (edge_index[0], edge_index[1])
        q = (x @ Wq + bq).reshape(n, H, OUT_DIM)
        k = (x @ Wk + bk).reshape(n, H, OUT_DIM)
        v = (x @ Wv + bv).reshape(n, H, OUT_DIM)
        alpha = jnp.einsum('ehc,ehc->eh', q[dst], k[src]) / np.sqrt(OUT_DIM)
        amax = jax.ops.segment_max(alpha, dst, num_segments=n)
        ex = jnp.exp(alpha - amax[dst])
        denom = jax.ops.segment_sum(ex, dst, num_segments=n)
        attn = ex / denom[dst]
        msg = attn[:, :, None] * v[src]
        agg = jax.ops.segment_sum(msg, dst, num_segments=n).reshape(n, HC)
        x_attn = agg + x @ Wskip + bskip
        x_lin = x_attn @ Wlin + blin
        h = x_lin + x_attn[:, :OUT_DIM]
        mu = jnp.mean(h, axis=-1, keepdims=True)
        var = jnp.mean((h - mu) ** 2, axis=-1, keepdims=True)
        return gamma * (h - mu) / jnp.sqrt(var + 1e-05) + beta

    def _L2_mix_ref(x, qkv_w, qkv_b, out_w, out_b, ln_gamma, ln_beta):
        import jax, jax.numpy as jnp
        import numpy as np
        HEADS = 8
        EPS_LN = 1e-05
        EPS_NORM = 1e-08
        B, N, C = x.shape
        h = HEADS
        d = C // h
        residual = x
        mu = jnp.mean(x, axis=-1, keepdims=True)
        var = jnp.var(x, axis=-1, keepdims=True)
        xn = (x - mu) / jnp.sqrt(var + EPS_LN) * ln_gamma + ln_beta
        qkv = xn @ qkv_w.T + qkv_b
        qkv = qkv.reshape(B, N, 3, h, d).transpose(2, 0, 3, 1, 4)
        q, k, v = (qkv[0], qkv[1], qkv[2])
        q = jax.nn.elu(q) + 1.0
        k = jax.nn.elu(k) + 1.0
        kv = jnp.einsum('bhnd,bhne->bhde', k, v)
        k_sum = jnp.sum(k, axis=2)
        out = jnp.einsum('bhnd,bhde->bhne', q, kv)
        normalizer = jnp.einsum('bhnd,bhd->bhn', q, k_sum)
        out = out / (normalizer[..., None] + EPS_NORM)
        out = out.transpose(0, 2, 1, 3).reshape(B, N, C)
        out = out @ out_w.T + out_b
        return out + residual

    def _L2_ffn_ref(x, w_gating, w1, w2):
        import jax, jax.numpy as jnp
        import numpy as np
        MIN_EXPERT_CAPACITY = 4
        EPS = 1e-09
        CAPACITY_FACTOR = 2.0

        def cumsum_exclusive(t, axis):
            return jnp.cumsum(t, axis=axis) - t

        def safe_one_hot(idx, depth):
            return jax.nn.one_hot(idx, depth + 1)[..., :depth]

        def top2_gating(x, w_gating):
            b, n, d = x.shape
            e = w_gating.shape[-1]
            raw_gates = jax.nn.softmax(jnp.einsum('bnd,de->bne', x, w_gating), axis=-1)
            gate_1 = jnp.max(raw_gates, axis=-1)
            index_1 = jnp.argmax(raw_gates, axis=-1)
            mask_1 = jax.nn.one_hot(index_1, e, dtype=raw_gates.dtype)
            gates_without_top1 = raw_gates * (1.0 - mask_1)
            gate_2 = jnp.max(gates_without_top1, axis=-1)
            index_2 = jnp.argmax(gates_without_top1, axis=-1)
            mask_2 = jax.nn.one_hot(index_2, e, dtype=raw_gates.dtype)
            denom = gate_1 + gate_2 + EPS
            gate_1 = gate_1 / denom
            gate_2 = gate_2 / denom
            density_1 = jnp.mean(mask_1, axis=-2)
            density_1_proxy = jnp.mean(raw_gates, axis=-2)
            loss = jnp.mean(density_1_proxy * density_1) * float(e * e)
            capacity = max(min(n, int(n * 2 * CAPACITY_FACTOR / e)), MIN_EXPERT_CAPACITY)
            cap_f = float(capacity)
            pos1 = cumsum_exclusive(mask_1, axis=-2) * mask_1
            mask_1 = mask_1 * (pos1 < cap_f).astype(mask_1.dtype)
            mask_1_count = jnp.sum(mask_1, axis=-2, keepdims=True)
            mask_1_flat = jnp.sum(mask_1, axis=-1)
            pos1 = jnp.sum(pos1, axis=-1)
            gate_1 = gate_1 * mask_1_flat
            pos2 = (cumsum_exclusive(mask_2, axis=-2) + mask_1_count) * mask_2
            mask_2 = mask_2 * (pos2 < cap_f).astype(mask_2.dtype)
            mask_2_flat = jnp.sum(mask_2, axis=-1)
            pos2 = jnp.sum(pos2, axis=-1)
            gate_2 = gate_2 * mask_2_flat
            combine = gate_1[..., None, None] * mask_1_flat[..., None, None] * jax.nn.one_hot(index_1, e, dtype=x.dtype)[..., None] * safe_one_hot(pos1.astype(jnp.int32), capacity)[..., None, :] + gate_2[..., None, None] * mask_2_flat[..., None, None] * jax.nn.one_hot(index_2, e, dtype=x.dtype)[..., None] * safe_one_hot(pos2.astype(jnp.int32), capacity)[..., None, :]
            dispatch = (combine > 0).astype(combine.dtype)
            return (dispatch, combine, loss)
        dispatch, combine, loss = top2_gating(x, w_gating)
        expert_inputs = jnp.einsum('bnd,bnec->ebcd', x, dispatch)
        hidden = jax.nn.relu(jnp.einsum('ebcd,edh->ebch', expert_inputs, w1))
        expert_outputs = jnp.einsum('ebch,ehd->ebcd', hidden, w2)
        output = jnp.einsum('ebcd,bnec->bnd', expert_outputs, combine)
        return output

    def _L3_gnn_ref(node_feats, edge_attrs, edge_feats, edge_index, W_up0, W_up1, W_mlp1, W_mlp2, W_mlp3, W_mlp4, W_out0, W_out1):
        import jax, jax.numpy as jnp
        import numpy as np
        MUL = 128
        N_NODES = 1250
        N_EDGES = 20000
        R_BASIS = 8
        HIDDEN = 64
        W_NUMEL = 4 * MUL
        SQRT3 = 3.0 ** 0.5
        SILU_2MOM = 1.679177
        AVG_NUM_NEIGHBORS = 10.0

        def _lin_irreps(x0, x1, W0, W1):
            y0 = x0 @ W0 / jnp.sqrt(jnp.float32(W0.shape[0]))
            y1 = jnp.einsum('num,uv->nvm', x1, W1) / jnp.sqrt(jnp.float32(W1.shape[0]))
            return (y0, y1)

        def _forward(node_feats, edge_attrs, edge_feats, edge_index, W_up0, W_up1, W_mlp1, W_mlp2, W_mlp3, W_mlp4, W_out0, W_out1):
            num_nodes = node_feats.shape[0]
            sender, receiver = (edge_index[0], edge_index[1])
            x0 = node_feats[:, :MUL]
            x1 = node_feats[:, MUL:].reshape(num_nodes, MUL, 3)
            x0, x1 = _lin_irreps(x0, x1, W_up0, W_up1)
            h = edge_feats
            for W in (W_mlp1, W_mlp2, W_mlp3):
                h = SILU_2MOM * jax.nn.silu(h @ W / jnp.sqrt(jnp.float32(W.shape[0])))
            tpw = h @ W_mlp4 / jnp.sqrt(jnp.float32(W_mlp4.shape[0]))
            w1, w2, w3, w4 = jnp.split(tpw, 4, axis=-1)
            s0 = x0[sender]
            s1 = x1[sender]
            y0 = edge_attrs[:, 0:1]
            y1 = edge_attrs[:, 1:4]
            p1 = w1 * s0 * y0
            p2 = (w2 * s0)[:, :, None] * y1[:, None, :]
            p3 = w3[:, :, None] * s1 * y0[:, None, :]
            p4 = w4 * jnp.einsum('eum,em->eu', s1, y1) / SQRT3
            m0 = jnp.concatenate([p1, p4], axis=-1)
            m1 = jnp.concatenate([p2, p3], axis=1)
            msg0 = jax.ops.segment_sum(m0, receiver, num_segments=num_nodes)
            msg1 = jax.ops.segment_sum(m1, receiver, num_segments=num_nodes)
            o0, o1 = _lin_irreps(msg0, msg1, W_out0, W_out1)
            out = jnp.concatenate([o0, o1.reshape(num_nodes, 3 * MUL)], axis=-1)
            return out / AVG_NUM_NEIGHBORS
        return _forward(node_feats, edge_attrs, edge_feats, edge_index, W_up0, W_up1, W_mlp1, W_mlp2, W_mlp3, W_mlp4, W_out0, W_out1)

    def _L3_mix_ref(x, Wq, bq, Wk, bk, Wv, bv, Wo, bo, W1, b1, W2, b2, g1, be1, g2, be2):
        import jax, jax.numpy as jnp
        import numpy as np
        EPS = 1e-06
        H = 8
        DH = 64
        LN_EPS = 1e-05

        def _layernorm(x, g, b):
            m = jnp.mean(x, axis=-1, keepdims=True)
            v = jnp.mean(jnp.square(x - m), axis=-1, keepdims=True)
            return (x - m) / jnp.sqrt(v + LN_EPS) * g + b

        def _flow_attention(x, Wq, bq, Wk, bk, Wv, bv, Wo, bo):
            B, L, D = x.shape
            S = L
            q = jax.nn.sigmoid((x @ Wq + bq).reshape(B, L, H, DH).transpose(0, 2, 1, 3))
            k = jax.nn.sigmoid((x @ Wk + bk).reshape(B, S, H, DH).transpose(0, 2, 1, 3))
            v = (x @ Wv + bv).reshape(B, S, H, DH).transpose(0, 2, 1, 3)
            sink_incoming = 1.0 / jnp.einsum('nhld,nhd->nhl', q + EPS, k.sum(axis=2) + EPS)
            source_outgoing = 1.0 / jnp.einsum('nhld,nhd->nhl', k + EPS, q.sum(axis=2) + EPS)
            conserved_sink = jnp.einsum('nhld,nhd->nhl', q + EPS, (k * source_outgoing[..., None]).sum(axis=2) + EPS)
            conserved_source = jnp.einsum('nhld,nhd->nhl', k + EPS, (q * sink_incoming[..., None]).sum(axis=2) + EPS)
            conserved_source = jnp.clip(conserved_source, -1.0, 1.0)
            sink_allocation = jax.nn.sigmoid(conserved_sink * (float(L) / float(S)))
            source_competition = jax.nn.softmax(conserved_source, axis=-1) * float(S)
            kv = jnp.einsum('nhld,nhlm->nhdm', k, v * source_competition[..., None])
            o = jnp.einsum('nhld,nhdm->nhlm', q * sink_incoming[..., None], kv)
            o = o * sink_allocation[..., None]
            o = o.transpose(0, 2, 1, 3).reshape(B, L, D)
            return o @ Wo + bo
        sa = _flow_attention(_layernorm(x, g1, be1), Wq, bq, Wk, bk, Wv, bv, Wo, bo)[0]
        x = x + sa
        h = _layernorm(x, g2, be2)
        h = jax.nn.gelu(h @ W1 + b1, approximate=False) @ W2 + b2
        return x + h

    def _L3_ffn_ref(x, input_patterns, process_input_weights, process_values, output_input_weights, output_patterns):
        import jax, jax.numpy as jnp
        import numpy as np
        K_INPUT, K_PROCESS, K_OUTPUT = (256, 128, 256)

        def _gelu(x):
            return jax.nn.gelu(x, approximate=False)
        B, S, d_model = x.shape
        n_in = input_patterns.shape[0]
        input_acts = _gelu(jnp.einsum('bsd,nd->bsn', x, input_patterns))
        top_in_acts, top_in_idx = jax.lax.top_k(input_acts, K_INPUT)
        bi = jnp.arange(B)[:, None, None]
        si = jnp.arange(S)[None, :, None]
        input_repr = jnp.zeros((B, S, n_in), dtype=x.dtype).at[bi, si, top_in_idx].set(top_in_acts)
        process_acts = _gelu(jnp.einsum('bsn,pn->bsp', input_repr, process_input_weights))
        top_p_acts, top_p_idx = jax.lax.top_k(process_acts, K_PROCESS)
        sel_values = process_values[top_p_idx]
        p_weights = jax.nn.softmax(top_p_acts, axis=-1)
        agg_value = jnp.einsum('bsk,bskd->bsd', p_weights, sel_values)
        output_acts = _gelu(jnp.einsum('bsd,od->bso', agg_value, output_input_weights))
        top_o_acts, top_o_idx = jax.lax.top_k(output_acts, K_OUTPUT)
        sel_patterns = output_patterns[top_o_idx]
        out = jnp.einsum('bsk,bskm->bsm', top_o_acts, sel_patterns)
        return out
    edge_index = jnp.stack([src, dst])
    xn = _layernorm(x, axis=-1)
    x = x + _L0_gnn_ref(xn, edge_index, L0_gnn_W_q, L0_gnn_b_q, L0_gnn_W_k, L0_gnn_b_k, L0_gnn_W_v, L0_gnn_b_v, L0_gnn_W_e, L0_gnn_b_e, L0_gnn_W_o, L0_gnn_b_o, L0_gnn_edge_emb, L0_gnn_edge_attn, L0_gnn_ln_g, L0_gnn_ln_b) + _L0_mix_ref(xn[None], L0_mix_Wqkv)[0]
    x = x + _L0_ffn_ref(_layernorm(x, axis=-1)[None], L0_ffn_Wg, L0_ffn_bg, L0_ffn_W1, L0_ffn_W3, L0_ffn_W2)[0]
    xn = _layernorm(x, axis=-1)
    x = x + _L1_gnn_ref(xn, src, dst, L1_gnn_W, L1_gnn_b) + _L1_mix_ref(xn[None], L1_mix_W_qkv, L1_mix_W_out, L1_mix_b_out)[0]
    x = x + _L1_ffn_ref(_layernorm(x, axis=-1)[None], L1_ffn_gate_w, L1_ffn_biases, L1_ffn_w1, L1_ffn_w3, L1_ffn_w2, L1_ffn_sw1, L1_ffn_sw3, L1_ffn_sw2)[0]
    xn = _layernorm(x, axis=-1)
    x = x + _L2_gnn_ref(xn, edge_index, L2_gnn_Wq, L2_gnn_bq, L2_gnn_Wk, L2_gnn_bk, L2_gnn_Wv, L2_gnn_bv, L2_gnn_Wskip, L2_gnn_bskip, L2_gnn_Wlin, L2_gnn_blin, L2_gnn_gamma, L2_gnn_beta) + _L2_mix_ref(xn[None], L2_mix_qkv_w, L2_mix_qkv_b, L2_mix_out_w, L2_mix_out_b, L2_mix_ln_gamma, L2_mix_ln_beta)[0]
    x = x + _L2_ffn_ref(_layernorm(x, axis=-1)[None], L2_ffn_w_gating, L2_ffn_w1, L2_ffn_w2)[0]
    xn = _layernorm(x, axis=-1)
    x = x + _L3_gnn_ref(xn, edge_attr_4, edge_attr_8, edge_index, L3_gnn_W_up0, L3_gnn_W_up1, L3_gnn_W_mlp1, L3_gnn_W_mlp2, L3_gnn_W_mlp3, L3_gnn_W_mlp4, L3_gnn_W_out0, L3_gnn_W_out1) + _L3_mix_ref(xn[None], L3_mix_Wq, L3_mix_bq, L3_mix_Wk, L3_mix_bk, L3_mix_Wv, L3_mix_bv, L3_mix_Wo, L3_mix_bo, L3_mix_W1, L3_mix_b1, L3_mix_W2, L3_mix_b2, L3_mix_g1, L3_mix_be1, L3_mix_g2, L3_mix_be2)[0]
    x = x + _L3_ffn_ref(_layernorm(x, axis=-1)[None], L3_ffn_input_patterns, L3_ffn_process_input_weights, L3_ffn_process_values, L3_ffn_output_input_weights, L3_ffn_output_patterns)[0]
    return x

_drawn_inputs = setup_inputs


def setup_inputs(seed=0):
    import zlib

    import numpy as np

    out = dict(_drawn_inputs(seed))
    spreads = {'L0_gnn_ln_g': (1.0, 0.2),
     'L0_gnn_ln_b': (0.0, 0.1),
     'L1_ffn_biases': (0.0, 0.1),
     'L2_gnn_bq': (0.0, 0.543),
     'L2_gnn_bk': (0.0, 2.0),
     'L2_gnn_bv': (0.0, 0.1),
     'L2_gnn_bskip': (0.0, 0.1),
     'L2_gnn_blin': (0.0, 0.1),
     'L2_gnn_gamma': (1.0, 0.2),
     'L2_gnn_beta': (0.0, 0.1),
     'L2_mix_qkv_b': (0.0, 0.1),
     'L2_mix_out_b': (0.0, 0.1),
     'L2_mix_ln_gamma': (1.0, 0.6),
     'L2_mix_ln_beta': (0.0, 0.1),
     'L3_mix_bq': (0.0, 2.0),
     'L3_mix_bk': (0.0, 2.0),
     'L3_mix_bv': (0.0, 0.8),
     'L3_mix_bo': (0.0, 0.361),
     'L3_mix_b1': (0.0, 0.8),
     'L3_mix_b2': (0.0, 0.359),
     'L3_mix_g1': (1.0, 0.6),
     'L3_mix_be1': (0.0, 0.8),
     'L3_mix_g2': (1.0, 0.6),
     'L3_mix_be2': (0.0, 0.8)}
    factors = {'L0_gnn_b_q': 8.0,
     'L0_gnn_b_k': 64.0,
     'L0_gnn_W_e': 2.842,
     'L0_gnn_b_e': 7.24,
     'L0_gnn_edge_emb': 64.0,
     'L0_ffn_bg': 3.351,
     'L1_gnn_b': 4.107,
     'L3_mix_Wq': 8.0,
     'L3_mix_Wk': 8.0,
     'L3_mix_Wv': 8.0,
     'L3_mix_Wo': 6.932,
     'L3_mix_W1': 3.057,
     'L3_mix_W2': 2.808,
     'L3_ffn_input_patterns': 8.0,
     'L3_ffn_process_input_weights': 8.0,
     'L3_ffn_process_values': 8.0,
     'L3_ffn_output_input_weights': 8.0,
     'L3_ffn_output_patterns': 8.0}
    for name, (base, spread) in spreads.items():
        noise = np.random.default_rng([zlib.crc32(name.encode()), seed]).standard_normal(out[name].shape)
        drawn = base * np.exp(spread * noise) if base else spread * noise
        out[name] = jnp.asarray(drawn.astype(out[name].dtype))
    for name, factor in factors.items():
        out[name] = (out[name] * factor).astype(out[name].dtype)
    return out
```

```python
from contextlib import ExitStack

import numpy as np

import concourse.bass as bass
from concourse import mybir

P = 128
NODES = 512
DIM = 512
TILES = NODES // P
CHUNKS = DIM // P
EDGES = 16384
EDGE_TILES = EDGES // P
HEADS = 8
HEAD = DIM // HEADS
BANK = 512

F32 = mybir.dt.float32
BF16 = mybir.dt.bfloat16
I32 = mybir.dt.int32
U32 = mybir.dt.uint32
ALU = mybir.AluOpType
ACT = mybir.ActivationFunctionType
AXIS = mybir.AxisListType
MASKED = -1.0e30


class Chain:

    def __init__(self, engine, sem):
        self.engine, self.sem, self.count = engine, sem, 0

    def __call__(self, instruction):
        self.count += 1
        instruction.then_inc(self.sem, 1)
        self.engine.wait_ge(self.sem, self.count)


class Load:

    def __init__(self, sem, value):
        self.sem, self.value = sem, value

    def wait(self, engine):
        engine.wait_ge(self.sem, self.value)


class Core:

    PER_STAGE = 20
    LOADS = 24

    def __init__(self, nc, stack):
        self.nc, self.stack = nc, stack
        taken = [nc.alloc_semaphore(f"stage_pool_{i}") for i in range(2 * self.PER_STAGE)]
        numbers = [s.num for s in taken]
        for s in taken:
            nc.release_semaphore(s)
        self.pools = [numbers[:self.PER_STAGE], numbers[self.PER_STAGE:]]
        self.turn, self.used = 0, None
        self.load_sems = [stack.enter_context(nc.semaphore(f"load_landed_{i}")) for i in range(self.LOADS)]
        self.gather_sems = [stack.enter_context(nc.semaphore(f"sender_rows_landed_{b}")) for b in range(2)]
        self.load_counts = [0] * self.LOADS
        self.loads = 0
        self.psum = stack.enter_context(nc.psum_tensor("banks", [P, 8, BANK], F32))
        self.names = 0

    def sb(self, name, shape, dtype=F32):
        return self.stack.enter_context(self.nc.sbuf_tensor(name, shape, dtype))

    def load(self, queue, dst, src):
        i = self.loads % self.LOADS
        self.loads += 1
        self.load_counts[i] += 16
        queue.dma_start(dst, src).then_inc(self.load_sems[i], 16)
        return Load(self.load_sems[i], self.load_counts[i])

    def section(self, first, chunks=4, width=512):
        return self.wpool[:, first * 2048:first * 2048 + chunks * width].rearrange("p (c n) -> p c n", c=chunks)

    def bank(self, i):
        return self.psum[:, i, :]


class Stage:

    def __init__(self, core, name):
        self.core, self.name, self.sems = core, name, []

    def __enter__(self):
        core = self.core
        if core.used:
            core.nc.gpsimd.sem_clear(range(min(core.used), max(core.used) + 1))
        core.turn ^= 1
        self.numbers = core.pools[core.turn]
        self.opened = core.nc.Block()
        self.block = self.opened.__enter__()
        return self

    def sem(self, name):
        s = self.core.nc.alloc_semaphore(name=f"{self.name}_{name}", num=self.numbers[len(self.sems)])
        self.sems.append(s)
        return s

    def chain(self, engine, name):
        return Chain(engine, self.sem(name))

    def __exit__(self, *exc):
        self.opened.__exit__(*exc)
        self.core.used = [s.num for s in self.sems]
        for s in self.sems:
            self.core.nc.release_semaphore(s)
        return False


def product(nc, core, out, pairs):
    n = len(pairs)
    for j, (left, right) in enumerate(pairs):
        if right is None:
            last = nc.tensor.transpose(out, left, core.ident[0:left.shape[0], 0:left.shape[0]])
        else:
            last = nc.tensor.matmul(out, left, right, start=(j == 0), stop=(j == n - 1))
    return last


class Tile:

    def __init__(self, parts, engine, loads=()):
        self.parts, self.engine, self.loads = parts, engine, loads


def products_stage(core, name, tiles, finish, issue=None, params=(), banks=8, ordered=False):
    nc = core.nc
    order = {"V": [t for t, x in enumerate(tiles) if x.engine == "V"],
             "A": [t for t, x in enumerate(tiles) if x.engine == "A"]}
    place = {t: i for ts in order.values() for i, t in enumerate(ts)}
    with Stage(core, name) as st:
        filled = st.sem("bank_filled")
        taken = {"V": st.sem("vector_took_bank"), "A": st.sem("scalar_took_bank")}
        chain_v, chain_a = st.chain(nc.vector, "vector_chain"), st.chain(nc.scalar, "scalar_chain")

        if issue is not None:
            @st.block.sync
            def _(sp):
                issue(sp)

        @st.block.tensor
        def _(pe):
            for t, tile in enumerate(tiles):
                for load in tile.loads:
                    load().wait(pe)
                if t >= banks:
                    pe.wait_ge(taken[tiles[t - banks].engine], place[t - banks] + 1)
                for rows, c0, c1, pairs in tile.parts:
                    last = product(nc, core, core.bank(t % banks)[0:rows, c0:c1], pairs)
                last.then_inc(filled, 1)

        if order["V"]:
            @st.block.vector
            def _(dve):
                for load in params:
                    load().wait(dve)
                for t in order["V"]:
                    dve.wait_ge(filled, t + 1)
                    if ordered and place[t] > 0:
                        dve.wait_ge(taken["V"], place[t])
                    finish(t, nc.vector, core.bank(t % banks), chain_v).then_inc(taken["V"], 1)

        if order["A"]:
            @st.block.scalar
            def _(act):
                for load in params:
                    load().wait(act)
                for t in order["A"]:
                    act.wait_ge(filled, t + 1)
                    finish(t, nc.scalar, core.bank(t % banks), chain_a).then_inc(taken["A"], 1)


def copy_out(nc, engine, out, in_):
    return nc.vector.tensor_copy(out, in_) if engine is nc.vector else nc.scalar.copy(out, in_)


def transpose_stage(core, name, dst, blocks):
    nc = core.nc
    tiles = [Tile([(P, i * P, (i + 1) * P, [(blocks(i, c), None)]) for i in range(TILES)], "VA"[c % 2])
             for c in range(CHUNKS)]
    products_stage(core, name, tiles, lambda t, e, ps, chain: copy_out(nc, e, dst[:, t, :], ps))


def rows_of(src):
    return lambda i, c: src[:, i, c * P:(c + 1) * P]


def norm_stage(core, name, src, dst, scale=None, shift=None, add_to=None, plain=None, issue=None, params=()):
    nc = core.nc
    stats, moments, deviation = core.stats, core.moments, core.deviation
    with Stage(core, name) as st:
        variance_ready, deviation_ready = st.sem("variance_ready"), st.sem("deviation_ready")
        chain = st.chain(nc.vector, "vector_chain")
        if issue is not None:
            @st.block.sync
            def _(sp):
                issue(sp)

        @st.block.scalar
        def _(act):
            act.wait_ge(variance_ready, 1)
            nc.scalar.activation(deviation[:, :, 1], deviation[:, :, 0], ACT.Sqrt).then_inc(deviation_ready, 1)

        @st.block.vector
        def _(dve):
            for load in params:
                load().wait(dve)
            for i in range(TILES):
                chain(nc.vector.bn_stats(stats[:, i, :], src[:, i, :]))
                chain(nc.vector.bn_aggr(moments[:, i, :], stats[:, i, :]))
            nc.vector.tensor_scalar(deviation[:, :, 0], moments[:, :, 1], 1e-5, None, ALU.add).then_inc(variance_ready, 1)
            dve.wait_ge(deviation_ready, 1)
            chain(nc.vector.reciprocal(deviation[:, :, 2], deviation[:, :, 1]))
            for i in range(TILES):
                out = plain if plain is not None else dst
                chain(nc.vector.tensor_scalar(dst[:, i, :], src[:, i, :], moments[:, i, 0:1], deviation[:, i, 2:3],
                                              ALU.subtract, ALU.mult))
                if scale is not None:
                    chain(nc.vector.tensor_tensor(dst[:, i, :], dst[:, i, :], scale, ALU.mult))
                    chain(nc.vector.tensor_tensor(dst[:, i, :], dst[:, i, :], shift, ALU.add))
                if add_to is not None:
                    chain(nc.vector.tensor_tensor(add_to[:, i, :], add_to[:, i, :], dst[:, i, :], ALU.add))


def softmax_stage(core, name, units, width, scale=1.0, mask=None, weigh=None, normal=False, keep=None,
                  turned=None, values=None, total_banks=(), finish=None, issue=None):
    nc = core.nc
    n, blocks = len(units), width // P
    scores, exps, turns, sums, negmax = core.scores, core.exps, core.turns, core.sums, core.negmax
    post = weigh is not None or normal

    def exps_of(u):
        return keep(u) if keep is not None else exps[:, u % 2, 0:width]

    def turned_of(u):
        return turned(u) if turned is not None else turns[:, u % 2, 0:blocks * P].rearrange("p (c n) -> p c n", c=blocks)

    with Stage(core, name) as st:
        scored, shifted, exponed = st.sem("scores_ready"), st.sem("maximum_ready"), st.sem("exponentials_ready")
        weighed, flipped, copied = st.sem("weighed_ready"), st.sem("transpose_ready"), st.sem("transpose_copied")
        valued = st.sem("values_ready")
        chain = st.chain(nc.vector, "vector_chain")
        if issue is not None:
            @st.block.sync
            def _(sp):
                issue(sp)

        @st.block.tensor
        def _(pe):
            def score(u):
                if u >= 2:
                    pe.wait_ge(shifted, u - 1)
                product(nc, core, core.bank(u % 2)[:, 0:width], units[u]).then_inc(scored, 1)

            def flip(u):
                pe.wait_ge(weighed if post else exponed, u + 1)
                if u >= 2:
                    pe.wait_ge(copied, u - 1)
                for c in range(blocks):
                    last = product(nc, core, core.bank(2 + u % 2)[:, c * P:(c + 1) * P],
                                   [(exps_of(u)[:, c * P:(c + 1) * P], None)])
                last.then_inc(flipped, 1)

            def value(u):
                pe.wait_ge(copied, u + 1)
                bank, c0, c1, pairs = values(u, turned_of(u))
                product(nc, core, core.bank(bank)[:, c0:c1], pairs).then_inc(valued, 1)

            score(0)
            for u in range(n):
                if u + 1 < n:
                    score(u + 1)
                flip(u)
                if values is not None and u >= 1:
                    value(u - 1)
            if values is not None:
                value(n - 1)

        @st.block.vector
        def _(dve):
            def shift(u):
                dve.wait_ge(scored, u + 1)
                if u >= 2:
                    dve.wait_ge(exponed, u - 1)
                if mask is not None:
                    chain(nc.vector.scalar_tensor_tensor(out=scores[:, u % 2, 0:width], in0=core.bank(u % 2)[:, 0:width],
                                                         scalar=scale, in1=mask(u), op0=ALU.mult, op1=ALU.add))
                else:
                    chain(nc.vector.tensor_scalar(scores[:, u % 2, 0:width], core.bank(u % 2)[:, 0:width], scale, None,
                                                  ALU.mult))
                nc.vector.tensor_reduce(negmax[:, u:u + 1], scores[:, u % 2, 0:width], AXIS.X, ALU.max,
                                        negate=True).then_inc(shifted, 1)

            def weigh_exps(u):
                dve.wait_ge(exponed, u + 1)
                e, s = exps_of(u), sums[:, u:u + 1]
                if weigh is not None:
                    chain(nc.vector.tensor_tensor(e, e, weigh(u), ALU.mult))
                    chain(nc.vector.tensor_reduce(s, e, AXIS.X, ALU.add))
                    chain(nc.vector.tensor_scalar(s, s, 0.5, None, ALU.max))
                chain(nc.vector.reciprocal(s, s))
                nc.vector.tensor_scalar(e, e, s, None, ALU.mult).then_inc(weighed, 1)

            shift(0)
            for u in range(n):
                if u + 1 < n:
                    shift(u + 1)
                if post:
                    weigh_exps(u)
            if finish is not None:
                dve.wait_ge(valued, n)
                dve.wait_ge(exponed, n)
                finish(chain)

        @st.block.scalar
        def _(act):
            def expo(u):
                act.wait_ge(shifted, u + 1)
                if u >= 2 and keep is None:
                    act.wait_ge(flipped, u - 1)
                nc.scalar.activation(exps_of(u), scores[:, u % 2, 0:width], ACT.Exp, bias=negmax[:, u:u + 1],
                                     accum_out=sums[:, u:u + 1]).then_inc(exponed, 1)

            def copy_turned(u):
                act.wait_ge(flipped, u + 1)
                if u >= 2 and values is not None and turned is None:
                    act.wait_ge(valued, u - 1)
                nc.scalar.copy(turned_of(u), core.bank(2 + u % 2)[:, 0:blocks * P].rearrange("p (c n) -> p c n", c=blocks)
                               ).then_inc(copied, 1)

            expo(0)
            for u in range(n):
                if u + 1 < n:
                    expo(u + 1)
                copy_turned(u)


def setup_stage(core, src_dram, dst_dram, x_dram):
    nc = core.nc
    with Stage(core, "setup") as st:
        landed, made = st.sem("inputs_landed"), st.sem("constants_made")
        x_landed = st.sem("x_landed")

        @st.block.sync
        def _(sp):
            sp.dma_start(core.src_i[:], src_dram).then_inc(landed, 16)
            sp.dma_start(core.dst_i[:], dst_dram).then_inc(landed, 16)
            sp.dma_start(core.x[:], x_dram.rearrange("(i p) d -> p i d", p=P)).then_inc(x_landed, 16)
            sp.wait_ge(x_landed, 16)

        @st.block.gpsimd
        def _(pool):
            nc.gpsimd.memset(core.ident[:], 0.0).then_inc(made, 1)
            nc.gpsimd.memset(core.ones[:], 1.0)
            pool.wait_ge(made, 1)
            nc.gpsimd.affine_select(out=core.ident[:], in_=core.ident[:], compare_op=ALU.not_equal, fill=1.0, base=0,
                                    pattern=[[-1, P]], channel_multiplier=1)
            nc.gpsimd.iota(core.iota_i[:], [[1, NODES]], base=0, channel_multiplier=0).then_inc(made, 1)

        @st.block.vector
        def _(dve):
            dve.wait_ge(landed, 32)
            nc.vector.tensor_copy(core.src_f[:], core.src_i[:])
            nc.vector.tensor_copy(core.dst_f[:], core.dst_i[:])
            dve.wait_ge(made, 2)
            nc.vector.tensor_copy(core.iota[:], core.iota_i[:])


def adjacency_stage(core):
    nc = core.nc
    with ExitStack() as local, Stage(core, "adjacency") as st:
        hot_src = local.enter_context(nc.sbuf_tensor("hot_src", [P, 2, NODES], BF16))
        hot_dst = local.enter_context(nc.sbuf_tensor("hot_dst", [P, 2, NODES], BF16))
        hot, counted = st.sem("one_hots_ready"), st.sem("edges_counted")
        steps = EDGE_TILES // 2

        def one_hots(t, b):
            nc.vector.tensor_scalar(hot_src[:, b, :], core.iota[:], core.src_f[:, bass.ds(t, 1)], None, ALU.is_equal)
            nc.vector.tensor_scalar(hot_dst[:, b, :], core.iota[:], core.dst_f[:, bass.ds(t, 1)], None,
                                    ALU.is_equal).then_inc(hot, 1)

        def count(pe, b, first, last):
            for m in range(TILES):
                done = nc.tensor.matmul(core.bank(m), hot_dst[:, b, m * P:(m + 1) * P], hot_src[:, b, :],
                                        start=first, stop=last, skip_group_check=True)
            done.then_inc(counted, 1)

        @st.block.vector
        def _(dve):
            one_hots(0, 0)
            one_hots(1, 1)
            with dve.Fori(1, steps) as s:
                for b in range(2):
                    dve.wait_ge(counted, 2 * s + b - 1)
                    one_hots(2 * s + b, b)
            dve.wait_ge(counted, 2 * steps)
            for m in range(TILES):
                nc.vector.tensor_copy(core.edges_to[:, m, :], core.bank(m))

        @st.block.tensor
        def _(pe):
            pe.wait_ge(hot, 1)
            count(pe, 0, True, False)
            pe.wait_ge(hot, 2)
            count(pe, 1, False, False)
            with pe.Fori(1, steps - 1) as s:
                for b in range(2):
                    pe.wait_ge(hot, 2 * s + b + 1)
                    count(pe, b, False, False)
            pe.wait_ge(hot, 2 * steps - 1)
            count(pe, 0, False, False)
            pe.wait_ge(hot, 2 * steps)
            count(pe, 1, False, True)


def weights(dram, cols=None):
    w = dram.rearrange("(c p) n -> p c n", p=P)
    return w if cols is None else w[:, :, cols[0]:cols[1]]


def linear_tiles(left, right, engines, loads=(), width=DIM):
    k = right.shape[1]
    return [Tile([(P, 0, width, [(left[:, c, i * P:(i + 1) * P], right[:, c, 0:width]) for c in range(k)])],
                 engines[i % len(engines)], loads) for i in range(TILES)]


def turned_tiles(right, weight, engines, loads=(), first=0):
    k, n = weight.shape[1], weight.shape[2] // P
    return [Tile([(P, 0, NODES, [(weight[:, c, m * P:(m + 1) * P], right[:, c, :]) for c in range(k)])],
                 engines[(first + m) % len(engines)], loads) for m in range(n)]


def layer0_gnn(core, w):
    nc = core.nc
    xn, xnT = core.xn, core.xnT
    with ExitStack() as local:
        def sb(name, shape, dtype=F32):
            return local.enter_context(nc.sbuf_tensor("g0_" + name, shape, dtype))
        part = [core.section(j) for j in range(12)]
        qT, kT, v, mixed, xe, mask = part[5:11]
        rows, cols = sb("rows", [P, 6, 512]), sb("cols", [P, 12])
        L = {}

        def issue(sp):
            L["cols"] = core.load(sp, cols[:], w["g0_cols"])
            for j, name in enumerate(["g0_WqT", "g0_WkT", "g0_WeT", "g0_WvT", "g0_WoT"]):
                L[name] = core.load(sp, part[j], weights(w[name]))
                if j == 1:
                    L["rows"] = core.load(sp, rows[:], w["g0_rows"].rearrange("(o r) n -> o r n", o=1).to_broadcast([P, 6, 512]))

        tiles = (turned_tiles(xnT, part[0], "A", [lambda: L["g0_WqT"]]) + turned_tiles(xnT, part[1], "V", [lambda: L["g0_WkT"]])
                 + linear_tiles(xnT, part[2], "V", [lambda: L["g0_WeT"]]) + linear_tiles(xnT, part[3], "V", [lambda: L["g0_WvT"]]))

        def finish(t, engine, ps, chain):
            m = t % 4
            if t < 4:
                return nc.scalar.activation(qT[:, m, :], ps, ACT.Identity, bias=cols[:, m:m + 1])
            if t < 8:
                return nc.vector.tensor_scalar(kT[:, m, :], ps, cols[:, 4 + m:5 + m], cols[:, 8 + m:9 + m], ALU.add, ALU.add)
            if t < 12:
                chain(nc.vector.tensor_tensor(xe[:, m, :], ps, rows[:, 1, :], ALU.add))
                return nc.vector.tensor_tensor(xe[:, m, :], xe[:, m, :], rows[:, 2, :], ALU.mult)
            chain(nc.vector.tensor_tensor(v[:, m, :], ps, rows[:, 0, :], ALU.add))
            return nc.vector.tensor_tensor(v[:, m, :], v[:, m, :], xe[:, m, :], ALU.add)

        with Stage(core, "g0_mask") as st:
            chain = st.chain(nc.vector, "vector_chain")

            @st.block.sync
            def _(sp):
                issue(sp)

            @st.block.vector
            def _(dve):
                chain(nc.vector.tensor_scalar(mask[:], core.edges_from[:], 0.5, None, ALU.is_lt))
                nc.vector.tensor_scalar(mask[:], mask[:], MASKED, None, ALU.mult)
        products_stage(core, "g0_qkv", tiles, finish, params=[lambda: L["rows"], lambda: L["cols"]])

        def head(x, h):
            return x[HEAD * (h % 2):HEAD * (h % 2) + HEAD, h // 2]
        order = [(h, i) for h in range(HEADS) for i in range(TILES)]
        units = [[(head(qT, h)[:, i * P:(i + 1) * P], head(kT, h))] for h, i in order]

        def values(u, turned):
            h, i = order[u]
            return 4 + i, h * HEAD, (h + 1) * HEAD, [(turned[:, c, :], v[:, c, h * HEAD:(h + 1) * HEAD]) for c in range(4)]

        def finish_attention(chain):
            chain(nc.vector.reciprocal(core.sums[:, 0:32], core.sums[:, 0:32]))
            s = core.sums[:, 0:32].rearrange("p (h i) -> p i h", i=4)
            for i in range(TILES):
                nc.vector.tensor_tensor(mixed[:, i, :].rearrange("p (h d) -> p h d", h=HEADS),
                                        core.bank(4 + i).rearrange("p (h d) -> p h d", h=HEADS),
                                        s[:, i, :].unsqueeze(2).to_broadcast([P, HEADS, HEAD]), ALU.mult)
        softmax_stage(core, "g0_attention", units, NODES, scale=HEAD ** -0.5, mask=lambda u: mask[:, order[u][1], :],
                      values=values, finish=finish_attention)
        transpose_stage(core, "g0_turn", qT, rows_of(mixed))

        def finish_out(t, engine, ps, chain):
            chain(nc.vector.tensor_tensor(v[:, t, :], ps, rows[:, 3, :], ALU.add))
            return nc.vector.tensor_tensor(v[:, t, :], v[:, t, :], xn[:, t, :], ALU.add)
        products_stage(core, "g0_out", linear_tiles(qT, part[4], "V", [lambda: L["g0_WoT"]]), finish_out)
        norm_stage(core, "g0_norm", v, core.branches, scale=rows[:, 4, :], shift=rows[:, 5, :])


def add_stage(core, name, pairs, out=None):
    nc = core.nc
    with Stage(core, name) as st:
        @st.block.vector
        def _(dve):
            for a, b in pairs:
                nc.vector.tensor_tensor(a, a, b, ALU.add)


def store_stage(core, out_dram, src):
    nc = core.nc
    with Stage(core, "store") as st:
        stored = st.sem("output_stored")

        @st.block.sync
        def _(sp):
            sp.dma_start(out_dram.rearrange("(i p) d -> p i d", p=P), src[:]).then_inc(stored, 16)
            sp.wait_ge(stored, 16)


LANDMARKS = 256
PINV_STEPS = 6


def pinv_stage(core, XT, Z, ZT):
    nc = core.nc
    big = lambda first: core.wpool[:, first * 4096:(first + 1) * 4096].rearrange("p (h c n) -> p h c n", h=HEADS, c=2)
    XZ, XZT, Q = big(3), big(4), big(5)
    with ExitStack() as local, Stage(core, "pinv") as st:
        seven, fifteen, thirteen = (local.enter_context(nc.sbuf_tensor(f"pinv_{n}", [P, 2, 256], F32))
                                    for n in ("seven", "fifteen", "thirteen"))
        tops = local.enter_context(nc.sbuf_tensor("pinv_tops", [P, 8], F32))
        all_sums = local.enter_context(nc.sbuf_tensor("pinv_sums", [P, 2, 16], F32))
        tops_ready, tops_shared, factor_ready = st.sem("tops_ready"), st.sem("tops_shared"), st.sem("factor_ready")
        chain = st.chain(nc.vector, "vector_chain")
        made, vec, act_ = st.sem("products_ready"), st.sem("vector_results"), st.sem("scalar_results")
        PE_STEP, V_STEP, A_STEP = 48, 32, 24

        def bank(h):
            return core.bank(h).rearrange("p (c n) -> p c n", c=2)

        @st.block.gpsimd
        def _(pool):
            pool.wait_ge(tops_ready, 1)
            nc.gpsimd.partition_all_reduce(tops[:, 2:4], tops[:, 0:2], P, bass.bass_isa.ReduceOp.max).then_inc(tops_shared, 1)

        @st.block.vector
        def _(dve):
            flat = lambda x: x.rearrange("p h c n -> p (h c) n")
            chain(nc.vector.tensor_reduce(all_sums[:, 0, :], flat(ZT), AXIS.X, ALU.add, apply_absolute_value=True))
            chain(nc.vector.tensor_reduce(all_sums[:, 1, :], flat(XT), AXIS.X, ALU.add, apply_absolute_value=True))
            nc.vector.tensor_reduce(tops[:, 0:2], all_sums[:], AXIS.X, ALU.max).then_inc(tops_ready, 1)
            for matrix, value in ((seven, 7.0), (fifteen, 15.0), (thirteen, 13.0)):
                chain(nc.vector.memset(matrix[:], 0.0))
                for c in range(2):
                    chain(nc.vector.tensor_scalar(matrix[:, c, c * P:(c + 1) * P], core.ident[:], value, None, ALU.mult))
            dve.wait_ge(tops_shared, 1)
            chain(nc.vector.tensor_tensor(tops[:, 4:5], tops[:, 2:3], tops[:, 3:4], ALU.mult))
            nc.vector.reciprocal(tops[:, 5:6], tops[:, 4:5]).then_inc(factor_ready, 1)
            dve.wait_ge(factor_ready, 1)
            for h in range(HEADS):
                nc.vector.tensor_scalar(ZT[:, h], ZT[:, h], tops[:, 5:6], None, ALU.mult).then_inc(vec, 1)
            with dve.Fori(0, PINV_STEPS) as s:
                for j, matrix in enumerate((seven, fifteen, thirteen)):
                    for h in range(HEADS):
                        dve.wait_ge(made, s * PE_STEP + (0, 16, 24)[j] + h + 1)
                        nc.vector.scalar_tensor_tensor(out=Q[:, h], in0=bank(h), scalar=-1.0, in1=matrix[:],
                                                       op0=ALU.mult, op1=ALU.add).then_inc(vec, 1)
                for h in range(HEADS):
                    dve.wait_ge(made, s * PE_STEP + 40 + h + 1)
                    nc.vector.tensor_copy(ZT[:, h], bank(h)).then_inc(vec, 1)

        @st.block.scalar
        def _(act):
            act.wait_ge(factor_ready, 1)
            for h in range(HEADS):
                nc.scalar.activation(Z[:, h], XT[:, h], ACT.Copy, scale=tops[:, 5:6]).then_inc(act_, 1)
            with act.Fori(0, PINV_STEPS) as s:
                for h in range(HEADS):
                    act.wait_ge(vec, s * V_STEP + 8 + h + 1)
                    nc.scalar.copy(XZ[:, h], bank(h)).then_inc(act_, 1)
                for h in range(HEADS):
                    act.wait_ge(made, s * PE_STEP + 8 + h + 1)
                    nc.scalar.copy(XZT[:, h], bank(h)).then_inc(act_, 1)
                for h in range(HEADS):
                    act.wait_ge(made, s * PE_STEP + 32 + h + 1)
                    nc.scalar.activation(Z[:, h], bank(h), ACT.Copy, scale=0.25).then_inc(act_, 1)

        @st.block.tensor
        def _(pe):
            def multiply(h, left_turned, right):
                for m in range(2):
                    last = product(nc, core, bank(h)[:, m, :],
                                   [(left_turned[:, h, c, m * P:(m + 1) * P], right[:, h, c, :]) for c in range(2)])
                last.then_inc(made, 1)

            def turn(h, matrix):
                for c in range(2):
                    for m in range(2):
                        last = nc.tensor.transpose(bank(h)[:, c, m * P:(m + 1) * P], matrix[:, h, m, c * P:(c + 1) * P],
                                                   core.ident[:])
                last.then_inc(made, 1)

            with pe.Fori(0, PINV_STEPS) as s:
                for h in range(HEADS):
                    pe.wait_ge(act_, s * A_STEP + h + 1)
                    pe.wait_ge(vec, s * V_STEP + h + 1)
                    multiply(h, XT, Z)
                for h in range(HEADS):
                    pe.wait_ge(act_, s * A_STEP + 8 + h + 1)
                    pe.wait_ge(vec, s * V_STEP + 8 + h + 1)
                    turn(h, XZ)
                for h in range(HEADS):
                    pe.wait_ge(act_, s * A_STEP + 16 + h + 1)
                    multiply(h, XZT, Q)
                for h in range(HEADS):
                    pe.wait_ge(vec, s * V_STEP + 16 + h + 1)
                    multiply(h, XZT, Q)
                for h in range(HEADS):
                    pe.wait_ge(vec, s * V_STEP + 24 + h + 1)
                    multiply(h, ZT, Q)
                for h in range(HEADS):
                    pe.wait_ge(act_, s * A_STEP + 24 + h + 1)
                    turn(h, Z)


def layer0_mixer(core, w):
    nc = core.nc
    with ExitStack() as local:
        def sb(name, shape, dtype=F32):
            return local.enter_context(nc.sbuf_tensor("m0_" + name, shape, dtype))
        qT, kT, v = sb("qT", [P, 4, 512]), sb("kT", [P, 4, 512]), sb("v", [P, 4, 512])
        qlT, klT = sb("qlT", [P, 4, LANDMARKS]), sb("klT", [P, 4, LANDMARKS])
        a3v, zav = sb("a3v", [P, 2, 512]), sb("zav", [P, 2, 512])
        Wqkv = core.section(0, 4, 3 * DIM)
        L = {}

        def issue(sp):
            for j in range(3):
                L[j] = core.load(sp, Wqkv[:, :, j * DIM:(j + 1) * DIM], weights(w["m0_Wqkv"], (j * DIM, (j + 1) * DIM)))

        def finish(t, engine, ps, chain):
            m = t % 4
            if t < 4:
                return nc.scalar.mul(qT[:, m, :], ps, HEAD ** -0.5)
            return copy_out(nc, engine, (kT if t < 8 else v)[:, m, :], ps)
        with Stage(core, "m0_load") as st:
            @st.block.sync
            def _(sp):
                issue(sp)
        products_stage(core, "m0_qkv",
                       turned_tiles(core.xnT, Wqkv[:, :, 0:DIM], "A", [lambda: L[0]])
                       + turned_tiles(core.xnT, Wqkv[:, :, DIM:2 * DIM], "V", [lambda: L[1]])
                       + linear_tiles(core.xnT, Wqkv[:, :, 2 * DIM:], "AV", [lambda: L[2]]), finish)
        with Stage(core, "m0_landmarks") as st:
            chain = st.chain(nc.vector, "vector_chain")

            @st.block.vector
            def _(dve):
                for full, marks in ((qT, qlT), (kT, klT)):
                    pairs = full[:].rearrange("p c (n two) -> p c n two", two=2)
                    chain(nc.vector.tensor_tensor(marks[:], pairs[:, :, :, 0], pairs[:, :, :, 1], ALU.add))
                    chain(nc.vector.tensor_scalar(marks[:], marks[:], 0.5, None, ALU.mult))

        def head(x, h):
            return x[HEAD * (h % 2):HEAD * (h % 2) + HEAD, h // 2]
        by_landmarks = [(h, i) for h in range(HEADS) for i in range(2)]

        def values3(u, turned):
            h, i = by_landmarks[u]
            return 4 + i, h * HEAD, (h + 1) * HEAD, [(turned[:, c, :], v[:, c, h * HEAD:(h + 1) * HEAD]) for c in range(4)]

        def per_head(x):
            return x.rearrange("p (h d) -> p h d", h=HEADS)

        def normalise(chain, count, tiles, dst, add=False):
            chain(nc.vector.reciprocal(core.sums[:, 0:count], core.sums[:, 0:count]))
            s = core.sums[:, 0:count].rearrange("p (h i) -> p i h", i=tiles)
            for i in range(tiles):
                chain(nc.vector.tensor_tensor(per_head(dst[:, i, :]), per_head(core.bank(4 + i)),
                                              s[:, i, :].unsqueeze(2).to_broadcast([P, HEADS, HEAD]), ALU.mult))
        softmax_stage(core, "m0_attn3", [[(head(qlT, h)[:, i * P:(i + 1) * P], head(kT, h))] for h, i in by_landmarks],
                      NODES, values=values3, finish=lambda chain: normalise(chain, 16, 2, a3v))

        big = lambda first: core.wpool[:, first * 4096:(first + 1) * 4096].rearrange("p (h c n) -> p h c n", h=HEADS, c=2)
        XT, Z, ZT = big(0), big(1), big(2)
        softmax_stage(core, "m0_attn2", [[(head(qlT, h)[:, i * P:(i + 1) * P], head(klT, h))] for h, i in by_landmarks],
                      LANDMARKS, normal=True, keep=lambda u: ZT[:, by_landmarks[u][0], by_landmarks[u][1], :],
                      turned=lambda u: XT[:, by_landmarks[u][0], :, by_landmarks[u][1] * P:(by_landmarks[u][1] + 1) * P])
        pinv_stage(core, XT, Z, ZT)

        products_stage(core, "m0_inverse_values",
                       [Tile([(P, h * HEAD, (h + 1) * HEAD, [(ZT[:, h, c, i * P:(i + 1) * P], a3v[:, c, h * HEAD:(h + 1) * HEAD])
                                                            for c in range(2)]) for h in range(HEADS)], "VA"[i])
                        for i in range(2)], lambda t, e, ps, chain: copy_out(nc, e, zav[:, t, :], ps))

        by_rows = [(h, i) for h in range(HEADS) for i in range(TILES)]

        def values1(u, turned):
            h, i = by_rows[u]
            return 4 + i, h * HEAD, (h + 1) * HEAD, [(turned[:, c, :], zav[:, c, h * HEAD:(h + 1) * HEAD]) for c in range(2)]

        def finish1(chain):
            normalise(chain, 32, TILES, qT)
            chain(nc.vector.tensor_tensor(core.branches[:], core.branches[:], qT[:], ALU.add))
        softmax_stage(core, "m0_attn1", [[(head(qT, h)[:, i * P:(i + 1) * P], head(klT, h))] for h, i in by_rows],
                      LANDMARKS, values=values1, finish=finish1)


def linear_attention(core, name, q_turned, k_rows, v_rows, out, epsilon=0.0, factor=None):
    nc = core.nc
    pairs = HEADS // 2
    with ExitStack() as local:
        def sb(n, shape):
            return local.enter_context(nc.sbuf_tensor(f"{name}_{n}", shape, F32))
        kv, k_sum, inverse = sb("kv", [P, pairs, P]), sb("k_sum", [P, pairs, 2]), sb("inverse", [P, 4, HEADS])
        with Stage(core, name + "_kv") as st:
            ready, chain = st.sem("products_ready"), st.chain(nc.vector, "vector_chain")

            @st.block.tensor
            def _(pe):
                for j in range(pairs):
                    cols = slice(j * P, (j + 1) * P)
                    last = product(nc, core, core.bank(0)[:, cols], [(k_rows[:, c, cols], v_rows[:, c, cols]) for c in range(4)])
                for j in range(pairs if factor is None else 0):
                    cols = slice(j * P, (j + 1) * P)
                    last = product(nc, core, core.bank(1)[:, 2 * j:2 * j + 2],
                                   [(k_rows[:, c, cols], core.ones[:, 0:2]) for c in range(4)])
                last.then_inc(ready, 1)

            @st.block.vector
            def _(dve):
                chain(nc.vector.memset(kv[:], 0.0))
                chain(nc.vector.memset(k_sum[:], 0.0))
                dve.wait_ge(ready, 1)
                for b in range(2):
                    half = slice(b * HEAD, (b + 1) * HEAD)
                    chain(nc.vector.tensor_copy(kv[half, :, half], core.bank(0)[half].rearrange("p (j n) -> p j n", j=pairs)[:, :, half]))
                    if factor is not None:
                        continue
                    chain(nc.vector.tensor_copy(k_sum[half, :, b], core.bank(1)[half, 0:2 * pairs].rearrange("p (j n) -> p j n", j=pairs)[:, :, b]))
        with Stage(core, name + "_out") as st:
            ready, taken, chain = st.sem("products_ready"), st.sem("banks_taken"), st.chain(nc.vector, "vector_chain")

            @st.block.tensor
            def _(pe):
                for i in range(TILES):
                    rows = slice(i * P, (i + 1) * P)
                    for j in range(pairs):
                        last = product(nc, core, core.bank(2 * i)[:, j * P:(j + 1) * P], [(q_turned[:, j, rows], kv[:, j, :])])
                    for j in range(pairs if factor is None else 0):
                        last = product(nc, core, core.bank(2 * i + 1)[:, 2 * j:2 * j + 2], [(q_turned[:, j, rows], k_sum[:, j, :])])
                    last.then_inc(ready, 1)

            @st.block.vector
            def _(dve):
                for i in range(TILES):
                    dve.wait_ge(ready, i + 1)
                    if factor is None:
                        chain(nc.vector.tensor_scalar(inverse[:, i, :], core.bank(2 * i + 1)[:, 0:HEADS], epsilon, None, ALU.add))
                        chain(nc.vector.reciprocal(inverse[:, i, :], inverse[:, i, :]))
                    by = inverse[:, i, :] if factor is None else factor[:, i, :]
                    chain(nc.vector.tensor_tensor(out[:, i, :].rearrange("p (h d) -> p h d", h=HEADS),
                                                  core.bank(2 * i).rearrange("p (h d) -> p h d", h=HEADS),
                                                  by.unsqueeze(2).to_broadcast([P, HEADS, HEAD]), ALU.mult))


def phi_stage(core, name, x, scratch):
    nc = core.nc
    with Stage(core, name) as st:
        clamped, exponed = st.sem("minimum_ready"), st.sem("exponential_ready")

        @st.block.vector
        def _(dve):
            for j, a in enumerate(x):
                nc.vector.tensor_scalar(scratch[j][:], a[:], 0.0, None, ALU.min).then_inc(clamped, 1)
            for j, a in enumerate(x):
                dve.wait_ge(exponed, j + 1)
                nc.vector.scalar_tensor_tensor(out=a[:], in0=a[:], scalar=0.0, in1=scratch[j][:], op0=ALU.max, op1=ALU.add)

        @st.block.scalar
        def _(act):
            for j in range(len(x)):
                act.wait_ge(clamped, j + 1)
                nc.scalar.activation(scratch[j][:], scratch[j][:], ACT.Exp).then_inc(exponed, 1)


def layer1_mixer(core, w):
    nc = core.nc
    part = [core.section(j) for j in range(12)]
    qT, k, v, s0, s1, out = part[4], part[5], part[6], part[7], part[8], part[9]
    with ExitStack() as local:
        rows = local.enter_context(nc.sbuf_tensor("m1_rows", [P, 1, 512], F32))
        L = {}
        with Stage(core, "m1_load") as st:
            @st.block.sync
            def _(sp):
                for j in range(3):
                    L[j] = core.load(sp, part[j], weights(w["m1_Wqkv"], (j * DIM, (j + 1) * DIM)))
                L[3] = core.load(sp, part[3], weights(w["m1_Wout"]))
                L["rows"] = core.load(sp, rows[:], w["m1_rows"].rearrange("(o r) n -> o r n", o=1).to_broadcast([P, 1, 512]))
        products_stage(core, "m1_qkv",
                       turned_tiles(core.xnT, part[0], "VA", [lambda: L[0]]) + linear_tiles(core.xnT, part[1], "VA", [lambda: L[1]])
                       + linear_tiles(core.xnT, part[2], "VA", [lambda: L[2]]),
                       lambda t, e, ps, chain: copy_out(nc, e, (qT, k, v)[t // 4][:, t % 4, :], ps))
        phi_stage(core, "m1_phi", (qT, k), (s0, s1))
        linear_attention(core, "m1", qT, k, v, out, 1e-6)
        transpose_stage(core, "m1_turn", s0, rows_of(out))

        def finish(t, e, ps, chain):
            chain(nc.vector.tensor_tensor(out[:, t, :], ps, rows[:, 0, :], ALU.add))
            return nc.vector.tensor_tensor(core.branches[:, t, :], core.branches[:, t, :], out[:, t, :], ALU.add)
        products_stage(core, "m1_out", linear_tiles(s0, part[3], "V", [lambda: L[3]]), finish, params=[lambda: L["rows"]])


def layer2_mixer(core, w):
    nc = core.nc
    part = [core.section(j) for j in range(12)]
    qT, k, v, s0, s1, out, normed, nT = part[4:12]
    with ExitStack() as local:
        rows = local.enter_context(nc.sbuf_tensor("m2_rows", [P, 5, 512], F32))
        cols = local.enter_context(nc.sbuf_tensor("m2_cols", [P, 4], F32))
        L = {}

        def issue(sp):
            L["rows"] = core.load(sp, rows[:], w["m2_rows"].rearrange("(o r) n -> o r n", o=1).to_broadcast([P, 5, 512]))
            L["cols"] = core.load(sp, cols[:], w["m2_cols"])
            for j in range(3):
                L[j] = core.load(sp, part[j], weights(w["m2_Wqkv"], (j * DIM, (j + 1) * DIM)))
            L[3] = core.load(sp, part[3], weights(w["m2_Wout"]))
        norm_stage(core, "m2_norm", core.xn, normed, scale=rows[:, 3, :], shift=rows[:, 4, :], issue=issue,
                   params=[lambda: L["rows"]])
        transpose_stage(core, "m2_turn_in", nT, rows_of(normed))

        def finish_qkv(t, e, ps, chain):
            m = t % 4
            if t < 4:
                return nc.scalar.activation(qT[:, m, :], ps, ACT.Identity, bias=cols[:, m:m + 1])
            return nc.vector.tensor_tensor((k if t < 8 else v)[:, m, :], ps, rows[:, t // 4 - 1, :], ALU.add)
        products_stage(core, "m2_qkv",
                       turned_tiles(nT, part[0], "A", [lambda: L[0]]) + linear_tiles(nT, part[1], "V", [lambda: L[1]])
                       + linear_tiles(nT, part[2], "V", [lambda: L[2]]), finish_qkv, params=[lambda: L["cols"]])
        phi_stage(core, "m2_phi", (qT, k), (s0, s1))
        linear_attention(core, "m2", qT, k, v, out, 1e-8)
        transpose_stage(core, "m2_turn_out", s0, rows_of(out))

        def finish(t, e, ps, chain):
            chain(nc.vector.tensor_tensor(out[:, t, :], ps, rows[:, 2, :], ALU.add))
            chain(nc.vector.tensor_tensor(out[:, t, :], out[:, t, :], core.xn[:, t, :], ALU.add))
            return nc.vector.tensor_tensor(core.branches[:, t, :], core.branches[:, t, :], out[:, t, :], ALU.add)
        products_stage(core, "m2_out", linear_tiles(s0, part[3], "V", [lambda: L[3]]), finish)


def gate_stage(core, name, weight, bias, experts, gate, rule):
    nc = core.nc
    with ExitStack() as local, Stage(core, name) as st:
        def sb(n, shape, dtype=F32):
            return local.enter_context(nc.sbuf_tensor(f"{name}_{n}", shape, dtype))
        w_sb, b_sb = sb("weight", [P, 4, experts]), sb("bias", [P, experts])
        scores, biased = sb("scores", [P, 4, experts]), sb("biased", [P, 4, experts])
        tops, tops_biased = sb("tops", [P, 4, 8]), sb("tops_biased", [P, 4, 8])
        index, index_f = sb("index", [P, 4, 8], U32), sb("index_f", [P, 4, 8])
        share, total = sb("share", [P, 4, 2]), sb("total", [P, 4])
        hot = sb("hot", [P, experts])
        weight_landed, bias_landed, ready = st.sem("weight_landed"), st.sem("bias_landed"), st.sem("scores_ready")
        tops_ready, shares_ready = st.sem("tops_ready"), st.sem("shares_ready")
        chain = st.chain(nc.vector, "vector_chain")

        @st.block.sync
        def _(sp):
            sp.dma_start(w_sb[:], weights(weight)).then_inc(weight_landed, 16)
            sp.dma_start(b_sb[:], bias.to_broadcast([P, experts])).then_inc(bias_landed, 16)

        @st.block.tensor
        def _(pe):
            pe.wait_ge(weight_landed, 16)
            for i in range(TILES):
                last = product(nc, core, core.bank(0)[:, i * experts:(i + 1) * experts],
                               [(core.xnT[:, c, i * P:(i + 1) * P], w_sb[:, c, :]) for c in range(4)])
            last.then_inc(ready, 1)

        @st.block.scalar
        def _(act):
            act.wait_ge(tops_ready, 1)
            if rule == "softmax":
                nc.scalar.activation(share[:, :, 1], share[:, :, 0], ACT.Exp).then_inc(shares_ready, 1)
            else:
                nc.scalar.activation(share[:], tops[:, :, 0:2], ACT.Sigmoid).then_inc(shares_ready, 1)

        @st.block.vector
        def _(dve):
            dve.wait_ge(bias_landed, 16)
            dve.wait_ge(ready, 1)
            chain(nc.vector.tensor_copy(scores[:], core.bank(0)[:, 0:4 * experts].rearrange("p (i e) -> p i e", i=4)))
            chain(nc.vector.tensor_tensor(biased[:], scores[:], b_sb[:].unsqueeze(1).to_broadcast([P, 4, experts]), ALU.add))
            for i in range(TILES):
                chain(nc.vector.max(tops_biased[:, i, :], biased[:, i, :]))
                chain(nc.vector.max_index(index[:, i, :], tops_biased[:, i, :], biased[:, i, :]))
            chain(nc.vector.tensor_copy(index_f[:], index[:]))
            if rule == "softmax":
                nc.vector.tensor_tensor(share[:, :, 0], tops_biased[:, :, 1], tops_biased[:, :, 0], ALU.subtract).then_inc(tops_ready, 1)
                dve.wait_ge(shares_ready, 1)
                chain(nc.vector.tensor_scalar(total[:], share[:, :, 1], 1.0, None, ALU.add))
                chain(nc.vector.reciprocal(share[:, :, 0], total[:]))
                chain(nc.vector.tensor_tensor(share[:, :, 1], share[:, :, 1], share[:, :, 0], ALU.mult))
            else:
                for i in range(TILES):
                    chain(nc.vector.max(tops[:, i, :], scores[:, i, :]))
                nc.vector.tensor_copy(total[:], tops[:, :, 0]).then_inc(tops_ready, 1)
                dve.wait_ge(shares_ready, 1)
                chain(nc.vector.tensor_tensor(total[:], share[:, :, 0], share[:, :, 1], ALU.add))
                chain(nc.vector.reciprocal(total[:], total[:]))
                chain(nc.vector.tensor_tensor(share[:], share[:], total[:].unsqueeze(2).to_broadcast([P, 4, 2]), ALU.mult))
                chain(nc.vector.memset(gate[:], 1.0))
            for i in range(TILES):
                chain(nc.vector.tensor_scalar(gate[:, i, 0:experts], core.iota[:, 0:experts], index_f[:, i, 0:1], share[:, i, 0:1],
                                              ALU.is_equal, ALU.mult))
                chain(nc.vector.tensor_scalar(hot[:], core.iota[:, 0:experts], index_f[:, i, 1:2], share[:, i, 1:2],
                                              ALU.is_equal, ALU.mult))
                chain(nc.vector.tensor_tensor(gate[:, i, 0:experts], gate[:, i, 0:experts], hot[:], ALU.add))


def experts_stage(core, name, w1, w3, w2, gate, experts):
    nc = core.nc
    hidden = 2 * DIM
    chunks = hidden // P
    W1 = [core.section(6 * b, 4, hidden) for b in range(2)]
    W3 = [core.section(6 * b + 2, 4, hidden) for b in range(2)]
    W2 = [core.section(6 * b + 4, chunks, DIM) for b in range(2)]
    with ExitStack() as local, Stage(core, name) as st:
        hT = local.enter_context(nc.sbuf_tensor(name + "_hT", [P, chunks, NODES], F32))
        silu = local.enter_context(nc.sbuf_tensor(name + "_silu", [P, 2, NODES], F32))
        landed = {(n, b): st.sem(f"{n}_landed_{b}") for n in ("w1", "w3", "w2") for b in range(2)}
        ready, silu_ready, hidden_ready = st.sem("products_ready"), st.sem("silu_ready"), st.sem("hidden_ready")
        y_ready, y_taken = st.sem("outputs_ready"), st.sem("outputs_added")
        pairs = experts // 2

        def load(sp, e, b):
            for n, dst, src in (("w1", W1, w1), ("w3", W3, w3), ("w2", W2, w2)):
                sp.dma_start(dst[b], src[bass.ds(e, 1)].rearrange("o (c p) n -> p (o c) n", p=P)).then_inc(landed[n, b], 16)

        @st.block.sync
        def _(sp):
            load(sp, 0, 0)
            load(sp, 1, 1)
            with sp.Fori(1, pairs) as s:
                for b in range(2):
                    sp.wait_ge(y_ready, 8 * s + 4 * b - 4)
                    load(sp, 2 * s + b, b)
            if experts % 2:
                sp.wait_ge(y_ready, 4 * (experts - 2))
                load(sp, experts - 1, 0)

        @st.block.tensor
        def _(pe):
            def one(e, b, use):
                pe.wait_ge(landed["w1", b], 16 * use)
                for m in range(chunks):
                    if m >= 2:
                        pe.wait_ge(hidden_ready, chunks * e + m - 1)
                    for j, W in enumerate((W1[b], W3[b])):
                        if m == 0 and j == 1:
                            pe.wait_ge(landed["w3", b], 16 * use)
                        product(nc, core, core.bank(2 * (m % 2) + j),
                                [(W[:, c, m * P:(m + 1) * P], core.xnT[:, c, :]) for c in range(4)]).then_inc(ready, 1)
                pe.wait_ge(landed["w2", b], 16 * use)
                pe.wait_ge(hidden_ready, chunks * e + chunks - 1)
                for i in range(TILES):
                    for c in range(chunks):
                        if i == 0 and c == chunks - 1:
                            pe.wait_ge(hidden_ready, chunks * e + chunks)
                        last = nc.tensor.matmul(core.bank(4 + i), hT[:, c, i * P:(i + 1) * P], W2[b][:, c, :],
                                                start=(c == 0), stop=(c == chunks - 1))
                    last.then_inc(y_ready, 1)
            with pe.Fori(0, pairs) as s:
                for b in range(2):
                    one(2 * s + b, b, s + 1)
            if experts % 2:
                one(experts - 1, 0, pairs + 1)

        @st.block.scalar
        def _(act):
            def one(e):
                for m in range(chunks):
                    act.wait_ge(ready, 2 * chunks * e + 2 * m + 1)
                    if m >= 2:
                        act.wait_ge(hidden_ready, chunks * e + m - 1)
                    nc.scalar.activation(silu[:, m % 2, :], core.bank(2 * (m % 2)), ACT.Silu).then_inc(silu_ready, 1)
            with act.Fori(0, pairs) as s:
                for b in range(2):
                    one(2 * s + b)
            if experts % 2:
                one(experts - 1)

        @st.block.vector
        def _(dve):
            def one(e):
                for m in range(chunks):
                    dve.wait_ge(silu_ready, chunks * e + m + 1)
                    dve.wait_ge(ready, 2 * chunks * e + 2 * m + 2)
                    nc.vector.tensor_tensor(hT[:, m, :], core.bank(2 * (m % 2) + 1), silu[:, m % 2, :], ALU.mult).then_inc(hidden_ready, 1)
                dve.wait_ge(hidden_ready, chunks * e + chunks)
                for i in range(TILES):
                    dve.wait_ge(y_ready, TILES * e + i + 1)
                    nc.vector.scalar_tensor_tensor(out=core.x[:, i, :], in0=core.bank(4 + i), scalar=gate[:, i, bass.ds(e, 1)],
                                                   in1=core.x[:, i, :], op0=ALU.mult, op1=ALU.add).then_inc(y_taken, 1)
            with dve.Fori(0, pairs) as s:
                for b in range(2):
                    one(2 * s + b)
            if experts % 2:
                one(experts - 1)


def layer0_ffn(core, w):
    with ExitStack() as local:
        gate = local.enter_context(core.nc.sbuf_tensor("f0_gate", [P, 4, 8], F32))
        gate_stage(core, "f0_gate_stage", w["f0_Wg"], w["f0_bg"], 8, gate, "softmax")
        experts_stage(core, "f0_experts", w["f0_W1"], w["f0_W3"], w["f0_W2"], gate, 8)


def layer1_ffn(core, w):
    with ExitStack() as local:
        gate = local.enter_context(core.nc.sbuf_tensor("f1_gate", [P, 4, 9], F32))
        gate_stage(core, "f1_gate_stage", w["f1_Wg"], w["f1_bg"], 8, gate, "sigmoid")
        experts_stage(core, "f1_experts", w["f1_W1"], w["f1_W3"], w["f1_W2"], gate, 9)


CAPACITY = 128
L2_EXPERTS = 16
L2_HIDDEN = 256


def capacity_gate_stage(core, weight, coefficient, place):
    nc = core.nc
    E = L2_EXPERTS
    with ExitStack() as local, Stage(core, "f2_gate") as st:
        def sb(n, shape, dtype=F32):
            return local.enter_context(nc.sbuf_tensor(f"f2g_{n}", shape, dtype))
        w_sb, raw, negmax, total = sb("weight", [P, 4, E]), sb("raw", [P, 4, E]), sb("negmax", [P, 4]), sb("total", [P, 4])
        tops, index, index_f = sb("tops", [P, 2, 4, 8]), sb("index", [P, 2, 4, 8], U32), sb("index_f", [P, 2, 4, 8])
        mask, position, kept = sb("mask", [P, 2, 4, E]), sb("position", [P, 2, 4, E]), sb("kept", [P, 2, 4, E])
        rest, share, before = sb("rest", [P, 4, E]), sb("share", [P, 2, 4]), sb("before", [P, P])
        landed, ready, maxima, expd = st.sem("weight_landed"), st.sem("logits_ready"), st.sem("maximum_ready"), st.sem("exp_ready")
        masks_ready, counted, kept_ready, total_ready = (st.sem("masks_ready"), st.sem("positions_ready"),
                                                         st.sem("kept_ready"), st.sem("expert_counts_ready"))
        before_ready = st.sem("before_ready")
        chain = st.chain(nc.vector, "vector_chain")

        @st.block.sync
        def _(sp):
            sp.dma_start(w_sb[:], weights(weight)).then_inc(landed, 16)

        @st.block.gpsimd
        def _(pool):
            nc.gpsimd.affine_select(out=before[:], in_=core.ones[:], compare_op=ALU.is_gt, fill=0.0, base=0,
                                    pattern=[[1, P]], channel_multiplier=-1).then_inc(before_ready, 1)

        @st.block.tensor
        def _(pe):
            pe.wait_ge(landed, 16)
            for i in range(TILES):
                last = product(nc, core, core.bank(0)[:, i * E:(i + 1) * E],
                               [(core.xnT[:, c, i * P:(i + 1) * P], w_sb[:, c, :]) for c in range(4)])
            last.then_inc(ready, 1)
            pe.wait_ge(masks_ready, 1)
            pe.wait_ge(before_ready, 1)
            for k in range(2):
                for i in range(TILES):
                    last = product(nc, core, core.bank(1)[:, (4 * k + i) * E:(4 * k + i + 1) * E],
                                   [(core.ones[:], mask[:, k, j, :]) for j in range(i)] + [(before[:], mask[:, k, i, :])])
            last.then_inc(counted, 1)
            pe.wait_ge(kept_ready, 1)
            product(nc, core, core.bank(2)[:, 0:E], [(core.ones[:], kept[:, 0, j, :]) for j in range(TILES)]).then_inc(total_ready, 1)

        @st.block.scalar
        def _(act):
            act.wait_ge(maxima, 1)
            for i in range(TILES):
                last = nc.scalar.activation(raw[:, i, :], core.bank(0)[:, i * E:(i + 1) * E], ACT.Exp, bias=negmax[:, i:i + 1],
                                            accum_out=total[:, i:i + 1])
                last.then_inc(expd, 1)

        @st.block.vector
        def _(dve):
            flat = lambda x: x[:].rearrange("p k i e -> p (k i) e")
            dve.wait_ge(ready, 1)
            nc.vector.tensor_reduce(negmax[:], core.bank(0)[:, 0:4 * E].rearrange("p (i e) -> p i e", i=4), AXIS.X, ALU.max,
                                    negate=True).then_inc(maxima, 1)
            dve.wait_ge(expd, TILES)
            chain(nc.vector.reciprocal(total[:], total[:]))
            chain(nc.vector.tensor_tensor(raw[:], raw[:], total[:].unsqueeze(2).to_broadcast([P, 4, E]), ALU.mult))
            for k, values in enumerate((raw, rest)):
                for i in range(TILES):
                    chain(nc.vector.max(tops[:, k, i, :], values[:, i, :]))
                    chain(nc.vector.max_index(index[:, k, i, :], tops[:, k, i, :], values[:, i, :]))
                chain(nc.vector.tensor_copy(index_f[:, k], index[:, k]))
                for i in range(TILES):
                    last = nc.vector.tensor_scalar(mask[:, k, i, :], core.iota[:, 0:E], index_f[:, k, i, 0:1], None, ALU.is_equal)
                    if k == 0 or i < TILES - 1:
                        chain(last)
                if k == 0:
                    chain(nc.vector.tensor_scalar(rest[:], mask[:, 0], -1.0, 1.0, ALU.mult, ALU.add))
                    chain(nc.vector.tensor_tensor(rest[:], rest[:], raw[:], ALU.mult))
            last.then_inc(masks_ready, 1)
            chain(nc.vector.tensor_tensor(total[:], tops[:, 0, :, 0], tops[:, 1, :, 0], ALU.add))
            chain(nc.vector.tensor_scalar(total[:], total[:], 1e-9, None, ALU.add))
            chain(nc.vector.reciprocal(total[:], total[:]))
            for k in range(2):
                chain(nc.vector.tensor_tensor(share[:, k], tops[:, k, :, 0], total[:], ALU.mult))
            dve.wait_ge(counted, 1)
            counts = core.bank(1)[:, 0:8 * E].rearrange("p (k i e) -> p k i e", k=2, i=4)
            chain(nc.vector.tensor_tensor(position[:, 0], counts[:, 0], mask[:, 0], ALU.mult))
            chain(nc.vector.tensor_scalar(kept[:, 0], position[:, 0], float(CAPACITY), None, ALU.is_lt))
            nc.vector.tensor_tensor(kept[:, 0], kept[:, 0], mask[:, 0], ALU.mult).then_inc(kept_ready, 1)
            dve.wait_ge(total_ready, 1)
            chain(nc.vector.tensor_copy(rest[:, 0, :], core.bank(2)[:, 0:E]))
            chain(nc.vector.tensor_tensor(position[:, 1], counts[:, 1], rest[:, 0:1, :].to_broadcast([P, 4, E]), ALU.add))
            chain(nc.vector.tensor_tensor(position[:, 1], position[:, 1], mask[:, 1], ALU.mult))
            chain(nc.vector.tensor_scalar(kept[:, 1], position[:, 1], float(CAPACITY), None, ALU.is_lt))
            chain(nc.vector.tensor_tensor(kept[:, 1], kept[:, 1], mask[:, 1], ALU.mult))
            chain(nc.vector.tensor_reduce(place[:].rearrange("p k i -> p (k i)"), flat(position), AXIS.X, ALU.add))
            chain(nc.vector.tensor_tensor(coefficient[:].rearrange("p k i e -> p (k i) e"), flat(kept),
                                          share[:].rearrange("p k i -> p (k i)").unsqueeze(2).to_broadcast([P, 8, E]), ALU.mult))


def layer2_ffn(core, w):
    nc = core.nc
    with ExitStack() as local:
        def sb(n, shape):
            return local.enter_context(nc.sbuf_tensor(f"f2_{n}", shape, F32))
        coefficient, place = sb("coefficient", [P, 2, 4, L2_EXPERTS]), sb("place", [P, 2, 4])
        capacity_gate_stage(core, w["f2_Wg"], coefficient, place)
        hot = sb("hot", [P, 4, CAPACITY])
        combine, dispatch = core.section(0), core.section(1)
        pick = lambda x, b: x[:, b, :].rearrange("p (i c) -> p i c", i=4)
        combineT, inT, y_in = core.section(2), core.section(3), core.section(4)
        hiddenT = core.section(5)
        W1 = [core.section(6 + b, 4, L2_HIDDEN) for b in range(2)]
        W2 = [core.section(8 + b, 2, DIM) for b in range(2)]
        pairs = L2_EXPERTS // 2
        with Stage(core, "f2_experts") as st:
            landed1, landed2 = [st.sem(f"w1_landed_{b}") for b in range(2)], [st.sem(f"w2_landed_{b}") for b in range(2)]
            combined, turned, entered = st.sem("combine_ready"), st.sem("combine_turned"), st.sem("inputs_ready")
            turn_copied, in_copied = st.sem("turned_copied"), st.sem("inputs_copied")
            hid_ready, hid_made, out_ready, out_copied = (st.sem("hidden_ready"), st.sem("hidden_made"),
                                                          st.sem("expert_outputs_ready"), st.sem("expert_outputs_copied"))
            y_ready, y_added = st.sem("row_outputs_ready"), st.sem("row_outputs_added")
            chained = st.sem("vector_chain")

            def load1(sp, e, b):
                sp.dma_start(W1[b], w["f2_W1"][bass.ds(e, 1)].rearrange("o (c p) n -> p (o c) n", p=P)).then_inc(landed1[b], 16)

            def load2(sp, e, b):
                sp.dma_start(W2[b], w["f2_W2"][bass.ds(e, 1)].rearrange("o (c p) n -> p (o c) n", p=P)).then_inc(landed2[b], 16)

            @st.block.sync
            def _(sp):
                for b in range(2):
                    load1(sp, b, b)
                    load2(sp, b, b)
                with sp.Fori(1, pairs) as s:
                    for b in range(2):
                        sp.wait_ge(hid_ready, 2 * s + b - 1)
                        load1(sp, 2 * s + b, b)
                    for b in range(2):
                        sp.wait_ge(out_ready, 2 * s + b - 1)
                        load2(sp, 2 * s + b, b)

            @st.block.tensor
            def _(pe):
                with pe.Fori(0, pairs) as s:
                    for b in range(2):
                        pe.wait_ge(combined, 2 * s + b + 1)
                        for i in range(TILES):
                            last = nc.tensor.transpose(core.bank(b)[:, i * P:(i + 1) * P], pick(combine, b)[:, i, :], core.ident[:])
                        last.then_inc(turned, 1)
                        for c in range(CHUNKS):
                            last = product(nc, core, core.bank(2 + b)[:, c * P:(c + 1) * P],
                                           [(core.xn[:, i, c * P:(c + 1) * P], pick(dispatch, b)[:, i, :]) for i in range(TILES)])
                        last.then_inc(entered, 1)
                    for b in range(2):
                        pe.wait_ge(landed1[b], 16 * s + 16)
                        pe.wait_ge(in_copied, 2 * s + b + 1)
                        for m in range(2):
                            last = product(nc, core, core.bank(b)[:, m * P:(m + 1) * P],
                                           [(W1[b][:, c, m * P:(m + 1) * P], inT[:, b, :].rearrange("p (c n) -> p c n", c=4)[:, c, :])
                                            for c in range(4)])
                        last.then_inc(hid_ready, 1)
                    for b in range(2):
                        pe.wait_ge(landed2[b], 16 * s + 16)
                        pe.wait_ge(hid_made, 2 * s + b + 1)
                        product(nc, core, core.bank(2 + b),
                                [(hiddenT[:, b, m * P:(m + 1) * P], W2[b][:, m, :]) for m in range(2)]).then_inc(out_ready, 1)
                    for b in range(2):
                        pe.wait_ge(out_copied, 2 * s + b + 1)
                        for i in range(TILES):
                            if b == 1:
                                pe.wait_ge(y_added, 8 * s + i + 1)
                            product(nc, core, core.bank(4 + i), [(combineT[:, b, i * P:(i + 1) * P], y_in[:, b, :])]).then_inc(y_ready, 1)

            @st.block.scalar
            def _(act):
                with act.Fori(0, pairs) as s:
                    for b in range(2):
                        act.wait_ge(turned, 2 * s + b + 1)
                        nc.scalar.copy(combineT[:, b, :], core.bank(b)).then_inc(turn_copied, 1)
                        act.wait_ge(entered, 2 * s + b + 1)
                        act.wait_ge(turn_copied, 2 * s + b + 1)
                        nc.scalar.copy(inT[:, b, :], core.bank(2 + b)).then_inc(in_copied, 1)
                    for b in range(2):
                        act.wait_ge(hid_ready, 2 * s + b + 1)
                        nc.scalar.activation(hiddenT[:, b, 0:2 * P], core.bank(b)[:, 0:2 * P], ACT.Relu).then_inc(hid_made, 1)
                    for b in range(2):
                        act.wait_ge(out_ready, 2 * s + b + 1)
                        nc.scalar.copy(y_in[:, b, :], core.bank(2 + b)).then_inc(out_copied, 1)

            @st.block.vector
            def _(dve):
                with dve.Fori(0, pairs) as s:
                    for b in range(2):
                        for i in range(TILES):
                            for k, dst in enumerate((pick(combine, b), hot)):
                                last = nc.vector.tensor_scalar(dst[:, i, :], core.iota[:, 0:CAPACITY], place[:, k, i:i + 1],
                                                               coefficient[:, k, i, bass.ds(2 * s + b, 1)], ALU.is_equal, ALU.mult)
                        last.then_inc(chained, 1)
                        dve.wait_ge(chained, 4 * s + 2 * b + 1)
                        nc.vector.tensor_tensor(pick(combine, b), pick(combine, b), hot[:], ALU.add).then_inc(chained, 1)
                        dve.wait_ge(chained, 4 * s + 2 * b + 2)
                        nc.vector.tensor_scalar(pick(dispatch, b), pick(combine, b), 0.0, None, ALU.is_gt).then_inc(combined, 1)
                    for b in range(2):
                        for i in range(TILES):
                            dve.wait_ge(y_ready, 8 * s + 4 * b + i + 1)
                            if b == 1:
                                dve.wait_ge(y_added, 8 * s + i + 1)
                            nc.vector.tensor_tensor(core.x[:, i, :], core.bank(4 + i), core.x[:, i, :], ALU.add).then_inc(y_added, 1)


def layer1_gnn(core, w):
    nc = core.nc
    part = [core.section(j) for j in range(12)]
    sumT, W = part[0], core.section(1, 8, DIM)
    with ExitStack() as local:
        rows = local.enter_context(nc.sbuf_tensor("g1_rows", [P, 1, 512], F32))
        inverse = local.enter_context(nc.sbuf_tensor("g1_inverse", [P, 4], F32))
        L = {}
        with Stage(core, "g1_degrees") as st:
            chain = st.chain(nc.vector, "vector_chain")

            @st.block.sync
            def _(sp):
                L["W"] = core.load(sp, W, weights(w["g1_W"]))
                L["rows"] = core.load(sp, rows[:], w["g1_rows"].rearrange("(o r) n -> o r n", o=1).to_broadcast([P, 1, 512]))

            @st.block.vector
            def _(dve):
                chain(nc.vector.tensor_reduce(inverse[:], core.edges_to[:], AXIS.X, ALU.add))
                chain(nc.vector.tensor_scalar(inverse[:], inverse[:], 1.0, None, ALU.max))
                chain(nc.vector.reciprocal(inverse[:], inverse[:]))
        products_stage(core, "g1_sums",
                       [Tile([(P, 0, NODES, [(core.xn[:, j, c * P:(c + 1) * P], core.edges_from[:, j, :]) for j in range(TILES)])],
                             "VA"[c % 2]) for c in range(CHUNKS)], lambda t, e, ps, chain: copy_out(nc, e, sumT[:, t, :], ps))

        def tiles():
            out = []
            for i in range(TILES):
                rows_i = slice(i * P, (i + 1) * P)
                out.append(Tile([(P, 0, DIM, [(sumT[:, c, rows_i], W[:, 4 + c, :]) for c in range(4)])], "V", [lambda: L["W"]]))
                out.append(Tile([(P, 0, DIM, [(core.xnT[:, c, rows_i], W[:, c, :]) for c in range(4)])], "V"))
            return out

        def finish(t, e, ps, chain):
            i = t // 2
            out = core.branches[:, i, :]
            if t % 2 == 0:
                return nc.vector.scalar_tensor_tensor(out=out, in0=ps, scalar=inverse[:, i:i + 1], in1=rows[:, 0, :],
                                                      op0=ALU.mult, op1=ALU.add)
            chain(nc.vector.tensor_tensor(out, ps, out, ALU.add))
            return nc.vector.tensor_scalar(out, out, 0.0, None, ALU.max)
        products_stage(core, "g1_out", tiles(), finish, params=[lambda: L["rows"]], ordered=True)


def layer2_gnn(core, w):
    nc = core.nc
    heads = 4
    with ExitStack() as local:
        def sb(name, shape):
            return local.enter_context(nc.sbuf_tensor("g2_" + name, shape, F32))
        rows, cols = sb("rows", [P, 7, 512]), sb("cols", [P, 48])
        v, turned = sb("v", [P, 4, 512]), sb("attention", [P, 4, 512])
        xT = core.section(8, 16, 512)
        Wq, Wk, Wv, Wskip = (core.section(j) for j in range(4))
        qT, kT, mask, h = core.section(4), core.section(5), core.section(6), core.section(7)
        L = {}

        def load_head(n):
            def issue(sp):
                for name, dst in (("g2_Wq", Wq), ("g2_Wk", Wk), ("g2_Wv", Wv), ("g2_Wskip", Wskip)):
                    L[name, n] = core.load(sp, dst, weights(w[name], (n * DIM, (n + 1) * DIM)))
            return issue
        with Stage(core, "g2_mask") as st:
            chain = st.chain(nc.vector, "vector_chain")

            @st.block.sync
            def _(sp):
                L["cols"] = core.load(sp, cols[:], w["g2_cols"])
                L["rows"] = core.load(sp, rows[:], w["g2_rows"].rearrange("(o r) n -> o r n", o=1).to_broadcast([P, 7, 512]))

            @st.block.vector
            def _(dve):
                chain(nc.vector.tensor_scalar(mask[:], core.edges_to[:], 0.5, None, ALU.is_lt))
                nc.vector.tensor_scalar(mask[:], mask[:], MASKED, None, ALU.mult)
        load_stage(core, "g2_load0", load_head(0))
        for n in range(heads):
            def finish(t, e, ps, chain):
                m = t % 4
                if t < 4:
                    return nc.scalar.activation(qT[:, m, :], ps, ACT.Identity, bias=cols[:, 4 * n + m:4 * n + m + 1])
                if t < 8:
                    return nc.scalar.activation(kT[:, m, :], ps, ACT.Identity, bias=cols[:, 16 + 4 * n + m:17 + 4 * n + m])
                return nc.vector.tensor_tensor(v[:, m, :], ps, rows[:, n, :], ALU.add)
            products_stage(core, f"g2_qkv{n}",
                           turned_tiles(core.xnT, Wq, "A", [lambda: L["g2_Wq", n]]) + turned_tiles(core.xnT, Wk, "A", [lambda: L["g2_Wk", n]])
                           + linear_tiles(core.xnT, Wv, "V", [lambda: L["g2_Wv", n]]), finish,
                           params=[lambda: L["rows"], lambda: L["cols"]])
            softmax_stage(core, f"g2_attention{n}",
                          [[(qT[:, c, i * P:(i + 1) * P], kT[:, c, :]) for c in range(4)] for i in range(TILES)], NODES,
                          scale=DIM ** -0.5, mask=lambda u: mask[:, u, :], weigh=lambda u: core.edges_to[:, u, :],
                          turned=lambda u: turned[:, :, u * P:(u + 1) * P])

            def finish_values(t, e, ps, chain):
                c = 4 * n + t
                return nc.scalar.activation(xT[:, c, :], ps, ACT.Identity, bias=cols[:, 32 + c:33 + c])
            products_stage(core, f"g2_values{n}",
                           [Tile([(P, 0, NODES, [(v[:, j, c * P:(c + 1) * P], turned[:, j, :]) for j in range(4)]
                                   + [(Wskip[:, k, c * P:(c + 1) * P], core.xnT[:, k, :]) for k in range(4)])], "A",
                                 [lambda: L["g2_Wskip", n]]) for c in range(CHUNKS)], finish_values)
            if n + 1 < heads:
                load_stage(core, f"g2_load{n + 1}", load_head(n + 1))
        Wlin = core.section(0, 16, 512)

        def issue_lin(sp):
            L["lin"] = core.load(sp, Wlin, weights(w["g2_Wlin"]))
        load_stage(core, "g2_load_lin", issue_lin)

        def finish_out(t, e, ps, chain):
            return nc.vector.tensor_tensor(v[:, t, :], ps, rows[:, 4, :], ALU.add)
        products_stage(core, "g2_lin", linear_tiles(xT, Wlin, "V", [lambda: L["lin"]]), finish_out)

        def finish_first(t, e, ps, chain):
            return nc.vector.tensor_tensor(v[:, t, :], ps, v[:, t, :], ALU.add)
        products_stage(core, "g2_first", [Tile([(P, c * P, (c + 1) * P, [(xT[:, c, i * P:(i + 1) * P], None)]) for c in range(CHUNKS)], "V")
                                          for i in range(TILES)], finish_first)
        norm_stage(core, "g2_norm", v, core.branches, scale=rows[:, 5, :], shift=rows[:, 6, :])


def load_stage(core, name, issue):
    with Stage(core, name) as st:
        @st.block.sync
        def _(sp):
            issue(sp)


MUL = 128
SILU_2MOM = 1.679177
GROUP = 4
BLOCKS = 8


def edges_stage(core, w, table, sums):
    nc = core.nc
    groups = EDGE_TILES // GROUP
    with ExitStack() as local, Stage(core, "g3_edges") as st:
        def sb(n, shape, dtype=F32):
            return local.enter_context(nc.sbuf_tensor("g3e_" + n, shape, dtype))
        attr = sb("attributes", [P, 4 * EDGE_TILES])
        W1, W2, W3, W4 = sb("mlp1", [8, 64]), sb("mlp2", [64, P]), sb("mlp3", [64, P]), sb("mlp4", [64, 4 * MUL])
        feat = sb("features", [8, 2, GROUP * P])
        hid = sb("hidden", [64, 3, GROUP * P])
        senders = sb("senders", [P, 2, GROUP], I32)
        t2, dot = sb("w2_s0", [P, 2, MUL]), sb("dot", [P, 2, MUL])
        gathered = [core.section(2 + b, GROUP, 4 * MUL) for b in range(2)]
        messages = [core.section(4 + 2 * b, GROUP, BLOCKS * MUL) for b in range(2)]
        hot = [core.section(8 + b, GROUP, NODES) for b in range(2)]
        params = st.sem("parameters_landed")
        feat_landed = [st.sem(f"features_landed_{b}") for b in range(2)]
        rows_landed = core.gather_sems
        attr_ready = st.sem("attributes_scaled")
        mlp_ready, mlp_made, tpw_ready = st.sem("mlp_products"), st.sem("mlp_silus"), st.sem("edge_weights_ready")
        t2_ready, m1a_made, message_ready = st.sem("w2_s0_ready"), st.sem("vector_a_made"), st.sem("messages_ready")
        summed, added = st.sem("group_summed"), st.sem("sums_added")
        chained, padded = st.sem("vector_chain"), st.sem("weights_padded")
        LINKS = 3

        @st.block.sync
        def _(sp):
            def features(g, b):
                sp.dma_start(feat[:, b, :], w["g3_feat"][:, bass.ds(g * GROUP * P, GROUP * P)]).then_inc(feat_landed[b], 16)
            for dst, name in ((attr, "g3_attr"), (W1, "g3_mlp1"), (W2, "g3_mlp2"), (W3, "g3_mlp3"), (W4, "g3_mlp4")):
                src = w[name].rearrange("p t m -> p (t m)") if name == "g3_attr" else w[name]
                sp.dma_start(dst[:, 0:src.shape[1]], src).then_inc(params, 16)
            features(0, 0)
            features(1, 1)
            with sp.Fori(1, groups // 2) as s:
                for b in range(2):
                    sp.wait_ge(mlp_ready, 3 * (2 * s + b) - 5)
                    features(2 * s + b, b)

        @st.block.gpsimd
        def _(pool):
            def gather(g, b, first):
                if not first:
                    pool.wait_ge(message_ready, GROUP * g - GROUP)
                nc.gpsimd.tensor_copy(senders[:, b, :], core.src_i[:, bass.ds(GROUP * g, GROUP)])
                pool.drain()
                for j in range(GROUP):
                    nc.gpsimd.indirect_dma_start(
                        out=gathered[b][:, j, :], out_offset=None, in_=table,
                        in_offset=bass.IndirectOffsetOnAxis(ap=senders[:, b, j:j + 1].bitcast(U32), axis=0)).then_inc(rows_landed[b], 16)
            gather(0, 0, True)
            gather(1, 1, True)
            with pool.Fori(1, groups // 2) as s:
                for b in range(2):
                    gather(2 * s + b, b, False)

        @st.block.tensor
        def _(pe):
            def layer(g, n, weight, right):
                if n == 0:
                    pe.wait_ge(feat_landed[g[1]], g[2])
                else:
                    pe.wait_ge(mlp_made, 3 * g[0] + n)
                product(nc, core, core.bank(0)[0:weight.shape[1], :], [(weight[:], right)]).then_inc(mlp_ready, 1)

            def edge_weights(g):
                pe.wait_ge(mlp_made, 3 * g[0] + 3)
                for j in range(GROUP):
                    if g[3]:
                        pe.wait_ge(message_ready, GROUP * g[0] - GROUP + j + 1)
                    product(nc, core, core.bank(4 + j), [(hid[:, 2, j * P:(j + 1) * P], W4[:])]).then_inc(tpw_ready, 1)

            def add_up(g, r, b, first):
                m, half = r // 2, r % 2
                if r == 0:
                    pe.wait_ge(message_ready, GROUP * g + GROUP)
                    pe.wait_ge(m1a_made, GROUP * g + GROUP)
                if not (first and r < 2):
                    pe.wait_ge(added, BLOCKS * g + r)
                product(nc, core, core.bank(1 + r % 2),
                        [(hot[b][:, j, m * P:(m + 1) * P], messages[b][:, j, half * BANK:(half + 1) * BANK])
                         for j in range(GROUP)]).then_inc(summed, 1)

            def group(g, b, use, first, sum_g, sum_first=False):
                info = (g, b, 16 * use, not first)
                layer(info, 0, W1, feat[:, b, :])
                for n, (weight, right) in enumerate(((W2, hid[:, 0, :]), (W3, hid[:, 1, :]))):
                    if sum_g is not None:
                        add_up(sum_g, n, 1 - b, sum_first)
                    layer(info, n + 1, weight, right)
                if sum_g is not None:
                    add_up(sum_g, 2, 1 - b, sum_first)
                edge_weights(info)
                if sum_g is not None:
                    for r in range(3, BLOCKS):
                        add_up(sum_g, r, 1 - b, sum_first)
            pe.wait_ge(params, 80)
            pe.wait_ge(padded, 2)
            group(0, 0, 1, True, None)
            group(1, 1, 1, False, 0, True)
            with pe.Fori(1, groups // 2) as s:
                for b in range(2):
                    group(2 * s + b, b, s + 1, False, 2 * s + b - 1)
            for r in range(BLOCKS):
                add_up(groups - 1, r, 1, False)

        @st.block.scalar
        def _(act):
            def group(g):
                for n in range(3):
                    act.wait_ge(mlp_ready, 3 * g + n + 1)
                    scale = 8 ** -0.5 if n == 0 else SILU_2MOM / 8
                    nc.scalar.activation(hid[:, n, :], core.bank(0)[0:64, :], ACT.Silu, scale=scale).then_inc(mlp_made, 1)

            def vectors_a(g, b):
                for j in range(GROUP):
                    act.wait_ge(t2_ready, GROUP * g + j + 1)
                    for m in range(3):
                        last = nc.scalar.activation(messages[b][:, j, (2 + 2 * m) * MUL:(3 + 2 * m) * MUL], t2[:, j % 2, :], ACT.Copy,
                                                    scale=attr[:, bass.ds(4 * GROUP * g + 4 * j + m + 1, 1)])
                    last.then_inc(m1a_made, 1)
            act.wait_ge(attr_ready, 1)
            with act.Fori(0, groups // 2) as s:
                for b in range(2):
                    group(2 * s + b)
                    vectors_a(2 * s + b, b)

        @st.block.vector
        def _(dve):
            def link(instruction, g, j, n):
                instruction.then_inc(chained, 1)
                dve.wait_ge(chained, (g * GROUP + j) * LINKS + n)

            def message(g, j, b, use, first):
                y = [attr[:, bass.ds(4 * GROUP * g + 4 * j + m, 1)] for m in range(4)]
                if j == 0:
                    dve.wait_ge(rows_landed[b], 16 * GROUP * use)
                dve.wait_ge(tpw_ready, GROUP * g + j + 1)
                part = [core.bank(4 + j)[:, k * MUL:(k + 1) * MUL] for k in range(4)]
                s = [gathered[b][:, j, k * MUL:(k + 1) * MUL] for k in range(4)]
                out = messages[b][:, j, :]
                if not (first and j < 2):
                    dve.wait_ge(m1a_made, GROUP * g + j - 1)
                nc.vector.tensor_tensor(t2[:, j % 2, :], part[1], s[0], ALU.mult).then_inc(t2_ready, 1)
                link(nc.vector.tensor_scalar(dot[:, j % 2, :], s[1], y[1], None, ALU.mult), g, j, 1)
                link(nc.vector.scalar_tensor_tensor(out=dot[:, j % 2, :], in0=s[2], scalar=y[2], in1=dot[:, j % 2, :],
                                                    op0=ALU.mult, op1=ALU.add), g, j, 2)
                link(nc.vector.scalar_tensor_tensor(out=dot[:, j % 2, :], in0=s[3], scalar=y[3], in1=dot[:, j % 2, :],
                                                    op0=ALU.mult, op1=ALU.add), g, j, 3)
                nc.vector.scalar_tensor_tensor(out=out[:, 0:MUL], in0=part[0], scalar=y[0], in1=s[0], op0=ALU.mult, op1=ALU.mult)
                nc.vector.scalar_tensor_tensor(out=out[:, MUL:2 * MUL], in0=part[3], scalar=3 ** -0.5, in1=dot[:, j % 2, :],
                                               op0=ALU.mult, op1=ALU.mult)
                nc.vector.scalar_tensor_tensor(out=out.rearrange("p (m two u) -> p m two u", two=2, u=MUL)[:, 1:4, 1, :],
                                               in0=part[2].unsqueeze(1).to_broadcast([P, 3, MUL]), scalar=y[0],
                                               in1=gathered[b][:, j, MUL:].rearrange("p (m u) -> p m u", m=3),
                                               op0=ALU.mult, op1=ALU.mult)
                nc.vector.tensor_scalar(hot[b][:, j, :], core.iota[:], core.dst_f[:, bass.ds(GROUP * g + j, 1)], None,
                                        ALU.is_equal).then_inc(message_ready, 1)

            def add(g, r):
                dve.wait_ge(summed, BLOCKS * g + r + 1)
                if r == 0:
                    dve.wait_ge(added, BLOCKS * g + 1)
                to = sums[:, r // 2, (r % 2) * BANK:(r % 2 + 1) * BANK]
                nc.vector.tensor_tensor(to, core.bank(1 + r % 2), to, ALU.add).then_inc(added, 1)

            def group(g, b, use, first, sum_g):
                if sum_g is not None:
                    for r in range(3):
                        add(sum_g, r)
                for j in range(GROUP):
                    message(g, j, b, use, first)
                    if sum_g is not None:
                        add(sum_g, 3 + j)
                if sum_g is not None:
                    add(sum_g, 7)
            nc.vector.memset(W2[:, 64:P], 0.0).then_inc(padded, 1)
            nc.vector.memset(W3[:, 64:P], 0.0).then_inc(padded, 1)
            dve.wait_ge(params, 80)
            nc.vector.tensor_scalar(attr[:], attr[:], SILU_2MOM / 8, None, ALU.mult).then_inc(attr_ready, 1)
            dve.wait_ge(attr_ready, 1)
            nc.vector.memset(sums[:], 0.0).then_inc(added, 1)
            group(0, 0, 1, True, None)
            group(1, 1, 1, False, 0)
            with dve.Fori(1, groups // 2) as s:
                for b in range(2):
                    group(2 * s + b, b, s + 1, False, 2 * s + b - 1)
            for r in range(BLOCKS):
                add(groups - 1, r)


def layer3_gnn(core, w):
    nc = core.nc
    with ExitStack() as local:
        def sb(name, shape):
            return local.enter_context(nc.sbuf_tensor("g3_" + name, shape, F32))
        Wup, Wout = sb("Wup", [P, 2 * MUL]), sb("Wout", [P, 2, 2 * MUL])
        upT, up = core.section(2), core.section(3)
        sums = core.section(0, 4, BLOCKS * MUL)
        L = {}

        def issue(sp):
            L["up"] = core.load(sp, Wup[:], w["g3_Wup"])
            L["out"] = core.load(sp, Wout[:], weights(w["g3_Wout"]))
        load_stage(core, "g3_load", issue)

        def blocks(i, c):
            return core.xn[:, i, 0:MUL] if c == 0 else core.xn[:, i, MUL:].rearrange("p (u m) -> p m u", m=3)[:, c - 1, :]
        transpose_stage(core, "g3_turn", upT, blocks)
        products_stage(core, "g3_up",
                       [Tile([(P, c * MUL, (c + 1) * MUL, [(upT[:, c, i * P:(i + 1) * P], Wup[:, (c > 0) * MUL:(c > 0) * MUL + MUL])])
                              for c in range(4)], "V", [lambda: L["up"]]) for i in range(TILES)],
                       lambda t, e, ps, chain: nc.vector.tensor_scalar(up[:, t, :], ps, MUL ** -0.5, None, ALU.mult))
        table = nc.dram_tensor("node_table", (NODES, 4 * MUL), F32, kind="Internal").ap()
        with Stage(core, "g3_table") as st:
            stored = st.sem("table_stored")

            @st.block.sync
            def _(sp):
                sp.dma_start(table.rearrange("(i p) d -> p i d", p=P), up).then_inc(stored, 16)
                sp.wait_ge(stored, 16)
        edges_stage(core, w, table, sums)
        sumsT = core.section(2, BLOCKS, NODES)
        products_stage(core, "g3_turn_sums",
                       [Tile([(P, i * P, (i + 1) * P, [(sums[:, i, c * MUL:(c + 1) * MUL], None)]) for i in range(TILES)], "VA"[c % 2])
                        for c in range(BLOCKS)], lambda t, e, ps, chain: copy_out(nc, e, sumsT[:, t, :], ps))
        scale = 1.0 / (16.0 * 10.0)

        def finish(t, e, ps, chain):
            out = core.branches[:, t, :]
            nc.vector.tensor_scalar(out[:, 0:MUL], ps[:, 0:MUL], scale, None, ALU.mult)
            return nc.vector.tensor_scalar(out[:, MUL:].rearrange("p (u m) -> p m u", m=3), ps[:, MUL:].rearrange("p (m u) -> p m u", m=3),
                                           scale, None, ALU.mult)
        products_stage(core, "g3_out",
                       [Tile([(P, k * MUL, (k + 1) * MUL,
                               [(sumsT[:, 2 * k + c, i * P:(i + 1) * P], Wout[:, c, (k > 0) * MUL:(k > 0) * MUL + MUL]) for c in range(2)])
                              for k in range(4)], "V", [lambda: L["out"]]) for i in range(TILES)], finish)


FLOW_EPS = 1e-6


def flow_stage(core, q, k, v, kse, tmp, factor):
    nc = core.nc
    with ExitStack() as local, Stage(core, "m3_flow") as st:
        sink_in, source_out, sink, source = (local.enter_context(nc.sbuf_tensor(f"m3f_{n}", [P, 4, HEADS], F32))
                                             for n in ("sink_in", "source_out", "sink", "source"))
        total = local.enter_context(nc.sbuf_tensor("m3f_total", [P, HEADS], F32))
        sigmoids, column_sums = st.sem("sigmoids_ready"), st.sem("column_sums_ready")
        weighted, clipped, expd = st.sem("weighted_ready"), st.sem("clipped_ready"), st.sem("allocations_ready")
        chain = st.chain(nc.vector, "vector_chain")

        def over_rows(bank, x):
            return product(nc, core, bank, [(core.ones[:], x[:, i, :]) for i in range(TILES)])

        by_head = lambda x: x.rearrange("p i (h d) -> p (i h) d", h=HEADS)
        spread = lambda x: x[:].rearrange("p i h -> p (i h)").unsqueeze(2).to_broadcast([P, 4 * HEADS, HEAD])

        @st.block.scalar
        def _(act):
            nc.scalar.activation(q, q, ACT.Sigmoid).then_inc(sigmoids, 1)
            nc.scalar.activation(k, k, ACT.Sigmoid).then_inc(sigmoids, 1)
            act.wait_ge(clipped, 1)
            nc.scalar.activation(sink[:], sink[:], ACT.Sigmoid).then_inc(expd, 1)
            nc.scalar.activation(source[:], source[:], ACT.Exp).then_inc(expd, 1)

        @st.block.tensor
        def _(pe):
            pe.wait_ge(sigmoids, 1)
            over_rows(core.bank(0), q).then_inc(column_sums, 1)
            pe.wait_ge(sigmoids, 2)
            over_rows(core.bank(1), k).then_inc(column_sums, 1)
            pe.wait_ge(weighted, 1)
            over_rows(core.bank(2), tmp[0]).then_inc(column_sums, 1)
            pe.wait_ge(weighted, 2)
            over_rows(core.bank(3), tmp[1]).then_inc(column_sums, 1)
            pe.wait_ge(expd, 2)
            over_rows(core.bank(4)[:, 0:HEADS], source).then_inc(column_sums, 1)

        @st.block.vector
        def _(dve):
            def against(x, bank, dst):
                chain(nc.vector.tensor_scalar(kse, bank, FLOW_EPS, None, ALU.add))
                for i in range(TILES):
                    chain(nc.vector.scalar_tensor_tensor(out=core.branch_tmp[:, i, :], in0=x[:, i, :], scalar=FLOW_EPS, in1=kse,
                                                         op0=ALU.add, op1=ALU.mult))
                chain(nc.vector.tensor_reduce(dst[:].rearrange("p i h -> p (i h)"), by_head(core.branch_tmp), AXIS.X, ALU.add))
            dve.wait_ge(sigmoids, 2)
            dve.wait_ge(column_sums, 1)
            against(k, core.bank(0), source_out)
            dve.wait_ge(column_sums, 2)
            against(q, core.bank(1), sink_in)
            chain(nc.vector.reciprocal(source_out[:], source_out[:]))
            chain(nc.vector.reciprocal(sink_in[:], sink_in[:]))
            nc.vector.tensor_tensor(by_head(tmp[0]), by_head(k), spread(source_out), ALU.mult).then_inc(weighted, 1)
            nc.vector.tensor_tensor(by_head(tmp[1]), by_head(q), spread(sink_in), ALU.mult).then_inc(weighted, 1)
            dve.wait_ge(column_sums, 3)
            against(q, core.bank(2), sink)
            dve.wait_ge(column_sums, 4)
            against(k, core.bank(3), source)
            nc.vector.tensor_scalar(source[:], source[:], -1.0, 1.0, ALU.max, ALU.min).then_inc(clipped, 1)
            dve.wait_ge(expd, 1)
            chain(nc.vector.tensor_tensor(factor[:], sink_in[:], sink[:], ALU.mult))
            dve.wait_ge(column_sums, 5)
            chain(nc.vector.reciprocal(total[:], core.bank(4)[:, 0:HEADS]))
            chain(nc.vector.tensor_scalar(total[:], total[:], float(NODES), None, ALU.mult))
            chain(nc.vector.tensor_tensor(source[:], source[:], total[:].unsqueeze(1).to_broadcast([P, 4, HEADS]), ALU.mult))
            chain(nc.vector.tensor_tensor(by_head(v), by_head(v), spread(source), ALU.mult))


def layer3_mixer(core, w):
    nc = core.nc
    part = [core.section(j) for j in range(12)]
    Wq, Wk, Wv, Wo, W1, q, k, v, s0, s1 = part[0:10]
    W1, W2 = core.section(4, 4, 256), core.section(10, 2, DIM)
    core.branch_tmp = part[11]
    with ExitStack() as local:
        rows = local.enter_context(nc.sbuf_tensor("m3_rows", [P, 9, 512], F32))
        cols = local.enter_context(nc.sbuf_tensor("m3_cols", [P, 2], F32))
        factor = local.enter_context(nc.sbuf_tensor("m3_factor", [P, 4, HEADS], F32))
        L = {}

        def issue(sp):
            L["rows"] = core.load(sp, rows[:], w["m3_rows"].rearrange("(o r) n -> o r n", o=1).to_broadcast([P, 9, 512]))
            for name, dst in (("Wq", Wq), ("Wk", Wk), ("Wv", Wv), ("Wo", Wo), ("W1", W1), ("W2", W2)):
                L[name] = core.load(sp, dst, weights(w["m3_" + name]))
            L["cols"] = core.load(sp, cols[:], w["m3_cols"])
        norm_stage(core, "m3_norm1", core.xn, s0, scale=rows[:, 5, :], shift=rows[:, 6, :], issue=issue, params=[lambda: L["rows"]])
        transpose_stage(core, "m3_turn1", s1, rows_of(s0))
        products_stage(core, "m3_qkv",
                       linear_tiles(s1, Wq, "V", [lambda: L["Wq"]]) + linear_tiles(s1, Wk, "V", [lambda: L["Wk"]])
                       + linear_tiles(s1, Wv, "V", [lambda: L["Wv"]]),
                       lambda t, e, ps, chain: nc.vector.tensor_tensor((q, k, v)[t // 4][:, t % 4, :], ps, rows[:, t // 4, :], ALU.add))
        flow_stage(core, q, k, v, core.scores[:, 0, :], (s0, s1), factor)
        qT, mixed = Wq, Wk
        transpose_stage(core, "m3_turn_q", qT, rows_of(q))
        linear_attention(core, "m3", qT, k, v, mixed, factor=factor)
        transpose_stage(core, "m3_turn_mixed", s0, rows_of(mixed))

        def finish_attention(t, e, ps, chain):
            chain(nc.vector.tensor_tensor(q[:, t, :], ps, rows[:, 3, :], ALU.add))
            return nc.vector.tensor_tensor(q[:, t, :], q[:, t, :], core.xn[:, t, :], ALU.add)
        products_stage(core, "m3_attention_out", linear_tiles(s0, Wo, "V", [lambda: L["Wo"]]), finish_attention)
        norm_stage(core, "m3_norm2", q, s0, scale=rows[:, 7, :], shift=rows[:, 8, :])
        transpose_stage(core, "m3_turn2", s1, rows_of(s0))
        uT = v
        products_stage(core, "m3_up", turned_tiles(s1, W1, "A", [lambda: L["W1"]]),
                       lambda t, e, ps, chain: nc.scalar.activation(uT[:, t, :], ps, ACT.Gelu, bias=cols[:, t:t + 1]),
                       params=[lambda: L["cols"]])

        def finish(t, e, ps, chain):
            chain(nc.vector.tensor_tensor(k[:, t, :], ps, rows[:, 4, :], ALU.add))
            chain(nc.vector.tensor_tensor(k[:, t, :], k[:, t, :], q[:, t, :], ALU.add))
            return nc.vector.tensor_tensor(core.branches[:, t, :], core.branches[:, t, :], k[:, t, :], ALU.add)
        products_stage(core, "m3_down", linear_tiles(uT[:, 0:2], W2, "V", [lambda: L["W2"]]), finish)


TOP = 128
PROCESS = 1024


def top_stage(core, acts, work, weights_out):
    nc = core.nc
    taken = -1.0e30
    with ExitStack() as local, Stage(core, "f3_top") as st:
        best, negmax, total = (local.enter_context(nc.sbuf_tensor(f"f3_{n}", [P, 4, s], F32))
                               for n, s in (("best", 8), ("negmax", 1), ("total", 1)))
        chain = st.chain(nc.vector, "vector_chain")
        maxima, expd = st.sem("maximum_ready"), st.sem("exp_ready")

        @st.block.scalar
        def _(act):
            for i in range(TILES):
                act.wait_ge(maxima, i + 1)
                nc.scalar.activation(weights_out[:, i, :], acts[:, i, :], ACT.Exp, bias=negmax[:, i, :]).then_inc(expd, 1)

        @st.block.vector
        def _(dve):
            for i in range(TILES):
                nc.vector.tensor_reduce(negmax[:, i, :], acts[:, i, :], AXIS.X, ALU.max, negate=True).then_inc(maxima, 1)
            for r in range(TOP // 8):
                for i in range(TILES):
                    src = acts if r == 0 else work
                    if r > 0 and i == 0:
                        pass
                    chain(nc.vector.max(best[:, i, :], src[:, i, :]))
                    chain(nc.vector.match_replace(work[:, i, :], best[:, i, :], src[:, i, :], taken))
            for i in range(TILES):
                dve.wait_ge(expd, i + 1)
                chain(nc.vector.scalar_tensor_tensor(out=weights_out[:, i, :], in0=work[:, i, :], scalar=taken,
                                                     in1=weights_out[:, i, :], op0=ALU.is_equal, op1=ALU.mult))
                chain(nc.vector.tensor_reduce(total[:, i, :], weights_out[:, i, :], AXIS.X, ALU.add))
                chain(nc.vector.reciprocal(total[:, i, :], total[:, i, :]))
                chain(nc.vector.tensor_scalar(weights_out[:, i, :], weights_out[:, i, :], total[:, i, :], None, ALU.mult))


def layer3_ffn(core, w):
    nc = core.nc
    inT = core.section(0, 2, NODES)
    acts, work, attention = core.section(1, 4, PROCESS), core.section(3, 4, PROCESS), core.section(5, 4, PROCESS)
    attentionT = core.section(1, 8, NODES)
    ip, pw = core.section(7, 4, 256), core.section(8, 2, PROCESS)
    pv, ow, op = core.section(9, 8, 256), core.section(10, 2, 256), core.section(11, 2, DIM)
    aggT = core.section(3, 2, NODES)
    outT = core.section(4, 2, NODES)
    L = {}

    def issue(sp):
        for name, dst in (("ip", ip), ("pw", pw), ("pv", pv), ("ow", ow), ("op", op)):
            L[name] = core.load(sp, dst, weights(w["f3_" + name]))

    load_stage(core, "f3_load", issue)
    products_stage(core, "f3_in", turned_tiles(core.xnT, ip, "A", [lambda: L["ip"]]),
                   lambda t, e, ps, chain: nc.scalar.activation(inT[:, t, :], ps, ACT.Gelu))
    products_stage(core, "f3_process",
                   [Tile([(P, 0, 512, [(inT[:, c, i * P:(i + 1) * P], pw[:, c, n * 512:(n + 1) * 512]) for c in range(2)])], "A",
                         [lambda: L["pw"]]) for i in range(TILES) for n in range(2)],
                   lambda t, e, ps, chain: nc.scalar.activation(acts[:, t // 2, (t % 2) * 512:(t % 2 + 1) * 512], ps, ACT.Gelu))
    top_stage(core, acts, work, attention)
    products_stage(core, "f3_turn",
                   [Tile([(P, i * P, (i + 1) * P, [(attention[:, i, c * P:(c + 1) * P], None)]) for i in range(TILES)], "VA"[c % 2])
                    for c in range(8)], lambda t, e, ps, chain: copy_out(nc, e, attentionT[:, t, :], ps))
    products_stage(core, "f3_values", turned_tiles(attentionT, pv, "VA", [lambda: L["pv"]]),
                   lambda t, e, ps, chain: copy_out(nc, e, aggT[:, t, :], ps))
    products_stage(core, "f3_outputs", turned_tiles(aggT, ow, "A", [lambda: L["ow"]]),
                   lambda t, e, ps, chain: nc.scalar.activation(outT[:, t, :], ps, ACT.Gelu))
    products_stage(core, "f3_patterns", linear_tiles(outT, op, "V", [lambda: L["op"]]),
                   lambda t, e, ps, chain: nc.vector.tensor_tensor(core.x[:, t, :], ps, core.x[:, t, :], ALU.add))


def prepare(core, name):
    norm_stage(core, name + "_norm", core.x, core.xn)
    transpose_stage(core, name + "_turn", core.xnT, rows_of(core.xn))


def run_layers(core, w):
    for layer in range(4):
        prepare(core, f"l{layer}a")
        GNN[layer](core, w)
        MIXER[layer](core, w)
        add_stage(core, f"l{layer}_branches", [(core.x[:], core.branches[:])])
        prepare(core, f"l{layer}b")
        FFN[layer](core, w)


GNN = [layer0_gnn, layer1_gnn, layer2_gnn, layer3_gnn]
MIXER = [layer0_mixer, layer1_mixer, layer2_mixer, layer3_mixer]
FFN = [layer0_ffn, layer1_ffn, layer2_ffn, layer3_ffn]




def build(nc, w, out_dram):
    with ExitStack() as stack:
        core = Core(nc, stack)
        sb = core.sb
        core.x, core.xn, core.xnT = (sb(n, [P, 4, 512]) for n in ("x", "xn", "xnT"))
        core.branches = sb("branches", [P, 4, 512])
        core.edges_to, core.edges_from = sb("edges_to", [P, 4, 512]), sb("edges_from", [P, 4, 512])
        core.ident, core.ones, core.iota = sb("ident", [P, P]), sb("ones", [P, P]), sb("iota", [P, NODES])
        core.src_i, core.dst_i = sb("src_i", [P, EDGE_TILES], I32), sb("dst_i", [P, EDGE_TILES], I32)
        core.src_f, core.dst_f = sb("src_f", [P, EDGE_TILES]), sb("dst_f", [P, EDGE_TILES])
        core.stats, core.moments, core.deviation = sb("stats", [P, 4, 6]), sb("moments", [P, 4, 2]), sb("deviation", [P, 4, 3])
        core.scores, core.exps, core.turns = (sb(n, [P, 2, 512]) for n in ("scores", "exps", "turns"))
        core.iota_i = core.scores[:, 0, :].bitcast(I32)
        core.sums, core.negmax = sb("sums", [P, 32]), sb("negmax", [P, 32])
        core.wpool = sb("wpool", [P, 24576])

        setup_stage(core, w["src"], w["dst"], w["x"])
        adjacency_stage(core)
        transpose_stage(core, "edges_from", core.edges_from, rows_of(core.edges_to))
        run_layers(core, w)
        store_stage(core, out_dram, core.x)


def columns(*vectors):
    return np.concatenate([np.reshape(v, (-1, P)).T for v in vectors], axis=1)


def row_pack(*vectors):
    return np.concatenate([np.reshape(v, (-1, DIM)) for v in vectors], axis=0)


def layout(a):
    g = a.__getitem__
    emb = np.concatenate([g("L0_gnn_edge_emb")] * HEADS)
    w = {
        "x": g("x"),
        "src": np.reshape(g("src"), (EDGE_TILES, P)).T, "dst": np.reshape(g("dst"), (EDGE_TILES, P)).T,
        "g0_WqT": g("L0_gnn_W_q").T, "g0_WkT": g("L0_gnn_W_k").T, "g0_WvT": g("L0_gnn_W_v").T,
        "g0_WeT": g("L0_gnn_W_e").T, "g0_WoT": g("L0_gnn_W_o").T,
        "g0_rows": row_pack(g("L0_gnn_b_v"), g("L0_gnn_b_e"), g("L0_gnn_edge_attn"), g("L0_gnn_b_o"),
                            g("L0_gnn_ln_g"), g("L0_gnn_ln_b")),
        "g0_cols": columns(g("L0_gnn_b_q"), g("L0_gnn_b_k"), emb),
        "m0_Wqkv": g("L0_mix_Wqkv"),
        "f0_Wg": g("L0_ffn_Wg"), "f0_bg": np.reshape(g("L0_ffn_bg"), (1, 8)),
        "f0_W1": g("L0_ffn_W1"), "f0_W3": g("L0_ffn_W3"), "f0_W2": g("L0_ffn_W2"),
        "g1_W": g("L1_gnn_W"), "g1_rows": row_pack(g("L1_gnn_b")),
        "m1_Wqkv": g("L1_mix_W_qkv"), "m1_Wout": g("L1_mix_W_out"), "m1_rows": row_pack(g("L1_mix_b_out")),
        "f1_Wg": g("L1_ffn_gate_w").T, "f1_bg": np.reshape(g("L1_ffn_biases"), (1, 8)),
        "f1_W1": np.concatenate([g("L1_ffn_w1"), g("L1_ffn_sw1")[None]]),
        "f1_W3": np.concatenate([g("L1_ffn_w3"), g("L1_ffn_sw3")[None]]),
        "f1_W2": np.concatenate([g("L1_ffn_w2"), g("L1_ffn_sw2")[None]]),
        "g2_Wq": g("L2_gnn_Wq"), "g2_Wk": g("L2_gnn_Wk"), "g2_Wv": g("L2_gnn_Wv"), "g2_Wskip": g("L2_gnn_Wskip"),
        "g2_Wlin": g("L2_gnn_Wlin"),
        "g2_rows": row_pack(g("L2_gnn_bv"), g("L2_gnn_blin"), g("L2_gnn_gamma"), g("L2_gnn_beta")),
        "g2_cols": columns(g("L2_gnn_bq"), g("L2_gnn_bk"), g("L2_gnn_bskip")),
        "m2_Wqkv": g("L2_mix_qkv_w").T, "m2_Wout": g("L2_mix_out_w").T,
        "m2_rows": row_pack(g("L2_mix_qkv_b")[DIM:], g("L2_mix_out_b"), g("L2_mix_ln_gamma"), g("L2_mix_ln_beta")),
        "m2_cols": columns(g("L2_mix_qkv_b")[:DIM]),
        "f2_Wg": g("L2_ffn_w_gating"), "f2_W1": g("L2_ffn_w1"), "f2_W2": g("L2_ffn_w2"),
        "g3_attr": np.reshape(g("edge_attr_4"), (EDGE_TILES, P, 4)).transpose(1, 0, 2),
        "g3_feat": g("edge_attr_8").T,
        "g3_Wup": np.concatenate([g("L3_gnn_W_up0"), g("L3_gnn_W_up1")], axis=1),
        "g3_mlp1": g("L3_gnn_W_mlp1"), "g3_mlp2": g("L3_gnn_W_mlp2"), "g3_mlp3": g("L3_gnn_W_mlp3"),
        "g3_mlp4": g("L3_gnn_W_mlp4"),
        "g3_Wout": np.concatenate([g("L3_gnn_W_out0"), g("L3_gnn_W_out1")], axis=1),
        "m3_Wq": g("L3_mix_Wq"), "m3_Wk": g("L3_mix_Wk"), "m3_Wv": g("L3_mix_Wv"), "m3_Wo": g("L3_mix_Wo"),
        "m3_W1": g("L3_mix_W1"), "m3_W2": g("L3_mix_W2"),
        "m3_rows": row_pack(*[g("L3_mix_" + n) for n in ("bq", "bk", "bv", "bo", "b2", "g1", "be1", "g2", "be2")]),
        "m3_cols": columns(g("L3_mix_b1")),
        "f3_ip": g("L3_ffn_input_patterns").T, "f3_pw": g("L3_ffn_process_input_weights").T,
        "f3_pv": g("L3_ffn_process_values"), "f3_ow": g("L3_ffn_output_input_weights").T,
        "f3_op": g("L3_ffn_output_patterns"),
    }
    return {name: np.ascontiguousarray(v) for name, v in w.items()}


def kernel(**inputs):
    import concourse.bacc as bacc
    from concourse.bass_utils import run_bass_kernel_spmd

    nc = bacc.Bacc("TRN2", target_bir_lowering=False, num_devices=1)
    arrays = layout({name: np.asarray(v) for name, v in inputs.items()})
    w = {name: nc.dram_tensor("in_" + name, v.shape, mybir.dt.from_np(v.dtype), kind="ExternalInput").ap()
         for name, v in arrays.items()}
    out = nc.dram_tensor("out", (NODES, DIM), F32, kind="ExternalOutput").ap()
    build(nc, w, out)
    r = run_bass_kernel_spmd(nc, [{"in_" + name: v for name, v in arrays.items()}], core_ids=[0])
    return r.results[0]["out"]
```

```python
from contextlib import ExitStack

import numpy as np

import concourse.bass as bass
from concourse import mybir

P = 128
NODES = 512
DIM = 512
TILES = NODES // P
CHUNKS = DIM // P
EDGES = 16384
EDGE_TILES = EDGES // P
HEADS = 8
HEAD = DIM // HEADS
BANK = 512

F32 = mybir.dt.float32
F32R = mybir.dt.float32r
BF16 = mybir.dt.bfloat16
F16 = mybir.dt.float16
I32 = mybir.dt.int32
U32 = mybir.dt.uint32
ALU = mybir.AluOpType
ACT = mybir.ActivationFunctionType
AXIS = mybir.AxisListType
MASKED = -1.0e30


class Chain:

    def __init__(self, engine, sem):
        self.engine, self.sem, self.count = engine, sem, 0

    def __call__(self, instruction):
        self.count += 1
        instruction.then_inc(self.sem, 1)
        self.engine.wait_ge(self.sem, self.count)


class Load:

    def __init__(self, sem, value):
        self.sem, self.value = sem, value

    def wait(self, engine):
        engine.wait_ge(self.sem, self.value)


class Core:

    PER_STAGE = 20
    LOADS = 24

    def __init__(self, nc, stack):
        self.nc, self.stack = nc, stack
        taken = [nc.alloc_semaphore(f"stage_pool_{i}") for i in range(2 * self.PER_STAGE)]
        numbers = [s.num for s in taken]
        for s in taken:
            nc.release_semaphore(s)
        self.pools = [numbers[:self.PER_STAGE], numbers[self.PER_STAGE:]]
        self.turn, self.used = 0, None
        self.load_sems = [stack.enter_context(nc.semaphore(f"load_landed_{i}")) for i in range(self.LOADS)]
        self.gather_sems = [stack.enter_context(nc.semaphore(f"sender_rows_landed_{b}")) for b in range(2)]
        self.load_counts = [0] * self.LOADS
        self.loads = 0
        self.psum = stack.enter_context(nc.psum_tensor("banks", [P, 8, BANK], F32))
        self.names = 0

    def sb(self, name, shape, dtype=F32):
        return self.stack.enter_context(self.nc.sbuf_tensor(name, shape, dtype))

    def load(self, queue, dst, src):
        i = self.loads % self.LOADS
        self.loads += 1
        self.load_counts[i] += 16
        queue.dma_start(dst, src).then_inc(self.load_sems[i], 16)
        return Load(self.load_sems[i], self.load_counts[i])

    def open_pool(self, local, sections):
        self.names += 1
        self.wpool = local.enter_context(self.nc.sbuf_tensor(f"pool_{self.names}", [P, sections * 2048], F32))

    def section(self, first, chunks=4, width=512):
        return self.wpool[:, first * 2048:first * 2048 + chunks * width].rearrange("p (c n) -> p c n", c=chunks)

    def bank(self, i):
        return self.psum[:, i, :]


class Stage:

    def __init__(self, core, name):
        self.core, self.name, self.sems = core, name, []

    def __enter__(self):
        core = self.core
        if core.used:
            core.nc.gpsimd.sem_clear(range(min(core.used), max(core.used) + 1))
        core.turn ^= 1
        self.numbers = core.pools[core.turn]
        self.opened = core.nc.Block()
        self.block = self.opened.__enter__()
        return self

    def sem(self, name):
        s = self.core.nc.alloc_semaphore(name=f"{self.name}_{name}", num=self.numbers[len(self.sems)])
        self.sems.append(s)
        return s

    def chain(self, engine, name):
        return Chain(engine, self.sem(name))

    def __exit__(self, *exc):
        self.opened.__exit__(*exc)
        self.core.used = [s.num for s in self.sems]
        for s in self.sems:
            self.core.nc.release_semaphore(s)
        return False


def product(nc, core, out, pairs):
    n = len(pairs)
    for j, (left, right) in enumerate(pairs):
        if right is None:
            last = nc.tensor.transpose(out, left, core.ident[0:left.shape[0], 0:left.shape[0]])
        else:
            last = nc.tensor.matmul(out, left, right, start=(j == 0), stop=(j == n - 1))
    return last


def split_product(nc, out, pairs, start=True, stop=True):
    n = len(pairs)
    for j, ((left, left_low), (right, right_low)) in enumerate(pairs):
        nc.tensor.matmul(out, left, right, start=start and j == 0, stop=False)
        nc.tensor.matmul(out, left, right_low, start=False, stop=False)
        last = nc.tensor.matmul(out, left_low, right, start=False, stop=stop and j == n - 1)
    return last


class Tile:

    def __init__(self, parts, engine, loads=()):
        self.parts, self.engine, self.loads = parts, engine, loads


def products_stage(core, name, tiles, finish, issue=None, params=(), banks=8, ordered=False):
    nc = core.nc
    order = {"V": [t for t, x in enumerate(tiles) if x.engine == "V"],
             "A": [t for t, x in enumerate(tiles) if x.engine == "A"]}
    place = {t: i for ts in order.values() for i, t in enumerate(ts)}
    with Stage(core, name) as st:
        filled = st.sem("bank_filled")
        taken = {"V": st.sem("vector_took_bank"), "A": st.sem("scalar_took_bank")}
        chain_v, chain_a = st.chain(nc.vector, "vector_chain"), st.chain(nc.scalar, "scalar_chain")

        if issue is not None:
            @st.block.sync
            def _(sp):
                issue(sp)

        @st.block.tensor
        def _(pe):
            for t, tile in enumerate(tiles):
                for load in tile.loads:
                    load().wait(pe)
                if t >= banks:
                    pe.wait_ge(taken[tiles[t - banks].engine], place[t - banks] + 1)
                for rows, c0, c1, pairs in tile.parts:
                    last = product(nc, core, core.bank(t % banks)[0:rows, c0:c1], pairs)
                last.then_inc(filled, 1)

        if order["V"]:
            @st.block.vector
            def _(dve):
                for load in params:
                    load().wait(dve)
                for t in order["V"]:
                    dve.wait_ge(filled, t + 1)
                    if ordered and place[t] > 0:
                        dve.wait_ge(taken["V"], place[t])
                    finish(t, nc.vector, core.bank(t % banks), chain_v).then_inc(taken["V"], 1)

        if order["A"]:
            @st.block.scalar
            def _(act):
                for load in params:
                    load().wait(act)
                for t in order["A"]:
                    act.wait_ge(filled, t + 1)
                    finish(t, nc.scalar, core.bank(t % banks), chain_a).then_inc(taken["A"], 1)


def copy_out(nc, engine, out, in_):
    return nc.vector.tensor_copy(out, in_) if engine is nc.vector else nc.scalar.copy(out, in_)


def transpose_stage(core, name, dst, blocks):
    nc = core.nc
    tiles = [Tile([(P, i * P, (i + 1) * P, [(blocks(i, c), None)]) for i in range(TILES)], "VA"[c % 2])
             for c in range(CHUNKS)]
    products_stage(core, name, tiles, lambda t, e, ps, chain: copy_out(nc, e, dst[:, t, :], ps))


def rows_of(src):
    return lambda i, c: src[:, i, c * P:(c + 1) * P]


def norm_stage(core, name, src, dst, scale=None, shift=None, add_to=None, plain=None, issue=None, params=()):
    nc = core.nc
    stats, moments, deviation = core.stats, core.moments, core.deviation
    with Stage(core, name) as st:
        variance_ready, deviation_ready = st.sem("variance_ready"), st.sem("deviation_ready")
        chain = st.chain(nc.vector, "vector_chain")
        if issue is not None:
            @st.block.sync
            def _(sp):
                issue(sp)

        @st.block.scalar
        def _(act):
            act.wait_ge(variance_ready, 1)
            nc.scalar.activation(deviation[:, :, 1], deviation[:, :, 0], ACT.Sqrt).then_inc(deviation_ready, 1)

        @st.block.vector
        def _(dve):
            for i in range(TILES):
                chain(nc.vector.bn_stats(stats[:, i, :], src[:, i, :]))
                chain(nc.vector.bn_aggr(moments[:, i, :], stats[:, i, :]))
            nc.vector.tensor_scalar(deviation[:, :, 0], moments[:, :, 1], 1e-5, None, ALU.add).then_inc(variance_ready, 1)
            dve.wait_ge(deviation_ready, 1)
            chain(nc.vector.reciprocal(deviation[:, :, 2], deviation[:, :, 1]))
            for load in params:
                load().wait(dve)
            for i in range(TILES):
                out = plain if plain is not None else dst
                chain(nc.vector.tensor_scalar(dst[:, i, :], src[:, i, :], moments[:, i, 0:1], deviation[:, i, 2:3],
                                              ALU.subtract, ALU.mult))
                if scale is not None:
                    chain(nc.vector.tensor_tensor(dst[:, i, :], dst[:, i, :], scale, ALU.mult))
                    chain(nc.vector.tensor_tensor(dst[:, i, :], dst[:, i, :], shift, ALU.add))
                if add_to is not None:
                    chain(nc.vector.tensor_tensor(add_to[:, i, :], add_to[:, i, :], dst[:, i, :], ALU.add))


def softmax_stage(core, name, units, width, scale=1.0, mask=None, weigh=None, normal=False, keep=None,
                  turned=None, values=None, total_banks=(), finish=None, issue=None):
    nc = core.nc
    n, blocks = len(units), width // P
    scores, exps, turns, sums, negmax = core.scores, core.exps, core.turns, core.sums, core.negmax
    post = weigh is not None or normal

    def exps_of(u):
        return keep(u) if keep is not None else exps[:, u % 2, 0:width]

    def turned_of(u):
        return turned(u) if turned is not None else turns[:, u % 2, 0:blocks * P].rearrange("p (c n) -> p c n", c=blocks)

    with Stage(core, name) as st:
        scored, shifted, exponed = st.sem("scores_ready"), st.sem("maximum_ready"), st.sem("exponentials_ready")
        weighed, flipped, copied = st.sem("weighed_ready"), st.sem("transpose_ready"), st.sem("transpose_copied")
        valued = st.sem("values_ready")
        chain = st.chain(nc.vector, "vector_chain")
        if issue is not None:
            @st.block.sync
            def _(sp):
                issue(sp)

        @st.block.tensor
        def _(pe):
            def score(u):
                if u >= 2:
                    pe.wait_ge(shifted, u - 1)
                product(nc, core, core.bank(u % 2)[:, 0:width], units[u]).then_inc(scored, 1)

            def flip(u):
                pe.wait_ge(weighed if post else exponed, u + 1)
                if u >= 2:
                    pe.wait_ge(copied, u - 1)
                for c in range(blocks):
                    last = product(nc, core, core.bank(2 + u % 2)[:, c * P:(c + 1) * P],
                                   [(exps_of(u)[:, c * P:(c + 1) * P], None)])
                last.then_inc(flipped, 1)

            def value(u):
                pe.wait_ge(copied, u + 1)
                bank, c0, c1, pairs = values(u, turned_of(u))
                product(nc, core, core.bank(bank)[:, c0:c1], pairs).then_inc(valued, 1)

            score(0)
            for u in range(n):
                if u + 1 < n:
                    score(u + 1)
                flip(u)
                if values is not None and u >= 1:
                    value(u - 1)
            if values is not None:
                value(n - 1)

        @st.block.vector
        def _(dve):
            def shift(u):
                dve.wait_ge(scored, u + 1)
                if u >= 2:
                    dve.wait_ge(exponed, u - 1)
                if mask is not None:
                    chain(nc.vector.scalar_tensor_tensor(out=scores[:, u % 2, 0:width], in0=core.bank(u % 2)[:, 0:width],
                                                         scalar=scale, in1=mask(u), op0=ALU.mult, op1=ALU.add))
                else:
                    chain(nc.vector.tensor_scalar(scores[:, u % 2, 0:width], core.bank(u % 2)[:, 0:width], scale, None,
                                                  ALU.mult))
                nc.vector.tensor_reduce(negmax[:, u:u + 1], scores[:, u % 2, 0:width], AXIS.X, ALU.max,
                                        negate=True).then_inc(shifted, 1)

            def weigh_exps(u):
                dve.wait_ge(exponed, u + 1)
                e, s = exps_of(u), sums[:, u:u + 1]
                if weigh is not None:
                    chain(nc.vector.tensor_tensor(e, e, weigh(u), ALU.mult))
                    chain(nc.vector.tensor_reduce(s, e, AXIS.X, ALU.add))
                    chain(nc.vector.tensor_scalar(s, s, 0.5, None, ALU.max))
                chain(nc.vector.reciprocal(s, s))
                nc.vector.tensor_scalar(e, e, s, None, ALU.mult).then_inc(weighed, 1)

            shift(0)
            for u in range(n):
                if u + 1 < n:
                    shift(u + 1)
                if post:
                    weigh_exps(u)
            if finish is not None:
                dve.wait_ge(valued, n)
                dve.wait_ge(exponed, n)
                finish(chain)

        @st.block.scalar
        def _(act):
            def expo(u):
                act.wait_ge(shifted, u + 1)
                if u >= 2 and keep is None:
                    act.wait_ge(flipped, u - 1)
                nc.scalar.activation(exps_of(u), scores[:, u % 2, 0:width], ACT.Exp, bias=negmax[:, u:u + 1],
                                     accum_out=sums[:, u:u + 1]).then_inc(exponed, 1)

            def copy_turned(u):
                act.wait_ge(flipped, u + 1)
                if u >= 2 and values is not None and turned is None:
                    act.wait_ge(valued, u - 1)
                nc.scalar.copy(turned_of(u), core.bank(2 + u % 2)[:, 0:blocks * P].rearrange("p (c n) -> p c n", c=blocks)
                               ).then_inc(copied, 1)

            expo(0)
            for u in range(n):
                if u + 1 < n:
                    expo(u + 1)
                copy_turned(u)


def setup_stage(core, src_dram, dst_dram, x_dram):
    nc = core.nc
    with Stage(core, "setup") as st:
        landed, made = st.sem("inputs_landed"), st.sem("constants_made")
        x_landed = st.sem("x_landed")

        @st.block.sync
        def _(sp):
            sp.dma_start(core.src_i[:], src_dram).then_inc(landed, 16)
            sp.dma_start(core.dst_i[:], dst_dram).then_inc(landed, 16)
            sp.dma_start(core.x[:], x_dram.rearrange("(i p) d -> p i d", p=P)).then_inc(x_landed, 16)
            sp.wait_ge(x_landed, 16)

        @st.block.gpsimd
        def _(pool):
            nc.gpsimd.memset(core.ident[:], 0.0).then_inc(made, 1)
            nc.gpsimd.memset(core.ones[:], 1.0)
            pool.wait_ge(made, 1)
            nc.gpsimd.affine_select(out=core.ident[:], in_=core.ident[:], compare_op=ALU.not_equal, fill=1.0, base=0,
                                    pattern=[[-1, P]], channel_multiplier=1)
            nc.gpsimd.iota(core.iota_i[:], [[1, NODES]], base=0, channel_multiplier=0).then_inc(made, 1)

        @st.block.vector
        def _(dve):
            dve.wait_ge(landed, 32)
            nc.vector.tensor_copy(core.src_f[:], core.src_i[:])
            nc.vector.tensor_copy(core.dst_f[:], core.dst_i[:])
            dve.wait_ge(made, 2)
            nc.vector.tensor_copy(core.iota[:], core.iota_i[:])
            nc.vector.tensor_copy(core.iota_half, core.iota_i[:])


def adjacency_stage(core):
    nc = core.nc
    with ExitStack() as local, Stage(core, "adjacency") as st:
        hot_src = local.enter_context(nc.sbuf_tensor("hot_src", [P, 2, NODES], BF16))
        hot_dst = local.enter_context(nc.sbuf_tensor("hot_dst", [P, 2, NODES], BF16))
        hot, counted = st.sem("one_hots_ready"), st.sem("edges_counted")
        steps = EDGE_TILES // 2

        def one_hots(t, b):
            nc.vector.tensor_scalar(hot_src[:, b, :], core.iota_half, core.src_f[:, bass.ds(t, 1)], None, ALU.is_equal)
            nc.vector.tensor_scalar(hot_dst[:, b, :], core.iota_half, core.dst_f[:, bass.ds(t, 1)], None,
                                    ALU.is_equal).then_inc(hot, 1)

        def count(pe, b, first, last):
            for m in range(TILES):
                done = nc.tensor.matmul(core.bank(m), hot_dst[:, b, m * P:(m + 1) * P], hot_src[:, b, :],
                                        start=first, stop=last, skip_group_check=True)
            done.then_inc(counted, 1)

        @st.block.vector
        def _(dve):
            one_hots(0, 0)
            one_hots(1, 1)
            with dve.Fori(1, steps) as s:
                for b in range(2):
                    dve.wait_ge(counted, 2 * s + b - 1)
                    one_hots(2 * s + b, b)
            dve.wait_ge(counted, 2 * steps)
            for m in range(TILES):
                nc.vector.tensor_copy(core.edges_to[:, m, :], core.bank(m))

        @st.block.tensor
        def _(pe):
            pe.wait_ge(hot, 1)
            count(pe, 0, True, False)
            pe.wait_ge(hot, 2)
            count(pe, 1, False, False)
            with pe.Fori(1, steps - 1) as s:
                for b in range(2):
                    pe.wait_ge(hot, 2 * s + b + 1)
                    count(pe, b, False, False)
            pe.wait_ge(hot, 2 * steps - 1)
            count(pe, 0, False, False)
            pe.wait_ge(hot, 2 * steps)
            count(pe, 1, False, True)


def weights(dram, cols=None):
    w = dram.rearrange("(c p) n -> p c n", p=P)
    return w if cols is None else w[:, :, cols[0]:cols[1]]


def linear_tiles(left, right, engines, loads=(), width=DIM):
    k = right.shape[1]
    return [Tile([(P, 0, width, [(left[:, c, i * P:(i + 1) * P], right[:, c, 0:width]) for c in range(k)])],
                 engines[i % len(engines)], loads) for i in range(TILES)]


def turned_tiles(right, weight, engines, loads=(), first=0):
    k, n = weight.shape[1], weight.shape[2] // P
    return [Tile([(P, 0, NODES, [(weight[:, c, m * P:(m + 1) * P], right[:, c, :]) for c in range(k)])],
                 engines[(first + m) % len(engines)], loads) for m in range(n)]


def layer0_gnn(core, w):
    nc = core.nc
    xn, xnT = core.xn, core.xnT
    with ExitStack() as local:
        core.open_pool(local, 11)

        def sb(name, shape, dtype=F32):
            return local.enter_context(nc.sbuf_tensor("g0_" + name, shape, dtype))
        part = [core.section(j) for j in range(11)]
        qT, kT, v, mixed, xe, mask = part[5:11]
        rows, cols = sb("rows", [P, 6, 512]), sb("cols", [P, 12])
        L = {}

        def issue(sp):
            L["cols"] = core.load(sp, cols[:], w["g0_cols"])
            for j, name in enumerate(["g0_WqT", "g0_WkT", "g0_WeT", "g0_WvT", "g0_WoT"]):
                L[name] = core.load(sp, part[j], weights(w[name]))
                if j == 1:
                    L["rows"] = core.load(sp, rows[:], w["g0_rows"].rearrange("(o r) n -> o r n", o=1).to_broadcast([P, 6, 512]))

        tiles = (turned_tiles(xnT, part[0], "A", [lambda: L["g0_WqT"]]) + turned_tiles(xnT, part[1], "V", [lambda: L["g0_WkT"]])
                 + linear_tiles(xnT, part[2], "V", [lambda: L["g0_WeT"]]) + linear_tiles(xnT, part[3], "V", [lambda: L["g0_WvT"]]))

        def finish(t, engine, ps, chain):
            m = t % 4
            if t < 4:
                return nc.scalar.activation(qT[:, m, :], ps, ACT.Identity, bias=cols[:, m:m + 1])
            if t < 8:
                return nc.vector.tensor_scalar(kT[:, m, :], ps, cols[:, 4 + m:5 + m], cols[:, 8 + m:9 + m], ALU.add, ALU.add)
            if t < 12:
                chain(nc.vector.tensor_tensor(xe[:, m, :], ps, rows[:, 1, :], ALU.add))
                return nc.vector.tensor_tensor(xe[:, m, :], xe[:, m, :], rows[:, 2, :], ALU.mult)
            chain(nc.vector.tensor_tensor(v[:, m, :], ps, rows[:, 0, :], ALU.add))
            return nc.vector.tensor_tensor(v[:, m, :], v[:, m, :], xe[:, m, :], ALU.add)

        prepare(core, "g0", issue)
        with Stage(core, "g0_mask") as st:
            chain = st.chain(nc.vector, "vector_chain")

            @st.block.vector
            def _(dve):
                chain(nc.vector.tensor_scalar(mask[:], core.edges_from[:], 0.5, None, ALU.is_lt))
                nc.vector.tensor_scalar(mask[:], mask[:], MASKED, None, ALU.mult)
        products_stage(core, "g0_qkv", tiles, finish, params=[lambda: L["rows"], lambda: L["cols"]])

        def head(x, h):
            return x[HEAD * (h % 2):HEAD * (h % 2) + HEAD, h // 2]
        order = [(h, i) for h in range(HEADS) for i in range(TILES)]
        units = [[(head(qT, h)[:, i * P:(i + 1) * P], head(kT, h))] for h, i in order]

        def values(u, turned):
            h, i = order[u]
            return 4 + i, h * HEAD, (h + 1) * HEAD, [(turned[:, c, :], v[:, c, h * HEAD:(h + 1) * HEAD]) for c in range(4)]

        def finish_attention(chain):
            chain(nc.vector.reciprocal(core.sums[:, 0:32], core.sums[:, 0:32]))
            s = core.sums[:, 0:32].rearrange("p (h i) -> p i h", i=4)
            for i in range(TILES):
                nc.vector.tensor_tensor(mixed[:, i, :].rearrange("p (h d) -> p h d", h=HEADS),
                                        core.bank(4 + i).rearrange("p (h d) -> p h d", h=HEADS),
                                        s[:, i, :].unsqueeze(2).to_broadcast([P, HEADS, HEAD]), ALU.mult)
        softmax_stage(core, "g0_attention", units, NODES, scale=HEAD ** -0.5, mask=lambda u: mask[:, order[u][1], :],
                      values=values, finish=finish_attention)
        transpose_stage(core, "g0_turn", qT, rows_of(mixed))

        def finish_out(t, engine, ps, chain):
            chain(nc.vector.tensor_tensor(v[:, t, :], ps, rows[:, 3, :], ALU.add))
            return nc.vector.tensor_tensor(v[:, t, :], v[:, t, :], xn[:, t, :], ALU.add)
        products_stage(core, "g0_out", linear_tiles(qT, part[4], "V", [lambda: L["g0_WoT"]]), finish_out)
        norm_stage(core, "g0_norm", v, core.branches, scale=rows[:, 4, :], shift=rows[:, 5, :])


def add_stage(core, name, pairs, out=None):
    nc = core.nc
    with Stage(core, name) as st:
        @st.block.vector
        def _(dve):
            for a, b in pairs:
                nc.vector.tensor_tensor(a, a, b, ALU.add)


def store_stage(core, out_dram, src):
    nc = core.nc
    with Stage(core, "store") as st:
        stored = st.sem("output_stored")

        @st.block.sync
        def _(sp):
            sp.dma_start(out_dram.rearrange("(i p) d -> p i d", p=P), src[:]).then_inc(stored, 16)
            sp.wait_ge(stored, 16)


LANDMARKS = 256
PINV_STEPS = 6


def pinv_stage(core, XT, Z, ZT):
    nc = core.nc
    big = lambda first: core.wpool[:, first * 4096:(first + 1) * 4096].rearrange("p (h c n) -> p h c n", h=HEADS, c=2)
    XZ, XZT, Q = big(3), big(4), big(5)
    with ExitStack() as local, Stage(core, "pinv") as st:
        seven, fifteen, thirteen = (local.enter_context(nc.sbuf_tensor(f"pinv_{n}", [P, 2, 256], F32))
                                    for n in ("seven", "fifteen", "thirteen"))
        tops = local.enter_context(nc.sbuf_tensor("pinv_tops", [P, 8], F32))
        all_sums = local.enter_context(nc.sbuf_tensor("pinv_sums", [P, 2, 16], F32))
        tops_ready, tops_shared, factor_ready = st.sem("tops_ready"), st.sem("tops_shared"), st.sem("factor_ready")
        chain = st.chain(nc.vector, "vector_chain")
        made, vec, act_ = st.sem("products_ready"), st.sem("vector_results"), st.sem("scalar_results")
        PE_STEP, V_STEP, A_STEP = 48, 32, 24

        def bank(h):
            return core.bank(h).rearrange("p (c n) -> p c n", c=2)

        @st.block.gpsimd
        def _(pool):
            pool.wait_ge(tops_ready, 1)
            nc.gpsimd.partition_all_reduce(tops[:, 2:4], tops[:, 0:2], P, bass.bass_isa.ReduceOp.max).then_inc(tops_shared, 1)

        @st.block.vector
        def _(dve):
            flat = lambda x: x.rearrange("p h c n -> p (h c) n")
            chain(nc.vector.tensor_reduce(all_sums[:, 0, :], flat(ZT), AXIS.X, ALU.add, apply_absolute_value=True))
            chain(nc.vector.tensor_reduce(all_sums[:, 1, :], flat(XT), AXIS.X, ALU.add, apply_absolute_value=True))
            nc.vector.tensor_reduce(tops[:, 0:2], all_sums[:], AXIS.X, ALU.max).then_inc(tops_ready, 1)
            for matrix, value in ((seven, 7.0), (fifteen, 15.0), (thirteen, 13.0)):
                chain(nc.vector.memset(matrix[:], 0.0))
                for c in range(2):
                    chain(nc.vector.tensor_scalar(matrix[:, c, c * P:(c + 1) * P], core.ident[:], value, None, ALU.mult))
            dve.wait_ge(tops_shared, 1)
            chain(nc.vector.tensor_tensor(tops[:, 4:5], tops[:, 2:3], tops[:, 3:4], ALU.mult))
            nc.vector.reciprocal(tops[:, 5:6], tops[:, 4:5]).then_inc(factor_ready, 1)
            dve.wait_ge(factor_ready, 1)
            for h in range(HEADS):
                nc.vector.tensor_scalar(ZT[:, h], ZT[:, h], tops[:, 5:6], None, ALU.mult).then_inc(vec, 1)
            with dve.Fori(0, PINV_STEPS) as s:
                for j, matrix in enumerate((seven, fifteen, thirteen)):
                    for h in range(HEADS):
                        dve.wait_ge(made, s * PE_STEP + (0, 16, 24)[j] + h + 1)
                        nc.vector.scalar_tensor_tensor(out=Q[:, h], in0=bank(h), scalar=-1.0, in1=matrix[:],
                                                       op0=ALU.mult, op1=ALU.add).then_inc(vec, 1)
                for h in range(HEADS):
                    dve.wait_ge(made, s * PE_STEP + 40 + h + 1)
                    nc.vector.tensor_copy(ZT[:, h], bank(h)).then_inc(vec, 1)

        @st.block.scalar
        def _(act):
            act.wait_ge(factor_ready, 1)
            for h in range(HEADS):
                nc.scalar.activation(Z[:, h], XT[:, h], ACT.Copy, scale=tops[:, 5:6]).then_inc(act_, 1)
            with act.Fori(0, PINV_STEPS) as s:
                for h in range(HEADS):
                    act.wait_ge(vec, s * V_STEP + 8 + h + 1)
                    nc.scalar.copy(XZ[:, h], bank(h)).then_inc(act_, 1)
                for h in range(HEADS):
                    act.wait_ge(made, s * PE_STEP + 8 + h + 1)
                    nc.scalar.copy(XZT[:, h], bank(h)).then_inc(act_, 1)
                for h in range(HEADS):
                    act.wait_ge(made, s * PE_STEP + 32 + h + 1)
                    nc.scalar.activation(Z[:, h], bank(h), ACT.Copy, scale=0.25).then_inc(act_, 1)

        @st.block.tensor
        def _(pe):
            def multiply(h, left_turned, right):
                for m in range(2):
                    last = product(nc, core, bank(h)[:, m, :],
                                   [(left_turned[:, h, c, m * P:(m + 1) * P], right[:, h, c, :]) for c in range(2)])
                last.then_inc(made, 1)

            def turn(h, matrix):
                for c in range(2):
                    for m in range(2):
                        last = nc.tensor.transpose(bank(h)[:, c, m * P:(m + 1) * P], matrix[:, h, m, c * P:(c + 1) * P],
                                                   core.ident[:])
                last.then_inc(made, 1)

            with pe.Fori(0, PINV_STEPS) as s:
                for h in range(HEADS):
                    pe.wait_ge(act_, s * A_STEP + h + 1)
                    pe.wait_ge(vec, s * V_STEP + h + 1)
                    multiply(h, XT, Z)
                for h in range(HEADS):
                    pe.wait_ge(act_, s * A_STEP + 8 + h + 1)
                    pe.wait_ge(vec, s * V_STEP + 8 + h + 1)
                    turn(h, XZ)
                for h in range(HEADS):
                    pe.wait_ge(act_, s * A_STEP + 16 + h + 1)
                    multiply(h, XZT, Q)
                for h in range(HEADS):
                    pe.wait_ge(vec, s * V_STEP + 16 + h + 1)
                    multiply(h, XZT, Q)
                for h in range(HEADS):
                    pe.wait_ge(vec, s * V_STEP + 24 + h + 1)
                    multiply(h, ZT, Q)
                for h in range(HEADS):
                    pe.wait_ge(act_, s * A_STEP + 24 + h + 1)
                    turn(h, Z)


def layer0_mixer(core, w):
    nc = core.nc
    with ExitStack() as local:
        core.open_pool(local, 12)

        def sb(name, shape, dtype=F32):
            return local.enter_context(nc.sbuf_tensor("m0_" + name, shape, dtype))
        qT, kT, v = sb("qT", [P, 4, 512]), sb("kT", [P, 4, 512]), sb("v", [P, 4, 512])
        qlT, klT = sb("qlT", [P, 4, LANDMARKS]), sb("klT", [P, 4, LANDMARKS])
        a3v, zav = sb("a3v", [P, 2, 512]), sb("zav", [P, 2, 512])
        Wqkv = core.section(0, 4, 3 * DIM)
        L = {}

        def issue(sp):
            for j in range(3):
                L[j] = core.load(sp, Wqkv[:, :, j * DIM:(j + 1) * DIM], weights(w["m0_Wqkv"], (j * DIM, (j + 1) * DIM)))

        def finish(t, engine, ps, chain):
            m = t % 4
            if t < 4:
                return nc.scalar.mul(qT[:, m, :], ps, HEAD ** -0.5)
            return copy_out(nc, engine, (kT if t < 8 else v)[:, m, :], ps)
        with Stage(core, "m0_load") as st:
            @st.block.sync
            def _(sp):
                issue(sp)
        products_stage(core, "m0_qkv",
                       turned_tiles(core.xnT, Wqkv[:, :, 0:DIM], "A", [lambda: L[0]])
                       + turned_tiles(core.xnT, Wqkv[:, :, DIM:2 * DIM], "V", [lambda: L[1]])
                       + linear_tiles(core.xnT, Wqkv[:, :, 2 * DIM:], "AV", [lambda: L[2]]), finish)
        with Stage(core, "m0_landmarks") as st:
            chain = st.chain(nc.vector, "vector_chain")

            @st.block.vector
            def _(dve):
                for full, marks in ((qT, qlT), (kT, klT)):
                    pairs = full[:].rearrange("p c (n two) -> p c n two", two=2)
                    chain(nc.vector.tensor_tensor(marks[:], pairs[:, :, :, 0], pairs[:, :, :, 1], ALU.add))
                    chain(nc.vector.tensor_scalar(marks[:], marks[:], 0.5, None, ALU.mult))

        def head(x, h):
            return x[HEAD * (h % 2):HEAD * (h % 2) + HEAD, h // 2]
        by_landmarks = [(h, i) for h in range(HEADS) for i in range(2)]

        def values3(u, turned):
            h, i = by_landmarks[u]
            return 4 + i, h * HEAD, (h + 1) * HEAD, [(turned[:, c, :], v[:, c, h * HEAD:(h + 1) * HEAD]) for c in range(4)]

        def per_head(x):
            return x.rearrange("p (h d) -> p h d", h=HEADS)

        def normalise(chain, count, tiles, dst, add=False):
            chain(nc.vector.reciprocal(core.sums[:, 0:count], core.sums[:, 0:count]))
            s = core.sums[:, 0:count].rearrange("p (h i) -> p i h", i=tiles)
            for i in range(tiles):
                chain(nc.vector.tensor_tensor(per_head(dst[:, i, :]), per_head(core.bank(4 + i)),
                                              s[:, i, :].unsqueeze(2).to_broadcast([P, HEADS, HEAD]), ALU.mult))
        softmax_stage(core, "m0_attn3", [[(head(qlT, h)[:, i * P:(i + 1) * P], head(kT, h))] for h, i in by_landmarks],
                      NODES, values=values3, finish=lambda chain: normalise(chain, 16, 2, a3v))

        big = lambda first: core.wpool[:, first * 4096:(first + 1) * 4096].rearrange("p (h c n) -> p h c n", h=HEADS, c=2)
        XT, Z, ZT = big(0), big(1), big(2)
        softmax_stage(core, "m0_attn2", [[(head(qlT, h)[:, i * P:(i + 1) * P], head(klT, h))] for h, i in by_landmarks],
                      LANDMARKS, normal=True, keep=lambda u: ZT[:, by_landmarks[u][0], by_landmarks[u][1], :],
                      turned=lambda u: XT[:, by_landmarks[u][0], :, by_landmarks[u][1] * P:(by_landmarks[u][1] + 1) * P])
        pinv_stage(core, XT, Z, ZT)

        products_stage(core, "m0_inverse_values",
                       [Tile([(P, h * HEAD, (h + 1) * HEAD, [(ZT[:, h, c, i * P:(i + 1) * P], a3v[:, c, h * HEAD:(h + 1) * HEAD])
                                                            for c in range(2)]) for h in range(HEADS)], "VA"[i])
                        for i in range(2)], lambda t, e, ps, chain: copy_out(nc, e, zav[:, t, :], ps))

        by_rows = [(h, i) for h in range(HEADS) for i in range(TILES)]

        def values1(u, turned):
            h, i = by_rows[u]
            return 4 + i, h * HEAD, (h + 1) * HEAD, [(turned[:, c, :], zav[:, c, h * HEAD:(h + 1) * HEAD]) for c in range(2)]

        def finish1(chain):
            normalise(chain, 32, TILES, qT)
            chain(nc.vector.tensor_tensor(core.branches[:], core.branches[:], qT[:], ALU.add))
        softmax_stage(core, "m0_attn1", [[(head(qT, h)[:, i * P:(i + 1) * P], head(klT, h))] for h, i in by_rows],
                      LANDMARKS, values=values1, finish=finish1)


def linear_attention(core, name, q_turned, k_rows, v_rows, out, epsilon=0.0, factor=None):
    nc = core.nc
    pairs = HEADS // 2
    with ExitStack() as local:
        def sb(n, shape):
            return local.enter_context(nc.sbuf_tensor(f"{name}_{n}", shape, F32))
        kv, k_sum, inverse = sb("kv", [P, pairs, P]), sb("k_sum", [P, pairs, 2]), sb("inverse", [P, 4, HEADS])
        with Stage(core, name + "_kv") as st:
            ready, chain = st.sem("products_ready"), st.chain(nc.vector, "vector_chain")

            @st.block.tensor
            def _(pe):
                for j in range(pairs):
                    cols = slice(j * P, (j + 1) * P)
                    last = product(nc, core, core.bank(0)[:, cols], [(k_rows[:, c, cols], v_rows[:, c, cols]) for c in range(4)])
                for j in range(pairs if factor is None else 0):
                    cols = slice(j * P, (j + 1) * P)
                    last = product(nc, core, core.bank(1)[:, 2 * j:2 * j + 2],
                                   [(k_rows[:, c, cols], core.ones[:, 0:2]) for c in range(4)])
                last.then_inc(ready, 1)

            @st.block.vector
            def _(dve):
                chain(nc.vector.memset(kv[:], 0.0))
                chain(nc.vector.memset(k_sum[:], 0.0))
                dve.wait_ge(ready, 1)
                for b in range(2):
                    half = slice(b * HEAD, (b + 1) * HEAD)
                    chain(nc.vector.tensor_copy(kv[half, :, half], core.bank(0)[half].rearrange("p (j n) -> p j n", j=pairs)[:, :, half]))
                    if factor is not None:
                        continue
                    chain(nc.vector.tensor_copy(k_sum[half, :, b], core.bank(1)[half, 0:2 * pairs].rearrange("p (j n) -> p j n", j=pairs)[:, :, b]))
        with Stage(core, name + "_out") as st:
            ready, taken, chain = st.sem("products_ready"), st.sem("banks_taken"), st.chain(nc.vector, "vector_chain")

            @st.block.tensor
            def _(pe):
                for i in range(TILES):
                    rows = slice(i * P, (i + 1) * P)
                    for j in range(pairs):
                        last = product(nc, core, core.bank(2 * i)[:, j * P:(j + 1) * P], [(q_turned[:, j, rows], kv[:, j, :])])
                    for j in range(pairs if factor is None else 0):
                        last = product(nc, core, core.bank(2 * i + 1)[:, 2 * j:2 * j + 2], [(q_turned[:, j, rows], k_sum[:, j, :])])
                    last.then_inc(ready, 1)

            @st.block.vector
            def _(dve):
                for i in range(TILES):
                    dve.wait_ge(ready, i + 1)
                    if factor is None:
                        chain(nc.vector.tensor_scalar(inverse[:, i, :], core.bank(2 * i + 1)[:, 0:HEADS], epsilon, None, ALU.add))
                        chain(nc.vector.reciprocal(inverse[:, i, :], inverse[:, i, :]))
                    by = inverse[:, i, :] if factor is None else factor[:, i, :]
                    chain(nc.vector.tensor_tensor(out[:, i, :].rearrange("p (h d) -> p h d", h=HEADS),
                                                  core.bank(2 * i).rearrange("p (h d) -> p h d", h=HEADS),
                                                  by.unsqueeze(2).to_broadcast([P, HEADS, HEAD]), ALU.mult))


def phi_stage(core, name, x, scratch):
    nc = core.nc
    with Stage(core, name) as st:
        clamped, exponed = st.sem("minimum_ready"), st.sem("exponential_ready")

        @st.block.vector
        def _(dve):
            for j, a in enumerate(x):
                nc.vector.tensor_scalar(scratch[j][:], a[:], 0.0, None, ALU.min).then_inc(clamped, 1)
            for j, a in enumerate(x):
                dve.wait_ge(exponed, j + 1)
                nc.vector.scalar_tensor_tensor(out=a[:], in0=a[:], scalar=0.0, in1=scratch[j][:], op0=ALU.max, op1=ALU.add)

        @st.block.scalar
        def _(act):
            for j in range(len(x)):
                act.wait_ge(clamped, j + 1)
                nc.scalar.activation(scratch[j][:], scratch[j][:], ACT.Exp).then_inc(exponed, 1)


def layer1_mixer(core, w):
    nc = core.nc
    with ExitStack() as local:
        core.open_pool(local, 10)
        part = [core.section(j) for j in range(10)]
        qT, k, v, s0, s1, out = part[4:10]
        rows = local.enter_context(nc.sbuf_tensor("m1_rows", [P, 1, 512], F32))
        L = {}
        with Stage(core, "m1_load") as st:
            @st.block.sync
            def _(sp):
                for j in range(3):
                    L[j] = core.load(sp, part[j], weights(w["m1_Wqkv"], (j * DIM, (j + 1) * DIM)))
                L[3] = core.load(sp, part[3], weights(w["m1_Wout"]))
                L["rows"] = core.load(sp, rows[:], w["m1_rows"].rearrange("(o r) n -> o r n", o=1).to_broadcast([P, 1, 512]))
        products_stage(core, "m1_qkv",
                       turned_tiles(core.xnT, part[0], "VA", [lambda: L[0]]) + linear_tiles(core.xnT, part[1], "VA", [lambda: L[1]])
                       + linear_tiles(core.xnT, part[2], "VA", [lambda: L[2]]),
                       lambda t, e, ps, chain: copy_out(nc, e, (qT, k, v)[t // 4][:, t % 4, :], ps))
        phi_stage(core, "m1_phi", (qT, k), (s0, s1))
        linear_attention(core, "m1", qT, k, v, out, 1e-6)
        transpose_stage(core, "m1_turn", s0, rows_of(out))

        def finish(t, e, ps, chain):
            chain(nc.vector.tensor_tensor(out[:, t, :], ps, rows[:, 0, :], ALU.add))
            return nc.vector.tensor_tensor(core.branches[:, t, :], core.branches[:, t, :], out[:, t, :], ALU.add)
        products_stage(core, "m1_out", linear_tiles(s0, part[3], "V", [lambda: L[3]]), finish, params=[lambda: L["rows"]])


def layer2_mixer(core, w):
    nc = core.nc
    with ExitStack() as local:
        core.open_pool(local, 12)
        part = [core.section(j) for j in range(12)]
        qT, k, v, s0, s1, out, normed, nT = part[4:12]
        rows = local.enter_context(nc.sbuf_tensor("m2_rows", [P, 5, 512], F32))
        cols = local.enter_context(nc.sbuf_tensor("m2_cols", [P, 4], F32))
        L = {}

        def issue(sp):
            def load_rows(first, n):
                return core.load(sp, rows[:, first:first + n], w["m2_rows"][first:first + n].rearrange("(o r) n -> o r n", o=1).to_broadcast([P, n, 512]))
            L["norm_rows"] = load_rows(3, 2)
            L["cols"] = core.load(sp, cols[:], w["m2_cols"])
            L[0] = core.load(sp, part[0], weights(w["m2_Wqkv"], (0, DIM)))
            L["rows"] = load_rows(0, 3)
            for j in range(1, 3):
                L[j] = core.load(sp, part[j], weights(w["m2_Wqkv"], (j * DIM, (j + 1) * DIM)))
            L[3] = core.load(sp, part[3], weights(w["m2_Wout"]))
        norm_stage(core, "m2_norm", core.xn, normed, scale=rows[:, 3, :], shift=rows[:, 4, :], issue=issue,
                   params=[lambda: L["norm_rows"]])
        transpose_stage(core, "m2_turn_in", nT, rows_of(normed))

        def finish_qkv(t, e, ps, chain):
            m = t % 4
            if t < 4:
                return nc.scalar.activation(qT[:, m, :], ps, ACT.Identity, bias=cols[:, m:m + 1])
            return nc.vector.tensor_tensor((k if t < 8 else v)[:, m, :], ps, rows[:, t // 4 - 1, :], ALU.add)
        products_stage(core, "m2_qkv",
                       turned_tiles(nT, part[0], "A", [lambda: L[0]]) + linear_tiles(nT, part[1], "V", [lambda: L[1]])
                       + linear_tiles(nT, part[2], "V", [lambda: L[2]]), finish_qkv, params=[lambda: L["cols"], lambda: L["rows"]])
        phi_stage(core, "m2_phi", (qT, k), (s0, s1))
        linear_attention(core, "m2", qT, k, v, out, 1e-8)
        transpose_stage(core, "m2_turn_out", s0, rows_of(out))

        def finish(t, e, ps, chain):
            chain(nc.vector.tensor_tensor(out[:, t, :], ps, rows[:, 2, :], ALU.add))
            chain(nc.vector.tensor_tensor(out[:, t, :], out[:, t, :], core.xn[:, t, :], ALU.add))
            return nc.vector.tensor_tensor(core.branches[:, t, :], core.branches[:, t, :], out[:, t, :], ALU.add)
        products_stage(core, "m2_out", linear_tiles(s0, part[3], "V", [lambda: L[3]]), finish)


def gate_stage(core, name, weight, bias, experts, gate, rule):
    nc = core.nc
    with ExitStack() as local, Stage(core, name) as st:
        def sb(n, shape, dtype=F32):
            return local.enter_context(nc.sbuf_tensor(f"{name}_{n}", shape, dtype))
        w_sb, b_sb = sb("weight", [P, 4, experts]), sb("bias", [P, experts])
        scores, biased = sb("scores", [P, 4, experts]), sb("biased", [P, 4, experts])
        tops, tops_biased = sb("tops", [P, 4, 8]), sb("tops_biased", [P, 4, 8])
        index, index_f = sb("index", [P, 4, 8], U32), sb("index_f", [P, 4, 8])
        share, total = sb("share", [P, 4, 2]), sb("total", [P, 4])
        hot = sb("hot", [P, experts])
        weight_landed, bias_landed, ready = st.sem("weight_landed"), st.sem("bias_landed"), st.sem("scores_ready")
        tops_ready, shares_ready = st.sem("tops_ready"), st.sem("shares_ready")
        chain = st.chain(nc.vector, "vector_chain")

        @st.block.sync
        def _(sp):
            sp.dma_start(w_sb[:], weights(weight)).then_inc(weight_landed, 16)
            sp.dma_start(b_sb[:], bias.to_broadcast([P, experts])).then_inc(bias_landed, 16)

        @st.block.tensor
        def _(pe):
            pe.wait_ge(weight_landed, 16)
            for i in range(TILES):
                last = product(nc, core, core.bank(0)[:, i * experts:(i + 1) * experts],
                               [(core.xnT[:, c, i * P:(i + 1) * P], w_sb[:, c, :]) for c in range(4)])
            last.then_inc(ready, 1)

        @st.block.scalar
        def _(act):
            act.wait_ge(tops_ready, 1)
            if rule == "softmax":
                nc.scalar.activation(share[:, :, 1], share[:, :, 0], ACT.Exp).then_inc(shares_ready, 1)
            else:
                nc.scalar.activation(share[:], tops[:, :, 0:2], ACT.Sigmoid).then_inc(shares_ready, 1)

        @st.block.vector
        def _(dve):
            dve.wait_ge(bias_landed, 16)
            dve.wait_ge(ready, 1)
            chain(nc.vector.tensor_copy(scores[:], core.bank(0)[:, 0:4 * experts].rearrange("p (i e) -> p i e", i=4)))
            chain(nc.vector.tensor_tensor(biased[:], scores[:], b_sb[:].unsqueeze(1).to_broadcast([P, 4, experts]), ALU.add))
            for i in range(TILES):
                chain(nc.vector.max(tops_biased[:, i, :], biased[:, i, :]))
                chain(nc.vector.max_index(index[:, i, :], tops_biased[:, i, :], biased[:, i, :]))
            chain(nc.vector.tensor_copy(index_f[:], index[:]))
            if rule == "softmax":
                nc.vector.tensor_tensor(share[:, :, 0], tops_biased[:, :, 1], tops_biased[:, :, 0], ALU.subtract).then_inc(tops_ready, 1)
                dve.wait_ge(shares_ready, 1)
                chain(nc.vector.tensor_scalar(total[:], share[:, :, 1], 1.0, None, ALU.add))
                chain(nc.vector.reciprocal(share[:, :, 0], total[:]))
                chain(nc.vector.tensor_tensor(share[:, :, 1], share[:, :, 1], share[:, :, 0], ALU.mult))
            else:
                for i in range(TILES):
                    chain(nc.vector.max(tops[:, i, :], scores[:, i, :]))
                nc.vector.tensor_copy(total[:], tops[:, :, 0]).then_inc(tops_ready, 1)
                dve.wait_ge(shares_ready, 1)
                chain(nc.vector.tensor_tensor(total[:], share[:, :, 0], share[:, :, 1], ALU.add))
                chain(nc.vector.reciprocal(total[:], total[:]))
                chain(nc.vector.tensor_tensor(share[:], share[:], total[:].unsqueeze(2).to_broadcast([P, 4, 2]), ALU.mult))
                chain(nc.vector.memset(gate[:], 1.0))
            for i in range(TILES):
                chain(nc.vector.tensor_scalar(gate[:, i, 0:experts], core.iota[:, 0:experts], index_f[:, i, 0:1], share[:, i, 0:1],
                                              ALU.is_equal, ALU.mult))
                chain(nc.vector.tensor_scalar(hot[:], core.iota[:, 0:experts], index_f[:, i, 1:2], share[:, i, 1:2],
                                              ALU.is_equal, ALU.mult))
                chain(nc.vector.tensor_tensor(gate[:, i, 0:experts], gate[:, i, 0:experts], hot[:], ALU.add))


PIECES = 6
RAW, RING = 3, 4


def first_pieces(core, name, local, w1, w3):
    raw = [local.enter_context(core.nc.sbuf_tensor(f"{name}_raw_{j}", [P, 4, 512], F32)) for j in range(RAW)]
    L = {}

    def issue(sp):
        for p, (matrix, half) in enumerate(((w1, 0), (w3, 0), (w1, 1))):
            L[p] = core.load(sp, raw[p][:], matrix[0:1, :, half * 512:(half + 1) * 512].rearrange("o (c p) n -> p (o c) n", p=P))
    return raw, L, issue


def experts_stage(core, name, w1, w3, w2, gate, experts, raw, first_loads):
    nc = core.nc
    chunks = 2 * DIM // P
    half = chunks // 2
    with ExitStack() as local, Stage(core, name) as st:
        def sb(n, shape, dtype=F32R):
            return local.enter_context(nc.sbuf_tensor(f"{name}_{n}", shape, dtype))
        high, low = ([sb(f"{part}_{j}", [P, 4, 512]) for j in range(RING)] for part in ("high", "low"))
        h_high, h_low = sb("hidden_high", [P, chunks, NODES]), sb("hidden_low", [P, chunks, NODES])
        x_high, x_low = sb("x_high", [P, 4, NODES]), sb("x_low", [P, 4, NODES])
        silu, h = core.scores, core.exps
        landed = [st.sem(f"piece_landed_{j}") for j in range(RAW)]
        high_ready, split = st.sem("high_pieces_ready"), st.sem("pieces_split")
        x_rounded, x_split = st.sem("x_high_ready"), st.sem("x_split")
        ready, silu_ready, h_ready = st.sem("products_ready"), st.sem("silu_ready"), st.sem("hidden_ready")
        h_rounded, h_split = st.sem("hidden_high_ready"), st.sem("hidden_split")
        halfway, y_ready, y_added = st.sem("first_w2_piece_used"), st.sem("outputs_ready"), st.sem("outputs_added")
        refills = st.sem("refills_begun")
        looped = (experts - 1) // 2

        def over_experts(engine, body):
            with engine.Fori(0, looped) as s:
                for b in range(2):
                    body(2 * s + b, b, False)
            for e in range(2 * looped, experts):
                body(e, e % 2, e == experts - 1)

        def piece_source(e, p):
            if p < 4:
                cols = slice((p // 2) * 512, (p // 2 + 1) * 512)
                return (w1, w3)[p % 2][bass.ds(e, 1), :, cols].rearrange("o (c p) n -> p (o c) n", p=P)
            rows = slice((p - 4) * 512, (p - 3) * 512)
            return w2[bass.ds(e, 1), rows, :].rearrange("o (c p) n -> p (o c) n", p=P)

        @st.block.sync
        def _(sp):
            def load(e, b, p):
                n = PIECES * b + p
                sp.wait_ge(split, PIECES * e + p - RAW + 1)
                sp.sem_inc(refills, 1)
                sp.dma_start(raw[n % RAW][:], piece_source(e, p)).then_inc(landed[n % RAW], 16)

            def ahead(e, b, last):
                for p in range(RAW, PIECES):
                    load(e, b, p)
                if not last:
                    for p in range(RAW):
                        load(e + 1, 1 - b, p)
            over_experts(sp, ahead)

        @st.block.tensor
        def _(pe):
            def one(e, b, last):
                for m in range(chunks):
                    if m >= 2:
                        pe.wait_ge(h_ready, chunks * e + m - 1)
                    for j in range(2):
                        p = 2 * (m // half) + j
                        if m % half == 0:
                            pe.wait_ge(split, PIECES * e + p + 1)
                        slot = (PIECES * b + p) % RING
                        cols = slice((m % half) * P, (m % half + 1) * P)
                        split_product(nc, core.bank(2 * (m % 2) + j),
                                      [((high[slot][:, c, cols], low[slot][:, c, cols]), (x_high[:, c, :], x_low[:, c, :]))
                                       for c in range(4)]).then_inc(ready, 1)
                for q in range(2):
                    pe.wait_ge(split, PIECES * e + 4 + q + 1)
                    pe.wait_ge(h_split, chunks * e + half * (q + 1))
                    slot = (PIECES * b + 4 + q) % RING
                    for i in range(TILES):
                        rows = slice(i * P, (i + 1) * P)
                        done = split_product(nc, core.bank(4 + i),
                                             [((h_high[:, half * q + c, rows], h_low[:, half * q + c, rows]),
                                               (high[slot][:, c, :], low[slot][:, c, :])) for c in range(half)],
                                             start=q == 0, stop=q == 1)
                        if q == 1:
                            done.then_inc(y_ready, 1)
                    if q == 0:
                        done.then_inc(halfway, 1)
            pe.wait_ge(x_split, CHUNKS)
            over_experts(pe, one)

        def uses(e, b, p):
            return 16 * (2 * e + p // RAW)

        @st.block.scalar
        def _(act):
            def high_piece(e, b, p, free=True, first=False):
                n = PIECES * b + p
                if free:
                    if p == 2:
                        act.wait_ge(halfway, e)
                    elif p == 3:
                        act.wait_ge(y_ready, TILES * e)
                    elif p >= 4:
                        act.wait_ge(ready, 2 * chunks * e + 2 * half)
                    else:
                        act.wait_ge(ready, 2 * chunks * e)
                if first:
                    first_loads[p].wait(act)
                else:
                    act.wait_ge(landed[n % RAW], uses(e, b, p))
                nc.scalar.copy(high[n % RING][:], raw[n % RAW][:]).then_inc(high_ready, 1)

            def one(e, b, last, first=False):
                for m in range(chunks):
                    act.wait_ge(ready, 2 * chunks * e + 2 * m + 1)
                    nc.scalar.activation(silu[:, m % 2, :], core.bank(2 * (m % 2)), ACT.Silu).then_inc(silu_ready, 1)
                    act.wait_ge(h_ready, chunks * e + m + 1)
                    nc.scalar.copy(h_high[:, m, :], h[:, m % 2, :]).then_inc(h_rounded, 1)
                    if m in (0, 1):
                        high_piece(e, b, 2 + m, free=not first, first=first and m == 0)
                    if m in (half, half + 1):
                        high_piece(e, b, m)
                if not last:
                    for p in range(2):
                        high_piece(e + 1, 1 - b, p)
            for c in range(CHUNKS):
                nc.scalar.copy(x_high[:, c, :], core.xnT[:, c, :]).then_inc(x_rounded, 1)
            for p in range(2):
                high_piece(0, 0, p, free=False, first=True)
            one(0, 0, False, first=True)
            one(1, 1, False)
            with act.Fori(1, looped) as s:
                for b in range(2):
                    one(2 * s + b, b, False)
            for e in range(2 * looped, experts):
                one(e, e % 2, e == experts - 1)

        @st.block.vector
        def _(dve):
            def low_piece(e, b, p):
                n = PIECES * b + p
                dve.wait_ge(high_ready, PIECES * e + p + 1)
                nc.vector.tensor_tensor(low[n % RING][:], raw[n % RAW][:], high[n % RING][:].bitcast(F32),
                                        ALU.subtract).then_inc(split, 1)

            def one(e, b, last):
                for m in range(chunks):
                    dve.wait_ge(silu_ready, chunks * e + m + 1)
                    dve.wait_ge(ready, 2 * chunks * e + 2 * m + 2)
                    nc.vector.tensor_tensor(h[:, m % 2, :], core.bank(2 * (m % 2) + 1), silu[:, m % 2, :], ALU.mult).then_inc(h_ready, 1)
                    dve.wait_ge(h_rounded, chunks * e + m + 1)
                    nc.vector.tensor_tensor(h_low[:, m, :], h[:, m % 2, :], h_high[:, m, :].bitcast(F32),
                                            ALU.subtract).then_inc(h_split, 1)
                    if m in (0, 1):
                        low_piece(e, b, 2 + m)
                    if m in (half, half + 1):
                        low_piece(e, b, m)
                if not last:
                    for p in range(2):
                        low_piece(e + 1, 1 - b, p)
                dve.wait_ge(h_split, chunks * e + chunks)
                for i in range(TILES):
                    dve.wait_ge(y_ready, TILES * e + i + 1)
                    nc.vector.scalar_tensor_tensor(out=core.x[:, i, :], in0=core.bank(4 + i), scalar=gate[:, i, bass.ds(e, 1)],
                                                   in1=core.x[:, i, :], op0=ALU.mult, op1=ALU.add).then_inc(y_added, 1)
            for c in range(CHUNKS):
                dve.wait_ge(x_rounded, c + 1)
                nc.vector.tensor_tensor(x_low[:, c, :], core.xnT[:, c, :], x_high[:, c, :].bitcast(F32),
                                        ALU.subtract).then_inc(x_split, 1)
            for p in range(2):
                low_piece(0, 0, p)
            over_experts(dve, one)


def layer0_ffn(core, w):
    with ExitStack() as local:
        gate = local.enter_context(core.nc.sbuf_tensor("f0_gate", [P, 4, 8], F32))
        raw, first_loads, issue = first_pieces(core, "f0", local, w["f0_W1"], w["f0_W3"])
        prepare(core, "f0", issue)
        gate_stage(core, "f0_gate_stage", w["f0_Wg"], w["f0_bg"], 8, gate, "softmax")
        experts_stage(core, "f0_experts", w["f0_W1"], w["f0_W3"], w["f0_W2"], gate, 8, raw, first_loads)


def layer1_ffn(core, w):
    with ExitStack() as local:
        gate = local.enter_context(core.nc.sbuf_tensor("f1_gate", [P, 4, 9], F32))
        raw, first_loads, issue = first_pieces(core, "f1", local, w["f1_W1"], w["f1_W3"])
        prepare(core, "f1", issue)
        gate_stage(core, "f1_gate_stage", w["f1_Wg"], w["f1_bg"], 8, gate, "sigmoid")
        experts_stage(core, "f1_experts", w["f1_W1"], w["f1_W3"], w["f1_W2"], gate, 9, raw, first_loads)


CAPACITY = 128
L2_EXPERTS = 16
L2_HIDDEN = 256


def capacity_gate_stage(core, weight, coefficient, place):
    nc = core.nc
    E = L2_EXPERTS
    with ExitStack() as local, Stage(core, "f2_gate") as st:
        def sb(n, shape, dtype=F32):
            return local.enter_context(nc.sbuf_tensor(f"f2g_{n}", shape, dtype))
        w_sb, raw, negmax, total = sb("weight", [P, 4, E]), sb("raw", [P, 4, E]), sb("negmax", [P, 4]), sb("total", [P, 4])
        tops, index, index_f = sb("tops", [P, 2, 4, 8]), sb("index", [P, 2, 4, 8], U32), sb("index_f", [P, 2, 4, 8])
        mask, position, kept = sb("mask", [P, 2, 4, E]), sb("position", [P, 2, 4, E]), sb("kept", [P, 2, 4, E])
        rest, share, before = sb("rest", [P, 4, E]), sb("share", [P, 2, 4]), sb("before", [P, P])
        landed, ready, maxima, expd = st.sem("weight_landed"), st.sem("logits_ready"), st.sem("maximum_ready"), st.sem("exp_ready")
        masks_ready, counted, kept_ready, total_ready = (st.sem("masks_ready"), st.sem("positions_ready"),
                                                         st.sem("kept_ready"), st.sem("expert_counts_ready"))
        before_ready = st.sem("before_ready")
        chain = st.chain(nc.vector, "vector_chain")

        @st.block.sync
        def _(sp):
            sp.dma_start(w_sb[:], weights(weight)).then_inc(landed, 16)

        @st.block.gpsimd
        def _(pool):
            nc.gpsimd.affine_select(out=before[:], in_=core.ones[:], compare_op=ALU.is_gt, fill=0.0, base=0,
                                    pattern=[[1, P]], channel_multiplier=-1).then_inc(before_ready, 1)

        @st.block.tensor
        def _(pe):
            pe.wait_ge(landed, 16)
            for i in range(TILES):
                last = product(nc, core, core.bank(0)[:, i * E:(i + 1) * E],
                               [(core.xnT[:, c, i * P:(i + 1) * P], w_sb[:, c, :]) for c in range(4)])
            last.then_inc(ready, 1)
            pe.wait_ge(masks_ready, 1)
            pe.wait_ge(before_ready, 1)
            for k in range(2):
                for i in range(TILES):
                    last = product(nc, core, core.bank(1)[:, (4 * k + i) * E:(4 * k + i + 1) * E],
                                   [(core.ones[:], mask[:, k, j, :]) for j in range(i)] + [(before[:], mask[:, k, i, :])])
            last.then_inc(counted, 1)
            pe.wait_ge(kept_ready, 1)
            product(nc, core, core.bank(2)[:, 0:E], [(core.ones[:], kept[:, 0, j, :]) for j in range(TILES)]).then_inc(total_ready, 1)

        @st.block.scalar
        def _(act):
            act.wait_ge(maxima, 1)
            for i in range(TILES):
                last = nc.scalar.activation(raw[:, i, :], core.bank(0)[:, i * E:(i + 1) * E], ACT.Exp, bias=negmax[:, i:i + 1],
                                            accum_out=total[:, i:i + 1])
                last.then_inc(expd, 1)

        @st.block.vector
        def _(dve):
            flat = lambda x: x[:].rearrange("p k i e -> p (k i) e")
            dve.wait_ge(ready, 1)
            nc.vector.tensor_reduce(negmax[:], core.bank(0)[:, 0:4 * E].rearrange("p (i e) -> p i e", i=4), AXIS.X, ALU.max,
                                    negate=True).then_inc(maxima, 1)
            dve.wait_ge(expd, TILES)
            chain(nc.vector.reciprocal(total[:], total[:]))
            chain(nc.vector.tensor_tensor(raw[:], raw[:], total[:].unsqueeze(2).to_broadcast([P, 4, E]), ALU.mult))
            for k, values in enumerate((raw, rest)):
                for i in range(TILES):
                    chain(nc.vector.max(tops[:, k, i, :], values[:, i, :]))
                    chain(nc.vector.max_index(index[:, k, i, :], tops[:, k, i, :], values[:, i, :]))
                chain(nc.vector.tensor_copy(index_f[:, k], index[:, k]))
                for i in range(TILES):
                    last = nc.vector.tensor_scalar(mask[:, k, i, :], core.iota[:, 0:E], index_f[:, k, i, 0:1], None, ALU.is_equal)
                    if k == 0 or i < TILES - 1:
                        chain(last)
                if k == 0:
                    chain(nc.vector.tensor_scalar(rest[:], mask[:, 0], -1.0, 1.0, ALU.mult, ALU.add))
                    chain(nc.vector.tensor_tensor(rest[:], rest[:], raw[:], ALU.mult))
            last.then_inc(masks_ready, 1)
            chain(nc.vector.tensor_tensor(total[:], tops[:, 0, :, 0], tops[:, 1, :, 0], ALU.add))
            chain(nc.vector.tensor_scalar(total[:], total[:], 1e-9, None, ALU.add))
            chain(nc.vector.reciprocal(total[:], total[:]))
            for k in range(2):
                chain(nc.vector.tensor_tensor(share[:, k], tops[:, k, :, 0], total[:], ALU.mult))
            dve.wait_ge(counted, 1)
            counts = core.bank(1)[:, 0:8 * E].rearrange("p (k i e) -> p k i e", k=2, i=4)
            chain(nc.vector.tensor_tensor(position[:, 0], counts[:, 0], mask[:, 0], ALU.mult))
            chain(nc.vector.tensor_scalar(kept[:, 0], position[:, 0], float(CAPACITY), None, ALU.is_lt))
            nc.vector.tensor_tensor(kept[:, 0], kept[:, 0], mask[:, 0], ALU.mult).then_inc(kept_ready, 1)
            dve.wait_ge(total_ready, 1)
            chain(nc.vector.tensor_copy(rest[:, 0, :], core.bank(2)[:, 0:E]))
            chain(nc.vector.tensor_tensor(position[:, 1], counts[:, 1], rest[:, 0:1, :].to_broadcast([P, 4, E]), ALU.add))
            chain(nc.vector.tensor_tensor(position[:, 1], position[:, 1], mask[:, 1], ALU.mult))
            chain(nc.vector.tensor_scalar(kept[:, 1], position[:, 1], float(CAPACITY), None, ALU.is_lt))
            chain(nc.vector.tensor_tensor(kept[:, 1], kept[:, 1], mask[:, 1], ALU.mult))
            chain(nc.vector.tensor_reduce(place[:].rearrange("p k i -> p (k i)"), flat(position), AXIS.X, ALU.add))
            chain(nc.vector.tensor_tensor(coefficient[:].rearrange("p k i e -> p (k i) e"), flat(kept),
                                          share[:].rearrange("p k i -> p (k i)").unsqueeze(2).to_broadcast([P, 8, E]), ALU.mult))


def layer2_ffn(core, w):
    nc = core.nc
    with ExitStack() as local:
        def sb(n, shape):
            return local.enter_context(nc.sbuf_tensor(f"f2_{n}", shape, F32))
        core.open_pool(local, 10)
        coefficient, place = sb("coefficient", [P, 2, 4, L2_EXPERTS]), sb("place", [P, 2, 4])
        hot = sb("hot", [P, 4, CAPACITY])
        combine, dispatch = core.section(0), core.section(1)
        pick = lambda x, b: x[:, b, :].rearrange("p (i c) -> p i c", i=4)
        combineT, inT, y_in = core.section(2), core.section(3), core.section(4)
        hiddenT = core.section(5)
        W1 = [core.section(6 + b, 4, L2_HIDDEN) for b in range(2)]
        W2 = [core.section(8 + b, 2, DIM) for b in range(2)]
        pairs = L2_EXPERTS // 2
        L1, L2 = [], []

        def issue(sp):
            for b in range(2):
                L1.append(core.load(sp, W1[b], w["f2_W1"][b:b + 1].rearrange("o (c p) n -> p (o c) n", p=P)))
                L2.append(core.load(sp, W2[b], w["f2_W2"][b:b + 1].rearrange("o (c p) n -> p (o c) n", p=P)))
        prepare(core, "f2", issue)
        capacity_gate_stage(core, w["f2_Wg"], coefficient, place)
        with Stage(core, "f2_experts") as st:
            landed1, landed2 = [st.sem(f"w1_landed_{b}") for b in range(2)], [st.sem(f"w2_landed_{b}") for b in range(2)]
            combined, turned, entered = st.sem("combine_ready"), st.sem("combine_turned"), st.sem("inputs_ready")
            turn_copied, in_copied = st.sem("turned_copied"), st.sem("inputs_copied")
            hid_ready, hid_made, out_ready, out_copied = (st.sem("hidden_ready"), st.sem("hidden_made"),
                                                          st.sem("expert_outputs_ready"), st.sem("expert_outputs_copied"))
            y_ready, y_added = st.sem("row_outputs_ready"), st.sem("row_outputs_added")
            chained = st.sem("vector_chain")

            def load1(sp, e, b):
                sp.dma_start(W1[b], w["f2_W1"][bass.ds(e, 1)].rearrange("o (c p) n -> p (o c) n", p=P)).then_inc(landed1[b], 16)

            def load2(sp, e, b):
                sp.dma_start(W2[b], w["f2_W2"][bass.ds(e, 1)].rearrange("o (c p) n -> p (o c) n", p=P)).then_inc(landed2[b], 16)

            @st.block.sync
            def _(sp):
                with sp.Fori(1, pairs) as s:
                    for b in range(2):
                        sp.wait_ge(hid_ready, 2 * s + b - 1)
                        load1(sp, 2 * s + b, b)
                    for b in range(2):
                        sp.wait_ge(out_ready, 2 * s + b - 1)
                        load2(sp, 2 * s + b, b)

            @st.block.tensor
            def _(pe):
                def pair(s, first=False):
                    for b in range(2):
                        pe.wait_ge(combined, 2 * s + b + 1)
                        for i in range(TILES):
                            last = nc.tensor.transpose(core.bank(b)[:, i * P:(i + 1) * P], pick(combine, b)[:, i, :], core.ident[:])
                        last.then_inc(turned, 1)
                        for c in range(CHUNKS):
                            last = product(nc, core, core.bank(2 + b)[:, c * P:(c + 1) * P],
                                           [(core.xn[:, i, c * P:(c + 1) * P], pick(dispatch, b)[:, i, :]) for i in range(TILES)])
                        last.then_inc(entered, 1)
                    for b in range(2):
                        if first:
                            L1[b].wait(pe)
                        else:
                            pe.wait_ge(landed1[b], 16 * s)
                        pe.wait_ge(in_copied, 2 * s + b + 1)
                        for m in range(2):
                            last = product(nc, core, core.bank(b)[:, m * P:(m + 1) * P],
                                           [(W1[b][:, c, m * P:(m + 1) * P], inT[:, b, :].rearrange("p (c n) -> p c n", c=4)[:, c, :])
                                            for c in range(4)])
                        last.then_inc(hid_ready, 1)
                    for b in range(2):
                        if first:
                            L2[b].wait(pe)
                        else:
                            pe.wait_ge(landed2[b], 16 * s)
                        pe.wait_ge(hid_made, 2 * s + b + 1)
                        product(nc, core, core.bank(2 + b),
                                [(hiddenT[:, b, m * P:(m + 1) * P], W2[b][:, m, :]) for m in range(2)]).then_inc(out_ready, 1)
                    for b in range(2):
                        pe.wait_ge(out_copied, 2 * s + b + 1)
                        for i in range(TILES):
                            if not (first and b == 0):
                                pe.wait_ge(y_added, 8 * s + 4 * b + i - 3)
                            product(nc, core, core.bank(4 + i), [(combineT[:, b, i * P:(i + 1) * P], y_in[:, b, :])]).then_inc(y_ready, 1)
                pair(0, first=True)
                with pe.Fori(1, pairs) as s:
                    pair(s)

            @st.block.scalar
            def _(act):
                with act.Fori(0, pairs) as s:
                    for b in range(2):
                        act.wait_ge(turned, 2 * s + b + 1)
                        nc.scalar.copy(combineT[:, b, :], core.bank(b)).then_inc(turn_copied, 1)
                        act.wait_ge(entered, 2 * s + b + 1)
                        act.wait_ge(turn_copied, 2 * s + b + 1)
                        nc.scalar.copy(inT[:, b, :], core.bank(2 + b)).then_inc(in_copied, 1)
                    for b in range(2):
                        act.wait_ge(hid_ready, 2 * s + b + 1)
                        nc.scalar.activation(hiddenT[:, b, 0:2 * P], core.bank(b)[:, 0:2 * P], ACT.Relu).then_inc(hid_made, 1)
                    for b in range(2):
                        act.wait_ge(out_ready, 2 * s + b + 1)
                        nc.scalar.copy(y_in[:, b, :], core.bank(2 + b)).then_inc(out_copied, 1)

            @st.block.vector
            def _(dve):
                def combine_pair(s, first=False):
                    for b in range(2):
                        if not first:
                            dve.wait_ge(entered, 2 * s + b - 1)
                        for i in range(TILES):
                            for k, dst in enumerate((pick(combine, b), hot)):
                                last = nc.vector.tensor_scalar(dst[:, i, :], core.iota[:, 0:CAPACITY], place[:, k, i:i + 1],
                                                               coefficient[:, k, i, bass.ds(2 * s + b, 1)], ALU.is_equal, ALU.mult)
                        last.then_inc(chained, 1)
                        dve.wait_ge(chained, 4 * s + 2 * b + 1)
                        nc.vector.tensor_tensor(pick(combine, b), pick(combine, b), hot[:], ALU.add).then_inc(chained, 1)
                        dve.wait_ge(chained, 4 * s + 2 * b + 2)
                        nc.vector.tensor_scalar(pick(dispatch, b), pick(combine, b), 0.0, None, ALU.is_gt).then_inc(combined, 1)

                def add_pair(s, first=False):
                    for b in range(2):
                        for i in range(TILES):
                            dve.wait_ge(y_ready, 8 * s + 4 * b + i + 1)
                            if not (first and b == 0):
                                dve.wait_ge(y_added, 8 * s + 4 * b + i - 3)
                            nc.vector.tensor_tensor(core.x[:, i, :], core.bank(4 + i), core.x[:, i, :], ALU.add).then_inc(y_added, 1)
                combine_pair(0, first=True)
                combine_pair(1)
                add_pair(0, first=True)
                with dve.Fori(1, pairs - 1) as s:
                    combine_pair(s + 1)
                    add_pair(s)
                add_pair(pairs - 1)


def layer1_gnn(core, w):
    nc = core.nc
    with ExitStack() as local:
        core.open_pool(local, 3)
        sumT, W = core.section(0), core.section(1, 8, DIM)
        rows = local.enter_context(nc.sbuf_tensor("g1_rows", [P, 1, 512], F32))
        inverse = local.enter_context(nc.sbuf_tensor("g1_inverse", [P, 4], F32))
        L = {}

        def issue(sp):
            L["W"] = core.load(sp, W, weights(w["g1_W"]))
            L["rows"] = core.load(sp, rows[:], w["g1_rows"].rearrange("(o r) n -> o r n", o=1).to_broadcast([P, 1, 512]))
        prepare(core, "g1", issue)
        with Stage(core, "g1_degrees") as st:
            chain = st.chain(nc.vector, "vector_chain")

            @st.block.vector
            def _(dve):
                chain(nc.vector.tensor_reduce(inverse[:], core.edges_to[:], AXIS.X, ALU.add))
                chain(nc.vector.tensor_scalar(inverse[:], inverse[:], 1.0, None, ALU.max))
                chain(nc.vector.reciprocal(inverse[:], inverse[:]))
        products_stage(core, "g1_sums",
                       [Tile([(P, 0, NODES, [(core.xn[:, j, c * P:(c + 1) * P], core.edges_from[:, j, :]) for j in range(TILES)])],
                             "VA"[c % 2]) for c in range(CHUNKS)], lambda t, e, ps, chain: copy_out(nc, e, sumT[:, t, :], ps))

        def tiles():
            out = []
            for i in range(TILES):
                rows_i = slice(i * P, (i + 1) * P)
                out.append(Tile([(P, 0, DIM, [(sumT[:, c, rows_i], W[:, 4 + c, :]) for c in range(4)])], "V", [lambda: L["W"]]))
                out.append(Tile([(P, 0, DIM, [(core.xnT[:, c, rows_i], W[:, c, :]) for c in range(4)])], "V"))
            return out

        def finish(t, e, ps, chain):
            i = t // 2
            out = core.branches[:, i, :]
            if t % 2 == 0:
                return nc.vector.scalar_tensor_tensor(out=out, in0=ps, scalar=inverse[:, i:i + 1], in1=rows[:, 0, :],
                                                      op0=ALU.mult, op1=ALU.add)
            chain(nc.vector.tensor_tensor(out, ps, out, ALU.add))
            return nc.vector.tensor_scalar(out, out, 0.0, None, ALU.max)
        products_stage(core, "g1_out", tiles(), finish, params=[lambda: L["rows"]], ordered=True)


def layer2_gnn(core, w):
    nc = core.nc
    heads = 4
    with ExitStack() as local:
        core.open_pool(local, 12)

        def sb(name, shape):
            return local.enter_context(nc.sbuf_tensor("g2_" + name, shape, F32))
        rows, cols = sb("rows", [P, 7, 512]), sb("cols", [P, 48])
        v, turned = sb("v", [P, 4, 512]), sb("attention", [P, 4, 512])
        xT = core.section(8, 16, 512)
        Wq, Wk, Wv, Wskip = (core.section(j) for j in range(4))
        qT, kT, mask, h = core.section(4), core.section(5), core.section(6), core.section(7)
        L = {}

        def load_head(n, names):
            def issue(sp):
                for name, dst in (("g2_Wq", Wq), ("g2_Wk", Wk), ("g2_Wv", Wv), ("g2_Wskip", Wskip)):
                    if name in names and n < heads:
                        L[name, n] = core.load(sp, dst, weights(w[name], (n * DIM, (n + 1) * DIM)))
            return issue
        before_attention, after_attention = ("g2_Wq", "g2_Wk", "g2_Wv"), ("g2_Wskip",)

        def issue(sp):
            L["cols"] = core.load(sp, cols[:], w["g2_cols"])
            load_head(0, before_attention)(sp)
            L["rows"] = core.load(sp, rows[:], w["g2_rows"].rearrange("(o r) n -> o r n", o=1).to_broadcast([P, 7, 512]))
        prepare(core, "g2", issue)
        with Stage(core, "g2_mask") as st:
            chain = st.chain(nc.vector, "vector_chain")

            @st.block.vector
            def _(dve):
                chain(nc.vector.tensor_scalar(mask[:], core.edges_to[:], 0.5, None, ALU.is_lt))
                nc.vector.tensor_scalar(mask[:], mask[:], MASKED, None, ALU.mult)
        Wlin = core.section(4, 16, 512)

        def issue_lin(sp):
            L["lin"] = core.load(sp, Wlin, weights(w["g2_Wlin"]))
        for n in range(heads):
            def finish(t, e, ps, chain):
                m = t % 4
                if t < 4:
                    return nc.scalar.activation(qT[:, m, :], ps, ACT.Identity, bias=cols[:, 4 * n + m:4 * n + m + 1])
                if t < 8:
                    return nc.scalar.activation(kT[:, m, :], ps, ACT.Identity, bias=cols[:, 16 + 4 * n + m:17 + 4 * n + m])
                return nc.vector.tensor_tensor(v[:, m, :], ps, rows[:, n, :], ALU.add)
            products_stage(core, f"g2_qkv{n}",
                           turned_tiles(core.xnT, Wq, "A", [lambda: L["g2_Wq", n]]) + turned_tiles(core.xnT, Wk, "A", [lambda: L["g2_Wk", n]])
                           + linear_tiles(core.xnT, Wv, "V", [lambda: L["g2_Wv", n]]), finish,
                           params=[lambda: L["rows"], lambda: L["cols"]], issue=load_head(n, after_attention))
            softmax_stage(core, f"g2_attention{n}",
                          [[(qT[:, c, i * P:(i + 1) * P], kT[:, c, :]) for c in range(4)] for i in range(TILES)], NODES,
                          scale=DIM ** -0.5, mask=lambda u: mask[:, u, :], weigh=lambda u: core.edges_to[:, u, :],
                          turned=lambda u: turned[:, :, u * P:(u + 1) * P], issue=load_head(n + 1, before_attention))

            def finish_values(t, e, ps, chain):
                c = 4 * n + t
                return nc.scalar.activation(xT[:, c, :], ps, ACT.Identity, bias=cols[:, 32 + c:33 + c])
            products_stage(core, f"g2_values{n}",
                           [Tile([(P, 0, NODES, [(v[:, j, c * P:(c + 1) * P], turned[:, j, :]) for j in range(4)]
                                   + [(Wskip[:, k, c * P:(c + 1) * P], core.xnT[:, k, :]) for k in range(4)])], "A",
                                 [lambda: L["g2_Wskip", n]]) for c in range(CHUNKS)], finish_values,
                           issue=issue_lin if n == heads - 1 else None)

        def finish_out(t, e, ps, chain):
            return nc.vector.tensor_tensor(v[:, t, :], ps, rows[:, 4, :], ALU.add)
        products_stage(core, "g2_lin", linear_tiles(xT, Wlin, "V", [lambda: L["lin"]]), finish_out)

        def finish_first(t, e, ps, chain):
            return nc.vector.tensor_tensor(v[:, t, :], ps, v[:, t, :], ALU.add)
        products_stage(core, "g2_first", [Tile([(P, c * P, (c + 1) * P, [(xT[:, c, i * P:(i + 1) * P], None)]) for c in range(CHUNKS)], "V")
                                          for i in range(TILES)], finish_first)
        norm_stage(core, "g2_norm", v, core.branches, scale=rows[:, 5, :], shift=rows[:, 6, :])


MUL = 128
SILU_2MOM = 1.679177
GROUP = 4
BLOCKS = 8


def edges_stage(core, w, table, sums):
    nc = core.nc
    groups = EDGE_TILES // GROUP
    with ExitStack() as local, Stage(core, "g3_edges") as st:
        def sb(n, shape, dtype=F32):
            return local.enter_context(nc.sbuf_tensor("g3e_" + n, shape, dtype))
        attr = sb("attributes", [P, 4 * EDGE_TILES])
        W1, W2, W3, W4 = sb("mlp1", [8, 64]), sb("mlp2", [64, P]), sb("mlp3", [64, P]), sb("mlp4", [64, 4 * MUL])
        feat = sb("features", [8, 2, GROUP * P])
        hid = sb("hidden", [64, 3, GROUP * P])
        senders = sb("senders", [P, 2, GROUP], I32)
        t2, dot = sb("w2_s0", [P, 2, MUL]), sb("dot", [P, 2, MUL])
        gathered = [core.section(2 + b, GROUP, 4 * MUL) for b in range(2)]
        raw = sb("messages", [P, 2, BLOCKS * MUL])
        high = [sb(f"messages_high_{b}", [P, GROUP, BLOCKS * MUL], F32R) for b in range(2)]
        low = [sb(f"messages_low_{b}", [P, GROUP, BLOCKS * MUL], F32R) for b in range(2)]
        hot = [sb(f"one_hots_{b}", [P, GROUP, NODES], F32R) for b in range(2)]
        params = st.sem("parameters_landed")
        feat_landed = [st.sem(f"features_landed_{b}") for b in range(2)]
        rows_landed = core.gather_sems
        attr_ready = st.sem("attributes_scaled")
        mlp_ready, mlp_made, tpw_ready = st.sem("mlp_products"), st.sem("mlp_silus"), st.sem("edge_weights_ready")
        t2_ready, vectors_ready, raw_ready = st.sem("w2_s0_ready"), st.sem("vector_a_ready"), st.sem("raw_messages_ready")
        high_ready, message_ready = st.sem("high_parts_ready"), st.sem("messages_ready")
        summed, added, kept = st.sem("group_summed"), st.sem("sums_added"), st.sem("kept_sums_ready")
        group_read = st.sem("group_read")
        chained, padded = st.sem("vector_chain"), st.sem("weights_padded")
        LINKS = 3
        MLP_BANK, SUM_BANK = 0, 1
        tpw_bank = lambda j: core.bank(2 + j % 2)

        @st.block.sync
        def _(sp):
            def features(g, b):
                sp.dma_start(feat[:, b, :], w["g3_feat"][:, bass.ds(g * GROUP * P, GROUP * P)]).then_inc(feat_landed[b], 16)
            for dst, name in ((attr, "g3_attr"), (W1, "g3_mlp1"), (W2, "g3_mlp2"), (W3, "g3_mlp3"), (W4, "g3_mlp4")):
                src = w[name].rearrange("p t m -> p (t m)") if name == "g3_attr" else w[name]
                sp.dma_start(dst[:, 0:src.shape[1]], src).then_inc(params, 16)
            features(0, 0)
            features(1, 1)
            with sp.Fori(1, groups // 2) as s:
                for b in range(2):
                    sp.wait_ge(mlp_ready, 3 * (2 * s + b) - 5)
                    features(2 * s + b, b)

        @st.block.gpsimd
        def _(pool):
            def gather(g, b, first):
                if not first:
                    pool.wait_ge(raw_ready, GROUP * g - GROUP)
                nc.gpsimd.tensor_copy(senders[:, b, :], core.src_i[:, bass.ds(GROUP * g, GROUP)])
                pool.drain()
                for j in range(GROUP):
                    nc.gpsimd.indirect_dma_start(
                        out=gathered[b][:, j, :], out_offset=None, in_=table,
                        in_offset=bass.IndirectOffsetOnAxis(ap=senders[:, b, j:j + 1].bitcast(U32), axis=0)).then_inc(rows_landed[b], 16)
            gather(0, 0, True)
            gather(1, 1, True)
            with pool.Fori(1, groups // 2) as s:
                for b in range(2):
                    gather(2 * s + b, b, False)

        @st.block.tensor
        def _(pe):
            hidden_weights = (W1, W2, W3)

            def layer(g, b, n, use):
                if n == 0:
                    pe.wait_ge(feat_landed[b], 16 * use)
                else:
                    pe.wait_ge(mlp_made, 3 * g + n)
                right = feat[:, b, :] if n == 0 else hid[:, n - 1, :]
                product(nc, core, core.bank(MLP_BANK)[0:hidden_weights[n].shape[1], :],
                        [(hidden_weights[n][:], right)]).then_inc(mlp_ready, 1)

            def edge_weights(g, j, first=False):
                if j == 0:
                    pe.wait_ge(mlp_made, 3 * g + 3)
                if not first:
                    pe.wait_ge(raw_ready, GROUP * g + j - 1)
                product(nc, core, tpw_bank(j), [(hid[:, 2, j * P:(j + 1) * P], W4[:])]).then_inc(tpw_ready, 1)

            def add_up(g, r, b, first=False, last=False):
                m, half = r // 2, r % 2
                if r == 0:
                    pe.wait_ge(message_ready, GROUP * g + GROUP)
                if half == 0 and not (first and r == 0):
                    pe.wait_ge(added, 4 * g + m + 1)
                out = core.bank(SUM_BANK if half == 0 else 4 + m)
                start, stop = (True, True) if half == 0 else (first, last)
                for j in range(GROUP):
                    for p, part in enumerate((high, low)):
                        done = nc.tensor.matmul(out, hot[b][:, j, m * P:(m + 1) * P],
                                                part[b][:, j, half * BANK:(half + 1) * BANK],
                                                start=start and j == 0 and p == 0, stop=stop and j == GROUP - 1 and p == 1,
                                                skip_group_check=half == 1)
                if half == 0:
                    done.then_inc(summed, 1)
                elif last:
                    done.then_inc(kept, 1)
                elif r == BLOCKS - 1:
                    done.then_inc(group_read, 1)

            def group(g, b, use, sum_g, has_next=True, sum_first=False):
                def between(*products):
                    for r in products if sum_g is not None else ():
                        add_up(sum_g, r, 1 - b, first=sum_first)
                edge_weights(g, 2)
                between(0)
                edge_weights(g, 3)
                between(1)
                if has_next:
                    layer(g + 1, 1 - b, 0, use)
                between(2)
                if has_next:
                    layer(g + 1, 1 - b, 1, use)
                between(3, 4)
                if has_next:
                    layer(g + 1, 1 - b, 2, use)
                between(5)
                if has_next:
                    edge_weights(g + 1, 0)
                    edge_weights(g + 1, 1)
                between(6, 7)
            pe.wait_ge(params, 80)
            pe.wait_ge(padded, 2)
            for n in range(3):
                layer(0, 0, n, 1)
            edge_weights(0, 0, first=True)
            edge_weights(0, 1, first=True)
            group(0, 0, 1, None)
            group(1, 1, 2, 0, sum_first=True)
            with pe.Fori(1, groups // 2 - 1) as s:
                for b in range(2):
                    group(2 * s + b, b, s + 1 + b, 2 * s + b - 1)
            group(groups - 2, 0, groups // 2, groups - 3)
            group(groups - 1, 1, 0, groups - 2, has_next=False)
            for r in range(BLOCKS):
                add_up(groups - 1, r, 1, last=True)

        @st.block.scalar
        def _(act):
            def hidden(g, n):
                act.wait_ge(mlp_ready, 3 * g + n + 1)
                scale = 8 ** -0.5 if n == 0 else SILU_2MOM / 8
                nc.scalar.activation(hid[:, n, :], core.bank(MLP_BANK)[0:64, :], ACT.Silu, scale=scale).then_inc(mlp_made, 1)

            def vectors(g, j):
                act.wait_ge(t2_ready, GROUP * g + j + 1)
                for m in range(3):
                    last = nc.scalar.activation(raw[:, j % 2, (2 + 2 * m) * MUL:(3 + 2 * m) * MUL], t2[:, j % 2, :], ACT.Copy,
                                                scale=attr[:, bass.ds(4 * GROUP * g + 4 * j + m + 1, 1)])
                last.then_inc(vectors_ready, 1)

            def high_part(g, j, b, reused):
                if j == 0 and reused:
                    act.wait_ge(group_read, g - 1)
                act.wait_ge(vectors_ready, GROUP * g + j + 1)
                act.wait_ge(raw_ready, GROUP * g + j + 1)
                nc.scalar.copy(high[b][:, j, :], raw[:, j % 2, :]).then_inc(high_ready, 1)

            def group(g, b, reused=True, has_next=True):
                high_part(g, 0, b, reused)
                high_part(g, 1, b, reused)
                vectors(g, 2)
                high_part(g, 2, b, reused)
                if has_next:
                    hidden(g + 1, 0)
                vectors(g, 3)
                high_part(g, 3, b, reused)
                if has_next:
                    hidden(g + 1, 1)
                    hidden(g + 1, 2)
                    vectors(g + 1, 0)
                    vectors(g + 1, 1)
            act.wait_ge(attr_ready, 1)
            for n in range(3):
                hidden(0, n)
            vectors(0, 0)
            vectors(0, 1)
            group(0, 0, reused=False)
            group(1, 1, reused=False)
            with act.Fori(1, groups // 2 - 1) as s:
                for b in range(2):
                    group(2 * s + b, b)
            group(groups - 2, 0)
            group(groups - 1, 1, has_next=False)

        @st.block.vector
        def _(dve):
            def link(instruction, g, j, n):
                instruction.then_inc(chained, 1)
                dve.wait_ge(chained, (g * GROUP + j) * LINKS + n)

            def message(g, j, b, use):
                y = [attr[:, bass.ds(4 * GROUP * g + 4 * j + m, 1)] for m in range(4)]
                if j == 0:
                    dve.wait_ge(rows_landed[b], 16 * GROUP * use)
                dve.wait_ge(tpw_ready, GROUP * g + j + 1)
                part = [tpw_bank(j)[:, k * MUL:(k + 1) * MUL] for k in range(4)]
                s = [gathered[b][:, j, k * MUL:(k + 1) * MUL] for k in range(4)]
                out = raw[:, j % 2, :]
                nc.vector.tensor_tensor(t2[:, j % 2, :], part[1], s[0], ALU.mult).then_inc(t2_ready, 1)
                link(nc.vector.tensor_scalar(dot[:, j % 2, :], s[1], y[1], None, ALU.mult), g, j, 1)
                nc.vector.scalar_tensor_tensor(out=out[:, 0:MUL], in0=part[0], scalar=y[0], in1=s[0], op0=ALU.mult, op1=ALU.mult)
                link(nc.vector.scalar_tensor_tensor(out=dot[:, j % 2, :], in0=s[2], scalar=y[2], in1=dot[:, j % 2, :],
                                                    op0=ALU.mult, op1=ALU.add), g, j, 2)
                nc.vector.scalar_tensor_tensor(out=out.rearrange("p (m two u) -> p m two u", two=2, u=MUL)[:, 1:4, 1, :],
                                               in0=part[2].unsqueeze(1).to_broadcast([P, 3, MUL]), scalar=y[0],
                                               in1=gathered[b][:, j, MUL:].rearrange("p (m u) -> p m u", m=3),
                                               op0=ALU.mult, op1=ALU.mult)
                link(nc.vector.scalar_tensor_tensor(out=dot[:, j % 2, :], in0=s[3], scalar=y[3], in1=dot[:, j % 2, :],
                                                    op0=ALU.mult, op1=ALU.add), g, j, 3)
                nc.vector.scalar_tensor_tensor(out=out[:, MUL:2 * MUL], in0=part[3], scalar=3 ** -0.5, in1=dot[:, j % 2, :],
                                               op0=ALU.mult, op1=ALU.mult).then_inc(raw_ready, 1)

            def low_part(g, j, b):
                dve.wait_ge(high_ready, GROUP * g + j + 1)
                nc.vector.tensor_scalar(hot[b][:, j, :], core.iota[:], core.dst_f[:, bass.ds(GROUP * g + j, 1)], None, ALU.is_equal)
                nc.vector.tensor_tensor(low[b][:, j, :], raw[:, j % 2, :], high[b][:, j, :].bitcast(F32),
                                        ALU.subtract).then_inc(message_ready, 1)

            def add(g, m):
                dve.wait_ge(summed, 4 * g + m + 1)
                if m == 0:
                    dve.wait_ge(added, 4 * g + 1)
                to = sums[:, m, 0:BANK]
                nc.vector.tensor_tensor(to, core.bank(SUM_BANK), to, ALU.add).then_inc(added, 1)

            def group(g, b, use, sum_g, has_next=True):
                low_part(g, 0, b)
                message(g, 2, b, use[0])
                if sum_g is not None:
                    add(sum_g, 0)
                low_part(g, 1, b)
                message(g, 3, b, use[0])
                low_part(g, 2, b)
                if sum_g is not None:
                    add(sum_g, 1)
                low_part(g, 3, b)
                if sum_g is not None:
                    add(sum_g, 2)
                if has_next:
                    message(g + 1, 0, 1 - b, use[1])
                if sum_g is not None:
                    add(sum_g, 3)
                if has_next:
                    message(g + 1, 1, 1 - b, use[1])
            nc.vector.memset(W2[:, 64:P], 0.0).then_inc(padded, 1)
            nc.vector.memset(W3[:, 64:P], 0.0).then_inc(padded, 1)
            dve.wait_ge(params, 80)
            nc.vector.tensor_scalar(attr[:], attr[:], SILU_2MOM / 8, None, ALU.mult).then_inc(attr_ready, 1)
            dve.wait_ge(attr_ready, 1)
            nc.vector.memset(sums[:], 0.0).then_inc(added, 1)
            message(0, 0, 0, 1)
            message(0, 1, 0, 1)
            group(0, 0, (1, 1), None)
            group(1, 1, (1, 2), 0)
            with dve.Fori(1, groups // 2 - 1) as s:
                for b in range(2):
                    group(2 * s + b, b, (s + 1, s + 1 + b), 2 * s + b - 1)
            group(groups - 2, 0, (groups // 2, groups // 2), groups - 3)
            group(groups - 1, 1, (groups // 2, None), groups - 2, has_next=False)
            for m in range(TILES):
                add(groups - 1, m)
            for m in range(TILES):
                dve.wait_ge(kept, m + 1)
                nc.vector.tensor_copy(sums[:, m, BANK:2 * BANK], core.bank(4 + m))


def layer3_gnn(core, w):
    nc = core.nc
    with ExitStack() as local:
        core.open_pool(local, 4)

        def sb(name, shape):
            return local.enter_context(nc.sbuf_tensor("g3_" + name, shape, F32))
        Wup, Wout = sb("Wup", [P, 2 * MUL]), sb("Wout", [P, 2, 2 * MUL])
        upT, up = core.section(2), core.section(3)
        sums = core.section(0, 4, BLOCKS * MUL)
        L = {}

        def issue(sp):
            L["up"] = core.load(sp, Wup[:], w["g3_Wup"])
            L["out"] = core.load(sp, Wout[:], weights(w["g3_Wout"]))
        prepare(core, "g3", issue)

        def blocks(i, c):
            return core.xn[:, i, 0:MUL] if c == 0 else core.xn[:, i, MUL:].rearrange("p (u m) -> p m u", m=3)[:, c - 1, :]
        transpose_stage(core, "g3_turn", upT, blocks)
        products_stage(core, "g3_up",
                       [Tile([(P, c * MUL, (c + 1) * MUL, [(upT[:, c, i * P:(i + 1) * P], Wup[:, (c > 0) * MUL:(c > 0) * MUL + MUL])])
                              for c in range(4)], "V", [lambda: L["up"]]) for i in range(TILES)],
                       lambda t, e, ps, chain: nc.vector.tensor_scalar(up[:, t, :], ps, MUL ** -0.5, None, ALU.mult))
        table = nc.dram_tensor("node_table", (NODES, 4 * MUL), F32, kind="Internal").ap()
        with Stage(core, "g3_table") as st:
            stored = st.sem("table_stored")

            @st.block.sync
            def _(sp):
                sp.dma_start(table.rearrange("(i p) d -> p i d", p=P), up).then_inc(stored, 16)
                sp.wait_ge(stored, 16)
        edges_stage(core, w, table, sums)
        sumsT = core.section(2, BLOCKS, NODES)
        products_stage(core, "g3_turn_sums",
                       [Tile([(P, i * P, (i + 1) * P, [(sums[:, i, c * MUL:(c + 1) * MUL], None)]) for i in range(TILES)], "VA"[c % 2])
                        for c in range(BLOCKS)], lambda t, e, ps, chain: copy_out(nc, e, sumsT[:, t, :], ps))
        scale = 1.0 / (16.0 * 10.0)

        def finish(t, e, ps, chain):
            out = core.branches[:, t, :]
            nc.vector.tensor_scalar(out[:, 0:MUL], ps[:, 0:MUL], scale, None, ALU.mult)
            return nc.vector.tensor_scalar(out[:, MUL:].rearrange("p (u m) -> p m u", m=3), ps[:, MUL:].rearrange("p (m u) -> p m u", m=3),
                                           scale, None, ALU.mult)
        products_stage(core, "g3_out",
                       [Tile([(P, k * MUL, (k + 1) * MUL,
                               [(sumsT[:, 2 * k + c, i * P:(i + 1) * P], Wout[:, c, (k > 0) * MUL:(k > 0) * MUL + MUL]) for c in range(2)])
                              for k in range(4)], "V", [lambda: L["out"]]) for i in range(TILES)], finish)


FLOW_EPS = 1e-6


def flow_stage(core, q, k, v, kse, tmp, factor):
    nc = core.nc
    with ExitStack() as local, Stage(core, "m3_flow") as st:
        sink_in, source_out, sink, source = (local.enter_context(nc.sbuf_tensor(f"m3f_{n}", [P, 4, HEADS], F32))
                                             for n in ("sink_in", "source_out", "sink", "source"))
        total = local.enter_context(nc.sbuf_tensor("m3f_total", [P, HEADS], F32))
        sigmoids, column_sums = st.sem("sigmoids_ready"), st.sem("column_sums_ready")
        weighted, clipped, expd = st.sem("weighted_ready"), st.sem("clipped_ready"), st.sem("allocations_ready")
        chain = st.chain(nc.vector, "vector_chain")

        def over_rows(bank, x):
            return product(nc, core, bank, [(core.ones[:], x[:, i, :]) for i in range(TILES)])

        by_head = lambda x: x.rearrange("p i (h d) -> p (i h) d", h=HEADS)
        spread = lambda x: x[:].rearrange("p i h -> p (i h)").unsqueeze(2).to_broadcast([P, 4 * HEADS, HEAD])

        @st.block.scalar
        def _(act):
            nc.scalar.activation(q, q, ACT.Sigmoid).then_inc(sigmoids, 1)
            nc.scalar.activation(k, k, ACT.Sigmoid).then_inc(sigmoids, 1)
            act.wait_ge(clipped, 1)
            nc.scalar.activation(sink[:], sink[:], ACT.Sigmoid).then_inc(expd, 1)
            nc.scalar.activation(source[:], source[:], ACT.Exp).then_inc(expd, 1)

        @st.block.tensor
        def _(pe):
            pe.wait_ge(sigmoids, 1)
            over_rows(core.bank(0), q).then_inc(column_sums, 1)
            pe.wait_ge(sigmoids, 2)
            over_rows(core.bank(1), k).then_inc(column_sums, 1)
            pe.wait_ge(weighted, 1)
            over_rows(core.bank(2), tmp[0]).then_inc(column_sums, 1)
            pe.wait_ge(weighted, 2)
            over_rows(core.bank(3), tmp[1]).then_inc(column_sums, 1)
            pe.wait_ge(expd, 2)
            over_rows(core.bank(4)[:, 0:HEADS], source).then_inc(column_sums, 1)

        @st.block.vector
        def _(dve):
            def against(x, bank, dst):
                chain(nc.vector.tensor_scalar(kse, bank, FLOW_EPS, None, ALU.add))
                for i in range(TILES):
                    chain(nc.vector.scalar_tensor_tensor(out=core.branch_tmp[:, i, :], in0=x[:, i, :], scalar=FLOW_EPS, in1=kse,
                                                         op0=ALU.add, op1=ALU.mult))
                chain(nc.vector.tensor_reduce(dst[:].rearrange("p i h -> p (i h)"), by_head(core.branch_tmp), AXIS.X, ALU.add))
            dve.wait_ge(sigmoids, 2)
            dve.wait_ge(column_sums, 1)
            against(k, core.bank(0), source_out)
            dve.wait_ge(column_sums, 2)
            against(q, core.bank(1), sink_in)
            chain(nc.vector.reciprocal(source_out[:], source_out[:]))
            chain(nc.vector.reciprocal(sink_in[:], sink_in[:]))
            nc.vector.tensor_tensor(by_head(tmp[0]), by_head(k), spread(source_out), ALU.mult).then_inc(weighted, 1)
            nc.vector.tensor_tensor(by_head(tmp[1]), by_head(q), spread(sink_in), ALU.mult).then_inc(weighted, 1)
            dve.wait_ge(column_sums, 3)
            against(q, core.bank(2), sink)
            dve.wait_ge(column_sums, 4)
            against(k, core.bank(3), source)
            nc.vector.tensor_scalar(source[:], source[:], -1.0, 1.0, ALU.max, ALU.min).then_inc(clipped, 1)
            dve.wait_ge(expd, 1)
            chain(nc.vector.tensor_tensor(factor[:], sink_in[:], sink[:], ALU.mult))
            dve.wait_ge(column_sums, 5)
            chain(nc.vector.reciprocal(total[:], core.bank(4)[:, 0:HEADS]))
            chain(nc.vector.tensor_scalar(total[:], total[:], float(NODES), None, ALU.mult))
            chain(nc.vector.tensor_tensor(source[:], source[:], total[:].unsqueeze(1).to_broadcast([P, 4, HEADS]), ALU.mult))
            chain(nc.vector.tensor_tensor(by_head(v), by_head(v), spread(source), ALU.mult))


def layer3_mixer(core, w):
    nc = core.nc
    with ExitStack() as local:
        core.open_pool(local, 12)
        part = [core.section(j) for j in range(12)]
        Wq, Wk, Wv, Wo, W1, q, k, v, s0, s1 = part[0:10]
        W1, W2 = core.section(4, 4, 256), core.section(10, 2, DIM)
        core.branch_tmp = part[11]
        rows = local.enter_context(nc.sbuf_tensor("m3_rows", [P, 9, 512], F32))
        cols = local.enter_context(nc.sbuf_tensor("m3_cols", [P, 2], F32))
        factor = local.enter_context(nc.sbuf_tensor("m3_factor", [P, 4, HEADS], F32))
        L = {}

        def issue(sp):
            def load_rows(first, n):
                return core.load(sp, rows[:, first:first + n], w["m3_rows"][first:first + n].rearrange("(o r) n -> o r n", o=1).to_broadcast([P, n, 512]))
            L["norm_rows"] = load_rows(5, 2)
            for name, dst in (("Wq", Wq), ("Wk", Wk), ("Wv", Wv), ("Wo", Wo), ("W1", W1), ("W2", W2)):
                L[name] = core.load(sp, dst, weights(w["m3_" + name]))
                if name == "Wq":
                    L["rows"] = load_rows(0, 5)
            L["norm2_rows"] = load_rows(7, 2)
            L["cols"] = core.load(sp, cols[:], w["m3_cols"])
        norm_stage(core, "m3_norm1", core.xn, s0, scale=rows[:, 5, :], shift=rows[:, 6, :], issue=issue, params=[lambda: L["norm_rows"]])
        transpose_stage(core, "m3_turn1", s1, rows_of(s0))
        products_stage(core, "m3_qkv",
                       linear_tiles(s1, Wq, "V", [lambda: L["Wq"]]) + linear_tiles(s1, Wk, "V", [lambda: L["Wk"]])
                       + linear_tiles(s1, Wv, "V", [lambda: L["Wv"]]),
                       lambda t, e, ps, chain: nc.vector.tensor_tensor((q, k, v)[t // 4][:, t % 4, :], ps, rows[:, t // 4, :], ALU.add),
                       params=[lambda: L["rows"]])
        flow_stage(core, q, k, v, core.scores[:, 0, :], (s0, s1), factor)
        qT, mixed = Wq, Wk
        transpose_stage(core, "m3_turn_q", qT, rows_of(q))
        linear_attention(core, "m3", qT, k, v, mixed, factor=factor)
        transpose_stage(core, "m3_turn_mixed", s0, rows_of(mixed))

        def finish_attention(t, e, ps, chain):
            chain(nc.vector.tensor_tensor(q[:, t, :], ps, rows[:, 3, :], ALU.add))
            return nc.vector.tensor_tensor(q[:, t, :], q[:, t, :], core.xn[:, t, :], ALU.add)
        products_stage(core, "m3_attention_out", linear_tiles(s0, Wo, "V", [lambda: L["Wo"]]), finish_attention)
        norm_stage(core, "m3_norm2", q, s0, scale=rows[:, 7, :], shift=rows[:, 8, :], params=[lambda: L["norm2_rows"]])
        transpose_stage(core, "m3_turn2", s1, rows_of(s0))
        uT = v
        products_stage(core, "m3_up", turned_tiles(s1, W1, "A", [lambda: L["W1"]]),
                       lambda t, e, ps, chain: nc.scalar.activation(uT[:, t, :], ps, ACT.Gelu, bias=cols[:, t:t + 1]),
                       params=[lambda: L["cols"]])

        def finish(t, e, ps, chain):
            chain(nc.vector.tensor_tensor(k[:, t, :], ps, rows[:, 4, :], ALU.add))
            chain(nc.vector.tensor_tensor(k[:, t, :], k[:, t, :], q[:, t, :], ALU.add))
            return nc.vector.tensor_tensor(core.branches[:, t, :], core.branches[:, t, :], k[:, t, :], ALU.add)
        products_stage(core, "m3_down", linear_tiles(uT[:, 0:2], W2, "V", [lambda: L["W2"]]), finish)


TOP = 128
PROCESS = 1024


def top_stage(core, acts, work, weights_out):
    nc = core.nc
    taken = -1.0e30
    with ExitStack() as local, Stage(core, "f3_top") as st:
        best, negmax, total = (local.enter_context(nc.sbuf_tensor(f"f3_{n}", [P, 4, s], F32))
                               for n, s in (("best", 8), ("negmax", 1), ("total", 1)))
        chain = st.chain(nc.vector, "vector_chain")
        maxima, expd = st.sem("maximum_ready"), st.sem("exp_ready")

        @st.block.scalar
        def _(act):
            for i in range(TILES):
                act.wait_ge(maxima, i + 1)
                nc.scalar.activation(weights_out[:, i, :], acts[:, i, :], ACT.Exp, bias=negmax[:, i, :]).then_inc(expd, 1)

        @st.block.vector
        def _(dve):
            for i in range(TILES):
                nc.vector.tensor_reduce(negmax[:, i, :], acts[:, i, :], AXIS.X, ALU.max, negate=True).then_inc(maxima, 1)
            for r in range(TOP // 8):
                for i in range(TILES):
                    src = acts if r == 0 else work
                    if r > 0 and i == 0:
                        pass
                    chain(nc.vector.max(best[:, i, :], src[:, i, :]))
                    chain(nc.vector.match_replace(work[:, i, :], best[:, i, :], src[:, i, :], taken))
            for i in range(TILES):
                dve.wait_ge(expd, i + 1)
                chain(nc.vector.scalar_tensor_tensor(out=weights_out[:, i, :], in0=work[:, i, :], scalar=taken,
                                                     in1=weights_out[:, i, :], op0=ALU.is_equal, op1=ALU.mult))
                chain(nc.vector.tensor_reduce(total[:, i, :], weights_out[:, i, :], AXIS.X, ALU.add))
                chain(nc.vector.reciprocal(total[:, i, :], total[:, i, :]))
                chain(nc.vector.tensor_scalar(weights_out[:, i, :], weights_out[:, i, :], total[:, i, :], None, ALU.mult))


def layer3_ffn(core, w):
    nc = core.nc
    with ExitStack() as local:
        core.open_pool(local, 12)
        inT = core.section(0, 2, NODES)
        acts, work, attention = core.section(1, 4, PROCESS), core.section(3, 4, PROCESS), core.section(5, 4, PROCESS)
        attentionT = core.section(1, 8, NODES)
        ip, pw = core.section(7, 4, 256), core.section(8, 2, PROCESS)
        pv, ow, op = core.section(9, 8, 256), core.section(10, 2, 256), core.section(11, 2, DIM)
        aggT = core.section(3, 2, NODES)
        outT = core.section(4, 2, NODES)
        L = {}

        def issue(sp):
            for name, dst in (("ip", ip), ("pw", pw), ("pv", pv), ("ow", ow), ("op", op)):
                L[name] = core.load(sp, dst, weights(w["f3_" + name]))

        prepare(core, "f3", issue)
        products_stage(core, "f3_in", turned_tiles(core.xnT, ip, "A", [lambda: L["ip"]]),
                       lambda t, e, ps, chain: nc.scalar.activation(inT[:, t, :], ps, ACT.Gelu))
        products_stage(core, "f3_process",
                       [Tile([(P, 0, 512, [(inT[:, c, i * P:(i + 1) * P], pw[:, c, n * 512:(n + 1) * 512]) for c in range(2)])], "A",
                             [lambda: L["pw"]]) for i in range(TILES) for n in range(2)],
                       lambda t, e, ps, chain: nc.scalar.activation(acts[:, t // 2, (t % 2) * 512:(t % 2 + 1) * 512], ps, ACT.Gelu))
        top_stage(core, acts, work, attention)
        products_stage(core, "f3_turn",
                       [Tile([(P, i * P, (i + 1) * P, [(attention[:, i, c * P:(c + 1) * P], None)]) for i in range(TILES)], "VA"[c % 2])
                        for c in range(8)], lambda t, e, ps, chain: copy_out(nc, e, attentionT[:, t, :], ps))
        products_stage(core, "f3_values", turned_tiles(attentionT, pv, "VA", [lambda: L["pv"]]),
                       lambda t, e, ps, chain: copy_out(nc, e, aggT[:, t, :], ps))
        products_stage(core, "f3_outputs", turned_tiles(aggT, ow, "A", [lambda: L["ow"]]),
                       lambda t, e, ps, chain: nc.scalar.activation(outT[:, t, :], ps, ACT.Gelu))
        products_stage(core, "f3_patterns", linear_tiles(outT, op, "V", [lambda: L["op"]]),
                       lambda t, e, ps, chain: nc.vector.tensor_tensor(core.x[:, t, :], ps, core.x[:, t, :], ALU.add))


def prepare(core, name, issue=None):
    norm_stage(core, name + "_norm", core.x, core.xn, issue=issue)
    transpose_stage(core, name + "_turn", core.xnT, rows_of(core.xn))


def run_layers(core, w):
    for layer in range(4):
        prepare(core, f"l{layer}a")
        GNN[layer](core, w)
        MIXER[layer](core, w)
        add_stage(core, f"l{layer}_branches", [(core.x[:], core.branches[:])])
        prepare(core, f"l{layer}b")
        FFN[layer](core, w)


GNN = [layer0_gnn, layer1_gnn, layer2_gnn, layer3_gnn]
MIXER = [layer0_mixer, layer1_mixer, layer2_mixer, layer3_mixer]
FFN = [layer0_ffn, layer1_ffn, layer2_ffn, layer3_ffn]




def build(nc, w, out_dram):
    with ExitStack() as stack:
        core = Core(nc, stack)
        sb = core.sb
        core.x, core.xn, core.xnT = (sb(n, [P, 4, 512]) for n in ("x", "xn", "xnT"))
        core.branches = sb("branches", [P, 4, 512])
        core.edges_to, core.edges_from = sb("edges_to", [P, 4, 512]), sb("edges_from", [P, 4, 512])
        core.ident, core.ones, core.iota = sb("ident", [P, P]), sb("ones", [P, P]), sb("iota", [P, NODES])
        core.src_i, core.dst_i = sb("src_i", [P, EDGE_TILES], I32), sb("dst_i", [P, EDGE_TILES], I32)
        core.src_f, core.dst_f = sb("src_f", [P, EDGE_TILES]), sb("dst_f", [P, EDGE_TILES])
        core.stats, core.moments, core.deviation = sb("stats", [P, 4, 6]), sb("moments", [P, 4, 2]), sb("deviation", [P, 4, 3])
        core.scores, core.exps, core.turns = (sb(n, [P, 2, 512]) for n in ("scores", "exps", "turns"))
        core.iota_half = core.exps[:, 0, 0:NODES // 2].bitcast(F16)
        core.iota_i = core.scores[:, 0, :].bitcast(I32)
        core.sums, core.negmax = sb("sums", [P, 32]), sb("negmax", [P, 32])

        setup_stage(core, w["src"], w["dst"], w["x"])
        adjacency_stage(core)
        transpose_stage(core, "edges_from", core.edges_from, rows_of(core.edges_to))
        run_layers(core, w)
        store_stage(core, out_dram, core.x)


def columns(*vectors):
    return np.concatenate([np.reshape(v, (-1, P)).T for v in vectors], axis=1)


def row_pack(*vectors):
    return np.concatenate([np.reshape(v, (-1, DIM)) for v in vectors], axis=0)


def layout(a):
    g = a.__getitem__
    emb = np.concatenate([g("L0_gnn_edge_emb")] * HEADS)
    w = {
        "x": g("x"),
        "src": np.reshape(g("src"), (EDGE_TILES, P)).T, "dst": np.reshape(g("dst"), (EDGE_TILES, P)).T,
        "g0_WqT": g("L0_gnn_W_q").T, "g0_WkT": g("L0_gnn_W_k").T, "g0_WvT": g("L0_gnn_W_v").T,
        "g0_WeT": g("L0_gnn_W_e").T, "g0_WoT": g("L0_gnn_W_o").T,
        "g0_rows": row_pack(g("L0_gnn_b_v"), g("L0_gnn_b_e"), g("L0_gnn_edge_attn"), g("L0_gnn_b_o"),
                            g("L0_gnn_ln_g"), g("L0_gnn_ln_b")),
        "g0_cols": columns(g("L0_gnn_b_q"), g("L0_gnn_b_k"), emb),
        "m0_Wqkv": g("L0_mix_Wqkv"),
        "f0_Wg": g("L0_ffn_Wg"), "f0_bg": np.reshape(g("L0_ffn_bg"), (1, 8)),
        "f0_W1": g("L0_ffn_W1"), "f0_W3": g("L0_ffn_W3"), "f0_W2": g("L0_ffn_W2"),
        "g1_W": g("L1_gnn_W"), "g1_rows": row_pack(g("L1_gnn_b")),
        "m1_Wqkv": g("L1_mix_W_qkv"), "m1_Wout": g("L1_mix_W_out"), "m1_rows": row_pack(g("L1_mix_b_out")),
        "f1_Wg": g("L1_ffn_gate_w").T, "f1_bg": np.reshape(g("L1_ffn_biases"), (1, 8)),
        "f1_W1": np.concatenate([g("L1_ffn_w1"), g("L1_ffn_sw1")[None]]),
        "f1_W3": np.concatenate([g("L1_ffn_w3"), g("L1_ffn_sw3")[None]]),
        "f1_W2": np.concatenate([g("L1_ffn_w2"), g("L1_ffn_sw2")[None]]),
        "g2_Wq": g("L2_gnn_Wq"), "g2_Wk": g("L2_gnn_Wk"), "g2_Wv": g("L2_gnn_Wv"), "g2_Wskip": g("L2_gnn_Wskip"),
        "g2_Wlin": g("L2_gnn_Wlin"),
        "g2_rows": row_pack(g("L2_gnn_bv"), g("L2_gnn_blin"), g("L2_gnn_gamma"), g("L2_gnn_beta")),
        "g2_cols": columns(g("L2_gnn_bq"), g("L2_gnn_bk"), g("L2_gnn_bskip")),
        "m2_Wqkv": g("L2_mix_qkv_w").T, "m2_Wout": g("L2_mix_out_w").T,
        "m2_rows": row_pack(g("L2_mix_qkv_b")[DIM:], g("L2_mix_out_b"), g("L2_mix_ln_gamma"), g("L2_mix_ln_beta")),
        "m2_cols": columns(g("L2_mix_qkv_b")[:DIM]),
        "f2_Wg": g("L2_ffn_w_gating"), "f2_W1": g("L2_ffn_w1"), "f2_W2": g("L2_ffn_w2"),
        "g3_attr": np.reshape(g("edge_attr_4"), (EDGE_TILES, P, 4)).transpose(1, 0, 2),
        "g3_feat": g("edge_attr_8").T,
        "g3_Wup": np.concatenate([g("L3_gnn_W_up0"), g("L3_gnn_W_up1")], axis=1),
        "g3_mlp1": g("L3_gnn_W_mlp1"), "g3_mlp2": g("L3_gnn_W_mlp2"), "g3_mlp3": g("L3_gnn_W_mlp3"),
        "g3_mlp4": g("L3_gnn_W_mlp4"),
        "g3_Wout": np.concatenate([g("L3_gnn_W_out0"), g("L3_gnn_W_out1")], axis=1),
        "m3_Wq": g("L3_mix_Wq"), "m3_Wk": g("L3_mix_Wk"), "m3_Wv": g("L3_mix_Wv"), "m3_Wo": g("L3_mix_Wo"),
        "m3_W1": g("L3_mix_W1"), "m3_W2": g("L3_mix_W2"),
        "m3_rows": row_pack(*[g("L3_mix_" + n) for n in ("bq", "bk", "bv", "bo", "b2", "g1", "be1", "g2", "be2")]),
        "m3_cols": columns(g("L3_mix_b1")),
        "f3_ip": g("L3_ffn_input_patterns").T, "f3_pw": g("L3_ffn_process_input_weights").T,
        "f3_pv": g("L3_ffn_process_values"), "f3_ow": g("L3_ffn_output_input_weights").T,
        "f3_op": g("L3_ffn_output_patterns"),
    }
    return {name: np.ascontiguousarray(v) for name, v in w.items()}


def kernel(**inputs):
    import concourse.bacc as bacc
    from concourse.bass_utils import run_bass_kernel_spmd

    nc = bacc.Bacc("TRN2", target_bir_lowering=False, num_devices=1)
    arrays = layout({name: np.asarray(v) for name, v in inputs.items()})
    w = {name: nc.dram_tensor("in_" + name, v.shape, mybir.dt.from_np(v.dtype), kind="ExternalInput").ap()
         for name, v in arrays.items()}
    out = nc.dram_tensor("out", (NODES, DIM), F32, kind="ExternalOutput").ap()
    build(nc, w, out)
    r = run_bass_kernel_spmd(nc, [{"in_" + name: v for name, v in arrays.items()}], core_ids=[0])
    return r.results[0]["out"]
```

```python
from contextlib import ExitStack

import numpy as np

import concourse.bass as bass
from concourse import mybir

P = 128
NODES = 512
DIM = 512
TILES = NODES // P
CHUNKS = DIM // P
EDGES = 16384
EDGE_TILES = EDGES // P
HEADS = 8
HEAD = DIM // HEADS
BANK = 512
SCRATCHES = 3

F32 = mybir.dt.float32
F32R = mybir.dt.float32r
BF16 = mybir.dt.bfloat16
F16 = mybir.dt.float16
I32 = mybir.dt.int32
U32 = mybir.dt.uint32
ALU = mybir.AluOpType
ACT = mybir.ActivationFunctionType
AXIS = mybir.AxisListType
MASKED = -1.0e30


class Chain:

    def __init__(self, engine, sem):
        self.engine, self.sem, self.count = engine, sem, 0

    def __call__(self, instruction):
        self.count += 1
        instruction.then_inc(self.sem, 1)
        self.engine.wait_ge(self.sem, self.count)


class Load:

    def __init__(self, sem, value):
        self.sem, self.value = sem, value

    def wait(self, engine):
        engine.wait_ge(self.sem, self.value)


class Core:

    PER_STAGE = 20
    LOADS = 24

    def __init__(self, nc, stack):
        self.nc, self.stack = nc, stack
        taken = [nc.alloc_semaphore(f"stage_pool_{i}") for i in range(2 * self.PER_STAGE)]
        numbers = [s.num for s in taken]
        for s in taken:
            nc.release_semaphore(s)
        self.pools = [numbers[:self.PER_STAGE], numbers[self.PER_STAGE:]]
        self.turn, self.used = 0, None
        self.load_sems = [stack.enter_context(nc.semaphore(f"load_landed_{i}")) for i in range(self.LOADS)]
        self.gather_sems = [stack.enter_context(nc.semaphore(f"sender_rows_landed_{b}")) for b in range(2)]
        self.load_counts = [0] * self.LOADS
        self.loads = 0
        self.psum = stack.enter_context(nc.psum_tensor("banks", [P, 8, BANK], F32))
        self.names = 0

    def sb(self, name, shape, dtype=F32):
        return self.stack.enter_context(self.nc.sbuf_tensor(name, shape, dtype))

    def load(self, queue, dst, src):
        i = self.loads % self.LOADS
        self.loads += 1
        self.load_counts[i] += 16
        queue.dma_start(dst, src).then_inc(self.load_sems[i], 16)
        return Load(self.load_sems[i], self.load_counts[i])

    def open_pool(self, local, sections):
        self.names += 1
        self.wpool = local.enter_context(self.nc.sbuf_tensor(f"pool_{self.names}", [P, sections * 2048], F32))

    def section(self, first, chunks=4, width=512):
        return self.wpool[:, first * 2048:first * 2048 + chunks * width].rearrange("p (c n) -> p c n", c=chunks)

    def bank(self, i):
        return self.psum[:, i, :]


class Stage:

    def __init__(self, core, name):
        self.core, self.name, self.sems = core, name, []

    def __enter__(self):
        core = self.core
        if core.used:
            core.nc.gpsimd.sem_clear(range(min(core.used), max(core.used) + 1))
        core.turn ^= 1
        self.numbers = core.pools[core.turn]
        self.opened = core.nc.Block()
        self.block = self.opened.__enter__()
        return self

    def sem(self, name):
        s = self.core.nc.alloc_semaphore(name=f"{self.name}_{name}", num=self.numbers[len(self.sems)])
        self.sems.append(s)
        return s

    def chain(self, engine, name):
        return Chain(engine, self.sem(name))

    def __exit__(self, *exc):
        self.opened.__exit__(*exc)
        self.core.used = [s.num for s in self.sems]
        for s in self.sems:
            self.core.nc.release_semaphore(s)
        return False


def product(nc, core, out, pairs):
    n = len(pairs)
    for j, (left, right) in enumerate(pairs):
        if right is None:
            last = nc.tensor.transpose(out, left, core.ident[0:left.shape[0], 0:left.shape[0]])
        else:
            last = nc.tensor.matmul(out, left, right, start=(j == 0), stop=(j == n - 1))
    return last


def split_product(nc, out, pairs, start=True, stop=True):
    n = len(pairs)
    for j, ((left, left_low), (right, right_low)) in enumerate(pairs):
        nc.tensor.matmul(out, left, right, start=start and j == 0, stop=False)
        nc.tensor.matmul(out, left, right_low, start=False, stop=False)
        last = nc.tensor.matmul(out, left_low, right, start=False, stop=stop and j == n - 1)
    return last


class Tile:

    def __init__(self, parts, engine, loads=()):
        self.parts, self.engine, self.loads = parts, engine, loads


def products_stage(core, name, tiles, finish, issue=None, params=(), banks=8, ordered=False):
    nc = core.nc
    order = {"V": [t for t, x in enumerate(tiles) if x.engine == "V"],
             "A": [t for t, x in enumerate(tiles) if x.engine == "A"]}
    place = {t: i for ts in order.values() for i, t in enumerate(ts)}
    with Stage(core, name) as st:
        filled = st.sem("bank_filled")
        taken = {"V": st.sem("vector_took_bank"), "A": st.sem("scalar_took_bank")}
        chain_v, chain_a = st.chain(nc.vector, "vector_chain"), st.chain(nc.scalar, "scalar_chain")

        if issue is not None:
            @st.block.sync
            def _(sp):
                issue(sp)

        @st.block.tensor
        def _(pe):
            for t, tile in enumerate(tiles):
                for load in tile.loads:
                    load().wait(pe)
                if t >= banks:
                    pe.wait_ge(taken[tiles[t - banks].engine], place[t - banks] + 1)
                for rows, c0, c1, pairs in tile.parts:
                    last = product(nc, core, core.bank(t % banks)[0:rows, c0:c1], pairs)
                last.then_inc(filled, 1)

        if order["V"]:
            @st.block.vector
            def _(dve):
                for load in params:
                    load().wait(dve)
                for t in order["V"]:
                    dve.wait_ge(filled, t + 1)
                    if ordered and place[t] > 0:
                        dve.wait_ge(taken["V"], place[t])
                    finish(t, nc.vector, core.bank(t % banks), chain_v).then_inc(taken["V"], 1)

        if order["A"]:
            @st.block.scalar
            def _(act):
                for load in params:
                    load().wait(act)
                for t in order["A"]:
                    act.wait_ge(filled, t + 1)
                    finish(t, nc.scalar, core.bank(t % banks), chain_a).then_inc(taken["A"], 1)


def copy_out(nc, engine, out, in_):
    return nc.vector.tensor_copy(out, in_) if engine is nc.vector else nc.scalar.copy(out, in_)


def transpose_stage(core, name, dst, blocks):
    nc = core.nc
    tiles = [Tile([(P, i * P, (i + 1) * P, [(blocks(i, c), None)]) for i in range(TILES)], "VA"[c % 2])
             for c in range(CHUNKS)]
    products_stage(core, name, tiles, lambda t, e, ps, chain: copy_out(nc, e, dst[:, t, :], ps))


def rows_of(src):
    return lambda i, c: src[:, i, c * P:(c + 1) * P]


def norm_turn_stage(core, name, src, dst, dstT=None, scale=None, shift=None, add=None, issue=None, params=(), also=None):
    nc = core.nc
    stats, moments, deviation = core.stats, core.moments, core.deviation
    with Stage(core, name) as st:
        added, variance_ready, deviation_ready = st.sem("sum_ready"), st.sem("variance_ready"), st.sem("deviation_ready")
        normed, turned = st.sem("rows_normed"), st.sem("rows_turned")
        chain = st.chain(nc.vector, "vector_chain")
        if issue is not None:
            @st.block.sync
            def _(sp):
                issue(sp)

        if add is not None:
            @st.block.gpsimd
            def _(pool):
                for i in range(TILES):
                    nc.gpsimd.tensor_tensor(src[:, i, :], src[:, i, :], add[:, i, :], ALU.add).then_inc(added, 1)

        @st.block.scalar
        def _(act):
            for i in range(TILES):
                act.wait_ge(variance_ready, i + 1)
                nc.scalar.activation(deviation[:, i, 1:2], deviation[:, i, 0:1], ACT.Sqrt).then_inc(deviation_ready, 1)
            for i in range(TILES if dstT is not None else 0):
                act.wait_ge(turned, i + 1)
                nc.scalar.copy(dstT[:, :, i * P:(i + 1) * P], core.bank(i).rearrange("p (c n) -> p c n", c=CHUNKS))

        @st.block.tensor
        def _(pe):
            for i in range(TILES if dstT is not None else 0):
                pe.wait_ge(normed, i + 1)
                product_of = [(core.bank(i)[:, c * P:(c + 1) * P], dst[:, i, c * P:(c + 1) * P]) for c in range(CHUNKS)]
                for out, block in product_of:
                    last = nc.tensor.transpose(out, block, core.ident[:])
                last.then_inc(turned, 1)

        @st.block.vector
        def _(dve):
            def statistics(i):
                if add is not None:
                    dve.wait_ge(added, i + 1)
                chain(nc.vector.bn_stats(stats[:, i, :], src[:, i, :]))
                chain(nc.vector.bn_aggr(moments[:, i, :], stats[:, i, :]))
                nc.vector.tensor_scalar(deviation[:, i, 0:1], moments[:, i, 1:2], 1e-5, None, ALU.add).then_inc(variance_ready, 1)

            def norm(i):
                dve.wait_ge(deviation_ready, i + 1)
                chain(nc.vector.reciprocal(deviation[:, i, 2:3], deviation[:, i, 1:2]))
                if scale is None:
                    last = nc.vector.tensor_scalar(dst[:, i, :], src[:, i, :], moments[:, i, 0:1], deviation[:, i, 2:3],
                                                   ALU.subtract, ALU.mult)
                else:
                    chain(nc.vector.scalar_tensor_tensor(out=dst[:, i, :], in0=src[:, i, :], scalar=moments[:, i, 0:1], in1=scale,
                                                         op0=ALU.subtract, op1=ALU.mult))
                    last = nc.vector.scalar_tensor_tensor(out=dst[:, i, :], in0=dst[:, i, :], scalar=deviation[:, i, 2:3],
                                                          in1=shift, op0=ALU.mult, op1=ALU.add)
                last.then_inc(normed, 1)
            statistics(0)
            statistics(1)
            for load in params:
                load().wait(dve)
            for i in range(TILES):
                norm(i)
                if i + 2 < TILES:
                    statistics(i + 2)
            if also is not None:
                also(chain)


def softmax_stage(core, name, units, width, scale=1.0, mask=None, weigh=None, normal=False, keep=None,
                  turned=None, values=None, per_value=1, finish=None, issue=None):
    nc = core.nc
    n, blocks = len(units), width // P
    scores, exps, sums, negmax = core.scores, core.exps, core.sums, core.negmax
    post = weigh is not None or normal

    def exps_of(u):
        return keep(u) if keep is not None else exps[:, u % SCRATCHES, 0:width]

    with Stage(core, name) as st:
        scored, shifted, exponed = st.sem("scores_ready"), st.sem("maximum_ready"), st.sem("exponentials_ready")
        weighed, flipped, copied = st.sem("weighed_ready"), st.sem("transpose_ready"), st.sem("transpose_copied")
        valued = st.sem("values_ready")
        chain = st.chain(nc.vector, "vector_chain")
        if issue is not None:
            @st.block.sync
            def _(sp):
                issue(sp)

        @st.block.tensor
        def _(pe):
            def score(u):
                if u >= 2:
                    pe.wait_ge(shifted, u - 1)
                product(nc, core, core.bank(u % 2)[:, 0:width], units[u]).then_inc(scored, 1)

            def flip(u):
                pe.wait_ge(weighed if post else exponed, u + 1)
                if u >= 2:
                    pe.wait_ge(copied, u - 1)
                for c in range(blocks):
                    last = product(nc, core, core.bank(2 + u % 2)[:, c * P:(c + 1) * P],
                                   [(exps_of(u)[:, c * P:(c + 1) * P], None)])
                last.then_inc(flipped, 1)

            def value(h):
                pe.wait_ge(copied, (h + 1) * per_value)
                out, pairs = values(h)
                product(nc, core, out, pairs).then_inc(valued, 1)

            score(0)
            score(1)
            for u in range(n):
                if u + 2 < n:
                    score(u + 2)
                flip(u)
                if values is not None and u > 0 and u % per_value == 0:
                    value(u // per_value - 1)
            if values is not None:
                value(n // per_value - 1)

        @st.block.vector
        def _(dve):
            def shift(u):
                dve.wait_ge(scored, u + 1)
                if u >= SCRATCHES:
                    dve.wait_ge(exponed, u - SCRATCHES + 1)
                if mask is not None:
                    chain(nc.vector.scalar_tensor_tensor(out=scores[:, u % SCRATCHES, 0:width], in0=core.bank(u % 2)[:, 0:width],
                                                         scalar=scale, in1=mask(u), op0=ALU.mult, op1=ALU.add))
                else:
                    chain(nc.vector.tensor_scalar(scores[:, u % SCRATCHES, 0:width], core.bank(u % 2)[:, 0:width], scale, None,
                                                  ALU.mult))
                nc.vector.tensor_reduce(negmax[:, u:u + 1], scores[:, u % SCRATCHES, 0:width], AXIS.X, ALU.max,
                                        negate=True).then_inc(shifted, 1)

            def weigh_exps(u):
                dve.wait_ge(exponed, u + 1)
                e, s = exps_of(u), sums[:, u:u + 1]
                if weigh is not None:
                    chain(nc.vector.tensor_tensor(e, e, weigh(u), ALU.mult))
                    chain(nc.vector.tensor_reduce(s, e, AXIS.X, ALU.add))
                    chain(nc.vector.tensor_scalar(s, s, 0.5, None, ALU.max))
                chain(nc.vector.reciprocal(s, s))
                nc.vector.tensor_scalar(e, e, s, None, ALU.mult).then_inc(weighed, 1)

            shift(0)
            shift(1)
            for u in range(n):
                if post:
                    weigh_exps(u)
                if u + 2 < n:
                    shift(u + 2)
            if finish is not None:
                dve.wait_ge(valued, n // per_value)
                dve.wait_ge(exponed, n)
                finish(chain)

        @st.block.scalar
        def _(act):
            def expo(u):
                act.wait_ge(shifted, u + 1)
                if u >= SCRATCHES and keep is None:
                    act.wait_ge(flipped, u - SCRATCHES + 1)
                nc.scalar.activation(exps_of(u), scores[:, u % SCRATCHES, 0:width], ACT.Exp, bias=negmax[:, u:u + 1],
                                     accum_out=sums[:, u:u + 1]).then_inc(exponed, 1)

            def copy_turned(u):
                act.wait_ge(flipped, u + 1)
                if values is not None and u >= 2 * per_value:
                    act.wait_ge(valued, u // per_value - 1)
                nc.scalar.copy(turned(u), core.bank(2 + u % 2)[:, 0:blocks * P].rearrange("p (c n) -> p c n", c=blocks)
                               ).then_inc(copied, 1)

            expo(0)
            expo(1)
            for u in range(n):
                copy_turned(u)
                if u + 2 < n:
                    expo(u + 2)


def setup_stage(core, src_dram, dst_dram, x_dram):
    nc = core.nc
    with Stage(core, "setup") as st:
        landed, made = st.sem("inputs_landed"), st.sem("constants_made")
        x_landed = st.sem("x_landed")

        @st.block.sync
        def _(sp):
            sp.dma_start(core.src_i[:], src_dram).then_inc(landed, 16)
            sp.dma_start(core.dst_i[:], dst_dram).then_inc(landed, 16)
            sp.dma_start(core.x[:], x_dram.rearrange("(i p) d -> p i d", p=P)).then_inc(x_landed, 16)
            sp.wait_ge(x_landed, 16)

        @st.block.gpsimd
        def _(pool):
            nc.gpsimd.memset(core.ident[:], 0.0).then_inc(made, 1)
            nc.gpsimd.memset(core.ones[:], 1.0)
            pool.wait_ge(made, 1)
            nc.gpsimd.affine_select(out=core.ident[:], in_=core.ident[:], compare_op=ALU.not_equal, fill=1.0, base=0,
                                    pattern=[[-1, P]], channel_multiplier=1)
            nc.gpsimd.iota(core.iota_i[:], [[1, NODES]], base=0, channel_multiplier=0).then_inc(made, 1)

        @st.block.vector
        def _(dve):
            dve.wait_ge(landed, 32)
            nc.vector.tensor_copy(core.src_f[:], core.src_i[:])
            nc.vector.tensor_copy(core.dst_f[:], core.dst_i[:])
            dve.wait_ge(made, 2)
            nc.vector.tensor_copy(core.iota[:], core.iota_i[:])
            nc.vector.tensor_copy(core.iota_half, core.iota_i[:])


def adjacency_stage(core):
    nc = core.nc
    with ExitStack() as local, Stage(core, "adjacency") as st:
        B = 4
        hot_src = local.enter_context(nc.sbuf_tensor("hot_src", [P, B, NODES], BF16))
        hot_dst = local.enter_context(nc.sbuf_tensor("hot_dst", [P, B, NODES], BF16))
        hot, counted = st.sem("one_hots_ready"), st.sem("edges_counted")
        steps = EDGE_TILES // B

        def one_hots(t, b):
            nc.vector.tensor_scalar(hot_src[:, b, :], core.iota_half, core.src_f[:, bass.ds(t, 1)], None, ALU.is_equal)
            nc.vector.tensor_scalar(hot_dst[:, b, :], core.iota_half, core.dst_f[:, bass.ds(t, 1)], None,
                                    ALU.is_equal).then_inc(hot, 1)

        def count(pe, t, b, first=False, last=False):
            pe.wait_ge(hot, t + 1)
            for m in range(TILES):
                done = nc.tensor.matmul(core.bank(m), hot_dst[:, b, m * P:(m + 1) * P], hot_src[:, b, :],
                                        start=first, stop=last, skip_group_check=True)
            done.then_inc(counted, 1)

        @st.block.vector
        def _(dve):
            for b in range(B):
                one_hots(b, b)
            with dve.Fori(1, steps) as s:
                for b in range(B):
                    dve.wait_ge(counted, B * s + b - B + 1)
                    one_hots(B * s + b, b)
            dve.wait_ge(counted, B * steps)
            for m in range(TILES):
                nc.vector.tensor_copy(core.edges_to[:, m, :], core.bank(m))

        @st.block.tensor
        def _(pe):
            for b in range(B):
                count(pe, b, b, first=b == 0)
            with pe.Fori(1, steps - 1) as s:
                for b in range(B):
                    count(pe, B * s + b, b)
            for b in range(B):
                count(pe, B * (steps - 1) + b, b, last=b == B - 1)


def weights(dram, cols=None):
    w = dram.rearrange("(c p) n -> p c n", p=P)
    return w if cols is None else w[:, :, cols[0]:cols[1]]


def linear_tiles(left, right, engines, loads=(), width=DIM):
    k = right.shape[1]
    return [Tile([(P, 0, width, [(left[:, c, i * P:(i + 1) * P], right[:, c, 0:width]) for c in range(k)])],
                 engines[i % len(engines)], loads) for i in range(TILES)]


def turned_tiles(right, weight, engines, loads=(), first=0):
    k, n = weight.shape[1], weight.shape[2] // P
    return [Tile([(P, 0, NODES, [(weight[:, c, m * P:(m + 1) * P], right[:, c, :]) for c in range(k)])],
                 engines[(first + m) % len(engines)], loads) for m in range(n)]


def layer0_gnn(core, w):
    nc = core.nc
    xn, xnT = core.xn, core.xnT
    with ExitStack() as local:
        core.open_pool(local, 10)

        def sb(name, shape, dtype=F32):
            return local.enter_context(nc.sbuf_tensor("g0_" + name, shape, dtype))
        part = [core.section(j) for j in range(10)]
        qT, kT, v, xe, mask = part[5:10]
        rows, cols = sb("rows", [P, 6, 512]), sb("cols", [P, 12])
        L = {}

        def issue(sp):
            L["cols"] = core.load(sp, cols[:], w["g0_cols"])
            for j, name in enumerate(["g0_WqT", "g0_WkT", "g0_WeT", "g0_WvT", "g0_WoT"]):
                L[name] = core.load(sp, part[j], weights(w[name]))
                if j == 1:
                    L["rows"] = core.load(sp, rows[:], w["g0_rows"].rearrange("(o r) n -> o r n", o=1).to_broadcast([P, 6, 512]))

        tiles = (turned_tiles(xnT, part[0], "A", [lambda: L["g0_WqT"]]) + turned_tiles(xnT, part[1], "V", [lambda: L["g0_WkT"]])
                 + linear_tiles(xnT, part[2], "V", [lambda: L["g0_WeT"]]) + linear_tiles(xnT, part[3], "V", [lambda: L["g0_WvT"]]))

        def finish(t, engine, ps, chain):
            m = t % 4
            if t < 4:
                return nc.scalar.activation(qT[:, m, :], ps, ACT.Identity, bias=cols[:, m:m + 1])
            if t < 8:
                return nc.vector.tensor_scalar(kT[:, m, :], ps, cols[:, 4 + m:5 + m], cols[:, 8 + m:9 + m], ALU.add, ALU.add)
            if t < 12:
                chain(nc.vector.tensor_tensor(xe[:, m, :], ps, rows[:, 1, :], ALU.add))
                return nc.vector.tensor_tensor(xe[:, m, :], xe[:, m, :], rows[:, 2, :], ALU.mult)
            chain(nc.vector.tensor_tensor(v[:, m, :], ps, rows[:, 0, :], ALU.add))
            return nc.vector.tensor_tensor(v[:, m, :], v[:, m, :], xe[:, m, :], ALU.add)

        
        def make_mask(chain):
            nc.vector.tensor_scalar(mask[:], core.edges_from[:], 0.5, MASKED, ALU.is_lt, ALU.mult)
        prepare(core, "g0", issue, also=make_mask)
        products_stage(core, "g0_qkv", tiles, finish, params=[lambda: L["rows"], lambda: L["cols"]])

        def head(x, h):
            return x[HEAD * (h % 2):HEAD * (h % 2) + HEAD, h // 2]
        order = [(h, i) for h in range(HEADS) for i in range(TILES)]
        units = [[(head(qT, h)[:, i * P:(i + 1) * P], head(kT, h))] for h, i in order]

        turns, mixedT = (part[0], part[1]), part[2]

        def values(h):
            return (core.bank(4 + h // 2)[HEAD * (h % 2):HEAD * (h % 2) + HEAD],
                    [(v[:, c, h * HEAD:(h + 1) * HEAD], turns[h % 2][:, c, :]) for c in range(4)])

        def finish_attention(chain):
            for c in range(CHUNKS):
                nc.vector.tensor_copy(mixedT[:, c, :], core.bank(4 + c))
        softmax_stage(core, "g0_attention", units, NODES, scale=HEAD ** -0.5, mask=lambda u: mask[:, order[u][1], :], normal=True,
                      turned=lambda u: turns[order[u][0] % 2][:, :, order[u][1] * P:(order[u][1] + 1) * P],
                      values=values, per_value=TILES, finish=finish_attention)

        def finish_out(t, engine, ps, chain):
            chain(nc.vector.tensor_tensor(v[:, t, :], ps, rows[:, 3, :], ALU.add))
            return nc.vector.tensor_tensor(v[:, t, :], v[:, t, :], xn[:, t, :], ALU.add)
        products_stage(core, "g0_out", linear_tiles(mixedT, part[4], "V", [lambda: L["g0_WoT"]]), finish_out)
        norm_turn_stage(core, "g0_norm", v, core.branches, scale=rows[:, 4, :], shift=rows[:, 5, :])


def store_stage(core, out_dram, src):
    nc = core.nc
    with Stage(core, "store") as st:
        stored = st.sem("output_stored")

        @st.block.sync
        def _(sp):
            sp.dma_start(out_dram.rearrange("(i p) d -> p i d", p=P), src[:]).then_inc(stored, 16)
            sp.wait_ge(stored, 16)


LANDMARKS = 256
PINV_STEPS = 6


def pinv_stage(core, XT, Z, ZT):
    nc = core.nc
    big = lambda first: core.wpool[:, first * 4096:(first + 1) * 4096].rearrange("p (h c n) -> p h c n", h=HEADS, c=2)
    XZ, XZT, Q = big(3), big(4), big(5)
    with ExitStack() as local, Stage(core, "pinv") as st:
        seven, fifteen, thirteen = (core.scores[:, j, :].rearrange("p (c n) -> p c n", c=2) for j in range(3))
        tops = local.enter_context(nc.sbuf_tensor("pinv_tops", [P, 8], F32))
        all_sums = local.enter_context(nc.sbuf_tensor("pinv_sums", [P, 2, 16], F32))
        tops_ready, tops_shared, factor_ready = st.sem("tops_ready"), st.sem("tops_shared"), st.sem("factor_ready")
        chain = st.chain(nc.vector, "vector_chain")
        made, vec, act_ = st.sem("products_ready"), st.sem("vector_results"), st.sem("scalar_results")
        PE_STEP, V_STEP, A_STEP = 48, 32, 24

        def bank(h):
            return core.bank(h).rearrange("p (c n) -> p c n", c=2)

        @st.block.gpsimd
        def _(pool):
            pool.wait_ge(tops_ready, 1)
            nc.gpsimd.partition_all_reduce(tops[:, 2:4], tops[:, 0:2], P, bass.bass_isa.ReduceOp.max).then_inc(tops_shared, 1)

        @st.block.vector
        def _(dve):
            flat = lambda x: x.rearrange("p h c n -> p (h c) n")
            chain(nc.vector.tensor_reduce(all_sums[:, 0, :], flat(ZT), AXIS.X, ALU.add, apply_absolute_value=True))
            chain(nc.vector.tensor_reduce(all_sums[:, 1, :], flat(XT), AXIS.X, ALU.add, apply_absolute_value=True))
            nc.vector.tensor_reduce(tops[:, 0:2], all_sums[:], AXIS.X, ALU.max).then_inc(tops_ready, 1)
            for matrix, value in ((seven, 7.0), (fifteen, 15.0), (thirteen, 13.0)):
                chain(nc.vector.memset(matrix, 0.0))
                for c in range(2):
                    chain(nc.vector.tensor_scalar(matrix[:, c, c * P:(c + 1) * P], core.ident[:], value, None, ALU.mult))
            dve.wait_ge(tops_shared, 1)
            chain(nc.vector.tensor_tensor(tops[:, 4:5], tops[:, 2:3], tops[:, 3:4], ALU.mult))
            nc.vector.reciprocal(tops[:, 5:6], tops[:, 4:5]).then_inc(factor_ready, 1)
            dve.wait_ge(factor_ready, 1)
            for h in range(HEADS):
                nc.vector.tensor_scalar(ZT[:, h], ZT[:, h], tops[:, 5:6], None, ALU.mult).then_inc(vec, 1)
            with dve.Fori(0, PINV_STEPS) as s:
                for j, matrix in enumerate((seven, fifteen, thirteen)):
                    for h in range(HEADS):
                        dve.wait_ge(made, s * PE_STEP + (0, 16, 24)[j] + h + 1)
                        nc.vector.scalar_tensor_tensor(out=Q[:, h], in0=bank(h), scalar=-1.0, in1=matrix,
                                                       op0=ALU.mult, op1=ALU.add).then_inc(vec, 1)
                for h in range(HEADS):
                    dve.wait_ge(made, s * PE_STEP + 40 + h + 1)
                    nc.vector.tensor_copy(ZT[:, h], bank(h)).then_inc(vec, 1)

        @st.block.scalar
        def _(act):
            act.wait_ge(factor_ready, 1)
            for h in range(HEADS):
                nc.scalar.activation(Z[:, h], XT[:, h], ACT.Copy, scale=tops[:, 5:6]).then_inc(act_, 1)
            with act.Fori(0, PINV_STEPS) as s:
                for h in range(HEADS):
                    act.wait_ge(vec, s * V_STEP + 8 + h + 1)
                    nc.scalar.copy(XZ[:, h], bank(h)).then_inc(act_, 1)
                for h in range(HEADS):
                    act.wait_ge(made, s * PE_STEP + 8 + h + 1)
                    nc.scalar.copy(XZT[:, h], bank(h)).then_inc(act_, 1)
                for h in range(HEADS):
                    act.wait_ge(made, s * PE_STEP + 32 + h + 1)
                    nc.scalar.activation(Z[:, h], bank(h), ACT.Copy, scale=0.25).then_inc(act_, 1)

        @st.block.tensor
        def _(pe):
            def multiply(h, left_turned, right):
                for m in range(2):
                    last = product(nc, core, bank(h)[:, m, :],
                                   [(left_turned[:, h, c, m * P:(m + 1) * P], right[:, h, c, :]) for c in range(2)])
                last.then_inc(made, 1)

            def turn(h, matrix):
                for c in range(2):
                    for m in range(2):
                        last = nc.tensor.transpose(bank(h)[:, c, m * P:(m + 1) * P], matrix[:, h, m, c * P:(c + 1) * P],
                                                   core.ident[:])
                last.then_inc(made, 1)

            with pe.Fori(0, PINV_STEPS) as s:
                for h in range(HEADS):
                    pe.wait_ge(act_, s * A_STEP + h + 1)
                    pe.wait_ge(vec, s * V_STEP + h + 1)
                    multiply(h, XT, Z)
                for h in range(HEADS):
                    pe.wait_ge(act_, s * A_STEP + 8 + h + 1)
                    pe.wait_ge(vec, s * V_STEP + 8 + h + 1)
                    turn(h, XZ)
                for h in range(HEADS):
                    pe.wait_ge(act_, s * A_STEP + 16 + h + 1)
                    multiply(h, XZT, Q)
                for h in range(HEADS):
                    pe.wait_ge(vec, s * V_STEP + 16 + h + 1)
                    multiply(h, XZT, Q)
                for h in range(HEADS):
                    pe.wait_ge(vec, s * V_STEP + 24 + h + 1)
                    multiply(h, ZT, Q)
                for h in range(HEADS):
                    pe.wait_ge(act_, s * A_STEP + 24 + h + 1)
                    turn(h, Z)


def layer0_mixer(core, w):
    nc = core.nc
    with ExitStack() as local:
        core.open_pool(local, 12)

        def sb(name, shape, dtype=F32):
            return local.enter_context(nc.sbuf_tensor("m0_" + name, shape, dtype))
        qT, kT, v = sb("qT", [P, 4, 512]), sb("kT", [P, 4, 512]), sb("v", [P, 4, 512])
        qlT, klT = sb("qlT", [P, 4, LANDMARKS]), sb("klT", [P, 4, LANDMARKS])
        a3v, zav = sb("a3v", [P, 2, 512]), sb("zav", [P, 2, 512])
        Wqkv = core.section(0, 4, 3 * DIM)
        L = {}

        def issue(sp):
            for j in range(3):
                L[j] = core.load(sp, Wqkv[:, :, j * DIM:(j + 1) * DIM], weights(w["m0_Wqkv"], (j * DIM, (j + 1) * DIM)))

        def finish(t, engine, ps, chain):
            m = t % 4
            if t < 4:
                return nc.scalar.mul(qT[:, m, :], ps, HEAD ** -0.5)
            return copy_out(nc, engine, (kT if t < 8 else v)[:, m, :], ps)
        with Stage(core, "m0_load") as st:
            @st.block.sync
            def _(sp):
                issue(sp)
        products_stage(core, "m0_qkv",
                       turned_tiles(core.xnT, Wqkv[:, :, 0:DIM], "A", [lambda: L[0]])
                       + turned_tiles(core.xnT, Wqkv[:, :, DIM:2 * DIM], "V", [lambda: L[1]])
                       + linear_tiles(core.xnT, Wqkv[:, :, 2 * DIM:], "AV", [lambda: L[2]]), finish)
        with Stage(core, "m0_landmarks") as st:
            chain = st.chain(nc.vector, "vector_chain")

            @st.block.vector
            def _(dve):
                for full, marks in ((qT, qlT), (kT, klT)):
                    pairs = full[:].rearrange("p c (n two) -> p c n two", two=2)
                    chain(nc.vector.tensor_tensor(marks[:], pairs[:, :, :, 0], pairs[:, :, :, 1], ALU.add))
                    chain(nc.vector.tensor_scalar(marks[:], marks[:], 0.5, None, ALU.mult))

        def head(x, h):
            return x[HEAD * (h % 2):HEAD * (h % 2) + HEAD, h // 2]
        by_landmarks = [(h, i) for h in range(HEADS) for i in range(2)]

        turns3 = [core.section(b, 4, LANDMARKS) for b in range(2)]

        def half_bank(h):
            return core.bank(4 + h // 4)[HEAD * (h % 2):HEAD * (h % 2) + HEAD, (h // 2) % 2 * LANDMARKS:((h // 2) % 2 + 1) * LANDMARKS]

        def values3(h):
            return half_bank(h), [(v[:, c, h * HEAD:(h + 1) * HEAD], turns3[h % 2][:, c, :]) for c in range(4)]
        a3vT = core.section(2, 4, LANDMARKS)

        def finish3(chain):
            for j in range(2):
                nc.vector.tensor_copy(a3vT[:, 2 * j:2 * j + 2, :], core.bank(4 + j).rearrange("p (c n) -> p c n", c=2))
        softmax_stage(core, "m0_attn3", [[(head(qlT, h)[:, i * P:(i + 1) * P], head(kT, h))] for h, i in by_landmarks],
                      NODES, normal=True, turned=lambda u: turns3[by_landmarks[u][0] % 2][:, :, by_landmarks[u][1] * P:(by_landmarks[u][1] + 1) * P],
                      values=values3, per_value=2, finish=finish3)
        products_stage(core, "m0_turn_values", [Tile([(P, c * P, (c + 1) * P, [(a3vT[:, c, i * P:(i + 1) * P], None)]) for c in range(CHUNKS)], "VA"[i])
                                                for i in range(2)], lambda t, e, ps, chain: copy_out(nc, e, a3v[:, t, :], ps))

        big = lambda first: core.wpool[:, first * 4096:(first + 1) * 4096].rearrange("p (h c n) -> p h c n", h=HEADS, c=2)
        XT, Z, ZT = big(0), big(1), big(2)
        softmax_stage(core, "m0_attn2", [[(head(qlT, h)[:, i * P:(i + 1) * P], head(klT, h))] for h, i in by_landmarks],
                      LANDMARKS, normal=True, keep=lambda u: ZT[:, by_landmarks[u][0], by_landmarks[u][1], :],
                      turned=lambda u: XT[:, by_landmarks[u][0], :, by_landmarks[u][1] * P:(by_landmarks[u][1] + 1) * P])
        pinv_stage(core, XT, Z, ZT)

        products_stage(core, "m0_inverse_values",
                       [Tile([(P, h * HEAD, (h + 1) * HEAD, [(ZT[:, h, c, i * P:(i + 1) * P], a3v[:, c, h * HEAD:(h + 1) * HEAD])
                                                            for c in range(2)]) for h in range(HEADS)], "VA"[i])
                        for i in range(2)], lambda t, e, ps, chain: copy_out(nc, e, zav[:, t, :], ps))

        by_rows = [(h, i) for h in range(HEADS) for i in range(TILES)]

        turns1 = [core.section(6 + b, 2, NODES) for b in range(2)]
        outT = core.section(8)

        def values1(h):
            return (core.bank(4 + h // 2)[HEAD * (h % 2):HEAD * (h % 2) + HEAD],
                    [(zav[:, c, h * HEAD:(h + 1) * HEAD], turns1[h % 2][:, c, :]) for c in range(2)])

        def finish1(chain):
            for c in range(CHUNKS):
                nc.vector.tensor_copy(outT[:, c, :], core.bank(4 + c))
        softmax_stage(core, "m0_attn1", [[(head(qT, h)[:, i * P:(i + 1) * P], head(klT, h))] for h, i in by_rows],
                      LANDMARKS, normal=True, turned=lambda u: turns1[by_rows[u][0] % 2][:, :, by_rows[u][1] * P:(by_rows[u][1] + 1) * P],
                      values=values1, per_value=TILES, finish=finish1)
        products_stage(core, "m0_turn_out", [Tile([(P, c * P, (c + 1) * P, [(outT[:, c, i * P:(i + 1) * P], None)]) for c in range(CHUNKS)], "V")
                                             for i in range(TILES)],
                       lambda t, e, ps, chain: nc.vector.tensor_tensor(core.branches[:, t, :], ps, core.branches[:, t, :], ALU.add))


def linear_attention(core, name, q_turned, k_rows, v_rows, out, epsilon=0.0, factor=None):
    nc = core.nc
    pairs = HEADS // 2
    with ExitStack() as local:
        def sb(n, shape):
            return local.enter_context(nc.sbuf_tensor(f"{name}_{n}", shape, F32))
        kv, k_sum, inverse = sb("kv", [P, pairs, P]), sb("k_sum", [P, pairs, 2]), sb("inverse", [P, 4, HEADS])
        with Stage(core, name + "_kv") as st:
            ready, chain = st.sem("products_ready"), st.chain(nc.vector, "vector_chain")

            @st.block.tensor
            def _(pe):
                for j in range(pairs):
                    cols = slice(j * P, (j + 1) * P)
                    last = product(nc, core, core.bank(0)[:, cols], [(k_rows[:, c, cols], v_rows[:, c, cols]) for c in range(4)])
                for j in range(pairs if factor is None else 0):
                    cols = slice(j * P, (j + 1) * P)
                    last = product(nc, core, core.bank(1)[:, 2 * j:2 * j + 2],
                                   [(k_rows[:, c, cols], core.ones[:, 0:2]) for c in range(4)])
                last.then_inc(ready, 1)

            @st.block.vector
            def _(dve):
                chain(nc.vector.memset(kv[:], 0.0))
                chain(nc.vector.memset(k_sum[:], 0.0))
                dve.wait_ge(ready, 1)
                for b in range(2):
                    half = slice(b * HEAD, (b + 1) * HEAD)
                    chain(nc.vector.tensor_copy(kv[half, :, half], core.bank(0)[half].rearrange("p (j n) -> p j n", j=pairs)[:, :, half]))
                    if factor is not None:
                        continue
                    chain(nc.vector.tensor_copy(k_sum[half, :, b], core.bank(1)[half, 0:2 * pairs].rearrange("p (j n) -> p j n", j=pairs)[:, :, b]))
        with Stage(core, name + "_out") as st:
            ready, taken, chain = st.sem("products_ready"), st.sem("banks_taken"), st.chain(nc.vector, "vector_chain")

            @st.block.tensor
            def _(pe):
                for i in range(TILES):
                    rows = slice(i * P, (i + 1) * P)
                    for j in range(pairs):
                        last = product(nc, core, core.bank(2 * i)[:, j * P:(j + 1) * P], [(q_turned[:, j, rows], kv[:, j, :])])
                    for j in range(pairs if factor is None else 0):
                        last = product(nc, core, core.bank(2 * i + 1)[:, 2 * j:2 * j + 2], [(q_turned[:, j, rows], k_sum[:, j, :])])
                    last.then_inc(ready, 1)

            @st.block.vector
            def _(dve):
                for i in range(TILES):
                    dve.wait_ge(ready, i + 1)
                    if factor is None:
                        chain(nc.vector.tensor_scalar(inverse[:, i, :], core.bank(2 * i + 1)[:, 0:HEADS], epsilon, None, ALU.add))
                        chain(nc.vector.reciprocal(inverse[:, i, :], inverse[:, i, :]))
                    by = inverse[:, i, :] if factor is None else factor[:, i, :]
                    chain(nc.vector.tensor_tensor(out[:, i, :].rearrange("p (h d) -> p h d", h=HEADS),
                                                  core.bank(2 * i).rearrange("p (h d) -> p h d", h=HEADS),
                                                  by.unsqueeze(2).to_broadcast([P, HEADS, HEAD]), ALU.mult))


def phi_stage(core, name, x, scratch):
    nc = core.nc
    with Stage(core, name) as st:
        clamped, exponed = st.sem("minimum_ready"), st.sem("exponential_ready")

        @st.block.vector
        def _(dve):
            for j, a in enumerate(x):
                nc.vector.tensor_scalar(scratch[j][:], a[:], 0.0, None, ALU.min).then_inc(clamped, 1)
            for j, a in enumerate(x):
                dve.wait_ge(exponed, j + 1)
                nc.vector.scalar_tensor_tensor(out=a[:], in0=a[:], scalar=0.0, in1=scratch[j][:], op0=ALU.max, op1=ALU.add)

        @st.block.scalar
        def _(act):
            for j in range(len(x)):
                act.wait_ge(clamped, j + 1)
                nc.scalar.activation(scratch[j][:], scratch[j][:], ACT.Exp).then_inc(exponed, 1)


def layer1_mixer(core, w):
    nc = core.nc
    with ExitStack() as local:
        core.open_pool(local, 10)
        part = [core.section(j) for j in range(10)]
        qT, k, v, s0, s1, out = part[4:10]
        rows = local.enter_context(nc.sbuf_tensor("m1_rows", [P, 1, 512], F32))
        L = {}
        with Stage(core, "m1_load") as st:
            @st.block.sync
            def _(sp):
                for j in range(3):
                    L[j] = core.load(sp, part[j], weights(w["m1_Wqkv"], (j * DIM, (j + 1) * DIM)))
                L[3] = core.load(sp, part[3], weights(w["m1_Wout"]))
                L["rows"] = core.load(sp, rows[:], w["m1_rows"].rearrange("(o r) n -> o r n", o=1).to_broadcast([P, 1, 512]))
        products_stage(core, "m1_qkv",
                       turned_tiles(core.xnT, part[0], "VA", [lambda: L[0]]) + linear_tiles(core.xnT, part[1], "VA", [lambda: L[1]])
                       + linear_tiles(core.xnT, part[2], "VA", [lambda: L[2]]),
                       lambda t, e, ps, chain: copy_out(nc, e, (qT, k, v)[t // 4][:, t % 4, :], ps))
        phi_stage(core, "m1_phi", (qT, k), (s0, s1))
        linear_attention(core, "m1", qT, k, v, out, 1e-6)
        transpose_stage(core, "m1_turn", s0, rows_of(out))

        def finish(t, e, ps, chain):
            chain(nc.vector.tensor_tensor(out[:, t, :], ps, rows[:, 0, :], ALU.add))
            return nc.vector.tensor_tensor(core.branches[:, t, :], core.branches[:, t, :], out[:, t, :], ALU.add)
        products_stage(core, "m1_out", linear_tiles(s0, part[3], "V", [lambda: L[3]]), finish, params=[lambda: L["rows"]])


def layer2_mixer(core, w):
    nc = core.nc
    with ExitStack() as local:
        core.open_pool(local, 12)
        part = [core.section(j) for j in range(12)]
        qT, k, v, s0, s1, out, normed, nT = part[4:12]
        rows = local.enter_context(nc.sbuf_tensor("m2_rows", [P, 5, 512], F32))
        cols = local.enter_context(nc.sbuf_tensor("m2_cols", [P, 4], F32))
        L = {}

        def issue(sp):
            def load_rows(first, n):
                return core.load(sp, rows[:, first:first + n], w["m2_rows"][first:first + n].rearrange("(o r) n -> o r n", o=1).to_broadcast([P, n, 512]))
            L["norm_rows"] = load_rows(3, 2)
            L["cols"] = core.load(sp, cols[:], w["m2_cols"])
            L[0] = core.load(sp, part[0], weights(w["m2_Wqkv"], (0, DIM)))
            L["rows"] = load_rows(0, 3)
            for j in range(1, 3):
                L[j] = core.load(sp, part[j], weights(w["m2_Wqkv"], (j * DIM, (j + 1) * DIM)))
            L[3] = core.load(sp, part[3], weights(w["m2_Wout"]))
        norm_turn_stage(core, "m2_norm", core.xn, normed, nT, scale=rows[:, 3, :], shift=rows[:, 4, :], issue=issue,
                   params=[lambda: L["norm_rows"]])

        def finish_qkv(t, e, ps, chain):
            m = t % 4
            if t < 4:
                return nc.scalar.activation(qT[:, m, :], ps, ACT.Identity, bias=cols[:, m:m + 1])
            return nc.vector.tensor_tensor((k if t < 8 else v)[:, m, :], ps, rows[:, t // 4 - 1, :], ALU.add)
        products_stage(core, "m2_qkv",
                       turned_tiles(nT, part[0], "A", [lambda: L[0]]) + linear_tiles(nT, part[1], "V", [lambda: L[1]])
                       + linear_tiles(nT, part[2], "V", [lambda: L[2]]), finish_qkv, params=[lambda: L["cols"], lambda: L["rows"]])
        phi_stage(core, "m2_phi", (qT, k), (s0, s1))
        linear_attention(core, "m2", qT, k, v, out, 1e-8)
        transpose_stage(core, "m2_turn_out", s0, rows_of(out))

        def finish(t, e, ps, chain):
            chain(nc.vector.tensor_tensor(out[:, t, :], ps, rows[:, 2, :], ALU.add))
            chain(nc.vector.tensor_tensor(out[:, t, :], out[:, t, :], core.xn[:, t, :], ALU.add))
            return nc.vector.tensor_tensor(core.branches[:, t, :], core.branches[:, t, :], out[:, t, :], ALU.add)
        products_stage(core, "m2_out", linear_tiles(s0, part[3], "V", [lambda: L[3]]), finish)


class Gate:

    def __init__(self, core, name, local, weight, bias, experts, columns, rule):
        def sb(n, shape, dtype=F32):
            return local.enter_context(core.nc.sbuf_tensor(f"{name}_{n}", shape, dtype))
        self.core, self.experts, self.rule, self.dram = core, experts, rule, (weight, bias)
        self.gate = sb("gate", [P, 4, columns])
        self.w_sb, self.b_sb = sb("weight", [P, 4, experts]), sb("bias", [P, experts])
        self.scores, self.biased = sb("scores", [P, 4, experts]), sb("biased", [P, 4, experts])
        self.tops, self.tops_biased = sb("tops", [P, 4, 8]), sb("tops_biased", [P, 4, 8])
        self.index, self.index_f = sb("index", [P, 4, 8], U32), sb("index_f", [P, 4, 8])
        self.share, self.total = sb("share", [P, 4, 2]), sb("total", [P, 4])
        self.hot = sb("hot", [P, 4, experts])

    def issue(self, queue):
        self.weight_load = self.core.load(queue, self.w_sb[:], weights(self.dram[0]))
        self.bias_load = self.core.load(queue, self.b_sb[:], self.dram[1].to_broadcast([P, self.experts]))

    def semaphores(self, st):
        self.ready, self.tops_ready, self.shares_ready = st.sem("gate_scores_ready"), st.sem("tops_ready"), st.sem("shares_ready")
        self.chain = st.chain(self.core.nc.vector, "gate_chain")

    def multiply(self, pe, bank):
        core, experts = self.core, self.experts
        self.bank = core.bank(bank)
        self.weight_load.wait(pe)
        for i in range(TILES):
            last = product(core.nc, core, self.bank[:, i * experts:(i + 1) * experts],
                           [(core.xnT[:, c, i * P:(i + 1) * P], self.w_sb[:, c, :]) for c in range(4)])
        last.then_inc(self.ready, 1)

    def activate(self, act):
        nc, share = self.core.nc, self.share
        act.wait_ge(self.tops_ready, 1)
        if self.rule == "softmax":
            nc.scalar.activation(share[:, :, 1], share[:, :, 0], ACT.Exp).then_inc(self.shares_ready, 1)
        else:
            nc.scalar.activation(share[:], self.tops[:, :, 0:2], ACT.Sigmoid).then_inc(self.shares_ready, 1)

    def choose(self, dve):
        core, chain, gate, experts = self.core, self.chain, self.gate, self.experts
        nc = core.nc
        scores, biased, tops, tops_biased = self.scores, self.biased, self.tops, self.tops_biased
        index, index_f, share, total, hot, b_sb = self.index, self.index_f, self.share, self.total, self.hot, self.b_sb
        self.bias_load.wait(dve)
        dve.wait_ge(self.ready, 1)
        chain(nc.vector.tensor_copy(scores[:], self.bank[:, 0:4 * experts].rearrange("p (i e) -> p i e", i=4)))
        chain(nc.vector.tensor_tensor(biased[:], scores[:], b_sb[:].unsqueeze(1).to_broadcast([P, 4, experts]), ALU.add))
        for i in range(TILES):
            last = nc.vector.max(tops_biased[:, i, :], biased[:, i, :])
        chain(last)
        for i in range(TILES):
            last = nc.vector.max_index(index[:, i, :], tops_biased[:, i, :], biased[:, i, :])
        chain(last)
        chain(nc.vector.tensor_copy(index_f[:], index[:]))
        if self.rule == "softmax":
            nc.vector.tensor_tensor(share[:, :, 0], tops_biased[:, :, 1], tops_biased[:, :, 0], ALU.subtract).then_inc(self.tops_ready, 1)
            dve.wait_ge(self.shares_ready, 1)
            chain(nc.vector.tensor_scalar(total[:], share[:, :, 1], 1.0, None, ALU.add))
            chain(nc.vector.reciprocal(share[:, :, 0], total[:]))
            chain(nc.vector.tensor_tensor(share[:, :, 1], share[:, :, 1], share[:, :, 0], ALU.mult))
        else:
            for i in range(TILES):
                chain(nc.vector.max(tops[:, i, :], scores[:, i, :]))
            nc.vector.tensor_copy(total[:], tops[:, :, 0]).then_inc(self.tops_ready, 1)
            dve.wait_ge(self.shares_ready, 1)
            chain(nc.vector.tensor_tensor(total[:], share[:, :, 0], share[:, :, 1], ALU.add))
            chain(nc.vector.reciprocal(total[:], total[:]))
            chain(nc.vector.tensor_tensor(share[:], share[:], total[:].unsqueeze(2).to_broadcast([P, 4, 2]), ALU.mult))
            chain(nc.vector.memset(gate[:], 1.0))
        for i in range(TILES):
            for k, dst in enumerate((gate, hot)):
                last = nc.vector.tensor_scalar(dst[:, i, 0:experts], core.iota[:, 0:experts], index_f[:, i, k:k + 1], share[:, i, k:k + 1],
                                               ALU.is_equal, ALU.mult)
        chain(last)
        chain(nc.vector.tensor_tensor(gate[:, :, 0:experts], gate[:, :, 0:experts], hot[:], ALU.add))


PIECES = 6
RAW, RING = 3, 4


def first_pieces(core, name, local, w1, w3, gate):
    raw = [local.enter_context(core.nc.sbuf_tensor(f"{name}_raw_{j}", [P, 4, 512], F32)) for j in range(RAW)]
    L = {}

    def issue(sp):
        gate.issue(sp)
        for p, (matrix, half) in enumerate(((w1, 0), (w3, 0), (w1, 1))):
            L[p] = core.load(sp, raw[p][:], matrix[0:1, :, half * 512:(half + 1) * 512].rearrange("o (c p) n -> p (o c) n", p=P))
    return raw, L, issue


def experts_stage(core, name, w1, w3, w2, gates, experts, raw, first_loads):
    nc = core.nc
    chunks = 2 * DIM // P
    half = chunks // 2
    with ExitStack() as local, Stage(core, name) as st:
        def sb(n, shape, dtype=F32R):
            return local.enter_context(nc.sbuf_tensor(f"{name}_{n}", shape, dtype))
        high, low = ([sb(f"{part}_{j}", [P, 4, 512]) for j in range(RING)] for part in ("high", "low"))
        h_high, h_low = sb("hidden_high", [P, chunks, NODES]), sb("hidden_low", [P, chunks, NODES])
        x_high, x_low = sb("x_high", [P, 4, NODES]), sb("x_low", [P, 4, NODES])
        silu, h = core.scores, core.exps
        landed = [st.sem(f"piece_landed_{j}") for j in range(RAW)]
        high_ready, split = st.sem("high_pieces_ready"), st.sem("pieces_split")
        x_rounded, x_split = st.sem("x_high_ready"), st.sem("x_split")
        ready, silu_ready, h_ready = st.sem("products_ready"), st.sem("silu_ready"), st.sem("hidden_ready")
        h_rounded, h_split = st.sem("hidden_high_ready"), st.sem("hidden_split")
        halfway, y_ready, y_added = st.sem("first_w2_piece_used"), st.sem("outputs_ready"), st.sem("outputs_added")
        refills = st.sem("refills_begun")
        gates.semaphores(st)
        gate = gates.gate
        looped = (experts - 1) // 2

        def over_experts(engine, body):
            with engine.Fori(0, looped) as s:
                for b in range(2):
                    body(2 * s + b, b, False)
            for e in range(2 * looped, experts):
                body(e, e % 2, e == experts - 1)

        def piece_source(e, p):
            if p < 4:
                cols = slice((p // 2) * 512, (p // 2 + 1) * 512)
                return (w1, w3)[p % 2][bass.ds(e, 1), :, cols].rearrange("o (c p) n -> p (o c) n", p=P)
            rows = slice((p - 4) * 512, (p - 3) * 512)
            return w2[bass.ds(e, 1), rows, :].rearrange("o (c p) n -> p (o c) n", p=P)

        @st.block.sync
        def _(sp):
            def load(e, b, p):
                n = PIECES * b + p
                sp.wait_ge(split, PIECES * e + p - RAW + 1)
                sp.sem_inc(refills, 1)
                sp.dma_start(raw[n % RAW][:], piece_source(e, p)).then_inc(landed[n % RAW], 16)

            def ahead(e, b, last):
                for p in range(RAW, PIECES):
                    load(e, b, p)
                if not last:
                    for p in range(RAW):
                        load(e + 1, 1 - b, p)
            over_experts(sp, ahead)

        @st.block.tensor
        def _(pe):
            def one(e, b, last):
                for m in range(chunks):
                    if m >= 2:
                        pe.wait_ge(h_ready, chunks * e + m - 1)
                    for j in range(2):
                        p = 2 * (m // half) + j
                        if m % half == 0:
                            pe.wait_ge(split, PIECES * e + p + 1)
                        slot = (PIECES * b + p) % RING
                        cols = slice((m % half) * P, (m % half + 1) * P)
                        split_product(nc, core.bank(2 * (m % 2) + j),
                                      [((high[slot][:, c, cols], low[slot][:, c, cols]), (x_high[:, c, :], x_low[:, c, :]))
                                       for c in range(4)]).then_inc(ready, 1)
                for q in range(2):
                    pe.wait_ge(split, PIECES * e + 4 + q + 1)
                    pe.wait_ge(h_split, chunks * e + half * (q + 1))
                    slot = (PIECES * b + 4 + q) % RING
                    for i in range(TILES):
                        rows = slice(i * P, (i + 1) * P)
                        done = split_product(nc, core.bank(4 + i),
                                             [((h_high[:, half * q + c, rows], h_low[:, half * q + c, rows]),
                                               (high[slot][:, c, :], low[slot][:, c, :])) for c in range(half)],
                                             start=q == 0, stop=q == 1)
                        if q == 1:
                            done.then_inc(y_ready, 1)
                    if q == 0:
                        done.then_inc(halfway, 1)
            gates.multiply(pe, 4)
            pe.wait_ge(x_split, CHUNKS)
            over_experts(pe, one)

        def uses(e, b, p):
            return 16 * (2 * e + p // RAW)

        @st.block.scalar
        def _(act):
            def high_piece(e, b, p, free=True, first=False):
                n = PIECES * b + p
                if free:
                    if p == 2:
                        act.wait_ge(halfway, e)
                    elif p == 3:
                        act.wait_ge(y_ready, TILES * e)
                    elif p >= 4:
                        act.wait_ge(ready, 2 * chunks * e + 2 * half)
                    else:
                        act.wait_ge(ready, 2 * chunks * e)
                if first:
                    first_loads[p].wait(act)
                else:
                    act.wait_ge(landed[n % RAW], uses(e, b, p))
                nc.scalar.copy(high[n % RING][:], raw[n % RAW][:]).then_inc(high_ready, 1)

            def one(e, b, last, first=False):
                for m in range(chunks):
                    act.wait_ge(ready, 2 * chunks * e + 2 * m + 1)
                    nc.scalar.activation(silu[:, m % 2, :], core.bank(2 * (m % 2)), ACT.Silu).then_inc(silu_ready, 1)
                    act.wait_ge(h_ready, chunks * e + m + 1)
                    nc.scalar.copy(h_high[:, m, :], h[:, m % 2, :]).then_inc(h_rounded, 1)
                    if m in (0, 1):
                        high_piece(e, b, 2 + m, free=not first, first=first and m == 0)
                    if m in (half, half + 1):
                        high_piece(e, b, m)
                if not last:
                    for p in range(2):
                        high_piece(e + 1, 1 - b, p)
            for c in range(CHUNKS):
                nc.scalar.copy(x_high[:, c, :], core.xnT[:, c, :]).then_inc(x_rounded, 1)
            for p in range(2):
                high_piece(0, 0, p, free=False, first=True)
            gates.activate(act)
            one(0, 0, False, first=True)
            one(1, 1, False)
            with act.Fori(1, looped) as s:
                for b in range(2):
                    one(2 * s + b, b, False)
            for e in range(2 * looped, experts):
                one(e, e % 2, e == experts - 1)

        @st.block.vector
        def _(dve):
            def low_piece(e, b, p):
                n = PIECES * b + p
                dve.wait_ge(high_ready, PIECES * e + p + 1)
                nc.vector.tensor_tensor(low[n % RING][:], raw[n % RAW][:], high[n % RING][:].bitcast(F32),
                                        ALU.subtract).then_inc(split, 1)

            def one(e, b, last):
                for m in range(chunks):
                    dve.wait_ge(silu_ready, chunks * e + m + 1)
                    dve.wait_ge(ready, 2 * chunks * e + 2 * m + 2)
                    nc.vector.tensor_tensor(h[:, m % 2, :], core.bank(2 * (m % 2) + 1), silu[:, m % 2, :], ALU.mult).then_inc(h_ready, 1)
                    dve.wait_ge(h_rounded, chunks * e + m + 1)
                    nc.vector.tensor_tensor(h_low[:, m, :], h[:, m % 2, :], h_high[:, m, :].bitcast(F32),
                                            ALU.subtract).then_inc(h_split, 1)
                    if m in (0, 1):
                        low_piece(e, b, 2 + m)
                    if m in (half, half + 1):
                        low_piece(e, b, m)
                if not last:
                    for p in range(2):
                        low_piece(e + 1, 1 - b, p)
                dve.wait_ge(h_split, chunks * e + chunks)
                for i in range(TILES):
                    dve.wait_ge(y_ready, TILES * e + i + 1)
                    nc.vector.scalar_tensor_tensor(out=core.x[:, i, :], in0=core.bank(4 + i), scalar=gate[:, i, bass.ds(e, 1)],
                                                   in1=core.x[:, i, :], op0=ALU.mult, op1=ALU.add).then_inc(y_added, 1)
            for c in range(CHUNKS):
                dve.wait_ge(x_rounded, c + 1)
                nc.vector.tensor_tensor(x_low[:, c, :], core.xnT[:, c, :], x_high[:, c, :].bitcast(F32),
                                        ALU.subtract).then_inc(x_split, 1)
            for p in range(2):
                low_piece(0, 0, p)
            gates.choose(dve)
            over_experts(dve, one)


def layer0_ffn(core, w):
    with ExitStack() as local:
        gates = Gate(core, "f0_gate", local, w["f0_Wg"], w["f0_bg"], 8, 8, "softmax")
        raw, first_loads, issue = first_pieces(core, "f0", local, w["f0_W1"], w["f0_W3"], gates)
        prepare(core, "f0", issue, add=core.branches)
        experts_stage(core, "f0_experts", w["f0_W1"], w["f0_W3"], w["f0_W2"], gates, 8, raw, first_loads)


def layer1_ffn(core, w):
    with ExitStack() as local:
        gates = Gate(core, "f1_gate", local, w["f1_Wg"], w["f1_bg"], 8, 9, "sigmoid")
        raw, first_loads, issue = first_pieces(core, "f1", local, w["f1_W1"], w["f1_W3"], gates)
        prepare(core, "f1", issue, add=core.branches)
        experts_stage(core, "f1_experts", w["f1_W1"], w["f1_W3"], w["f1_W2"], gates, 9, raw, first_loads)


CAPACITY = 128
L2_EXPERTS = 16
L2_HIDDEN = 256


def capacity_gate_stage(core, w_sb, weight_load, coefficient, place):
    nc = core.nc
    E = L2_EXPERTS
    with ExitStack() as local, Stage(core, "f2_gate") as st:
        def sb(n, shape, dtype=F32):
            return local.enter_context(nc.sbuf_tensor(f"f2g_{n}", shape, dtype))
        raw, negmax, total = sb("raw", [P, 4, E]), sb("negmax", [P, 4]), sb("total", [P, 4])
        tops, index, index_f = sb("tops", [P, 2, 4, 8]), sb("index", [P, 2, 4, 8], U32), sb("index_f", [P, 2, 4, 8])
        mask, position, kept = sb("mask", [P, 2, 4, E]), sb("position", [P, 2, 4, E]), sb("kept", [P, 2, 4, E])
        rest, share, before = sb("rest", [P, 4, E]), sb("share", [P, 2, 4]), sb("before", [P, P])
        ready, maxima, expd = st.sem("logits_ready"), st.sem("maximum_ready"), st.sem("exp_ready")
        masks_ready, counted, kept_ready, total_ready = (st.sem("masks_ready"), st.sem("positions_ready"),
                                                         st.sem("kept_ready"), st.sem("expert_counts_ready"))
        before_ready = st.sem("before_ready")
        chain = st.chain(nc.vector, "vector_chain")

        @st.block.gpsimd
        def _(pool):
            nc.gpsimd.affine_select(out=before[:], in_=core.ones[:], compare_op=ALU.is_gt, fill=0.0, base=0,
                                    pattern=[[1, P]], channel_multiplier=-1).then_inc(before_ready, 1)

        @st.block.tensor
        def _(pe):
            weight_load.wait(pe)
            for i in range(TILES):
                last = product(nc, core, core.bank(0)[:, i * E:(i + 1) * E],
                               [(core.xnT[:, c, i * P:(i + 1) * P], w_sb[:, c, :]) for c in range(4)])
            last.then_inc(ready, 1)
            pe.wait_ge(masks_ready, 1)
            pe.wait_ge(before_ready, 1)
            for k in range(2):
                for i in range(TILES):
                    last = product(nc, core, core.bank(1)[:, (4 * k + i) * E:(4 * k + i + 1) * E],
                                   [(core.ones[:], mask[:, k, j, :]) for j in range(i)] + [(before[:], mask[:, k, i, :])])
            last.then_inc(counted, 1)
            pe.wait_ge(kept_ready, 1)
            product(nc, core, core.bank(2)[:, 0:E], [(core.ones[:], kept[:, 0, j, :]) for j in range(TILES)]).then_inc(total_ready, 1)

        @st.block.scalar
        def _(act):
            act.wait_ge(maxima, 1)
            for i in range(TILES):
                last = nc.scalar.activation(raw[:, i, :], core.bank(0)[:, i * E:(i + 1) * E], ACT.Exp, bias=negmax[:, i:i + 1],
                                            accum_out=total[:, i:i + 1])
                last.then_inc(expd, 1)

        @st.block.vector
        def _(dve):
            flat = lambda x: x[:].rearrange("p k i e -> p (k i) e")
            dve.wait_ge(ready, 1)
            nc.vector.tensor_reduce(negmax[:], core.bank(0)[:, 0:4 * E].rearrange("p (i e) -> p i e", i=4), AXIS.X, ALU.max,
                                    negate=True).then_inc(maxima, 1)
            dve.wait_ge(expd, TILES)
            chain(nc.vector.reciprocal(total[:], total[:]))
            chain(nc.vector.tensor_tensor(raw[:], raw[:], total[:].unsqueeze(2).to_broadcast([P, 4, E]), ALU.mult))
            for k, values in enumerate((raw, rest)):
                for i in range(TILES):
                    last = nc.vector.max(tops[:, k, i, :], values[:, i, :])
                chain(last)
                for i in range(TILES):
                    last = nc.vector.max_index(index[:, k, i, :], tops[:, k, i, :], values[:, i, :])
                chain(last)
                chain(nc.vector.tensor_copy(index_f[:, k], index[:, k]))
                for i in range(TILES):
                    last = nc.vector.tensor_scalar(mask[:, k, i, :], core.iota[:, 0:E], index_f[:, k, i, 0:1], None, ALU.is_equal)
                if k == 0:
                    chain(last)
                    chain(nc.vector.tensor_scalar(rest[:], mask[:, 0], -1.0, 1.0, ALU.mult, ALU.add))
                    chain(nc.vector.tensor_tensor(rest[:], rest[:], raw[:], ALU.mult))
            last.then_inc(masks_ready, 1)
            chain(nc.vector.tensor_tensor(total[:], tops[:, 0, :, 0], tops[:, 1, :, 0], ALU.add))
            chain(nc.vector.tensor_scalar(total[:], total[:], 1e-9, None, ALU.add))
            chain(nc.vector.reciprocal(total[:], total[:]))
            for k in range(2):
                chain(nc.vector.tensor_tensor(share[:, k], tops[:, k, :, 0], total[:], ALU.mult))
            dve.wait_ge(counted, 1)
            counts = core.bank(1)[:, 0:8 * E].rearrange("p (k i e) -> p k i e", k=2, i=4)
            chain(nc.vector.tensor_tensor(position[:, 0], counts[:, 0], mask[:, 0], ALU.mult))
            chain(nc.vector.tensor_scalar(kept[:, 0], position[:, 0], float(CAPACITY), None, ALU.is_lt))
            nc.vector.tensor_tensor(kept[:, 0], kept[:, 0], mask[:, 0], ALU.mult).then_inc(kept_ready, 1)
            dve.wait_ge(total_ready, 1)
            chain(nc.vector.tensor_copy(rest[:, 0, :], core.bank(2)[:, 0:E]))
            chain(nc.vector.tensor_tensor(position[:, 1], counts[:, 1], rest[:, 0:1, :].to_broadcast([P, 4, E]), ALU.add))
            chain(nc.vector.tensor_tensor(position[:, 1], position[:, 1], mask[:, 1], ALU.mult))
            chain(nc.vector.tensor_scalar(kept[:, 1], position[:, 1], float(CAPACITY), None, ALU.is_lt))
            chain(nc.vector.tensor_tensor(kept[:, 1], kept[:, 1], mask[:, 1], ALU.mult))
            chain(nc.vector.tensor_reduce(place[:].rearrange("p k i -> p (k i)"), flat(position), AXIS.X, ALU.add))
            chain(nc.vector.tensor_tensor(coefficient[:].rearrange("p k i e -> p (k i) e"), flat(kept),
                                          share[:].rearrange("p k i -> p (k i)").unsqueeze(2).to_broadcast([P, 8, E]), ALU.mult))


def layer2_ffn(core, w):
    nc = core.nc
    with ExitStack() as local:
        def sb(n, shape):
            return local.enter_context(nc.sbuf_tensor(f"f2_{n}", shape, F32))
        core.open_pool(local, 10)
        coefficient, place = sb("coefficient", [P, 2, 4, L2_EXPERTS]), sb("place", [P, 2, 4])
        hot = sb("hot", [P, 4, CAPACITY])
        combine = core.section(0)
        dispatch, xn_high, xn_low = (local.enter_context(nc.sbuf_tensor(f"f2_{n}", [P, 4, width], F32R))
                                     for n, width in (("dispatch", 2 * CAPACITY), ("xn_high", DIM), ("xn_low", DIM)))
        pick = lambda x, b: x[:, b, :].rearrange("p (i c) -> p i c", i=4)
        combineT, inT, y_in = core.section(2), core.section(3, 4, 2 * CAPACITY), core.section(4)
        hiddenT = core.section(5)
        W1 = [core.section(6 + b, 4, L2_HIDDEN) for b in range(2)]
        W2 = [core.section(8 + b, 2, DIM) for b in range(2)]
        pairs = L2_EXPERTS // 2
        L1, L2, gate_loads = [], [], []
        gate_weight = sb("gate_weight", [P, 4, L2_EXPERTS])

        def issue(sp):
            gate_loads.append(core.load(sp, gate_weight[:], weights(w["f2_Wg"])))
            for b in range(2):
                L1.append(core.load(sp, W1[b], w["f2_W1"][b:b + 1].rearrange("o (c p) n -> p (o c) n", p=P)))
                L2.append(core.load(sp, W2[b], w["f2_W2"][b:b + 1].rearrange("o (c p) n -> p (o c) n", p=P)))
        prepare(core, "f2", issue, add=core.branches)
        capacity_gate_stage(core, gate_weight, gate_loads[0], coefficient, place)
        with Stage(core, "f2_experts") as st:
            landed1, landed2 = [st.sem(f"w1_landed_{b}") for b in range(2)], [st.sem(f"w2_landed_{b}") for b in range(2)]
            combined, turned, entered = st.sem("combine_ready"), st.sem("combine_turned"), st.sem("inputs_ready")
            turn_copied, in_copied = st.sem("turned_copied"), st.sem("inputs_copied")
            hid_ready, hid_made, out_ready, out_copied = (st.sem("hidden_ready"), st.sem("hidden_made"),
                                                          st.sem("expert_outputs_ready"), st.sem("expert_outputs_copied"))
            y_ready, y_added = st.sem("row_outputs_ready"), st.sem("row_outputs_added")
            xn_rounded, xn_split = st.sem("xn_high_ready"), st.sem("xn_split")
            chained = st.sem("vector_chain")

            def load1(sp, e, b):
                sp.dma_start(W1[b], w["f2_W1"][bass.ds(e, 1)].rearrange("o (c p) n -> p (o c) n", p=P)).then_inc(landed1[b], 16)

            def load2(sp, e, b):
                sp.dma_start(W2[b], w["f2_W2"][bass.ds(e, 1)].rearrange("o (c p) n -> p (o c) n", p=P)).then_inc(landed2[b], 16)

            @st.block.sync
            def _(sp):
                with sp.Fori(1, pairs) as s:
                    for b in range(2):
                        sp.wait_ge(hid_ready, 2 * s + b - 1)
                        load1(sp, 2 * s + b, b)
                    for b in range(2):
                        sp.wait_ge(out_ready, 2 * s + b - 1)
                        load2(sp, 2 * s + b, b)

            @st.block.tensor
            def _(pe):
                def pair(s, first=False):
                    for b in range(2):
                        pe.wait_ge(combined, 2 * s + b + 1)
                        for i in range(TILES):
                            last = nc.tensor.transpose(core.bank(b)[:, i * P:(i + 1) * P], pick(combine, b)[:, i, :], core.ident[:])
                        last.then_inc(turned, 1)
                    if first:
                        pe.wait_ge(xn_split, TILES)
                    for c in range(CHUNKS):
                        for i in range(TILES):
                            for j, part in enumerate((xn_high, xn_low)):
                                last = nc.tensor.matmul(core.bank(2 + c // 2)[:, c % 2 * 2 * CAPACITY:(c % 2 + 1) * 2 * CAPACITY],
                                                        part[:, i, c * P:(c + 1) * P], dispatch[:, i, :],
                                                        start=i == 0 and j == 0, stop=i == TILES - 1 and j == 1)
                        if c % 2 == 1:
                            last.then_inc(entered, 1)
                    for b in range(2):
                        if first:
                            L1[b].wait(pe)
                        else:
                            pe.wait_ge(landed1[b], 16 * s)
                        if b == 0:
                            pe.wait_ge(in_copied, 2 * s + 2)
                        for m in range(2):
                            last = product(nc, core, core.bank(b)[:, m * P:(m + 1) * P],
                                           [(W1[b][:, c, m * P:(m + 1) * P], inT[:, c, b * CAPACITY:(b + 1) * CAPACITY])
                                            for c in range(4)])
                        last.then_inc(hid_ready, 1)
                    for b in range(2):
                        if first:
                            L2[b].wait(pe)
                        else:
                            pe.wait_ge(landed2[b], 16 * s)
                        pe.wait_ge(hid_made, 2 * s + b + 1)
                        product(nc, core, core.bank(2 + b),
                                [(hiddenT[:, b, m * P:(m + 1) * P], W2[b][:, m, :]) for m in range(2)]).then_inc(out_ready, 1)
                    for b in range(2):
                        pe.wait_ge(out_copied, 2 * s + b + 1)
                        for i in range(TILES):
                            if not (first and b == 0):
                                pe.wait_ge(y_added, 8 * s + 4 * b + i - 3)
                            product(nc, core, core.bank(4 + i), [(combineT[:, b, i * P:(i + 1) * P], y_in[:, b, :])]).then_inc(y_ready, 1)
                pair(0, first=True)
                with pe.Fori(1, pairs) as s:
                    pair(s)

            @st.block.scalar
            def _(act):
                for i in range(TILES):
                    nc.scalar.copy(xn_high[:, i, :], core.xn[:, i, :]).then_inc(xn_rounded, 1)
                with act.Fori(0, pairs) as s:
                    for b in range(2):
                        act.wait_ge(turned, 2 * s + b + 1)
                        nc.scalar.copy(combineT[:, b, :], core.bank(b)).then_inc(turn_copied, 1)
                    for half in range(2):
                        act.wait_ge(entered, 2 * s + half + 1)
                        act.wait_ge(turn_copied, 2 * s + half + 1)
                        nc.scalar.copy(inT[:, 2 * half:2 * half + 2, :],
                                       core.bank(2 + half).rearrange("p (c n) -> p c n", c=2)).then_inc(in_copied, 1)
                    for b in range(2):
                        act.wait_ge(hid_ready, 2 * s + b + 1)
                        nc.scalar.activation(hiddenT[:, b, 0:2 * P], core.bank(b)[:, 0:2 * P], ACT.Relu).then_inc(hid_made, 1)
                    for b in range(2):
                        act.wait_ge(out_ready, 2 * s + b + 1)
                        nc.scalar.copy(y_in[:, b, :], core.bank(2 + b)).then_inc(out_copied, 1)

            @st.block.vector
            def _(dve):
                def combine_pair(s, first=False):
                    for b in range(2):
                        if not first and b == 0:
                            dve.wait_ge(entered, 2 * s)
                        for i in range(TILES):
                            for k, dst in enumerate((pick(combine, b), hot)):
                                last = nc.vector.tensor_scalar(dst[:, i, :], core.iota[:, 0:CAPACITY], place[:, k, i:i + 1],
                                                               coefficient[:, k, i, bass.ds(2 * s + b, 1)], ALU.is_equal, ALU.mult)
                        last.then_inc(chained, 1)
                        dve.wait_ge(chained, 4 * s + 2 * b + 1)
                        nc.vector.tensor_tensor(pick(combine, b), pick(combine, b), hot[:], ALU.add).then_inc(chained, 1)
                        dve.wait_ge(chained, 4 * s + 2 * b + 2)
                        nc.vector.tensor_scalar(dispatch[:, :, b * CAPACITY:(b + 1) * CAPACITY], pick(combine, b), 0.0, None,
                                                ALU.is_gt).then_inc(combined, 1)

                def add_pair(s, first=False):
                    for b in range(2):
                        for i in range(TILES):
                            dve.wait_ge(y_ready, 8 * s + 4 * b + i + 1)
                            if not (first and b == 0):
                                dve.wait_ge(y_added, 8 * s + 4 * b + i - 3)
                            nc.vector.tensor_tensor(core.x[:, i, :], core.bank(4 + i), core.x[:, i, :], ALU.add).then_inc(y_added, 1)
                combine_pair(0, first=True)
                for i in range(TILES):
                    dve.wait_ge(xn_rounded, i + 1)
                    nc.vector.tensor_tensor(xn_low[:, i, :], core.xn[:, i, :], xn_high[:, i, :].bitcast(F32),
                                            ALU.subtract).then_inc(xn_split, 1)
                combine_pair(1)
                add_pair(0, first=True)
                with dve.Fori(1, pairs - 1) as s:
                    combine_pair(s + 1)
                    add_pair(s)
                add_pair(pairs - 1)


def layer1_gnn(core, w):
    nc = core.nc
    with ExitStack() as local:
        core.open_pool(local, 3)
        sumT, W = core.section(0), core.section(1, 8, DIM)
        rows = local.enter_context(nc.sbuf_tensor("g1_rows", [P, 1, 512], F32))
        inverse = local.enter_context(nc.sbuf_tensor("g1_inverse", [P, 4], F32))
        L = {}

        def issue(sp):
            L["W"] = core.load(sp, W, weights(w["g1_W"]))
            L["rows"] = core.load(sp, rows[:], w["g1_rows"].rearrange("(o r) n -> o r n", o=1).to_broadcast([P, 1, 512]))

        def degrees(chain):
            chain(nc.vector.tensor_reduce(inverse[:], core.edges_to[:], AXIS.X, ALU.add))
            chain(nc.vector.tensor_scalar(inverse[:], inverse[:], 1.0, None, ALU.max))
            nc.vector.reciprocal(inverse[:], inverse[:])
        prepare(core, "g1", issue, also=degrees)
        products_stage(core, "g1_sums",
                       [Tile([(P, 0, NODES, [(core.xn[:, j, c * P:(c + 1) * P], core.edges_from[:, j, :]) for j in range(TILES)])],
                             "VA"[c % 2]) for c in range(CHUNKS)], lambda t, e, ps, chain: copy_out(nc, e, sumT[:, t, :], ps))

        def tiles():
            out = []
            for i in range(TILES):
                rows_i = slice(i * P, (i + 1) * P)
                out.append(Tile([(P, 0, DIM, [(sumT[:, c, rows_i], W[:, 4 + c, :]) for c in range(4)])], "V", [lambda: L["W"]]))
                out.append(Tile([(P, 0, DIM, [(core.xnT[:, c, rows_i], W[:, c, :]) for c in range(4)])], "V"))
            return out

        def finish(t, e, ps, chain):
            i = t // 2
            out = core.branches[:, i, :]
            if t % 2 == 0:
                return nc.vector.scalar_tensor_tensor(out=out, in0=ps, scalar=inverse[:, i:i + 1], in1=rows[:, 0, :],
                                                      op0=ALU.mult, op1=ALU.add)
            chain(nc.vector.tensor_tensor(out, ps, out, ALU.add))
            return nc.vector.tensor_scalar(out, out, 0.0, None, ALU.max)
        products_stage(core, "g1_out", tiles(), finish, params=[lambda: L["rows"]], ordered=True)


def layer2_gnn(core, w):
    nc = core.nc
    heads = 4
    with ExitStack() as local:
        core.open_pool(local, 12)

        def sb(name, shape):
            return local.enter_context(nc.sbuf_tensor("g2_" + name, shape, F32))
        rows, cols = sb("rows", [P, 7, 512]), sb("cols", [P, 48])
        v, turned = sb("v", [P, 4, 512]), sb("attention", [P, 4, 512])
        xT = core.section(8, 16, 512)
        Wq, Wk, Wv, Wskip = (core.section(j) for j in range(4))
        qT, kT, mask, h = core.section(4), core.section(5), core.section(6), core.section(7)
        L = {}

        def load_head(n, names):
            def issue(sp):
                for name, dst in (("g2_Wq", Wq), ("g2_Wk", Wk), ("g2_Wv", Wv), ("g2_Wskip", Wskip)):
                    if name in names and n < heads:
                        L[name, n] = core.load(sp, dst, weights(w[name], (n * DIM, (n + 1) * DIM)))
            return issue
        before_attention, after_attention = ("g2_Wq", "g2_Wk", "g2_Wv"), ("g2_Wskip",)

        def issue(sp):
            L["cols"] = core.load(sp, cols[:], w["g2_cols"])
            load_head(0, before_attention)(sp)
            L["rows"] = core.load(sp, rows[:], w["g2_rows"].rearrange("(o r) n -> o r n", o=1).to_broadcast([P, 7, 512]))
        
        def make_mask(chain):
            nc.vector.tensor_scalar(mask[:], core.edges_to[:], 0.5, MASKED, ALU.is_lt, ALU.mult)
        prepare(core, "g2", issue, also=make_mask)
        Wlin = core.section(4, 16, 512)

        def issue_lin(sp):
            L["lin"] = core.load(sp, Wlin, weights(w["g2_Wlin"]))
        for n in range(heads):
            def finish(t, e, ps, chain):
                m = t % 4
                if t < 4:
                    return nc.scalar.activation(qT[:, m, :], ps, ACT.Identity, bias=cols[:, 4 * n + m:4 * n + m + 1])
                if t < 8:
                    return nc.scalar.activation(kT[:, m, :], ps, ACT.Identity, bias=cols[:, 16 + 4 * n + m:17 + 4 * n + m])
                return nc.vector.tensor_tensor(v[:, m, :], ps, rows[:, n, :], ALU.add)
            products_stage(core, f"g2_qkv{n}",
                           turned_tiles(core.xnT, Wq, "A", [lambda: L["g2_Wq", n]]) + turned_tiles(core.xnT, Wk, "A", [lambda: L["g2_Wk", n]])
                           + linear_tiles(core.xnT, Wv, "V", [lambda: L["g2_Wv", n]]), finish,
                           params=[lambda: L["rows"], lambda: L["cols"]], issue=load_head(n, after_attention))
            softmax_stage(core, f"g2_attention{n}",
                          [[(qT[:, c, i * P:(i + 1) * P], kT[:, c, :]) for c in range(4)] for i in range(TILES)], NODES,
                          scale=DIM ** -0.5, mask=lambda u: mask[:, u, :], weigh=lambda u: core.edges_to[:, u, :],
                          turned=lambda u: turned[:, :, u * P:(u + 1) * P], issue=load_head(n + 1, before_attention))

            def finish_values(t, e, ps, chain):
                c = 4 * n + t
                return nc.scalar.activation(xT[:, c, :], ps, ACT.Identity, bias=cols[:, 32 + c:33 + c])
            products_stage(core, f"g2_values{n}",
                           [Tile([(P, 0, NODES, [(v[:, j, c * P:(c + 1) * P], turned[:, j, :]) for j in range(4)]
                                   + [(Wskip[:, k, c * P:(c + 1) * P], core.xnT[:, k, :]) for k in range(4)])], "A",
                                 [lambda: L["g2_Wskip", n]]) for c in range(CHUNKS)], finish_values,
                           issue=issue_lin if n == heads - 1 else None)

        def finish_out(t, e, ps, chain):
            return nc.vector.tensor_tensor(v[:, t, :], ps, rows[:, 4, :], ALU.add)
        products_stage(core, "g2_lin", linear_tiles(xT, Wlin, "V", [lambda: L["lin"]]), finish_out)

        def finish_first(t, e, ps, chain):
            return nc.vector.tensor_tensor(v[:, t, :], ps, v[:, t, :], ALU.add)
        products_stage(core, "g2_first", [Tile([(P, c * P, (c + 1) * P, [(xT[:, c, i * P:(i + 1) * P], None)]) for c in range(CHUNKS)], "V")
                                          for i in range(TILES)], finish_first)
        norm_turn_stage(core, "g2_norm", v, core.branches, scale=rows[:, 5, :], shift=rows[:, 6, :])


MUL = 128
SILU_2MOM = 1.679177
GROUP = 4
BLOCKS = 8


def edges_stage(core, w, table, sums, attr, W1, W_raw, loads):
    nc = core.nc
    groups = EDGE_TILES // GROUP
    with ExitStack() as local, Stage(core, "g3_edges") as st:
        def sb(n, shape, dtype=F32):
            return local.enter_context(nc.sbuf_tensor("g3e_" + n, shape, dtype))
        W_high = [sb(f"mlp{n + 2}_high", [P, width], F32R) for n, width in enumerate((P, P, 4 * MUL))]
        W_low = [sb(f"mlp{n + 2}_low", [64, width], F32R) for n, width in enumerate((P, P, 4 * MUL))]
        feat = sb("features", [8, 2, GROUP * P])
        hid = core.exps
        hid_parts = sb("hidden_parts", [P, 3, GROUP * P], F32R)
        senders = sb("senders", [P, 2, GROUP], I32)
        t2, dot = (core.scores[:, j, 0:2 * MUL].rearrange("p (b u) -> p b u", b=2) for j in range(2))
        gathered = [core.section(2 + b, GROUP, 4 * MUL) for b in range(2)]
        raw = sb("messages", [P, 2, BLOCKS * MUL])
        high = [sb(f"messages_high_{b}", [P, GROUP, BLOCKS * MUL], F32R) for b in range(2)]
        low = [sb(f"messages_low_{b}", [P, GROUP, BLOCKS * MUL], F32R) for b in range(2)]
        hot = [sb(f"one_hots_{b}", [P, GROUP, NODES], F32R) for b in range(2)]
        feat_landed = [st.sem(f"features_landed_{b}") for b in range(2)]
        rows_landed = core.gather_sems
        attr_ready = st.sem("attributes_scaled")
        mlp_ready, mlp_made, tpw_ready = st.sem("mlp_products"), st.sem("mlp_silus"), st.sem("edge_weights_ready")
        t2_ready, vectors_ready, raw_ready = st.sem("w2_s0_ready"), st.sem("vector_a_ready"), st.sem("raw_messages_ready")
        high_ready, message_ready = st.sem("high_parts_ready"), st.sem("messages_ready")
        summed, added, kept = st.sem("group_summed"), st.sem("sums_added"), st.sem("kept_sums_ready")
        group_read = st.sem("group_read")
        chained, weights_split = st.sem("vector_chain"), st.sem("weights_split")
        silu_ready, hid_rounded = st.sem("silus_ready"), st.sem("hidden_high_ready")
        LINKS = 3
        MLP_BANK, SUM_BANK = 0, 1
        tpw_bank = lambda j: core.bank(2 + j % 2)

        @st.block.sync
        def _(sp):
            def features(g, b):
                sp.dma_start(feat[:, b, :], w["g3_feat"][:, bass.ds(g * GROUP * P, GROUP * P)]).then_inc(feat_landed[b], 16)
            features(0, 0)
            features(1, 1)
            with sp.Fori(1, groups // 2) as s:
                for b in range(2):
                    sp.wait_ge(mlp_ready, 3 * (2 * s + b) - 5)
                    features(2 * s + b, b)

        @st.block.gpsimd
        def _(pool):
            def gather(g, b, first):
                if not first:
                    pool.wait_ge(raw_ready, GROUP * g - GROUP)
                nc.gpsimd.tensor_copy(senders[:, b, :], core.src_i[:, bass.ds(GROUP * g, GROUP)])
                pool.drain()
                for j in range(GROUP):
                    nc.gpsimd.indirect_dma_start(
                        out=gathered[b][:, j, :], out_offset=None, in_=table,
                        in_offset=bass.IndirectOffsetOnAxis(ap=senders[:, b, j:j + 1].bitcast(U32), axis=0)).then_inc(rows_landed[b], 16)

            def low_hidden(g, b, use):
                pool.wait_ge(rows_landed[b], 16 * GROUP * use)
                for n in range(3):
                    pool.wait_ge(hid_rounded, 3 * g + n + 1)
                    nc.gpsimd.tensor_tensor(hid_parts[64:P, n, :], hid[64:P, n, :], hid_parts[64:P, n, :].bitcast(F32),
                                            ALU.subtract).then_inc(mlp_made, 1)
                pool.wait_ge(mlp_made, 3 * g + 3)
            gather(0, 0, True)
            low_hidden(0, 0, 1)
            gather(1, 1, True)
            with pool.Fori(0, groups // 2 - 1) as s:
                for b in range(2):
                    low_hidden(2 * s + b + 1, 1 - b, s + 1 + b)
                    gather(2 * s + b + 2, b, False)
            low_hidden(groups - 1, 1, groups // 2)

        @st.block.tensor
        def _(pe):
            def hidden_product(out, n, cols, transposed):
                first = (W_high[n - 1][:], hid_parts[:, n - 1, cols])
                second = (W_low[n - 1][:], hid_parts[0:64, n - 1, cols])
                for j, (weight, hidden) in enumerate((first, second)):
                    left, right = (hidden, weight) if transposed else (weight, hidden)
                    last = nc.tensor.matmul(out, left, right, start=j == 0, stop=j == 1)
                return last

            def layer(g, b, n, use):
                if n == 0:
                    pe.wait_ge(feat_landed[b], 16 * use)
                else:
                    pe.wait_ge(mlp_made, 3 * g + n)
                if n == 0:
                    last = product(nc, core, core.bank(MLP_BANK), [(W1[:], feat[:, b, :])])
                else:
                    last = hidden_product(core.bank(MLP_BANK), n, slice(0, GROUP * P), False)
                last.then_inc(mlp_ready, 1)

            def edge_weights(g, j, first=False):
                if j == 0:
                    pe.wait_ge(mlp_made, 3 * g + 3)
                if not first:
                    pe.wait_ge(raw_ready, GROUP * g + j - 1)
                hidden_product(tpw_bank(j), 3, slice(j * P, (j + 1) * P), True).then_inc(tpw_ready, 1)

            def add_up(g, r, b, first=False, last=False):
                m, half = r // 2, r % 2
                if r == 0:
                    pe.wait_ge(message_ready, GROUP * g + GROUP)
                if half == 0 and not (first and r == 0):
                    pe.wait_ge(added, 4 * g + m + 1)
                out = core.bank(SUM_BANK if half == 0 else 4 + m)
                start, stop = (True, True) if half == 0 else (first, last)
                for j in range(GROUP):
                    for p, part in enumerate((high, low)):
                        done = nc.tensor.matmul(out, hot[b][:, j, m * P:(m + 1) * P],
                                                part[b][:, j, half * BANK:(half + 1) * BANK],
                                                start=start and j == 0 and p == 0, stop=stop and j == GROUP - 1 and p == 1,
                                                skip_group_check=half == 1)
                if half == 0:
                    done.then_inc(summed, 1)
                elif last:
                    done.then_inc(kept, 1)
                elif r == BLOCKS - 1:
                    done.then_inc(group_read, 1)

            def group(g, b, use, sum_g, has_next=True, sum_first=False):
                def between(*products):
                    for r in products if sum_g is not None else ():
                        add_up(sum_g, r, 1 - b, first=sum_first)
                if has_next:
                    layer(g + 1, 1 - b, 0, use)
                edge_weights(g, 2)
                between(0)
                edge_weights(g, 3)
                between(1)
                if has_next:
                    layer(g + 1, 1 - b, 1, use)
                between(2, 3)
                if has_next:
                    layer(g + 1, 1 - b, 2, use)
                between(4, 5)
                if has_next:
                    edge_weights(g + 1, 0)
                    edge_weights(g + 1, 1)
                between(6, 7)
            pe.wait_ge(weights_split, 6)
            for n in range(3):
                layer(0, 0, n, 1)
            edge_weights(0, 0, first=True)
            edge_weights(0, 1, first=True)
            group(0, 0, 1, None)
            group(1, 1, 2, 0, sum_first=True)
            with pe.Fori(1, groups // 2 - 1) as s:
                for b in range(2):
                    group(2 * s + b, b, s + 1 + b, 2 * s + b - 1)
            group(groups - 2, 0, groups // 2, groups - 3)
            group(groups - 1, 1, 0, groups - 2, has_next=False)
            for r in range(BLOCKS):
                add_up(groups - 1, r, 1, last=True)

        @st.block.scalar
        def _(act):
            def hidden(g, n):
                act.wait_ge(mlp_ready, 3 * g + n + 1)
                scale = 8 ** -0.5 if n == 0 else SILU_2MOM / 8
                nc.scalar.activation(hid[:, n, :], core.bank(MLP_BANK), ACT.Silu, scale=scale).then_inc(silu_ready, 1)
                act.wait_ge(silu_ready, 3 * g + n + 1)
                nc.scalar.copy(hid_parts[:, n, :], hid[:, n, :]).then_inc(hid_rounded, 1)

            def vectors(g, j):
                act.wait_ge(t2_ready, GROUP * g + j + 1)
                for m in range(3):
                    last = nc.scalar.activation(raw[:, j % 2, (2 + 2 * m) * MUL:(3 + 2 * m) * MUL], t2[:, j % 2, :], ACT.Copy,
                                                scale=attr[:, bass.ds(4 * GROUP * g + 4 * j + m + 1, 1)])
                last.then_inc(vectors_ready, 1)

            def high_part(g, j, b, reused):
                if j == 0 and reused:
                    act.wait_ge(group_read, g - 1)
                act.wait_ge(vectors_ready, GROUP * g + j + 1)
                act.wait_ge(raw_ready, GROUP * g + j + 1)
                nc.scalar.copy(high[b][:, j, :], raw[:, j % 2, :]).then_inc(high_ready, 1)

            def group(g, b, reused=True, has_next=True):
                high_part(g, 0, b, reused)
                if has_next:
                    hidden(g + 1, 0)
                high_part(g, 1, b, reused)
                vectors(g, 2)
                high_part(g, 2, b, reused)
                if has_next:
                    hidden(g + 1, 1)
                vectors(g, 3)
                high_part(g, 3, b, reused)
                if has_next:
                    hidden(g + 1, 2)
                    vectors(g + 1, 0)
                    vectors(g + 1, 1)
            act.wait_ge(attr_ready, 1)
            for n in range(3):
                hidden(0, n)
            vectors(0, 0)
            vectors(0, 1)
            group(0, 0, reused=False)
            group(1, 1, reused=False)
            with act.Fori(1, groups // 2 - 1) as s:
                for b in range(2):
                    group(2 * s + b, b)
            group(groups - 2, 0)
            group(groups - 1, 1, has_next=False)

        @st.block.vector
        def _(dve):
            def link(instruction, g, j, n):
                instruction.then_inc(chained, 1)
                dve.wait_ge(chained, (g * GROUP + j) * LINKS + n)

            def message(g, j, b, use):
                y = [attr[:, bass.ds(4 * GROUP * g + 4 * j + m, 1)] for m in range(4)]
                if j == 0:
                    dve.wait_ge(rows_landed[b], 16 * GROUP * use)
                dve.wait_ge(tpw_ready, GROUP * g + j + 1)
                part = [tpw_bank(j)[:, k * MUL:(k + 1) * MUL] for k in range(4)]
                s = [gathered[b][:, j, k * MUL:(k + 1) * MUL] for k in range(4)]
                out = raw[:, j % 2, :]
                nc.vector.tensor_tensor(t2[:, j % 2, :], part[1], s[0], ALU.mult).then_inc(t2_ready, 1)
                link(nc.vector.tensor_scalar(dot[:, j % 2, :], s[1], y[1], None, ALU.mult), g, j, 1)
                nc.vector.scalar_tensor_tensor(out=out[:, 0:MUL], in0=part[0], scalar=y[0], in1=s[0], op0=ALU.mult, op1=ALU.mult)
                link(nc.vector.scalar_tensor_tensor(out=dot[:, j % 2, :], in0=s[2], scalar=y[2], in1=dot[:, j % 2, :],
                                                    op0=ALU.mult, op1=ALU.add), g, j, 2)
                nc.vector.scalar_tensor_tensor(out=out.rearrange("p (m two u) -> p m two u", two=2, u=MUL)[:, 1:4, 1, :],
                                               in0=part[2].unsqueeze(1).to_broadcast([P, 3, MUL]), scalar=y[0],
                                               in1=gathered[b][:, j, MUL:].rearrange("p (m u) -> p m u", m=3),
                                               op0=ALU.mult, op1=ALU.mult)
                link(nc.vector.scalar_tensor_tensor(out=dot[:, j % 2, :], in0=s[3], scalar=y[3], in1=dot[:, j % 2, :],
                                                    op0=ALU.mult, op1=ALU.add), g, j, 3)
                nc.vector.scalar_tensor_tensor(out=out[:, MUL:2 * MUL], in0=part[3], scalar=3 ** -0.5, in1=dot[:, j % 2, :],
                                               op0=ALU.mult, op1=ALU.mult).then_inc(raw_ready, 1)

            def low_part(g, j, b):
                dve.wait_ge(high_ready, GROUP * g + j + 1)
                nc.vector.tensor_scalar(hot[b][:, j, :], core.iota[:], core.dst_f[:, bass.ds(GROUP * g + j, 1)], None, ALU.is_equal)
                nc.vector.tensor_tensor(low[b][:, j, :], raw[:, j % 2, :], high[b][:, j, :].bitcast(F32),
                                        ALU.subtract).then_inc(message_ready, 1)

            def add(g, m):
                dve.wait_ge(summed, 4 * g + m + 1)
                if m == 0:
                    dve.wait_ge(added, 4 * g + 1)
                to = sums[:, m, 0:BANK]
                nc.vector.tensor_tensor(to, core.bank(SUM_BANK), to, ALU.add).then_inc(added, 1)

            def group(g, b, use, sum_g, has_next=True):
                low_part(g, 0, b)
                message(g, 2, b, use[0])
                if sum_g is not None:
                    add(sum_g, 0)
                low_part(g, 1, b)
                message(g, 3, b, use[0])
                if sum_g is not None:
                    add(sum_g, 1)
                low_part(g, 2, b)
                low_part(g, 3, b)
                if sum_g is not None:
                    add(sum_g, 2)
                if has_next:
                    message(g + 1, 0, 1 - b, use[1])
                    message(g + 1, 1, 1 - b, use[1])
                if sum_g is not None:
                    add(sum_g, 3)
            for load in loads:
                load.wait(dve)
            for n in range(3):
                nc.vector.tensor_copy(W_high[n][:], W_raw[n]).then_inc(weights_split, 1)
            dve.wait_ge(weights_split, 3)
            for n in range(3):
                nc.vector.tensor_tensor(W_low[n][:], W_raw[n][0:64], W_high[n][0:64].bitcast(F32), ALU.subtract).then_inc(weights_split, 1)
            nc.vector.tensor_scalar(attr[:], attr[:], SILU_2MOM / 8, None, ALU.mult).then_inc(attr_ready, 1)
            dve.wait_ge(attr_ready, 1)
            nc.vector.memset(sums[:], 0.0).then_inc(added, 1)
            message(0, 0, 0, 1)
            message(0, 1, 0, 1)
            group(0, 0, (1, 1), None)
            group(1, 1, (1, 2), 0)
            with dve.Fori(1, groups // 2 - 1) as s:
                for b in range(2):
                    group(2 * s + b, b, (s + 1, s + 1 + b), 2 * s + b - 1)
            group(groups - 2, 0, (groups // 2, groups // 2), groups - 3)
            group(groups - 1, 1, (groups // 2, None), groups - 2, has_next=False)
            for m in range(TILES):
                add(groups - 1, m)
            for m in range(TILES):
                dve.wait_ge(kept, m + 1)
                nc.vector.tensor_copy(sums[:, m, BANK:2 * BANK], core.bank(4 + m))


def layer3_gnn(core, w):
    nc = core.nc
    with ExitStack() as local:
        core.open_pool(local, 4)

        def sb(name, shape):
            return local.enter_context(nc.sbuf_tensor("g3_" + name, shape, F32))
        attr, W1 = sb("attributes", [P, 4 * EDGE_TILES]), sb("mlp1", [8, P])
        W_raw = [core.exps[:, 0, 0:P], core.exps[:, 1, 0:P], core.scores[:, 2, :]]
        mlp_loads = []
        Wup, Wout = sb("Wup", [P, 2 * MUL]), sb("Wout", [P, 2, 2 * MUL])
        upT, up = core.section(2), core.section(3)
        sums = core.section(0, 4, BLOCKS * MUL)
        L = {}

        def issue(sp):
            L["up"] = core.load(sp, Wup[:], w["g3_Wup"])
            L["out"] = core.load(sp, Wout[:], weights(w["g3_Wout"]))
            for cols in (slice(0, 64), slice(64, P)):
                mlp_loads.append(core.load(sp, W1[:, cols], w["g3_mlp1"]))
                for rows in (slice(0, 64), slice(64, P)):
                    for n in range(2):
                        mlp_loads.append(core.load(sp, W_raw[n][rows, cols], w[f"g3_mlp{n + 2}"]))
            for rows in (slice(0, 64), slice(64, P)):
                mlp_loads.append(core.load(sp, W_raw[2][rows], w["g3_mlp4"]))
            mlp_loads.append(core.load(sp, attr[:], w["g3_attr"].rearrange("p t m -> p (t m)")))
        prepare(core, "g3", issue)

        def blocks(i, c):
            return core.xn[:, i, 0:MUL] if c == 0 else core.xn[:, i, MUL:].rearrange("p (u m) -> p m u", m=3)[:, c - 1, :]
        transpose_stage(core, "g3_turn", upT, blocks)
        products_stage(core, "g3_up",
                       [Tile([(P, c * MUL, (c + 1) * MUL, [(upT[:, c, i * P:(i + 1) * P], Wup[:, (c > 0) * MUL:(c > 0) * MUL + MUL])])
                              for c in range(4)], "V", [lambda: L["up"]]) for i in range(TILES)],
                       lambda t, e, ps, chain: nc.vector.tensor_scalar(up[:, t, :], ps, MUL ** -0.5, None, ALU.mult))
        table = nc.dram_tensor("node_table", (NODES, 4 * MUL), F32, kind="Internal").ap()
        with Stage(core, "g3_table") as st:
            stored = st.sem("table_stored")

            @st.block.sync
            def _(sp):
                sp.dma_start(table.rearrange("(i p) d -> p i d", p=P), up).then_inc(stored, 16)
                sp.wait_ge(stored, 16)
        edges_stage(core, w, table, sums, attr, W1, W_raw, mlp_loads)
        sumsT = core.section(2, BLOCKS, NODES)
        products_stage(core, "g3_turn_sums",
                       [Tile([(P, i * P, (i + 1) * P, [(sums[:, i, c * MUL:(c + 1) * MUL], None)]) for i in range(TILES)], "VA"[c % 2])
                        for c in range(BLOCKS)], lambda t, e, ps, chain: copy_out(nc, e, sumsT[:, t, :], ps))
        scale = 1.0 / (16.0 * 10.0)

        def finish(t, e, ps, chain):
            out = core.branches[:, t, :]
            nc.vector.tensor_scalar(out[:, 0:MUL], ps[:, 0:MUL], scale, None, ALU.mult)
            return nc.vector.tensor_scalar(out[:, MUL:].rearrange("p (u m) -> p m u", m=3), ps[:, MUL:].rearrange("p (m u) -> p m u", m=3),
                                           scale, None, ALU.mult)
        products_stage(core, "g3_out",
                       [Tile([(P, k * MUL, (k + 1) * MUL,
                               [(sumsT[:, 2 * k + c, i * P:(i + 1) * P], Wout[:, c, (k > 0) * MUL:(k > 0) * MUL + MUL]) for c in range(2)])
                              for k in range(4)], "V", [lambda: L["out"]]) for i in range(TILES)], finish)


FLOW_EPS = 1e-6


def flow_stage(core, q, k, v, kse, tmp, factor):
    nc = core.nc
    with ExitStack() as local, Stage(core, "m3_flow") as st:
        sink_in, source_out, sink, source = (local.enter_context(nc.sbuf_tensor(f"m3f_{n}", [P, 4, HEADS], F32))
                                             for n in ("sink_in", "source_out", "sink", "source"))
        total = local.enter_context(nc.sbuf_tensor("m3f_total", [P, HEADS], F32))
        sigmoids, column_sums = st.sem("sigmoids_ready"), st.sem("column_sums_ready")
        weighted, clipped, expd = st.sem("weighted_ready"), st.sem("clipped_ready"), st.sem("allocations_ready")
        chain = st.chain(nc.vector, "vector_chain")

        def over_rows(bank, x):
            return product(nc, core, bank, [(core.ones[:], x[:, i, :]) for i in range(TILES)])

        by_head = lambda x: x.rearrange("p i (h d) -> p (i h) d", h=HEADS)
        spread = lambda x: x[:].rearrange("p i h -> p (i h)").unsqueeze(2).to_broadcast([P, 4 * HEADS, HEAD])

        @st.block.scalar
        def _(act):
            nc.scalar.activation(q, q, ACT.Sigmoid).then_inc(sigmoids, 1)
            nc.scalar.activation(k, k, ACT.Sigmoid).then_inc(sigmoids, 1)
            act.wait_ge(clipped, 1)
            nc.scalar.activation(sink[:], sink[:], ACT.Sigmoid).then_inc(expd, 1)
            nc.scalar.activation(source[:], source[:], ACT.Exp).then_inc(expd, 1)

        @st.block.tensor
        def _(pe):
            pe.wait_ge(sigmoids, 1)
            over_rows(core.bank(0), q).then_inc(column_sums, 1)
            pe.wait_ge(sigmoids, 2)
            over_rows(core.bank(1), k).then_inc(column_sums, 1)
            pe.wait_ge(weighted, 1)
            over_rows(core.bank(2), tmp[0]).then_inc(column_sums, 1)
            pe.wait_ge(weighted, 2)
            over_rows(core.bank(3), tmp[1]).then_inc(column_sums, 1)
            pe.wait_ge(expd, 2)
            over_rows(core.bank(4)[:, 0:HEADS], source).then_inc(column_sums, 1)

        @st.block.vector
        def _(dve):
            def against(x, bank, dst):
                chain(nc.vector.tensor_scalar(kse, bank, FLOW_EPS, None, ALU.add))
                for i in range(TILES):
                    chain(nc.vector.scalar_tensor_tensor(out=core.branch_tmp[:, i, :], in0=x[:, i, :], scalar=FLOW_EPS, in1=kse,
                                                         op0=ALU.add, op1=ALU.mult))
                chain(nc.vector.tensor_reduce(dst[:].rearrange("p i h -> p (i h)"), by_head(core.branch_tmp), AXIS.X, ALU.add))
            dve.wait_ge(sigmoids, 2)
            dve.wait_ge(column_sums, 1)
            against(k, core.bank(0), source_out)
            dve.wait_ge(column_sums, 2)
            against(q, core.bank(1), sink_in)
            chain(nc.vector.reciprocal(source_out[:], source_out[:]))
            chain(nc.vector.reciprocal(sink_in[:], sink_in[:]))
            nc.vector.tensor_tensor(by_head(tmp[0]), by_head(k), spread(source_out), ALU.mult).then_inc(weighted, 1)
            nc.vector.tensor_tensor(by_head(tmp[1]), by_head(q), spread(sink_in), ALU.mult).then_inc(weighted, 1)
            dve.wait_ge(column_sums, 3)
            against(q, core.bank(2), sink)
            dve.wait_ge(column_sums, 4)
            against(k, core.bank(3), source)
            nc.vector.tensor_scalar(source[:], source[:], -1.0, 1.0, ALU.max, ALU.min).then_inc(clipped, 1)
            dve.wait_ge(expd, 1)
            chain(nc.vector.tensor_tensor(factor[:], sink_in[:], sink[:], ALU.mult))
            dve.wait_ge(column_sums, 5)
            chain(nc.vector.reciprocal(total[:], core.bank(4)[:, 0:HEADS]))
            chain(nc.vector.tensor_scalar(total[:], total[:], float(NODES), None, ALU.mult))
            chain(nc.vector.tensor_tensor(source[:], source[:], total[:].unsqueeze(1).to_broadcast([P, 4, HEADS]), ALU.mult))
            chain(nc.vector.tensor_tensor(by_head(v), by_head(v), spread(source), ALU.mult))


def layer3_mixer(core, w):
    nc = core.nc
    with ExitStack() as local:
        core.open_pool(local, 12)
        part = [core.section(j) for j in range(12)]
        Wq, Wk, Wv, Wo, W1, q, k, v, s0, s1 = part[0:10]
        W1, W2 = core.section(4, 4, 256), core.section(10, 2, DIM)
        core.branch_tmp = part[11]
        rows = local.enter_context(nc.sbuf_tensor("m3_rows", [P, 9, 512], F32))
        cols = local.enter_context(nc.sbuf_tensor("m3_cols", [P, 2], F32))
        factor = local.enter_context(nc.sbuf_tensor("m3_factor", [P, 4, HEADS], F32))
        L = {}

        def issue(sp):
            def load_rows(first, n):
                return core.load(sp, rows[:, first:first + n], w["m3_rows"][first:first + n].rearrange("(o r) n -> o r n", o=1).to_broadcast([P, n, 512]))
            L["norm_rows"] = load_rows(5, 2)
            for name, dst in (("Wq", Wq), ("Wk", Wk), ("Wv", Wv), ("Wo", Wo), ("W1", W1), ("W2", W2)):
                L[name] = core.load(sp, dst, weights(w["m3_" + name]))
                if name == "Wq":
                    L["rows"] = load_rows(0, 5)
            L["norm2_rows"] = load_rows(7, 2)
            L["cols"] = core.load(sp, cols[:], w["m3_cols"])
        norm_turn_stage(core, "m3_norm1", core.xn, s0, s1, scale=rows[:, 5, :], shift=rows[:, 6, :], issue=issue, params=[lambda: L["norm_rows"]])
        products_stage(core, "m3_qkv",
                       linear_tiles(s1, Wq, "V", [lambda: L["Wq"]]) + linear_tiles(s1, Wk, "V", [lambda: L["Wk"]])
                       + linear_tiles(s1, Wv, "V", [lambda: L["Wv"]]),
                       lambda t, e, ps, chain: nc.vector.tensor_tensor((q, k, v)[t // 4][:, t % 4, :], ps, rows[:, t // 4, :], ALU.add),
                       params=[lambda: L["rows"]])
        flow_stage(core, q, k, v, core.scores[:, 0, :], (s0, s1), factor)
        qT, mixed = Wq, Wk
        transpose_stage(core, "m3_turn_q", qT, rows_of(q))
        linear_attention(core, "m3", qT, k, v, mixed, factor=factor)
        transpose_stage(core, "m3_turn_mixed", s0, rows_of(mixed))

        def finish_attention(t, e, ps, chain):
            chain(nc.vector.tensor_tensor(q[:, t, :], ps, rows[:, 3, :], ALU.add))
            return nc.vector.tensor_tensor(q[:, t, :], q[:, t, :], core.xn[:, t, :], ALU.add)
        products_stage(core, "m3_attention_out", linear_tiles(s0, Wo, "V", [lambda: L["Wo"]]), finish_attention)
        norm_turn_stage(core, "m3_norm2", q, s0, s1, scale=rows[:, 7, :], shift=rows[:, 8, :], params=[lambda: L["norm2_rows"]])
        uT = v
        products_stage(core, "m3_up", turned_tiles(s1, W1, "A", [lambda: L["W1"]]),
                       lambda t, e, ps, chain: nc.scalar.activation(uT[:, t, :], ps, ACT.Gelu, bias=cols[:, t:t + 1]),
                       params=[lambda: L["cols"]])

        def finish(t, e, ps, chain):
            chain(nc.vector.tensor_tensor(k[:, t, :], ps, rows[:, 4, :], ALU.add))
            chain(nc.vector.tensor_tensor(k[:, t, :], k[:, t, :], q[:, t, :], ALU.add))
            return nc.vector.tensor_tensor(core.branches[:, t, :], core.branches[:, t, :], k[:, t, :], ALU.add)
        products_stage(core, "m3_down", linear_tiles(uT[:, 0:2], W2, "V", [lambda: L["W2"]]), finish)


TOP = 128
PROCESS = 1024


def top_stage(core, acts, work, weights_out):
    nc = core.nc
    taken = -1.0e30
    with ExitStack() as local, Stage(core, "f3_top") as st:
        best, negmax, total = (local.enter_context(nc.sbuf_tensor(f"f3_{n}", [P, 4, s], F32))
                               for n, s in (("best", 8), ("negmax", 1), ("total", 1)))
        chain = st.chain(nc.vector, "vector_chain")
        maxima, expd = st.sem("maximum_ready"), st.sem("exp_ready")
        found, replaced = st.sem("eight_largest_found"), st.sem("eight_largest_replaced")

        @st.block.scalar
        def _(act):
            for i in range(TILES):
                act.wait_ge(maxima, i + 1)
                nc.scalar.activation(weights_out[:, i, :], acts[:, i, :], ACT.Exp, bias=negmax[:, i, :]).then_inc(expd, 1)

        @st.block.vector
        def _(dve):
            for r in range(TOP // 8):
                src = acts if r == 0 else work
                for i in range(TILES):
                    if r > 0:
                        dve.wait_ge(replaced, (r - 1) * TILES + i + 1)
                    nc.vector.max(best[:, i, :], src[:, i, :]).then_inc(found, 1)
                for i in range(TILES):
                    dve.wait_ge(found, r * TILES + i + 1)
                    if r == 0:
                        nc.vector.tensor_scalar(negmax[:, i, :], best[:, i, 0:1], -1.0, None, ALU.mult).then_inc(maxima, 1)
                    nc.vector.match_replace(work[:, i, :], best[:, i, :], src[:, i, :], taken).then_inc(replaced, 1)
            dve.wait_ge(replaced, TOP // 8 * TILES)
            for i in range(TILES):
                dve.wait_ge(expd, i + 1)
                chain(nc.vector.scalar_tensor_tensor(out=weights_out[:, i, :], in0=work[:, i, :], scalar=taken,
                                                     in1=weights_out[:, i, :], op0=ALU.is_equal, op1=ALU.mult))
                chain(nc.vector.tensor_reduce(total[:, i, :], weights_out[:, i, :], AXIS.X, ALU.add))
                chain(nc.vector.reciprocal(total[:, i, :], total[:, i, :]))
                chain(nc.vector.tensor_scalar(weights_out[:, i, :], weights_out[:, i, :], total[:, i, :], None, ALU.mult))


def layer3_ffn(core, w):
    nc = core.nc
    with ExitStack() as local:
        core.open_pool(local, 12)
        inT = core.section(0, 2, NODES)
        acts, work, attention = core.section(1, 4, PROCESS), core.section(3, 4, PROCESS), core.section(5, 4, PROCESS)
        attentionT = core.section(1, 8, NODES)
        ip, pw = core.section(7, 4, 256), core.section(8, 2, PROCESS)
        pv, ow, op = core.section(9, 8, 256), core.section(10, 2, 256), core.section(11, 2, DIM)
        aggT = core.section(3, 2, NODES)
        outT = core.section(4, 2, NODES)
        L = {}

        def issue(sp):
            for name, dst in (("ip", ip), ("pw", pw), ("pv", pv), ("ow", ow), ("op", op)):
                L[name] = core.load(sp, dst, weights(w["f3_" + name]))

        prepare(core, "f3", issue, add=core.branches)
        products_stage(core, "f3_in", turned_tiles(core.xnT, ip, "A", [lambda: L["ip"]]),
                       lambda t, e, ps, chain: nc.scalar.activation(inT[:, t, :], ps, ACT.Gelu))
        products_stage(core, "f3_process",
                       [Tile([(P, 0, 512, [(inT[:, c, i * P:(i + 1) * P], pw[:, c, n * 512:(n + 1) * 512]) for c in range(2)])], "A",
                             [lambda: L["pw"]]) for i in range(TILES) for n in range(2)],
                       lambda t, e, ps, chain: nc.scalar.activation(acts[:, t // 2, (t % 2) * 512:(t % 2 + 1) * 512], ps, ACT.Gelu))
        top_stage(core, acts, work, attention)
        products_stage(core, "f3_turn",
                       [Tile([(P, i * P, (i + 1) * P, [(attention[:, i, c * P:(c + 1) * P], None)]) for i in range(TILES)], "VA"[c % 2])
                        for c in range(8)], lambda t, e, ps, chain: copy_out(nc, e, attentionT[:, t, :], ps))
        products_stage(core, "f3_values", turned_tiles(attentionT, pv, "VA", [lambda: L["pv"]]),
                       lambda t, e, ps, chain: copy_out(nc, e, aggT[:, t, :], ps))
        products_stage(core, "f3_outputs", turned_tiles(aggT, ow, "A", [lambda: L["ow"]]),
                       lambda t, e, ps, chain: nc.scalar.activation(outT[:, t, :], ps, ACT.Gelu))
        products_stage(core, "f3_patterns", linear_tiles(outT, op, "V", [lambda: L["op"]]),
                       lambda t, e, ps, chain: nc.vector.tensor_tensor(core.x[:, t, :], ps, core.x[:, t, :], ALU.add))


def prepare(core, name, issue=None, add=None, also=None):
    norm_turn_stage(core, name + "_norm", core.x, core.xn, core.xnT, add=add, issue=issue, also=also)


def run_layers(core, w):
    for layer in range(4):
        GNN[layer](core, w)
        MIXER[layer](core, w)
        FFN[layer](core, w)


GNN = [layer0_gnn, layer1_gnn, layer2_gnn, layer3_gnn]
MIXER = [layer0_mixer, layer1_mixer, layer2_mixer, layer3_mixer]
FFN = [layer0_ffn, layer1_ffn, layer2_ffn, layer3_ffn]




def build(nc, w, out_dram):
    with ExitStack() as stack:
        core = Core(nc, stack)
        sb = core.sb
        core.x, core.xn, core.xnT = (sb(n, [P, 4, 512]) for n in ("x", "xn", "xnT"))
        core.branches = sb("branches", [P, 4, 512])
        core.edges_to, core.edges_from = sb("edges_to", [P, 4, 512]), sb("edges_from", [P, 4, 512])
        core.ident, core.ones, core.iota = sb("ident", [P, P]), sb("ones", [P, P]), sb("iota", [P, NODES])
        core.src_i, core.dst_i = sb("src_i", [P, EDGE_TILES], I32), sb("dst_i", [P, EDGE_TILES], I32)
        core.src_f, core.dst_f = sb("src_f", [P, EDGE_TILES]), sb("dst_f", [P, EDGE_TILES])
        core.stats, core.moments, core.deviation = sb("stats", [P, 4, 6]), sb("moments", [P, 4, 2]), sb("deviation", [P, 4, 3])
        core.scores, core.exps = (sb(n, [P, SCRATCHES, 512]) for n in ("scores", "exps"))
        core.iota_half = core.exps[:, 0, 0:NODES // 2].bitcast(F16)
        core.iota_i = core.scores[:, 0, :].bitcast(I32)
        core.sums, core.negmax = sb("sums", [P, 32]), sb("negmax", [P, 32])

        setup_stage(core, w["src"], w["dst"], w["x"])
        adjacency_stage(core)
        transpose_stage(core, "edges_from", core.edges_from, rows_of(core.edges_to))
        run_layers(core, w)
        store_stage(core, out_dram, core.x)


def columns(*vectors):
    return np.concatenate([np.reshape(v, (-1, P)).T for v in vectors], axis=1)


def row_pack(*vectors):
    return np.concatenate([np.reshape(v, (-1, DIM)) for v in vectors], axis=0)


def layout(a):
    g = a.__getitem__
    emb = np.concatenate([g("L0_gnn_edge_emb")] * HEADS)
    w = {
        "x": g("x"),
        "src": np.reshape(g("src"), (EDGE_TILES, P)).T, "dst": np.reshape(g("dst"), (EDGE_TILES, P)).T,
        "g0_WqT": g("L0_gnn_W_q").T, "g0_WkT": g("L0_gnn_W_k").T, "g0_WvT": g("L0_gnn_W_v").T,
        "g0_WeT": g("L0_gnn_W_e").T, "g0_WoT": g("L0_gnn_W_o").T,
        "g0_rows": row_pack(g("L0_gnn_b_v"), g("L0_gnn_b_e"), g("L0_gnn_edge_attn"), g("L0_gnn_b_o"),
                            g("L0_gnn_ln_g"), g("L0_gnn_ln_b")),
        "g0_cols": columns(g("L0_gnn_b_q"), g("L0_gnn_b_k"), emb),
        "m0_Wqkv": g("L0_mix_Wqkv"),
        "f0_Wg": g("L0_ffn_Wg"), "f0_bg": np.reshape(g("L0_ffn_bg"), (1, 8)),
        "f0_W1": g("L0_ffn_W1"), "f0_W3": g("L0_ffn_W3"), "f0_W2": g("L0_ffn_W2"),
        "g1_W": g("L1_gnn_W"), "g1_rows": row_pack(g("L1_gnn_b")),
        "m1_Wqkv": g("L1_mix_W_qkv"), "m1_Wout": g("L1_mix_W_out"), "m1_rows": row_pack(g("L1_mix_b_out")),
        "f1_Wg": g("L1_ffn_gate_w").T, "f1_bg": np.reshape(g("L1_ffn_biases"), (1, 8)),
        "f1_W1": np.concatenate([g("L1_ffn_w1"), g("L1_ffn_sw1")[None]]),
        "f1_W3": np.concatenate([g("L1_ffn_w3"), g("L1_ffn_sw3")[None]]),
        "f1_W2": np.concatenate([g("L1_ffn_w2"), g("L1_ffn_sw2")[None]]),
        "g2_Wq": g("L2_gnn_Wq"), "g2_Wk": g("L2_gnn_Wk"), "g2_Wv": g("L2_gnn_Wv"), "g2_Wskip": g("L2_gnn_Wskip"),
        "g2_Wlin": g("L2_gnn_Wlin"),
        "g2_rows": row_pack(g("L2_gnn_bv"), g("L2_gnn_blin"), g("L2_gnn_gamma"), g("L2_gnn_beta")),
        "g2_cols": columns(g("L2_gnn_bq"), g("L2_gnn_bk"), g("L2_gnn_bskip")),
        "m2_Wqkv": g("L2_mix_qkv_w").T, "m2_Wout": g("L2_mix_out_w").T,
        "m2_rows": row_pack(g("L2_mix_qkv_b")[DIM:], g("L2_mix_out_b"), g("L2_mix_ln_gamma"), g("L2_mix_ln_beta")),
        "m2_cols": columns(g("L2_mix_qkv_b")[:DIM]),
        "f2_Wg": g("L2_ffn_w_gating"), "f2_W1": g("L2_ffn_w1"), "f2_W2": g("L2_ffn_w2"),
        "g3_attr": np.reshape(g("edge_attr_4"), (EDGE_TILES, P, 4)).transpose(1, 0, 2),
        "g3_feat": g("edge_attr_8").T,
        "g3_Wup": np.concatenate([g("L3_gnn_W_up0"), g("L3_gnn_W_up1")], axis=1),
        "g3_mlp1": g("L3_gnn_W_mlp1"), "g3_mlp2": g("L3_gnn_W_mlp2"), "g3_mlp3": g("L3_gnn_W_mlp3"),
        "g3_mlp4": g("L3_gnn_W_mlp4"),
        "g3_Wout": np.concatenate([g("L3_gnn_W_out0"), g("L3_gnn_W_out1")], axis=1),
        "m3_Wq": g("L3_mix_Wq"), "m3_Wk": g("L3_mix_Wk"), "m3_Wv": g("L3_mix_Wv"), "m3_Wo": g("L3_mix_Wo"),
        "m3_W1": g("L3_mix_W1"), "m3_W2": g("L3_mix_W2"),
        "m3_rows": row_pack(*[g("L3_mix_" + n) for n in ("bq", "bk", "bv", "bo", "b2", "g1", "be1", "g2", "be2")]),
        "m3_cols": columns(g("L3_mix_b1")),
        "f3_ip": g("L3_ffn_input_patterns").T, "f3_pw": g("L3_ffn_process_input_weights").T,
        "f3_pv": g("L3_ffn_process_values"), "f3_ow": g("L3_ffn_output_input_weights").T,
        "f3_op": g("L3_ffn_output_patterns"),
    }
    return {name: np.ascontiguousarray(v) for name, v in w.items()}


def kernel(**inputs):
    import concourse.bacc as bacc
    from concourse.bass_utils import run_bass_kernel_spmd

    nc = bacc.Bacc("TRN2", target_bir_lowering=False, num_devices=1)
    arrays = layout({name: np.asarray(v) for name, v in inputs.items()})
    w = {name: nc.dram_tensor("in_" + name, v.shape, mybir.dt.from_np(v.dtype), kind="ExternalInput").ap()
         for name, v in arrays.items()}
    out = nc.dram_tensor("out", (NODES, DIM), F32, kind="ExternalOutput").ap()
    build(nc, w, out)
    r = run_bass_kernel_spmd(nc, [{"in_" + name: v for name, v in arrays.items()}], core_ids=[0])
    return r.results[0]["out"]
```
